# Optimizing a Trainium2 kernel written in Bass

```python
import numpy as np
import jax
import jax.numpy as jnp

def _softmax(x, axis=-1):
    return jax.nn.softmax(x, axis=axis)

def _gelu(x):
    return jax.nn.gelu(x, approximate=True)

def _silu(x):
    return jax.nn.silu(x)

def _sigmoid(x):
    return jax.nn.sigmoid(x)

def _layernorm(x, axis=-1, eps=1e-05):
    m = jnp.mean(x, axis=axis, keepdims=True)
    v = jnp.var(x, axis=axis, keepdims=True)
    return (x - m) / jnp.sqrt(v + eps)

def _scatter_add(tgt, idx, src, axis=0):
    return tgt.at[idx].add(src)

def _segment_sum(src, seg, n):
    return jax.ops.segment_sum(src, seg, n)
kernel_name = 'mk_prb_d4_jaxref_r8_b90dbd'

def setup_inputs(seed: int=0):
    np.random.seed(seed)
    _w = jnp.asarray

    def _L0_attn_setup():
        import jax, jax.numpy as jnp
        import numpy as np
        D_MODEL = 128
        N_HEADS = 16
        WINDOW = 128
        TOPK_RATIO = 0.25
        N_GLOBAL = 64
        B, N = (2, 256)
        key = jax.random.key(seed)
        ks = jax.random.split(key, 8)
        s = 0.02
        return {'x': jax.random.normal(ks[0], (B, N, D_MODEL), jnp.float32), 'Wq': jax.random.normal(ks[1], (D_MODEL, D_MODEL), jnp.float32) * s, 'bq': jnp.zeros((D_MODEL,), jnp.float32), 'Wk': jax.random.normal(ks[2], (D_MODEL, D_MODEL), jnp.float32) * s, 'bk': jnp.zeros((D_MODEL,), jnp.float32), 'Wv': jax.random.normal(ks[3], (D_MODEL, D_MODEL), jnp.float32) * s, 'bv': jnp.zeros((D_MODEL,), jnp.float32), 'Wo': jax.random.normal(ks[4], (D_MODEL, D_MODEL), jnp.float32) * s, 'bo': jnp.zeros((D_MODEL,), jnp.float32), 'Ws': jax.random.normal(ks[5], (N_HEADS, D_MODEL), jnp.float32) * s, 'bs': jnp.zeros((N_HEADS,), jnp.float32)}
    _L0_attn_in = _L0_attn_setup()

    def _L0_ffn_setup():
        import jax, jax.numpy as jnp
        import numpy as np
        D_MODEL = 128
        D_FF = 512
        N_EXPERTS = 8
        D_EXPERT = D_FF // N_EXPERTS
        TOP_K = 2
        LB_WEIGHT = 0.01
        B, S = (4, 256)

        def _top_k_softmax(logits, k):
            vals, _ = jax.lax.top_k(logits, k)
            thresh = vals[..., -1:]
            masked = jnp.where(logits >= thresh, logits, -jnp.inf)
            return jax.nn.softmax(masked, axis=-1)
        key = jax.random.key(seed)
        ks = jax.random.split(key, 8)
        x = jax.random.normal(ks[0], (B, S, D_MODEL), dtype=jnp.float32)
        w1 = jax.random.normal(ks[1], (N_EXPERTS, D_MODEL, D_EXPERT), dtype=jnp.float32) * (1.0 / np.sqrt(D_MODEL))
        b1 = jnp.zeros((N_EXPERTS, D_EXPERT), dtype=jnp.float32)
        w2 = jax.random.normal(ks[2], (N_EXPERTS, D_EXPERT, D_MODEL), dtype=jnp.float32) * (1.0 / np.sqrt(D_EXPERT))
        b2 = jnp.zeros((N_EXPERTS, D_MODEL), dtype=jnp.float32)
        centroids = jax.random.normal(ks[3], (N_EXPERTS, D_MODEL), dtype=jnp.float32) * 0.02
        w_route = jax.random.normal(ks[4], (N_EXPERTS, D_MODEL), dtype=jnp.float32) * (1.0 / np.sqrt(D_MODEL))
        return {'x': x, 'w1': w1, 'b1': b1, 'w2': w2, 'b2': b2, 'centroids': centroids, 'w_route': w_route}
    _L0_ffn_in = _L0_ffn_setup()

    def _L1_attn_setup():
        import jax, jax.numpy as jnp
        import numpy as np
        B, N, DIM_IN, DIM_INNER, DIM_OUT, WINDOW = (4, 512, 128, 128, 128, 128)
        key = jax.random.key(seed)
        k1, k2, k3, k4 = jax.random.split(key, 4)
        x = jax.random.normal(k1, (B, N, DIM_IN), dtype=jnp.float32)
        w_qkv = jax.random.normal(k2, (DIM_IN, 3 * DIM_INNER), dtype=jnp.float32) / np.sqrt(DIM_IN)
        w_out = jax.random.normal(k3, (DIM_INNER, DIM_OUT), dtype=jnp.float32) / np.sqrt(DIM_INNER)
        b_out = jax.random.normal(k4, (DIM_OUT,), dtype=jnp.float32) * 0.01
        return {'x': x, 'w_qkv': w_qkv, 'w_out': w_out, 'b_out': b_out}
    _L1_attn_in = _L1_attn_setup()

    def _L1_ffn_setup():
        import jax, jax.numpy as jnp
        import numpy as np
        D = 128
        E = 8
        key = jax.random.key(seed)
        ks = jax.random.split(key, 7)
        s = 1.0 / np.sqrt(D)
        x = jax.random.normal(ks[0], (4, 256, D), dtype=jnp.float32)
        Wg = jax.random.uniform(ks[1], (D, E), minval=-s, maxval=s, dtype=jnp.float32)
        bg = jax.random.uniform(ks[2], (E,), minval=-s, maxval=s, dtype=jnp.float32)
        W1 = jax.random.uniform(ks[3], (E, D, D), minval=-s, maxval=s, dtype=jnp.float32)
        b1 = jax.random.uniform(ks[4], (E, D), minval=-s, maxval=s, dtype=jnp.float32)
        W2 = jax.random.uniform(ks[5], (E, D, D), minval=-s, maxval=s, dtype=jnp.float32)
        b2 = jax.random.uniform(ks[6], (E, D), minval=-s, maxval=s, dtype=jnp.float32)
        return {'x': x, 'Wg': Wg, 'bg': bg, 'W1': W1, 'b1': b1, 'W2': W2, 'b2': b2}
    _L1_ffn_in = _L1_ffn_setup()

    def _L2_attn_setup():
        import jax, jax.numpy as jnp
        import numpy as np
        D = 128
        HS = 128
        NKV = 2

        def apply_rope(x):
            d = x.shape[-1]
            T = x.shape[-2]
            positions = jnp.arange(0, d, 2, dtype=jnp.float32)
            theta = 10000.0 ** (-2.0 * positions / d)
            angles = jnp.arange(T, dtype=jnp.float32)[:, None] * theta[None, :]
            cos, sin = (jnp.cos(angles), jnp.sin(angles))
            xr = x.reshape(x.shape[:-1] + (d // 2, 2))
            out = jnp.stack([xr[..., 0] * cos - xr[..., 1] * sin, xr[..., 1] * cos + xr[..., 0] * sin], axis=-1)
            return out.reshape(x.shape)
        key = jax.random.key(seed)
        k1, k2, k3, k4, k5 = jax.random.split(key, 5)
        B, T = (4, 256)
        x = jax.random.normal(k1, (B, T, D), dtype=jnp.float32)
        s = 1.0 / np.sqrt(D)
        Wq = jax.random.normal(k2, (NKV, HS, D), dtype=jnp.float32) * s
        Wk = jax.random.normal(k3, (HS, D), dtype=jnp.float32) * s
        Wv = jax.random.normal(k4, (HS, D), dtype=jnp.float32) * s
        Wo = jax.random.normal(k5, (D, NKV * HS), dtype=jnp.float32) * (1.0 / np.sqrt(NKV * HS))
        return {'x': x, 'Wq': Wq, 'Wk': Wk, 'Wv': Wv, 'Wo': Wo}
    _L2_attn_in = _L2_attn_setup()

    def _L2_ffn_setup():
        import jax, jax.numpy as jnp
        import numpy as np
        S, B, D = (128, 2, 128)
        E, TOPK = (15, 3)
        F = 128
        FS = 256

        def _uinit(k, shape, out_dim):
            std = out_dim ** (-0.5)
            return jax.random.uniform(k, shape, jnp.float32, -std, std)
        key = jax.random.key(seed)
        ks = jax.random.split(key, 10)
        return {'x': jax.random.normal(ks[0], (S, B, D), jnp.float32), 'gate_w': jax.random.normal(ks[1], (E, D), jnp.float32) * D ** (-0.5), 'fc1_w': _uinit(ks[2], (E, 2 * F, D), 2 * F), 'fc1_b': _uinit(ks[3], (E, 2 * F), 2 * F), 'geglu_mult': jnp.ones((E, F), jnp.float32), 'fc2_w': _uinit(ks[4], (E, D, F), D), 'fc2_b': _uinit(ks[5], (E, D), D), 's_fc1_w': _uinit(ks[6], (2 * FS, D), 2 * FS), 's_fc1_b': _uinit(ks[7], (2 * FS,), 2 * FS), 's_geglu_mult': jnp.ones((FS,), jnp.float32), 's_fc2_w': _uinit(ks[8], (D, FS), D), 's_fc2_b': _uinit(ks[9], (D,), D)}
    _L2_ffn_in = _L2_ffn_setup()

    def _L3_attn_setup():
        import jax, jax.numpy as jnp
        import numpy as np
        B, L, D, H, W = (2, 512, 128, 16, 128)
        E = D // H

        def _ln(x, g, b):
            m = jnp.mean(x, axis=-1, keepdims=True)
            v = jnp.mean((x - m) ** 2, axis=-1, keepdims=True)
            return (x - m) / jnp.sqrt(v + 1e-05) * g + b

        def _swa(xn, Wqkv, bqkv, Wp, bp):
            b_, l_, d_ = xn.shape
            nb = l_ // W
            qkv = xn @ Wqkv + bqkv
            q, k, v = jnp.split(qkv, 3, axis=-1)

            def heads(t):
                return t.reshape(b_, l_, H, E).transpose(0, 2, 1, 3)
            q, k, v = (heads(q), heads(k), heads(v))

            def blk(t):
                return t.reshape(b_, H, nb, W, E)
            qb, kb, vb = (blk(q), blk(k), blk(v))
            kprev = jnp.pad(kb, ((0, 0), (0, 0), (1, 0), (0, 0), (0, 0)))[:, :, :nb]
            vprev = jnp.pad(vb, ((0, 0), (0, 0), (1, 0), (0, 0), (0, 0)))[:, :, :nb]
            kc = jnp.concatenate([kprev, kb], axis=3)
            vc = jnp.concatenate([vprev, vb], axis=3)
            scores = jnp.einsum('bhnre,bhnse->bhnrs', qb, kc) / np.float32(np.sqrt(E))
            r = jnp.arange(W)[:, None]
            s = jnp.arange(2 * W)[None, :]
            band = (s >= r + 1) & (s <= r + W)
            first = band & (s >= W)
            mask = jnp.concatenate([first[None], jnp.broadcast_to(band, (nb - 1, W, 2 * W))], axis=0)
            scores = jnp.where(mask[None, None], scores, jnp.float32(-1e+30))
            attn = jax.nn.softmax(scores, axis=-1)
            out = jnp.einsum('bhnrs,bhnse->bhnre', attn, vc)
            out = out.reshape(b_, H, l_, E).transpose(0, 2, 1, 3).reshape(b_, l_, d_)
            return out @ Wp + bp

        def _linattn(xn, Wqkv, bqkv, Wo, bo):
            b_, l_, d_ = xn.shape
            C = 128
            nc = l_ // C
            qkv = xn @ Wqkv + bqkv
            q, k, v = jnp.split(qkv, 3, axis=-1)
            q = q.reshape(b_, l_, H, E)
            k = k.reshape(b_, l_, H, E)
            v = v.reshape(b_, l_, H, E)
            q = jax.nn.elu(q * np.float32(E ** (-0.5))) + np.float32(1.0001)
            k = jax.nn.elu(k) + np.float32(1.0001)

            def chunks(t):
                return t.reshape(b_, nc, C, H, E).transpose(1, 0, 3, 2, 4)
            qc, kc, vc = (chunks(q), chunks(k), chunks(v))
            tril = jnp.tril(jnp.ones((C, C), jnp.float32))

            def step(carry, inp):
                S, z = carry
                qi, ki, vi = inp
                A = jnp.einsum('bhce,bhde->bhcd', qi, ki) * tril
                num = jnp.einsum('bhce,bhef->bhcf', qi, S) + jnp.einsum('bhcd,bhdf->bhcf', A, vi)
                den = jnp.einsum('bhce,bhe->bhc', qi, z) + A.sum(-1)
                o = num / (den[..., None] + 1e-06)
                S = S + jnp.einsum('bhce,bhcf->bhef', ki, vi)
                z = z + ki.sum(2)
                return ((S, z), o)
            S0 = jnp.zeros((b_, H, E, E), jnp.float32)
            z0 = jnp.zeros((b_, H, E), jnp.float32)
            _, out = jax.lax.scan(step, (S0, z0), (qc, kc, vc))
            out = out.transpose(1, 0, 3, 2, 4).reshape(b_, l_, d_)
            return out @ Wo + bo
        key = jax.random.key(seed)
        ks = jax.random.split(key, 9)

        def w(k, shape, s=0.02):
            return jax.random.normal(k, shape, jnp.float32) * s
        return {'x': jax.random.normal(ks[0], (B, L, D), jnp.float32), 'g1': jnp.ones((D,), jnp.float32), 'b1': jnp.zeros((D,), jnp.float32), 'Wqkv_a': w(ks[1], (D, 3 * D)), 'bqkv_a': jnp.zeros((3 * D,), jnp.float32), 'Wp_a': w(ks[2], (D, D)), 'bp_a': jnp.zeros((D,), jnp.float32), 'Wqkv_s': w(ks[3], (D, 3 * D)), 'bqkv_s': jnp.zeros((3 * D,), jnp.float32), 'Wo_s': w(ks[4], (D, D)), 'bo_s': jnp.zeros((D,), jnp.float32), 'Wo': w(ks[5], (D, D)), 'bo': jnp.zeros((D,), jnp.float32), 'gm': jnp.ones((D,), jnp.float32), 'bm': jnp.zeros((D,), jnp.float32), 'W1': w(ks[6], (D, 4 * D)), 'b1m': jnp.zeros((4 * D,), jnp.float32), 'W2': w(ks[7], (4 * D, D)), 'b2m': jnp.zeros((D,), jnp.float32)}
    _L3_attn_in = _L3_attn_setup()

    def _L3_ffn_setup():
        import jax, jax.numpy as jnp
        import numpy as np
        MAX_VAL = 100.0
        key = jax.random.key(seed)
        k1, k2, k3 = jax.random.split(key, 3)
        B, S, D_IN, D_OUT = (4, 1024, 128, 128)
        x = jax.random.normal(k1, (B, S, D_IN), dtype=jnp.float32)
        weights = jax.random.normal(k2, (D_OUT, D_IN), dtype=jnp.float32)
        scale = jnp.ones((D_OUT,), dtype=jnp.float32)
        bias = jax.random.normal(k3, (D_OUT,), dtype=jnp.float32)
        return {'x': x, 'weights': weights, 'scale': scale, 'bias': bias}
    _L3_ffn_in = _L3_ffn_setup()
    _d = {'L0_attn_x': _L0_attn_in['x'], 'L0_attn_Wq': _L0_attn_in['Wq'], 'L0_attn_bq': _L0_attn_in['bq'], 'L0_attn_Wk': _L0_attn_in['Wk'], 'L0_attn_bk': _L0_attn_in['bk'], 'L0_attn_Wv': _L0_attn_in['Wv'], 'L0_attn_bv': _L0_attn_in['bv'], 'L0_attn_Wo': _L0_attn_in['Wo'], 'L0_attn_bo': _L0_attn_in['bo'], 'L0_attn_Ws': _L0_attn_in['Ws'], 'L0_attn_bs': _L0_attn_in['bs'], 'L0_ffn_w1': _L0_ffn_in['w1'], 'L0_ffn_b1': _L0_ffn_in['b1'], 'L0_ffn_w2': _L0_ffn_in['w2'], 'L0_ffn_b2': _L0_ffn_in['b2'], 'L0_ffn_centroids': _L0_ffn_in['centroids'], 'L0_ffn_w_route': _L0_ffn_in['w_route'], 'L1_attn_w_qkv': _L1_attn_in['w_qkv'], 'L1_attn_w_out': _L1_attn_in['w_out'], 'L1_attn_b_out': _L1_attn_in['b_out'], 'L1_ffn_Wg': _L1_ffn_in['Wg'], 'L1_ffn_bg': _L1_ffn_in['bg'], 'L1_ffn_W1': _L1_ffn_in['W1'], 'L1_ffn_b1': _L1_ffn_in['b1'], 'L1_ffn_W2': _L1_ffn_in['W2'], 'L1_ffn_b2': _L1_ffn_in['b2'], 'L2_attn_Wq': _L2_attn_in['Wq'], 'L2_attn_Wk': _L2_attn_in['Wk'], 'L2_attn_Wv': _L2_attn_in['Wv'], 'L2_attn_Wo': _L2_attn_in['Wo'], 'L2_ffn_gate_w': _L2_ffn_in['gate_w'], 'L2_ffn_fc1_w': _L2_ffn_in['fc1_w'], 'L2_ffn_fc1_b': _L2_ffn_in['fc1_b'], 'L2_ffn_geglu_mult': _L2_ffn_in['geglu_mult'], 'L2_ffn_fc2_w': _L2_ffn_in['fc2_w'], 'L2_ffn_fc2_b': _L2_ffn_in['fc2_b'], 'L2_ffn_s_fc1_w': _L2_ffn_in['s_fc1_w'], 'L2_ffn_s_fc1_b': _L2_ffn_in['s_fc1_b'], 'L2_ffn_s_geglu_mult': _L2_ffn_in['s_geglu_mult'], 'L2_ffn_s_fc2_w': _L2_ffn_in['s_fc2_w'], 'L2_ffn_s_fc2_b': _L2_ffn_in['s_fc2_b'], 'L3_attn_g1': _L3_attn_in['g1'], 'L3_attn_b1': _L3_attn_in['b1'], 'L3_attn_Wqkv_a': _L3_attn_in['Wqkv_a'], 'L3_attn_bqkv_a': _L3_attn_in['bqkv_a'], 'L3_attn_Wp_a': _L3_attn_in['Wp_a'], 'L3_attn_bp_a': _L3_attn_in['bp_a'], 'L3_attn_Wqkv_s': _L3_attn_in['Wqkv_s'], 'L3_attn_bqkv_s': _L3_attn_in['bqkv_s'], 'L3_attn_Wo_s': _L3_attn_in['Wo_s'], 'L3_attn_bo_s': _L3_attn_in['bo_s'], 'L3_attn_Wo': _L3_attn_in['Wo'], 'L3_attn_bo': _L3_attn_in['bo'], 'L3_attn_gm': _L3_attn_in['gm'], 'L3_attn_bm': _L3_attn_in['bm'], 'L3_attn_W1': _L3_attn_in['W1'], 'L3_attn_b1m': _L3_attn_in['b1m'], 'L3_attn_W2': _L3_attn_in['W2'], 'L3_attn_b2m': _L3_attn_in['b2m'], 'L3_ffn_weights': _L3_ffn_in['weights'], 'L3_ffn_scale': _L3_ffn_in['scale'], 'L3_ffn_bias': _L3_ffn_in['bias']}
    _x0 = _d['L0_attn_x']
    _d['L0_attn_x'] = jax.random.normal(jax.random.fold_in(jax.random.key(seed), 1), (4, 1024, 128), dtype=_x0.dtype)
    del _x0
    return _d

def reference(L0_attn_x, L0_attn_Wq, L0_attn_bq, L0_attn_Wk, L0_attn_bk, L0_attn_Wv, L0_attn_bv, L0_attn_Wo, L0_attn_bo, L0_attn_Ws, L0_attn_bs, L0_ffn_w1, L0_ffn_b1, L0_ffn_w2, L0_ffn_b2, L0_ffn_centroids, L0_ffn_w_route, L1_attn_w_qkv, L1_attn_w_out, L1_attn_b_out, L1_ffn_Wg, L1_ffn_bg, L1_ffn_W1, L1_ffn_b1, L1_ffn_W2, L1_ffn_b2, L2_attn_Wq, L2_attn_Wk, L2_attn_Wv, L2_attn_Wo, L2_ffn_gate_w, L2_ffn_fc1_w, L2_ffn_fc1_b, L2_ffn_geglu_mult, L2_ffn_fc2_w, L2_ffn_fc2_b, L2_ffn_s_fc1_w, L2_ffn_s_fc1_b, L2_ffn_s_geglu_mult, L2_ffn_s_fc2_w, L2_ffn_s_fc2_b, L3_attn_g1, L3_attn_b1, L3_attn_Wqkv_a, L3_attn_bqkv_a, L3_attn_Wp_a, L3_attn_bp_a, L3_attn_Wqkv_s, L3_attn_bqkv_s, L3_attn_Wo_s, L3_attn_bo_s, L3_attn_Wo, L3_attn_bo, L3_attn_gm, L3_attn_bm, L3_attn_W1, L3_attn_b1m, L3_attn_W2, L3_attn_b2m, L3_ffn_weights, L3_ffn_scale, L3_ffn_bias):

    def _L0_attn_ref(x, Wq, bq, Wk, bk, Wv, bv, Wo, bo, Ws, bs):
        import jax, jax.numpy as jnp
        import numpy as np
        D_MODEL = 128
        N_HEADS = 16
        WINDOW = 128
        TOPK_RATIO = 0.25
        N_GLOBAL = 64
        B, N = (2, 256)
        Bx, Nx, C = x.shape
        H, D = (N_HEADS, C // N_HEADS)
        scale = 1.0 / jnp.sqrt(jnp.asarray(D, x.dtype))

        def heads(t):
            return t.reshape(Bx, Nx, H, D).transpose(0, 2, 1, 3)
        q = heads(x @ Wq.T + bq)
        k = heads(x @ Wk.T + bk)
        v = heads(x @ Wv.T + bv)
        attn = jnp.einsum('bhnd,bhmd->bhnm', q, k) * scale
        idx = jnp.arange(Nx)
        band = jnp.abs(idx[:, None] - idx[None, :]) <= WINDOW
        attn = jnp.where(band[None, None], attn, -jnp.inf)
        local_out = jnp.einsum('bhnm,bhmd->bhnd', jax.nn.softmax(attn, axis=-1), v)
        k_tokens = max(int(Nx * TOPK_RATIO), 1)
        scores = (x @ Ws.T + bs).transpose(0, 2, 1)
        top_idx = jax.lax.top_k(scores, k_tokens)[1]
        gather = lambda t: jnp.take_along_axis(t, top_idx[..., None], axis=2)
        k_t, v_t = (gather(k), gather(v))
        attn_t = jnp.einsum('bhnd,bhkd->bhnk', q, k_t) * scale
        topk_out = jnp.einsum('bhnk,bhkd->bhnd', jax.nn.softmax(attn_t, axis=-1), v_t)
        k_g, v_g = (k[:, :, :N_GLOBAL], v[:, :, :N_GLOBAL])
        attn_g = jnp.einsum('bhnd,bhgd->bhng', q, k_g) * scale
        global_out = jnp.einsum('bhng,bhgd->bhnd', jax.nn.softmax(attn_g, axis=-1), v_g)
        out = (local_out + topk_out + global_out) / 3.0
        out = out.transpose(0, 2, 1, 3).reshape(Bx, Nx, C)
        return out @ Wo.T + bo

    def _L0_ffn_ref(x, w1, b1, w2, b2, centroids, w_route):
        import jax, jax.numpy as jnp
        import numpy as np
        D_MODEL = 128
        D_FF = 512
        N_EXPERTS = 8
        D_EXPERT = D_FF // N_EXPERTS
        TOP_K = 2
        LB_WEIGHT = 0.01
        B, S = (4, 256)

        def _top_k_softmax(logits, k):
            vals, _ = jax.lax.top_k(logits, k)
            thresh = vals[..., -1:]
            masked = jnp.where(logits >= thresh, logits, -jnp.inf)
            return jax.nn.softmax(masked, axis=-1)
        eps = 1e-12
        x_norm = x / jnp.maximum(jnp.linalg.norm(x, axis=-1, keepdims=True), eps)
        c_norm = centroids / jnp.maximum(jnp.linalg.norm(centroids, axis=-1, keepdims=True), eps)
        cos_scores = jnp.einsum('bsd,ed->bse', x_norm, c_norm)
        route_scores = jnp.einsum('bsd,ed->bse', x, w_route)
        logits = cos_scores + route_scores
        gates = _top_k_softmax(logits, TOP_K)
        h = jax.nn.gelu(jnp.einsum('bsd,edh->bseh', x, w1) + b1, approximate=False)
        expert_out = jnp.einsum('bseh,ehd->bsed', h, w2) + b2
        out = jnp.einsum('bse,bsed->bsd', gates, expert_out)
        return out

    def _L1_attn_ref(x, w_qkv, w_out, b_out):
        import jax, jax.numpy as jnp
        import numpy as np
        B, N, DIM_IN, DIM_INNER, DIM_OUT, WINDOW = (4, 512, 128, 128, 128, 128)
        b, n, _ = x.shape
        w = WINDOW
        scale = DIM_INNER ** (-0.5)
        qkv = jnp.einsum('bnd,de->bne', x, w_qkv)
        q, k, v = jnp.split(qkv, 3, axis=-1)
        nw = n // w
        win = lambda t: t.reshape(b, nw, w, DIM_INNER)
        q, k, v = (win(q), win(k), win(v))
        kp = jnp.pad(k, ((0, 0), (1, 0), (0, 0), (0, 0)))
        k2 = jnp.concatenate([kp[:, :-1], kp[:, 1:]], axis=2)
        v2 = k2
        sim = jnp.einsum('bwid,bwjd->bwij', q, k2) * scale
        i, j = (w, 2 * w)
        mask = jnp.triu(jnp.ones((i, j), dtype=bool), j - i + 1)
        mask_value = -jnp.finfo(sim.dtype).max
        sim = jnp.where(mask[None, None], mask_value, sim)
        attn = jax.nn.softmax(sim, axis=-1)
        out = jnp.einsum('bwij,bwjd->bwid', attn, v2)
        out = out.reshape(b, n, DIM_INNER)[:, :n]
        return jnp.einsum('bnd,de->bne', out, w_out) + b_out

    def _L1_ffn_ref(x, Wg, bg, W1, b1, W2, b2):
        import jax, jax.numpy as jnp
        import numpy as np
        D = 128
        E = 8
        N, T, d = x.shape
        x_flat = x.reshape(N * T, d)
        logits = x_flat @ Wg + bg
        probs = jax.nn.softmax(logits, axis=-1)
        assignments = jnp.argmax(probs, axis=-1)
        h = jnp.einsum('nd,edh->neh', x_flat, W1) + b1[None]
        h = jax.nn.gelu(h, approximate=False)
        eo = jnp.einsum('neh,ehd->ned', h, W2) + b2[None]
        selected = jnp.take_along_axis(eo, assignments[:, None, None], axis=1)[:, 0, :]
        w = jnp.take_along_axis(probs, assignments[:, None], axis=1)
        out = (w * selected).reshape(N, T, d)
        return out

    def _L2_attn_ref(x, Wq, Wk, Wv, Wo):
        import jax, jax.numpy as jnp
        import numpy as np
        D = 128
        HS = 128
        NKV = 2

        def apply_rope(x):
            d = x.shape[-1]
            T = x.shape[-2]
            positions = jnp.arange(0, d, 2, dtype=jnp.float32)
            theta = 10000.0 ** (-2.0 * positions / d)
            angles = jnp.arange(T, dtype=jnp.float32)[:, None] * theta[None, :]
            cos, sin = (jnp.cos(angles), jnp.sin(angles))
            xr = x.reshape(x.shape[:-1] + (d // 2, 2))
            out = jnp.stack([xr[..., 0] * cos - xr[..., 1] * sin, xr[..., 1] * cos + xr[..., 0] * sin], axis=-1)
            return out.reshape(x.shape)
        B, T, _ = x.shape
        k = apply_rope(x @ Wk.T)
        v = x @ Wv.T
        q = jnp.einsum('btd,hkd->bhtk', x, Wq)
        q = apply_rope(q)
        scale = HS ** (-0.5)
        scores = jnp.einsum('bhtk,bsk->bhts', q, k) * scale
        causal = jnp.tril(jnp.ones((T, T), dtype=bool))
        scores = jnp.where(causal, scores, -jnp.inf)
        w = jax.nn.softmax(scores, axis=-1)
        out = jnp.einsum('bhts,bsk->bhtk', w, v)
        out = out.transpose(0, 2, 1, 3).reshape(B, T, NKV * HS)
        return out @ Wo.T

    def _L2_ffn_ref(x, gate_w, fc1_w, fc1_b, geglu_mult, fc2_w, fc2_b, s_fc1_w, s_fc1_b, s_geglu_mult, s_fc2_w, s_fc2_b):
        import jax, jax.numpy as jnp
        import numpy as np
        S, B, D = (128, 2, 128)
        E, TOPK = (15, 3)
        F = 128
        FS = 256

        def _uinit(k, shape, out_dim):
            std = out_dim ** (-0.5)
            return jax.random.uniform(k, shape, jnp.float32, -std, std)
        s, b, d = x.shape
        xt = x.reshape(-1, d)
        T = xt.shape[0]
        logits = xt @ gate_w.T
        scores = jax.nn.softmax(logits, axis=-1)
        topk_w, topk_idx = jax.lax.top_k(scores, TOPK)
        topk_w = topk_w / (jnp.sum(topk_w, axis=-1, keepdims=True) + 1e-20)
        comb = jnp.zeros((T, E), xt.dtype).at[jnp.arange(T)[:, None], topk_idx].add(topk_w)
        h = jnp.einsum('td,efd->etf', xt, fc1_w) + fc1_b[:, None, :]
        xh, g = (h[..., :F], h[..., F:])
        a = jax.nn.gelu(g, approximate=False) * xh * geglu_mult[:, None, :]
        yexp = jnp.einsum('etf,edf->etd', a, fc2_w) + fc2_b[:, None, :]
        y = jnp.einsum('etd,te->td', yexp, comb)
        hs = xt @ s_fc1_w.T + s_fc1_b
        xs, gs = (hs[..., :FS], hs[..., FS:])
        as_ = jax.nn.gelu(gs, approximate=False) * xs * s_geglu_mult
        ys = as_ @ s_fc2_w.T + s_fc2_b
        return (y + ys).reshape(s, b, d)

    def _L3_attn_ref(x, g1, b1, Wqkv_a, bqkv_a, Wp_a, bp_a, Wqkv_s, bqkv_s, Wo_s, bo_s, Wo, bo, gm, bm, W1, b1m, W2, b2m):
        import jax, jax.numpy as jnp
        import numpy as np
        B, L, D, H, W = (2, 512, 128, 16, 128)
        E = D // H

        def _ln(x, g, b):
            m = jnp.mean(x, axis=-1, keepdims=True)
            v = jnp.mean((x - m) ** 2, axis=-1, keepdims=True)
            return (x - m) / jnp.sqrt(v + 1e-05) * g + b

        def _swa(xn, Wqkv, bqkv, Wp, bp):
            b_, l_, d_ = xn.shape
            nb = l_ // W
            qkv = xn @ Wqkv + bqkv
            q, k, v = jnp.split(qkv, 3, axis=-1)

            def heads(t):
                return t.reshape(b_, l_, H, E).transpose(0, 2, 1, 3)
            q, k, v = (heads(q), heads(k), heads(v))

            def blk(t):
                return t.reshape(b_, H, nb, W, E)
            qb, kb, vb = (blk(q), blk(k), blk(v))
            kprev = jnp.pad(kb, ((0, 0), (0, 0), (1, 0), (0, 0), (0, 0)))[:, :, :nb]
            vprev = jnp.pad(vb, ((0, 0), (0, 0), (1, 0), (0, 0), (0, 0)))[:, :, :nb]
            kc = jnp.concatenate([kprev, kb], axis=3)
            vc = jnp.concatenate([vprev, vb], axis=3)
            scores = jnp.einsum('bhnre,bhnse->bhnrs', qb, kc) / np.float32(np.sqrt(E))
            r = jnp.arange(W)[:, None]
            s = jnp.arange(2 * W)[None, :]
            band = (s >= r + 1) & (s <= r + W)
            first = band & (s >= W)
            mask = jnp.concatenate([first[None], jnp.broadcast_to(band, (nb - 1, W, 2 * W))], axis=0)
            scores = jnp.where(mask[None, None], scores, jnp.float32(-1e+30))
            attn = jax.nn.softmax(scores, axis=-1)
            out = jnp.einsum('bhnrs,bhnse->bhnre', attn, vc)
            out = out.reshape(b_, H, l_, E).transpose(0, 2, 1, 3).reshape(b_, l_, d_)
            return out @ Wp + bp

        def _linattn(xn, Wqkv, bqkv, Wo, bo):
            b_, l_, d_ = xn.shape
            C = 128
            nc = l_ // C
            qkv = xn @ Wqkv + bqkv
            q, k, v = jnp.split(qkv, 3, axis=-1)
            q = q.reshape(b_, l_, H, E)
            k = k.reshape(b_, l_, H, E)
            v = v.reshape(b_, l_, H, E)
            q = jax.nn.elu(q * np.float32(E ** (-0.5))) + np.float32(1.0001)
            k = jax.nn.elu(k) + np.float32(1.0001)

            def chunks(t):
                return t.reshape(b_, nc, C, H, E).transpose(1, 0, 3, 2, 4)
            qc, kc, vc = (chunks(q), chunks(k), chunks(v))
            tril = jnp.tril(jnp.ones((C, C), jnp.float32))

            def step(carry, inp):
                S, z = carry
                qi, ki, vi = inp
                A = jnp.einsum('bhce,bhde->bhcd', qi, ki) * tril
                num = jnp.einsum('bhce,bhef->bhcf', qi, S) + jnp.einsum('bhcd,bhdf->bhcf', A, vi)
                den = jnp.einsum('bhce,bhe->bhc', qi, z) + A.sum(-1)
                o = num / (den[..., None] + 1e-06)
                S = S + jnp.einsum('bhce,bhcf->bhef', ki, vi)
                z = z + ki.sum(2)
                return ((S, z), o)
            S0 = jnp.zeros((b_, H, E, E), jnp.float32)
            z0 = jnp.zeros((b_, H, E), jnp.float32)
            _, out = jax.lax.scan(step, (S0, z0), (qc, kc, vc))
            out = out.transpose(1, 0, 3, 2, 4).reshape(b_, l_, d_)
            return out @ Wo + bo
        xn = _ln(x, g1, b1)
        attn_out = _swa(xn, Wqkv_a, bqkv_a, Wp_a, bp_a)
        ssm_out = _linattn(xn, Wqkv_s, bqkv_s, Wo_s, bo_s)
        mixed = (attn_out + ssm_out) @ Wo + bo
        x1 = x + mixed
        h = _ln(x1, gm, bm)
        mlp = jax.nn.gelu(h @ W1 + b1m, approximate=False) @ W2 + b2m
        return x1 + mlp

    def _L3_ffn_ref(x, weights, scale, bias):
        import jax, jax.numpy as jnp
        import numpy as np
        MAX_VAL = 100.0
        w = (weights >= 0.0).astype(x.dtype) * 2.0 - 1.0
        y = jnp.einsum('bsi,oi->bso', x, w)
        y = y * scale + bias
        y = jnp.clip(y, -MAX_VAL, MAX_VAL)
        return y
    x = L0_attn_x
    xn = _layernorm(x, axis=-1)
    x = x + _L0_attn_ref(xn, L0_attn_Wq, L0_attn_bq, L0_attn_Wk, L0_attn_bk, L0_attn_Wv, L0_attn_bv, L0_attn_Wo, L0_attn_bo, L0_attn_Ws, L0_attn_bs) + _L0_ffn_ref(xn, L0_ffn_w1, L0_ffn_b1, L0_ffn_w2, L0_ffn_b2, L0_ffn_centroids, L0_ffn_w_route)
    xn = _layernorm(x, axis=-1)
    x = x + _L1_attn_ref(xn, L1_attn_w_qkv, L1_attn_w_out, L1_attn_b_out) + _L1_ffn_ref(xn, L1_ffn_Wg, L1_ffn_bg, L1_ffn_W1, L1_ffn_b1, L1_ffn_W2, L1_ffn_b2)
    xn = _layernorm(x, axis=-1)
    x = x + _L2_attn_ref(xn, L2_attn_Wq, L2_attn_Wk, L2_attn_Wv, L2_attn_Wo) + _L2_ffn_ref(xn, L2_ffn_gate_w, L2_ffn_fc1_w, L2_ffn_fc1_b, L2_ffn_geglu_mult, L2_ffn_fc2_w, L2_ffn_fc2_b, L2_ffn_s_fc1_w, L2_ffn_s_fc1_b, L2_ffn_s_geglu_mult, L2_ffn_s_fc2_w, L2_ffn_s_fc2_b)
    xn = _layernorm(x, axis=-1)
    x = x + _L3_attn_ref(xn, L3_attn_g1, L3_attn_b1, L3_attn_Wqkv_a, L3_attn_bqkv_a, L3_attn_Wp_a, L3_attn_bp_a, L3_attn_Wqkv_s, L3_attn_bqkv_s, L3_attn_Wo_s, L3_attn_bo_s, L3_attn_Wo, L3_attn_bo, L3_attn_gm, L3_attn_bm, L3_attn_W1, L3_attn_b1m, L3_attn_W2, L3_attn_b2m) + _L3_ffn_ref(xn, L3_ffn_weights, L3_ffn_scale, L3_ffn_bias)
    return x

_drawn_inputs = setup_inputs


def setup_inputs(seed=0):
    import zlib

    import numpy as np

    out = dict(_drawn_inputs(seed))
    spreads = {'L0_attn_bq': (0.0, 0.8),
     'L0_attn_bk': (0.0, 0.8),
     'L0_attn_bv': (0.0, 0.1),
     'L0_attn_bo': (0.0, 0.1),
     'L0_attn_bs': (0.0, 0.1),
     'L0_ffn_b1': (0.0, 0.1),
     'L0_ffn_b2': (0.0, 0.1),
     'L2_ffn_geglu_mult': (1.0, 0.6),
     'L2_ffn_s_geglu_mult': (1.0, 0.6),
     'L3_attn_g1': (1.0, 0.6),
     'L3_attn_b1': (0.0, 0.8),
     'L3_attn_bqkv_a': (0.0, 0.8),
     'L3_attn_bp_a': (0.0, 0.8),
     'L3_attn_bqkv_s': (0.0, 0.8),
     'L3_attn_bo_s': (0.0, 0.8),
     'L3_attn_bo': (0.0, 0.8),
     'L3_attn_gm': (1.0, 0.6),
     'L3_attn_bm': (0.0, 0.8),
     'L3_attn_b1m': (0.0, 0.8),
     'L3_attn_b2m': (0.0, 0.8),
     'L3_ffn_scale': (1.0, 0.2)}
    factors = {'L0_attn_Wq': 8.0,
     'L0_attn_Wk': 8.0,
     'L0_attn_Wv': 8.0,
     'L0_attn_Ws': 8.0,
     'L1_attn_b_out': 4.796,
     'L1_ffn_bg': 4.664,
     'L1_ffn_b1': 8.0,
     'L1_ffn_b2': 4.416,
     'L2_ffn_fc1_b': 8.0,
     'L2_ffn_s_fc1_b': 8.0,
     'L3_attn_Wqkv_a': 8.0,
     'L3_attn_Wp_a': 8.0,
     'L3_attn_Wqkv_s': 8.0,
     'L3_attn_Wo_s': 8.0,
     'L3_attn_Wo': 8.0,
     'L3_attn_W1': 8.0,
     'L3_attn_W2': 8.0}
    for name, (base, spread) in spreads.items():
        noise = np.random.default_rng([zlib.crc32(name.encode()), seed]).standard_normal(out[name].shape)
        drawn = base * np.exp(spread * noise) if base else spread * noise
        out[name] = jnp.asarray(drawn.astype(out[name].dtype))
    for name, factor in factors.items():
        out[name] = (out[name] * factor).astype(out[name].dtype)
    return out
```

```python
from contextlib import ExitStack

import numpy as np

import concourse.bass as bass
from concourse import mybir

F32 = mybir.dt.float32
BF16 = mybir.dt.bfloat16
ACT = mybir.ActivationFunctionType
ALU = mybir.AluOpType
AX = mybir.AxisListType.X

P = 128
B, N, D = 4, 1024, 128
T = B * N
NT = T // P
TPB = N // P
CH = 4
NC = NT // CH
CW = CH * P
H, E = 16, 8
HEADS = B * H
KQ = 9 * E
MROW = 96
NEG = -1.0e30
LOW = -3.0e38


class Ev:

    def __init__(self, sem, prime):
        self.sem, self.prime = sem, prime

    def at(self, i):
        return i + (self.prime + 1)


class Chain:

    def __init__(self, eng, sem):
        self.eng, self.sem, self.n, self.base = eng, sem, 0, 0

    def step(self, ins):
        ins.then_inc(self.sem, 1)
        self.n += 1

    def wait(self):
        self.eng.wait_ge(self.sem, self.base + self.n)

    def link(self, ins):
        self.step(ins)
        self.wait()


class Prog:

    def __init__(self, nc, dram, out):
        self.nc, self.d, self.out = nc, dram, out
        self.names = 0

        self.stage = []

    def sem(self, ctx, name):
        self.names += 1
        self.stage.append(self.nc.alloc_semaphore(f"{name}_{self.names}"))
        return self.stage[-1]

    def end(self):
        self.nc.clear_and_free_semaphores(self.stage)
        self.stage = []
        self.nc.all_engine_barrier()

    def ev(self, ctx, name, prime=0):
        return Ev(self.sem(ctx, name), prime)

    def sb(self, ctx, name, shape, dt=F32):
        self.names += 1
        return ctx.enter_context(self.nc.sbuf_tensor(f"{name}_{self.names}", shape, dt))


def hold(eng, gate, sem, value):
    eng.wait_ge(sem, value)
    eng.sem_inc(gate, 1)


def ds(i, n=1):
    return bass.ds(i, n)


def one(ap, i):
    s = ap[:, ds(i, 1)]
    names = "abcdef"[:len(s.shape) - 2]
    if len(s.shape) == 3:
        return s.rearrange("p o a -> p (o a)")
    return s.rearrange(f"p o {' '.join(names)} -> p (o {names[0]}) {' '.join(names[1:])}")


def bc(ap, n):
    return ap.unsqueeze(len(ap.shape)).broadcast_to([*ap.shape, n])


def load_constants(pr):
    nc, d = pr.nc, pr.d
    with ExitStack() as ctx:
        loaded = pr.sem(ctx, "loaded")
        with nc.Block() as block:
            @block.sync
            def _(sp):
                sp.dma_start(pr.X[:], d["x"].rearrange("p (t d) -> p t d", d=D)).then_inc(loaded, 16)
                sp.dma_start(pr.idf[:], d["ident_f"]).then_inc(loaded, 16)
                sp.dma_start(pr.idb[:], d["ident_b"]).then_inc(loaded, 16)
                sp.wait_ge(loaded, 48)


def statistics(pr, norm=False, of=None):
    nc = pr.nc
    of = pr.X if of is None else of
    with ExitStack() as ctx:
        stats = pr.sb(ctx, "stats", [P, CH, 6])
        mv = pr.sb(ctx, "mv", [P, CH, 2])
        var = pr.sb(ctx, "var", [P, NT])
        std = pr.sb(ctx, "std", [P, NT])
        ssq = pr.sb(ctx, "ssq", [P, NT])
        nrm = pr.sb(ctx, "nrm", [P, NT])
        dv = pr.sem(ctx, "dv")
        eps = pr.sb(ctx, "eps", [P, 1])
        var_done = pr.sem(ctx, "var_done")
        std_done = pr.sem(ctx, "std_done")
        with nc.Block() as block:
            @block.vector
            def _(v):
                v.memset(eps[:], 1e-5).then_inc(var_done, 1)
                per = CH + CH + 2
                with v.Fori(0, NC) as k:
                    c = Chain(v, dv)
                    c.base = k * per
                    for t in range(CH):
                        c.step(v.bn_stats(stats[:, t, :], one(of, k * CH + t)))
                    c.wait()
                    v.sem_inc(pr.gate_v, 1)
                    for t in range(CH):
                        c.step(v.bn_aggr(mv[:, t, :], stats[:, t, :]))
                    c.wait()
                    c.step(v.tensor_copy(pr.mean[:, ds(k * CH, CH)], mv[:, :, 0]))
                    c.step(v.tensor_copy(var[:, ds(k * CH, CH)], mv[:, :, 1]))
                v.wait_ge(dv, NC * per)
                v.sem_inc(var_done, 1)
                v.wait_ge(std_done, 1)
                v.reciprocal(pr.rstd[:], std[:]).then_inc(dv, 1)
                v.wait_ge(dv, NC * per + 1)
                if norm:
                    v.scalar_tensor_tensor(out=ssq[:], in0=var[:], scalar=float(D), in1=pr.rstd[:],
                                           op0=ALU.mult, op1=ALU.mult).then_inc(dv, 1)
                    v.wait_ge(dv, NC * per + 2)
                    v.tensor_tensor(ssq[:], ssq[:], pr.rstd[:], ALU.mult).then_inc(var_done, 1)
                    v.wait_ge(std_done, 2)
                    v.tensor_scalar(nrm[:], nrm[:], 1e-12, None, ALU.max).then_inc(dv, 1)
                    v.wait_ge(dv, NC * per + 3)
                    v.reciprocal(pr.inorm[:], nrm[:])

            @block.scalar
            def _(act):
                act.wait_ge(var_done, 2)
                nc.scalar.activation(std[:], var[:], ACT.Sqrt, bias=eps[:]).then_inc(std_done, 1)
                if norm:
                    act.wait_ge(var_done, 3)
                    nc.scalar.activation(nrm[:], ssq[:], ACT.Sqrt).then_inc(std_done, 1)




def split_rows(pr, ctx, name):
    return (pr.sb(ctx, name + "32", [P, 2, CW]), pr.sb(ctx, name + "_parts", [P, 2, 3, CW], BF16),
            pr.sb(ctx, name + "_rest", [P, CW]))


def l0_project(pr):
    nc, d = pr.nc, pr.d
    with ExitStack() as ctx:
        wq = pr.sb(ctx, "wq", [P, D])
        wk = pr.sb(ctx, "wk", [P, D])
        wkv = pr.sb(ctx, "wkv", [P, 2 * D])
        ws = pr.sb(ctx, "ws", [P, H])
        wroute = pr.sb(ctx, "wroute", [P, 16])
        cent = pr.sb(ctx, "cent", [8, D])
        cn2 = pr.sb(ctx, "cn2", [8, 1])
        csq = pr.sb(ctx, "csq", [8, D])
        bq = pr.sb(ctx, "bq", [P, 1])
        bk = pr.sb(ctx, "bk", [P, 1])
        bs = pr.sb(ctx, "bs", [H, 1])
        bkv = pr.sb(ctx, "bkv", [P, 2 * D])
        xnc = pr.sb(ctx, "xnc", [P, 2, CH, D])
        chunk = pr.sb(ctx, "chunk", [P, 2, CW])
        q32, qparts, qrest = split_rows(pr, ctx, "q")
        k32, kparts, krest = split_rows(pr, ctx, "k")
        kv32 = pr.sb(ctx, "kv32", [P, CH, 2 * D])
        kvrest = pr.sb(ctx, "kvrest", [P, CH, 2 * D])
        kvhalf = pr.sb(ctx, "kvhalf", [P, CH, 2 * D], BF16)
        srow = pr.sb(ctx, "srow", [H, 2, CW])
        loaded = pr.sem(ctx, "weights_loaded")
        dv = pr.sem(ctx, "dv_steps")
        pl = pr.sem(ctx, "pool_steps")
        setup = pr.sem(ctx, "centroids_steps")
        xn_ready = pr.ev(ctx, "xn_ready")
        turned = pr.ev(ctx, "xn_turned", 2)
        chunk_ready = pr.ev(ctx, "chunk_ready", 1)
        chunk_kept = pr.ev(ctx, "chunk_kept", 2)
        q_sum = pr.ev(ctx, "q_sum")
        k_sum = pr.ev(ctx, "k_sum")
        kv_sum = pr.ev(ctx, "kv_sum")
        s_sum = pr.ev(ctx, "s_sum")
        r_sum = pr.ev(ctx, "r_sum", 2)
        q_taken = pr.ev(ctx, "q_taken", 1)
        k_taken = pr.ev(ctx, "k_taken", 1)
        kv_taken = pr.ev(ctx, "kv_taken", 1)
        s_taken = pr.ev(ctx, "s_taken", 1)
        r_taken = pr.ev(ctx, "r_taken", 1)
        q_split = pr.ev(ctx, "q_split", 2)
        k_split = pr.ev(ctx, "k_split", 2)
        qk_stored = [pr.sem(ctx, f"qk_stored{u}") for u in range(2)]
        s_stored = [pr.sem(ctx, f"s_stored{u}") for u in range(2)]
        turn_ps, q_ps, k_ps, s_ps, r_ps = pr.ps[:, 0], pr.ps[:, 1], pr.ps[:, 2], pr.ps[:, 5], pr.ps[:, 6]
        kv_ps = pr.ps[:, 3:5]
        cent_ps = pr.ps[:, 7]
        WEIGHTS = 10 * 16

        def chunks(eng, body):
            with eng.Fori(0, NC // 2) as j:
                for u in range(2):
                    body(j * 2 + u, u, j)

        with nc.Block() as block:
            @block.sync
            def _(sp):
                for dst, src in ((wq, "wq"), (wk, "wk"), (wkv, "wkv"), (ws, "ws"), (cent, "cent"), (bq, "bq"),
                                 (bk, "bk"), (bs, "bs")):
                    sp.dma_start(dst[:], d[src]).then_inc(loaded, 16)
                sp.dma_start(bkv[:], d["bkv"].broadcast_to([P, 2 * D])).then_inc(loaded, 16)
                sp.dma_start(wroute[:, 0:8], d["wroute"]).then_inc(loaded, 16)
                for u in range(2):
                    sp.sem_inc(qk_stored[u], 32)
                    sp.sem_inc(s_stored[u], 16)

                def store(k, u, j):
                    sp.wait_ge(q_split.sem, q_split.at(k))
                    sp.dma_start(pr.q_dram[:, :, ds(u * CW, CW)].rearrange("a (b p) t -> b p a t", p=P)[ds(j, 1)]
                                 .rearrange("b p a t -> (b p) a t"), qparts[:, u]).then_inc(qk_stored[u], 16)
                    sp.wait_ge(k_split.sem, k_split.at(k))
                    sp.dma_start(pr.k_dram[:, :, ds(u * CW, CW)].rearrange("a (b p) t -> b p a t", p=P)[ds(j, 1)]
                                 .rearrange("b p a t -> (b p) a t"), kparts[:, u]).then_inc(qk_stored[u], 16)
                    sp.wait_ge(s_taken.sem, s_taken.at(k))
                    sp.dma_start(pr.s_dram.rearrange("(b h) t -> b h t", h=H)[ds(j, 1), :, u * CW:(u + 1) * CW]
                                 .rearrange("b h t -> (b h) t"), srow[:, u]).then_inc(s_stored[u], 16)

                chunks(sp, store)
                for u in range(2):
                    sp.wait_ge(qk_stored[u], 32 + 32 * NC // 2)
                    sp.wait_ge(s_stored[u], 16 + 16 * NC // 2)

            @block.gpsimd
            def _(pool):
                pool.sem_inc(chunk_kept.sem, 2)
                pool.sem_inc(q_split.sem, 2)
                pool.sem_inc(k_split.sem, 2)

                def part(k, u, j):
                    c = Chain(pool, pl)
                    c.base = k * 6
                    hold(pool, pr.gate_p, chunk_ready.sem, chunk_ready.at(k))
                    pool.tensor_copy(pr.xt[:, ds(k * CW, CW)], chunk[:, u]).then_inc(chunk_kept.sem, 1)
                    for taken, split, x32, parts, rest in ((q_taken, q_split, q32, qparts, qrest),
                                                           (k_taken, k_split, k32, kparts, krest)):
                        hold(pool, pr.gate_p, taken.sem, taken.at(k))
                        c.link(pool.tensor_tensor(rest[:], x32[:, u], parts[:, u, 0], ALU.subtract))
                        pool.sem_inc(pr.gate_p, 1)
                        c.link(pool.tensor_copy(parts[:, u, 1], rest[:]))
                        pool.sem_inc(pr.gate_p, 1)
                        c.step(pool.tensor_tensor(parts[:, u, 2], rest[:], parts[:, u, 1], ALU.subtract))
                        c.wait()
                        pool.sem_inc(split.sem, 1)

                chunks(pool, part)

            @block.vector
            def _(v):
                v.wait_ge(loaded, WEIGHTS)
                v.memset(pr.va[:, :, :, E:E + 1], 1.0).then_inc(dv, 1)
                v.tensor_tensor(csq[:], cent[:], cent[:], ALU.mult).then_inc(dv, 1)
                v.wait_ge(dv, 2)
                v.reduce_sum(cn2[:], csq[:], AX).then_inc(setup, 1)
                v.wait_ge(setup, 2)
                v.tensor_scalar(cn2[:], cn2[:], 1e-12, None, ALU.max).then_inc(dv, 1)
                v.wait_ge(dv, 3)
                v.reciprocal(cn2[:], cn2[:]).then_inc(dv, 1)
                v.wait_ge(dv, 4)
                v.tensor_scalar(cent[:], cent[:], cn2[:], None, ALU.mult).then_inc(setup, 1)
                v.wait_ge(setup, 4)
                v.tensor_copy(wroute[:, 8:16], cent_ps[:, 0:8]).then_inc(setup, 1)
                v.sem_inc(kv_taken.sem, 1)

                def part(k, u, j):
                    c = Chain(v, dv)
                    c.base = k * 10 + 4
                    v.wait_ge(turned.sem, turned.at(k - 2))
                    c.link(v.tensor_tensor(xnc[:, u], pr.X[:, ds(k * CH, CH), :], bc(pr.mean[:, ds(k * CH, CH)], D),
                                           ALU.subtract))
                    v.tensor_tensor(xnc[:, u], xnc[:, u], bc(pr.rstd[:, ds(k * CH, CH)], D),
                                    ALU.mult).then_inc(xn_ready.sem, 1)
                    v.wait_ge(kv_sum.sem, kv_sum.at(k))
                    c.step(v.tensor_tensor(kv32[:, 0:2], kv_ps[:, 0].rearrange("p (t c) -> p t c", t=2),
                                           bkv[:].unsqueeze(1).broadcast_to([P, 2, 2 * D]), ALU.add))
                    c.link(v.tensor_tensor(kv32[:, 2:4], kv_ps[:, 1].rearrange("p (t c) -> p t c", t=2),
                                           bkv[:].unsqueeze(1).broadcast_to([P, 2, 2 * D]), ALU.add))
                    v.sem_inc(kv_taken.sem, 1)
                    heads = kv32[:].rearrange("p t (h c) -> p h t c", c=2 * E)
                    c.step(v.tensor_copy(pr.va[:, ds(j * H, H), u * CH:(u + 1) * CH, 0:E], heads[:, :, :, E:2 * E]))
                    c.link(v.tensor_copy(kvhalf[:], kv32[:]))
                    c.step(v.tensor_tensor(kvrest[:], kv32[:], kvhalf[:], ALU.subtract))
                    pv = pr.kvp[:, ds(j * H, H), u * CH:(u + 1) * CH, :]
                    c.wait()
                    v.sem_inc(pr.gate_v, 1)
                    c.link(v.tensor_copy(pv[:, :, :, 0:16], kvhalf[:].rearrange("p t (h c) -> p h t c", c=16)))
                    c.link(v.tensor_copy(kvhalf[:], kvrest[:]))
                    v.sem_inc(pr.gate_v, 1)
                    c.step(v.tensor_copy(pv[:, :, :, 16:32], kvhalf[:].rearrange("p t (h c) -> p h t c", c=16)))
                    c.step(v.tensor_tensor(pv[:, :, :, 32:48], kvrest[:].rearrange("p t (h c) -> p h t c", c=16),
                                           kvhalf[:].rearrange("p t (h c) -> p h t c", c=16), ALU.subtract))
                    c.wait()
                    v.sem_inc(pr.gate_v, 1)
                    assert c.n == 10

                chunks(v, part)

            @block.scalar
            def _(act):
                act.wait_ge(setup, 1)
                nc.scalar.activation(cn2[:], cn2[:], ACT.Sqrt).then_inc(setup, 1)
                nc.scalar.preload_act_table(ACT.Identity)
                for e in (chunk_ready, q_taken, k_taken, s_taken, r_taken):
                    act.sem_inc(e.sem, 1)

                def part(k, u, j):
                    act.wait_ge(r_sum.sem, r_sum.at(k - 2))
                    act.wait_ge(chunk_kept.sem, chunk_kept.at(k - 2))
                    act.wait_ge(turned.sem, turned.at(k))
                    nc.scalar.activation(chunk[:, u], turn_ps, ACT.Copy).then_inc(chunk_ready.sem, 1)
                    act.wait_ge(qk_stored[u], j * 32 + 32)
                    for total, taken, split, ps, bias, x32, parts in (
                            (q_sum, q_taken, q_split, q_ps, bq, q32, qparts),
                            (k_sum, k_taken, k_split, k_ps, bk, k32, kparts)):
                        act.wait_ge(split.sem, split.at(k - 2))
                        act.wait_ge(total.sem, total.at(k))
                        nc.scalar.activation(x32[:, u], ps, ACT.Identity, bias=bias[:])
                        nc.scalar.activation(parts[:, u, 0], ps, ACT.Identity, bias=bias[:]).then_inc(taken.sem, 1)
                    act.wait_ge(s_stored[u], j * 16 + 16)
                    act.wait_ge(s_sum.sem, s_sum.at(k))
                    nc.scalar.activation(srow[:, u], s_ps[0:H], ACT.Identity, bias=bs[:]).then_inc(s_taken.sem, 1)
                    hold(act, pr.gate_a, r_sum.sem, r_sum.at(k))
                    nc.scalar.activation(pr.logits[:, ds(k * CH, CH), :],
                                         r_ps[:, 0:CH * 16].rearrange("p (t c) -> p t c", c=16),
                                         ACT.Copy).then_inc(r_taken.sem, 1)

                chunks(act, part)

            @block.tensor
            def _(pe):
                pe.wait_ge(loaded, WEIGHTS)
                pe.sem_inc(turned.sem, 2)
                pe.sem_inc(r_sum.sem, 2)
                pe.wait_ge(setup, 3)
                pe.transpose(cent_ps[:, 0:8], cent[:], pr.idf[0:8, 0:8]).then_inc(setup, 1)
                pe.wait_ge(setup, 5)

                def part(k, u, j):
                    pe.wait_ge(xn_ready.sem, xn_ready.at(k))
                    pe.wait_ge(chunk_ready.sem, chunk_ready.at(k - 1))
                    for t in range(CH):
                        mm = pe.transpose(turn_ps[:, t * P:(t + 1) * P], xnc[:, u, t], pr.idf[:])
                    mm.then_inc(turned.sem, 1)
                    pe.wait_ge(chunk_ready.sem, chunk_ready.at(k))
                    pe.wait_ge(q_taken.sem, q_taken.at(k - 1))
                    pe.matmul(q_ps, wq[:], chunk[:, u], start=True, stop=True).then_inc(q_sum.sem, 1)
                    pe.wait_ge(k_taken.sem, k_taken.at(k - 1))
                    pe.matmul(k_ps, wk[:], chunk[:, u], start=True, stop=True).then_inc(k_sum.sem, 1)
                    pe.wait_ge(kv_taken.sem, kv_taken.at(k - 1))
                    for t in range(CH):
                        mm = pe.matmul(kv_ps[:, t // 2, (t % 2) * 2 * D:(t % 2 + 1) * 2 * D],
                                       chunk[:, u, t * P:(t + 1) * P], wkv[:], start=True, stop=True)
                    mm.then_inc(kv_sum.sem, 1)
                    pe.wait_ge(s_taken.sem, s_taken.at(k - 1))
                    pe.matmul(s_ps[0:H], ws[:], chunk[:, u], start=True, stop=True).then_inc(s_sum.sem, 1)
                    pe.wait_ge(r_taken.sem, r_taken.at(k - 1))
                    for t in range(CH):
                        mm = pe.matmul(r_ps[:, t * 16:(t + 1) * 16], chunk[:, u, t * P:(t + 1) * P], wroute[:],
                                       start=True, stop=True)
                    mm.then_inc(r_sum.sem, 1)

                chunks(pe, part)


def l0_select(pr):
    nc, d = pr.nc, pr.d
    TOP = N // 4
    NE = 8
    with ExitStack() as ctx:
        s0 = pr.sb(ctx, "s0", [HEADS, N])
        s1 = pr.sb(ctx, "s1", [HEADS, N])
        ones = pr.sb(ctx, "ones", [HEADS, N])
        best = pr.sb(ctx, "best", [HEADS, 8])
        lg = pr.sb(ctx, "lg", [P, NT, NE])
        w8 = pr.sb(ctx, "w8", [P, NT, NE])
        w8b = pr.sb(ctx, "w8b", [P, NT, NE])
        m1 = pr.sb(ctx, "m1", [P, NT])
        m2 = pr.sb(ctx, "m2", [P, NT])
        cnt = pr.sb(ctx, "cnt", [P, NT])
        loaded = pr.sem(ctx, "scores_loaded")
        dv = pr.sem(ctx, "dv_steps")
        slots_ready = pr.sem(ctx, "slots_ready")
        slots_turned = pr.sem(ctx, "slots_turned")
        lg_ready = pr.sem(ctx, "lg_ready")
        exp_done = pr.sem(ctx, "exp_done")
        with nc.Block() as block:
            @block.sync
            def _(sp):
                sp.dma_start(s0[:], pr.s_dram).then_inc(loaded, 16)

            @block.vector
            def _(v):
                c = Chain(v, dv)
                c.link(v.tensor_tensor(w8[:], pr.logits[:, :, 8:16], bc(pr.inorm[:], NE), ALU.mult))
                c.link(v.tensor_tensor(lg[:], w8[:], pr.logits[:, :, 0:8], ALU.add))
                c.link(v.reduce_max(m1[:], lg[:], AX))
                v.tensor_tensor(w8[:], lg[:], bc(m1[:], NE), ALU.subtract).then_inc(lg_ready, 1)
                c.link(v.tensor_tensor(w8b[:], lg[:], bc(m1[:], NE), ALU.is_ge))
                c.link(v.reduce_sum(cnt[:], w8b[:], AX))
                c.link(v.scalar_tensor_tensor(out=w8b[:], in0=w8b[:], scalar=LOW, in1=lg[:], op0=ALU.mult,
                                              op1=ALU.add))
                c.link(v.reduce_max(m2[:], w8b[:], AX))
                c.link(v.tensor_scalar(cnt[:], cnt[:], 2.0, None, ALU.is_ge))
                c.link(v.tensor_tensor(m1[:], m1[:], cnt[:], ALU.mult))
                c.link(v.tensor_scalar(cnt[:], cnt[:], 1.0, -LOW, ALU.subtract, ALU.mult))
                c.link(v.tensor_tensor(m1[:], m1[:], cnt[:], ALU.add))
                c.link(v.tensor_tensor(m2[:], m2[:], m1[:], ALU.max))
                c.link(v.tensor_tensor(lg[:], lg[:], bc(m2[:], NE), ALU.is_ge))
                v.wait_ge(exp_done, 1)
                c.link(v.tensor_tensor(w8b[:], w8[:], lg[:], ALU.mult))
                c.link(v.reduce_sum(m1[:], w8b[:], AX))
                c.link(v.reciprocal(m2[:], m1[:]))
                c.link(v.tensor_tensor(pr.gates[:, :, 0:NE], w8b[:], bc(m2[:], NE), ALU.mult))
                v.wait_ge(loaded, 16)
                c.step(v.memset(ones[:], 1.0))
                c.link(v.tensor_copy(s1[:], s0[:]))
                for r in range(TOP // 8):
                    c.link(v.max(best[:], s1[:]))
                    c.link(v.match_replace(s1[:], best[:], s1[:], LOW))
                c.link(v.tensor_tensor(s1[:], s1[:], s0[:], ALU.not_equal))
                c.link(v.tensor_tensor_scan(s0[:], ones[:], s1[:], 0.0, ALU.mult, ALU.add))
                c.link(v.tensor_tensor(s0[:], s0[:], s1[:], ALU.mult))
                v.tensor_scalar(s0[:], s0[:], -1.0, None, ALU.add).then_inc(slots_ready, 1)
                v.wait_ge(slots_turned, 1)
                v.tensor_copy(pr.slot[:], pr.ps[:, 0].rearrange("p (t n) -> p n t", n=HEADS))

            @block.scalar
            def _(act):
                act.wait_ge(lg_ready, 1)
                nc.scalar.activation(w8[:], w8[:], ACT.Exp).then_inc(exp_done, 1)

            @block.tensor
            def _(pe):
                pe.wait_ge(slots_ready, 1)
                for t in range(TPB):
                    mm = pe.transpose(pr.ps[:, 0, t * HEADS:(t + 1) * HEADS], s0[:, t * P:(t + 1) * P],
                                      pr.idf[0:HEADS, 0:HEADS])
                mm.then_inc(slots_turned, 1)


def l0_attention(pr):
    nc, d = pr.nc, pr.d
    TOP, GLOB, V3 = N // 4, 64, 3
    SLOTS = TOP // P
    SCALE = float(E) ** -0.5
    KM = MROW + 2 * V3
    G_SEL, G_TURN, G_LOC, G_TOP, G_GLOB, G_MAX, NG = 0, 1, 2, 10, 14, 15, 16
    LG_TOP, LG_GLOB, NL = 4, 6, 7
    with ExitStack() as ctx:
        qst = [pr.sb(ctx, f"q_stack{u}", [P, N], BF16) for u in range(2)]
        kst = [pr.sb(ctx, f"k_stack{u}", [P, N], BF16) for u in range(2)]
        ksel = [pr.sb(ctx, f"k_selected{u}", [P, TOP], BF16) for u in range(2)]
        kglob = [pr.sb(ctx, f"k_global{u}", [P, GLOB], BF16) for u in range(2)]
        krep = pr.sb(ctx, "k_repeated", [P, SLOTS, KQ], BF16)
        vsel = [pr.sb(ctx, f"v_selected{u}", [P, SLOTS, E + 1]) for u in range(2)]
        hot = [pr.sb(ctx, f"one_hot{u}", [P, TPB, TOP], BF16) for u in range(2)]
        slot8 = pr.sb(ctx, "slot8", [P, TPB])
        places = pr.sb(ctx, "places", [P, TOP])
        mask = pr.sb(ctx, "band_mask", [P, 3 * P], BF16)
        mx = pr.sb(ctx, "maxima", [P, V3, TPB])
        mrow = [pr.sb(ctx, f"max_rows{u}", [P, TPB, KM], BF16) for u in range(2)]
        p_loc = pr.sb(ctx, "p_local", [P, TPB, 3 * P])
        p_top = pr.sb(ctx, "p_top", [P, SLOTS, N])
        p_glob = pr.sb(ctx, "p_global", [GLOB, N])
        rec = pr.sb(ctx, "rec", [P, TPB, V3])
        norm = pr.sb(ctx, "normed", [P, TPB, V3, E])
        zeroed = pr.sem(ctx, "zeroed")
        consts = pr.sem(ctx, "consts")
        stacks = [pr.sem(ctx, f"stacks{u}") for u in range(2)]
        first_part = pr.sem(ctx, "first_part")
        inverted = pr.sem(ctx, "inverted")
        psteps = pr.sem(ctx, "pool_steps")
        hot_ready = pr.ev(ctx, "hot_ready", 1)
        glob_ready = pr.ev(ctx, "glob_ready")
        scored = pr.ev(ctx, "scored_by_query", 2 * NG)
        reduced = pr.ev(ctx, "reduced", 2)
        rows_ready = pr.ev(ctx, "max_rows_ready")
        keyed = pr.ev(ctx, "scored_by_key", 2 * NL)
        exped = pr.ev(ctx, "exped", 2)
        summed = pr.ev(ctx, "values_summed")
        normed = pr.ev(ctx, "values_normed", 2)
        parts_q = pr.q_dram
        parts_k = pr.k_dram

        def heads(eng, first, step, last):
            first()
            with eng.Fori(0, HEADS // 2 - 1) as j:
                for u in range(2):
                    step(j * 2 + u, u)
            step(HEADS - 2, 0)
            last()

        def av_ps(u):
            return pr.ps[:, 6 + u, 0:TPB * V3 * (E + 1)].rearrange("p (t v c) -> p t v c", v=V3, c=E + 1)

        with nc.Block() as block:
            @block.sync
            def _(sp):
                sp.dma_start(mask[:], d["mask_band"]).then_inc(consts, 16)
                sp.dma_start(places[:], d["places"]).then_inc(consts, 16)
                sp.wait_ge(zeroed, 12)
                for u in range(2):
                    for v3, t in ((0, kst[u]), (1, ksel[u]), (2, kglob[u])):
                        sp.dma_start(t[MROW:KM, :], d["max_marks"][v3, :, 0:t.shape[1]]).then_inc(consts, 16)

                def load(n, u, j):
                    sp.wait_ge(keyed.sem, keyed.at((n - 2) * NL + NL - 1))
                    for a in range(3):
                        rows = slice(a * 3 * E, (a + 1) * 3 * E)
                        sp.dma_start(qst[u][rows],
                                     parts_q[:, ds(n * E, E), :]).then_inc(stacks[u], 16)
                        sp.dma_start(kst[u][rows],
                                     parts_k[a:a + 1, ds(n * E, E), :].broadcast_to([3, E, N])).then_inc(stacks[u], 16)

                with sp.Fori(0, HEADS // 2) as j:
                    for u in range(2):
                        load(j * 2 + u, u, j)

            @block.gpsimd
            def _(pool):
                for u in range(2):
                    for t in (qst[u], kst[u], ksel[u], kglob[u], mrow[u]):
                        pool.memset(t[:], 0.0).then_inc(zeroed, 1)
                    pool.memset(vsel[u][:], 1.0).then_inc(zeroed, 1)
                pool.wait_ge(consts, 16 * 8)
                pool.sem_inc(hot_ready.sem, 1)

                def one_hots(n, u, j):
                    c = Chain(pool, psteps)
                    c.base = n * 1
                    hold(pool, pr.gate_p, scored.sem, scored.at((n - 2) * NG + G_SEL))
                    hold(pool, pr.gate_p, hot_ready.sem, hot_ready.at(n - 1))
                    c.link(pool.tensor_copy(slot8[:], one(pr.slot, n)))
                    pool.sem_inc(pr.gate_p, 1)
                    for t in range(TPB):
                        ins = pool.tensor_scalar(hot[u][:, t], places[:], slot8[:, t:t + 1], None, ALU.is_equal)
                    ins.then_inc(hot_ready.sem, 1)
                    hold(pool, pr.gate_p, keyed.sem, keyed.at((n - 2) * NL + NL - 1))
                    hold(pool, pr.gate_p, stacks[u], j * 96 + 96)
                    pool.tensor_copy(kglob[u][0:KQ], kst[u][0:KQ, 0:GLOB]).then_inc(glob_ready.sem, 1)

                with pool.Fori(0, HEADS // 2) as j:
                    for u in range(2):
                        one_hots(j * 2 + u, u, j)

            @block.vector
            def _(v):
                v.sem_inc(reduced.sem, 2)
                v.sem_inc(normed.sem, 2)
                v.wait_ge(zeroed, 12)

                def take(n, u, g):
                    v.wait_ge(scored.sem, scored.at(n * NG + g))
                    return pr.ps[:, g % 2]

                def maxima(n, u):
                    ps = take(n, u, G_SEL)
                    sel = ps[:, 0:SLOTS * 48].rearrange("p (s a c) -> p s a c", s=SLOTS, a=3)
                    for s in range(SLOTS):
                        v.tensor_copy(krep[:, s].rearrange("p (a i e) -> p a i e", a=3, i=3),
                                      sel[:, s, :, 0:E].unsqueeze(2).broadcast_to([P, 3, 3, E]))
                    v.tensor_reduce(vsel[u][:, :, 0:E], sel[:, :, :, E:2 * E].rearrange("p s a e -> p s e a"),
                                    AX, ALU.add).then_inc(reduced.sem, 1)
                    ps = take(n, u, G_TURN)
                    v.tensor_copy(ksel[u][0:KQ], ps[0:KQ, 0:TOP // 2].bitcast(BF16)).then_inc(reduced.sem, 1)
                    for t in range(TPB):
                        ps = take(n, u, G_LOC + t)
                        lo, hi = (P if t == 0 else 0), (2 * P if t == TPB - 1 else 3 * P)
                        v.reduce_max(mx[:, 0, t:t + 1], ps[:, lo:hi], AX).then_inc(reduced.sem, 1)
                    for t in range(0, TPB, 2):
                        ps = take(n, u, G_TOP + t // 2)
                        v.reduce_max(mx[:, 1, t:t + 2], ps.rearrange("p (t k) -> p t k", t=2),
                                     AX).then_inc(reduced.sem, 1)
                    ps = take(n, u, G_GLOB)
                    v.reduce_max(mx[:, 2, :], ps.rearrange("p (t k) -> p t k", t=TPB), AX).then_inc(reduced.sem, 1)
                    v.wait_ge(reduced.sem, reduced.at(n * NG + G_GLOB))
                    first = mrow[u][:, :, MROW:MROW + V3].rearrange("p t v -> p v t")
                    second = mrow[u][:, :, MROW + V3:KM].rearrange("p t v -> p v t")
                    v.tensor_scalar(first, mx[:], -1.0, None, ALU.mult).then_inc(first_part, 1)
                    v.wait_ge(first_part, n + 1)
                    v.scalar_tensor_tensor(out=second, in0=mx[:], scalar=-1.0, in1=first, op0=ALU.mult,
                                           op1=ALU.subtract).then_inc(rows_ready.sem, 1)
                    ps = take(n, u, G_MAX)
                    v.tensor_copy(qst[u][MROW:KM], ps[MROW:KM].bitcast(BF16)).then_inc(reduced.sem, 1)

                def normalise(n, u):
                    v.wait_ge(summed.sem, summed.at(n))
                    sums = av_ps(u)
                    v.reciprocal(rec[:], sums[:, :, :, E]).then_inc(inverted, 1)
                    v.wait_ge(inverted, n * 2 + 1)
                    v.tensor_tensor(norm[:], sums[:, :, :, 0:E], bc(rec[:], E), ALU.mult).then_inc(normed.sem, 1)
                    hold(v, pr.gate_v, normed.sem, normed.at(n))
                    v.reduce_sum(one(pr.o, n), norm[:].rearrange("p t v e -> p t e v"), AX)\
                        .then_inc(inverted, 1)

                def step(n, u):
                    maxima(n + 1, 1 - u)
                    normalise(n, u)

                heads(v, lambda: maxima(0, 0), step, lambda: normalise(HEADS - 1, 1))

            @block.scalar
            def _(act):
                nc.scalar.preload_act_table(ACT.Exp)
                act.sem_inc(exped.sem, 2)

                def exps(n, u):
                    for g in range(NL):
                        i = u * NL + g
                        ps = pr.ps[:, 2 + 2 * (i % 2):4 + 2 * (i % 2)]
                        act.wait_ge(keyed.sem, keyed.at(n * NL + g))
                        if g < LG_TOP:
                            a, b = 2 * g, 2 * g + 1
                            if g == 0:
                                nc.scalar.activation(p_loc[:, a, P:], ps[:, 0, P:3 * P], ACT.Exp, scale=SCALE)
                                ins = nc.scalar.activation(p_loc[:, b], ps[:, 1, 0:3 * P], ACT.Exp, scale=SCALE)
                            elif g == LG_TOP - 1:
                                nc.scalar.activation(p_loc[:, a], ps[:, 0, 0:3 * P], ACT.Exp, scale=SCALE)
                                ins = nc.scalar.activation(p_loc[:, b, 0:2 * P], ps[:, 1, 0:2 * P], ACT.Exp,
                                                           scale=SCALE)
                            else:
                                ins = nc.scalar.activation(p_loc[:, a:b + 1], ps[:, :, 0:3 * P], ACT.Exp, scale=SCALE)
                        elif g < LG_GLOB:
                            ins = nc.scalar.activation(p_top[:, g - LG_TOP].rearrange("p (a t) -> p a t", a=2), ps,
                                                       ACT.Exp, scale=SCALE)
                        else:
                            ins = nc.scalar.activation(p_glob[:].rearrange("p (a t) -> p a t", a=2), ps[0:GLOB],
                                                       ACT.Exp, scale=SCALE)
                        ins.then_inc(exped.sem, 1)

                with act.Fori(0, HEADS // 2) as j:
                    for u in range(2):
                        exps(j * 2 + u, u)

            @block.tensor
            def _(pe):
                pe.sem_inc(scored.sem, 2 * NG)
                pe.sem_inc(keyed.sem, 2 * NL)
                pe.wait_ge(consts, 16 * 8)
                pe.wait_ge(zeroed, 12)

                def query_group(n, u, g):
                    pe.wait_ge(reduced.sem, reduced.at(n * NG + g - 2))
                    ps = pr.ps[:, g % 2]
                    if g == G_SEL:
                        pe.wait_ge(hot_ready.sem, hot_ready.at(n))
                        for s in range(SLOTS):
                            for t in range(TPB):
                                mm = pe.matmul(ps[:, s * 48:(s + 1) * 48], hot[u][:, t, s * P:(s + 1) * P],
                                               one(pr.kvp, n)[:, t], start=t == 0, stop=t == TPB - 1)
                    elif g == G_TURN:
                        pe.wait_ge(reduced.sem, reduced.at(n * NG + G_SEL))
                        for s in range(SLOTS):
                            mm = pe.transpose(ps[0:KQ, s * 64:(s + 1) * 64].bitcast(BF16), krep[:, s], pr.idb[:])
                    elif g < G_TOP:
                        t = g - G_LOC
                        if t == 0:
                            pe.wait_ge(stacks[u], 96 * (n_half(n, u) + 1))
                        lo, hi = (P if t == 0 else 0), (2 * P if t == TPB - 1 else 3 * P)
                        pe.matmul(ps[:, lo:hi], qst[u][0:KQ, t * P:(t + 1) * P],
                                  kst[u][0:KQ, (t - 1) * P + lo:(t - 1) * P + hi], start=True, stop=False)
                        mm = pe.matmul(ps[:, lo:hi], pr.idb[:], mask[:, lo:hi], start=False, stop=True)
                    elif g < G_GLOB:
                        if g == G_TOP:
                            pe.wait_ge(reduced.sem, reduced.at(n * NG + G_TURN))
                        for i in range(2):
                            t = 2 * (g - G_TOP) + i
                            mm = pe.matmul(ps[:, i * TOP:(i + 1) * TOP], qst[u][0:KQ, t * P:(t + 1) * P],
                                           ksel[u][0:KQ, :], start=True, stop=True)
                    elif g == G_GLOB:
                        for t in range(TPB):
                            mm = pe.matmul(ps[:, t * GLOB:(t + 1) * GLOB], qst[u][0:KQ, t * P:(t + 1) * P],
                                           kst[u][0:KQ, 0:GLOB], start=True, stop=True)
                    else:
                        pe.wait_ge(rows_ready.sem, rows_ready.at(n))
                        for t in range(TPB):
                            mm = pe.transpose(ps[0:KM, t * 64:(t + 1) * 64].bitcast(BF16), mrow[u][:, t], pr.idb[:])
                    mm.then_inc(scored.sem, 1)

                def n_half(n, u):
                    return n // 2 if isinstance(n, int) else pr.half

                def key_group(n, u, g):
                    pe.wait_ge(exped.sem, exped.at(n * NL + g - 2))
                    if g == 0:
                        pe.wait_ge(reduced.sem, reduced.at(n * NG + G_MAX))
                    i = u * NL + g
                    ps = pr.ps[:, 2 + 2 * (i % 2):4 + 2 * (i % 2)]
                    if g < LG_TOP:
                        for i in range(2):
                            t = 2 * g + i
                            lo, hi = (P if t == 0 else 0), (2 * P if t == TPB - 1 else 3 * P)
                            pe.matmul(ps[:, i, lo:hi], kst[u][0:KM, t * P:(t + 1) * P],
                                      qst[u][0:KM, (t - 1) * P + lo:(t - 1) * P + hi], start=True, stop=False)
                            mm = pe.matmul(ps[:, i, lo:hi], pr.idb[:], mask[:, lo:hi], start=False, stop=True)
                    elif g < LG_GLOB:
                        for i in range(2):
                            mm = pe.matmul(ps[:, i], ksel[u][0:KM, (g - LG_TOP) * P:(g - LG_TOP + 1) * P],
                                           qst[u][0:KM, i * CW:(i + 1) * CW], start=True, stop=True)
                    else:
                        pe.wait_ge(glob_ready.sem, glob_ready.at(n))
                        for i in range(2):
                            mm = pe.matmul(ps[0:GLOB, i], kglob[u][0:KM, :], qst[u][0:KM, i * CW:(i + 1) * CW],
                                           start=True, stop=True)
                    mm.then_inc(keyed.sem, 1)

                def values(n, u, g):
                    if g == LG_TOP:
                        return
                    hold(pe, pr.gate_e, exped.sem, exped.at(n * NL + g))
                    sums = av_ps(u)
                    if g == 0:
                        pe.wait_ge(normed.sem, normed.at(n - 2))
                    if g < LG_TOP:
                        va = one(pr.va, n)
                        done = [[0], [1, 2], [3, 4], [5, 6, 7]][g]
                        for t in done:
                            keys = [k for k in (t - 1, t, t + 1) if 0 <= k < TPB]
                            for k in keys:
                                pe.matmul(sums[:, t, 0], p_loc[:, k, (t - k + 1) * P:(t - k + 2) * P], va[:, k],
                                          start=k == keys[0], stop=k == keys[-1])
                    elif g < LG_GLOB:
                        for t in range(TPB):
                            for s in range(SLOTS):
                                pe.matmul(sums[:, t, 1], p_top[:, s, t * P:(t + 1) * P], vsel[u][:, s],
                                          start=s == 0, stop=s == SLOTS - 1)
                    else:
                        va = one(pr.va, n)
                        for t in range(TPB):
                            mm = pe.matmul(sums[:, t, 2], p_glob[:, t * P:(t + 1) * P], va[0:GLOB, 0],
                                           start=True, stop=True)
                        mm.then_inc(summed.sem, 1)

                def step(n, u):
                    for g in range(NG):
                        if g % 2 == 0 and g // 2 < NL:
                            key_group(n, u, g // 2)
                        if n_next(n):
                            query_group(n + 1, 1 - u, g)
                        if g % 2 == 1 and 1 <= g // 2 <= NL:
                            values(n, u, g // 2 - 1)

                def n_next(n):
                    return not isinstance(n, int) or n + 1 < HEADS

                for g in range(NG):
                    query_group(0, 0, g)
                with pe.Fori(0, HEADS // 2 - 1) as j:
                    for u in range(2):
                        pr.half = j + u
                        step(j * 2 + u, u)
                step(HEADS - 2, 0)
                step(HEADS - 1, 1)


def out_project(pr, w_name, bias_name, scale):
    nc, d = pr.nc, pr.d
    with ExitStack() as ctx:
        wo = pr.sb(ctx, "wo", [P, D])
        bo = pr.sb(ctx, "bo", [1, D])
        ones = pr.sb(ctx, "ones", [1, P])
        oc = pr.sb(ctx, "o_chunk", [P, 2, CH, H, E])
        ot = pr.sb(ctx, "o_turned", [P, 2, CW])
        loaded = pr.sem(ctx, "loaded")
        set_up = pr.sem(ctx, "set_up")
        gathered = pr.ev(ctx, "gathered")
        turned = pr.ev(ctx, "turned", 2)
        taken = pr.ev(ctx, "taken", 1)
        summed = pr.ev(ctx, "summed", 2)
        added = pr.ev(ctx, "added", 2)

        def chunks(eng, body):
            with eng.Fori(0, NC // 2) as j:
                for u in range(2):
                    body(j * 2 + u, u, j)

        with nc.Block() as block:
            @block.sync
            def _(sp):
                sp.dma_start(wo[:], d[w_name]).then_inc(loaded, 16)
                sp.dma_start(bo[:], d[bias_name]).then_inc(loaded, 16)

            @block.vector
            def _(v):
                v.memset(ones[:], 1.0).then_inc(set_up, 1)
                v.sem_inc(added.sem, 2)

                def part(k, u, j):
                    v.wait_ge(turned.sem, turned.at(k - 2))
                    v.tensor_scalar(oc[:, u].rearrange("p t h e -> p h t e"),
                                    pr.o[:, ds(j * H, H), u * CH:(u + 1) * CH, :], scale, None,
                                    ALU.mult).then_inc(gathered.sem, 1)
                    v.wait_ge(summed.sem, summed.at(k))
                    v.tensor_tensor(pr.X[:, ds(k * CH, CH), :], pr.X[:, ds(k * CH, CH), :],
                                    pr.ps[:, 2 + u].rearrange("p (t d) -> p t d", d=D), ALU.add).then_inc(added.sem, 1)

                chunks(v, part)

            @block.scalar
            def _(act):
                act.sem_inc(taken.sem, 1)

                def part(k, u, j):
                    act.wait_ge(summed.sem, summed.at(k - 2))
                    act.wait_ge(turned.sem, turned.at(k))
                    nc.scalar.activation(ot[:, u], pr.ps[:, 0], ACT.Copy).then_inc(taken.sem, 1)

                chunks(act, part)

            @block.tensor
            def _(pe):
                pe.sem_inc(turned.sem, 2)
                pe.sem_inc(summed.sem, 2)
                pe.wait_ge(loaded, 32)
                pe.wait_ge(set_up, 1)

                def part(k, u, j):
                    pe.wait_ge(taken.sem, taken.at(k - 1))
                    pe.wait_ge(gathered.sem, gathered.at(k))
                    for t in range(CH):
                        mm = pe.transpose(pr.ps[:, 0, t * P:(t + 1) * P], oc[:, u, t].rearrange("p h e -> p (h e)"),
                                          pr.idf[:])
                    mm.then_inc(turned.sem, 1)
                    pe.wait_ge(added.sem, added.at(k - 2))
                    pe.wait_ge(taken.sem, taken.at(k))
                    for t in range(CH):
                        s = pr.ps[:, 2 + u, t * D:(t + 1) * D]
                        pe.matmul(s, ot[:, u, t * P:(t + 1) * P], wo[:], start=True, stop=False)
                        mm = pe.matmul(s, ones[:], bo[:], start=False, stop=True)
                    mm.then_inc(summed.sem, 1)

                chunks(pe, part)


def experts(pr, name, ne, width, glu, nb=None):
    nc, d = pr.nc, pr.d
    UE = P // width
    NU = ne // UE
    nb = nb or ne
    with ExitStack() as ctx:
        w1 = pr.sb(ctx, "w1", [P, NU, (2 if glu else 1) * P])
        b1 = pr.sb(ctx, "b1", [P, NU, 2 if glu else 1])
        w2 = pr.sb(ctx, "w2", [P, NU, D])
        b2 = pr.sb(ctx, "b2", [nb, D])
        mult = pr.sb(ctx, "mult", [P, NU]) if glu else None
        gc = pr.sb(ctx, "gates_chunk", [P, 2, CH, nb])
        gt = pr.sb(ctx, "gates_turned", [nb, 2, CW])
        hid = pr.sb(ctx, "hidden", [P, 2, CW])
        gel = pr.sb(ctx, "gelu", [P, 2, CW]) if glu else None
        acc = pr.sb(ctx, "sums", [P, 2, CH, D])
        loaded = pr.sem(ctx, "weights_loaded")
        scaled = pr.sem(ctx, "w2_scaled")
        gates_ready = pr.ev(ctx, "gates_ready")
        gates_turned = pr.ev(ctx, "gates_turned")
        gates_kept = pr.ev(ctx, "gates_kept", 1)
        bias_sum = pr.ev(ctx, "bias_sum")
        acc_ready = pr.ev(ctx, "acc_ready", 1)
        h_sum = pr.ev(ctx, "h_sum")
        gelu_done = pr.ev(ctx, "gelu_done", 2)
        hidden_ready = pr.ev(ctx, "hidden_ready", 2) if glu else gelu_done
        y_sum = pr.ev(ctx, "y_sum", 2 * ne)
        y_added = pr.ev(ctx, "y_added", 2 * ne)
        x_added = pr.ev(ctx, "x_added", 2)

        def chunks(eng, body):
            with eng.Fori(0, NC // 2) as j:
                for u in range(2):
                    body(j * 2 + u, u)

        def h_ps(i):
            return pr.ps[:, i % 2]

        def g_ps(i):
            return pr.ps[:, 2 + i % 2]

        with nc.Block() as block:
            @block.sync
            def _(sp):
                sp.dma_start(w1[:], d[name + "_w1"]).then_inc(loaded, 16)
                sp.dma_start(b1[:], d[name + "_b1"]).then_inc(loaded, 16)
                sp.dma_start(w2[:], d[name + "_w2"]).then_inc(loaded, 16)
                sp.dma_start(b2[:], d[name + "_b2"]).then_inc(loaded, 16)
                if glu:
                    sp.dma_start(mult[:], d[name + "_mult"]).then_inc(loaded, 16)

            @block.gpsimd
            def _(pool):
                pool.sem_inc(x_added.sem, 2)

                def add(k, u):
                    hold(pool, pr.gate_p, y_added.sem, y_added.at(k * ne + ne - 1))
                    pool.tensor_tensor(pr.X[:, ds(k * CH, CH), :], pr.X[:, ds(k * CH, CH), :], acc[:, u],
                                       ALU.add).then_inc(x_added.sem, 1)

                chunks(pool, add)

            @block.vector
            def _(v):
                v.wait_ge(loaded, 16 * (5 if glu else 4))
                if glu:
                    v.tensor_tensor(w2[:], w2[:], bc(mult[:], D), ALU.mult).then_inc(scaled, 1)
                    v.sem_inc(hidden_ready.sem, 2)
                v.sem_inc(y_added.sem, 2 * ne)

                def gate_hidden(k, u, i):
                    v.wait_ge(y_sum.sem, y_sum.at(k * ne + i - 2))
                    v.wait_ge(gelu_done.sem, gelu_done.at(k * NU + i))
                    n = u * NU + i
                    v.scalar_tensor_tensor(out=hid[:, n % 2], in0=h_ps(n), scalar=b1[:, i, 0:1],
                                           in1=gel[:, n % 2], op0=ALU.add, op1=ALU.mult)\
                        .then_inc(hidden_ready.sem, 1)

                def part(k, u):
                    if glu:
                        gate_hidden(k, u, 0)
                    v.wait_ge(acc_ready.sem, acc_ready.at(k))
                    for e in range(ne):
                        if glu and e + 1 < ne:
                            gate_hidden(k, u, e + 1)
                        n = u * ne + e
                        v.wait_ge(y_added.sem, y_added.at(k * ne + e - 1))
                        v.wait_ge(y_sum.sem, y_sum.at(k * ne + e))
                        for t in range(CH):
                            ins = v.scalar_tensor_tensor(out=acc[:, u, t], in0=pr.ps[:, 4 + n % 2, t * D:(t + 1) * D],
                                                         scalar=gc[:, u, t, e:e + 1], in1=acc[:, u, t],
                                                         op0=ALU.mult, op1=ALU.add)
                        ins.then_inc(y_added.sem, 1)

                chunks(v, part)

            @block.scalar
            def _(act):
                nc.scalar.preload_act_table(ACT.Gelu)
                act.sem_inc(gates_kept.sem, 1)
                act.sem_inc(acc_ready.sem, 1)
                act.sem_inc(gelu_done.sem, 2)
                act.wait_ge(loaded, 16 * (5 if glu else 4))

                def part(k, u):
                    hold(act, pr.gate_a, y_added.sem, y_added.at((k - 2) * ne + ne - 1))
                    nc.scalar.activation(gc[:, u], pr.gates[:, ds(k * CH, CH), 0:nb], ACT.Copy)\
                        .then_inc(gates_ready.sem, 1)
                    act.wait_ge(gates_turned.sem, gates_turned.at(k))
                    nc.scalar.activation(gt[:, u], pr.ps[0:nb, 6], ACT.Copy).then_inc(gates_kept.sem, 1)
                    act.wait_ge(bias_sum.sem, bias_sum.at(k))
                    act.wait_ge(x_added.sem, x_added.at(k - 2))
                    nc.scalar.activation(acc[:, u], pr.ps[:, 7].rearrange("p (t d) -> p t d", d=D), ACT.Copy)\
                        .then_inc(acc_ready.sem, 1)
                    for i in range(NU):
                        n = u * NU + i
                        act.wait_ge(y_sum.sem, y_sum.at(k * ne + (i - 2) * UE + UE - 1))
                        act.wait_ge(h_sum.sem, h_sum.at(k * NU + i))
                        if glu:
                            act.wait_ge(hidden_ready.sem, hidden_ready.at(k * NU + i - 2))
                        nc.scalar.activation(gel[:, n % 2] if glu else hid[:, n % 2], g_ps(n) if glu else h_ps(n),
                                             ACT.Gelu, bias=b1[:, i, 1:2] if glu else b1[:, i, 0:1])\
                            .then_inc(gelu_done.sem, 1)

                chunks(act, part)

            @block.tensor
            def _(pe):
                pe.sem_inc(y_sum.sem, 2 * ne)
                pe.wait_ge(loaded, 16 * (5 if glu else 4))
                if glu:
                    pe.wait_ge(scaled, 1)

                def first(k, u, i):
                    n = u * NU + i
                    pe.wait_ge(gelu_done.sem, gelu_done.at(k * NU + i - 2))
                    if glu:
                        pe.wait_ge(hidden_ready.sem, hidden_ready.at(k * NU + i - 2))
                    x = pr.xt[:, ds(k * CW, CW)]
                    mm = pe.matmul(h_ps(n), w1[:, i, 0:P], x, start=True, stop=True)
                    if glu:
                        mm = pe.matmul(g_ps(n), w1[:, i, P:2 * P], x, start=True, stop=True)
                    mm.then_inc(h_sum.sem, 1)

                def second(k, u, i):
                    pe.wait_ge(hidden_ready.sem, hidden_ready.at(k * NU + i))
                    for s in range(UE):
                        n = u * ne + i * UE + s
                        r = slice(s * width, (s + 1) * width)
                        pe.wait_ge(y_added.sem, y_added.at(k * ne + i * UE + s - 2))
                        for t in range(CH):
                            mm = pe.matmul(pr.ps[:, 4 + n % 2, t * D:(t + 1) * D],
                                           hid[r, (u * NU + i) % 2, t * P:(t + 1) * P], w2[r, i], start=True, stop=True)
                        mm.then_inc(y_sum.sem, 1)

                def part(k, u):
                    first(k, u, 0)
                    pe.wait_ge(gates_ready.sem, gates_ready.at(k))
                    pe.wait_ge(gates_kept.sem, gates_kept.at(k - 1))
                    for t in range(CH):
                        mm = pe.transpose(pr.ps[0:nb, 6, t * P:(t + 1) * P], gc[:, u, t], pr.idf[:])
                    mm.then_inc(gates_turned.sem, 1)
                    if NU > 1:
                        first(k, u, 1)
                    pe.wait_ge(gates_kept.sem, gates_kept.at(k))
                    pe.wait_ge(acc_ready.sem, acc_ready.at(k - 1))
                    for t in range(CH):
                        mm = pe.matmul(pr.ps[:, 7, t * D:(t + 1) * D], gt[:, u, t * P:(t + 1) * P], b2[:],
                                       start=True, stop=True)
                    mm.then_inc(bias_sum.sem, 1)
                    for i in range(NU):
                        second(k, u, i)
                        if i + 2 < NU:
                            first(k, u, i + 2)

                chunks(pe, part)


def store_output(pr):
    nc = pr.nc
    with ExitStack() as ctx:
        stored = pr.sem(ctx, "stored")
        with nc.Block() as block:
            @block.sync
            def _(sp):
                sp.dma_start(pr.out.rearrange("p (t d) -> p t d", d=D), pr.X[:]).then_inc(stored, 16)
                sp.wait_ge(stored, 16)


def two_a_turn(eng, body):
    with eng.Fori(0, NC // 2) as j:
        for u in range(2):
            body(j * 2 + u, u, j)


def l1_attention(pr):
    nc, d = pr.nc, pr.d
    SCALE = float(D) ** -0.5
    with ExitStack() as ctx:
        wq, wk, wo = (pr.sb(ctx, n, [P, D]) for n in ("wq", "wk", "wo"))
        wroute = pr.sb(ctx, "wroute", [P, 8])
        mask = pr.sb(ctx, "causal_mask", [P, P], BF16)
        xnc = pr.sb(ctx, "xnc", [P, 2, CH, D])
        chunk = pr.sb(ctx, "chunk", [P, 2, CW])
        qt = pr.sb(ctx, "q_turned", [P, 2, CW])
        kt = pr.sb(ctx, "k_turned", [P, 2, P + CW])
        kn = pr.sb(ctx, "k_by_token", [P, 2, 1 + CH, D])
        mx = pr.sb(ctx, "mx", [P, 2, CH])
        nmx = pr.sb(ctx, "minus_mx", [P, 2, CH])
        sums = pr.sb(ctx, "sums", [P, 2, CH])
        rec = pr.sb(ctx, "rec", [P, 2, CH])
        prob = pr.sb(ctx, "prob", [P, 2, CH, 2 * P])
        pt = pr.sb(ctx, "prob_turned", [P, 2, CH, 2, P])
        ot = pr.sb(ctx, "out_turned", [P, 2, CW])
        loaded = pr.sem(ctx, "weights_loaded")
        zeroed = pr.sem(ctx, "zeroed")
        xn_sub = pr.ev(ctx, "xn_sub")
        xn_ready = pr.ev(ctx, "xn_ready")
        turned = pr.ev(ctx, "xn_turned", 2)
        chunk_ready = pr.ev(ctx, "chunk_ready", 1)
        chunk_kept = pr.ev(ctx, "chunk_kept", 2)
        q_sum, k_sum, kn_sum, r_sum = (pr.ev(ctx, n, 2) for n in ("q_sum", "k_sum", "kn_sum", "r_sum"))
        q_taken, k_taken, kn_taken, r_taken = (pr.ev(ctx, n, 1) for n in ("q_tak", "k_tak", "kn_tak", "r_tak"))
        k_passed = pr.ev(ctx, "k_passed", 1)
        scored = pr.ev(ctx, "scored", 2)
        maxed = pr.ev(ctx, "maxed")
        minus_ready = pr.ev(ctx, "minus_ready")
        exped = pr.ev(ctx, "exped", 2)
        p_turned = pr.ev(ctx, "p_turned", 4)
        p_taken = pr.ev(ctx, "p_taken", 2)
        o_sum = pr.ev(ctx, "o_sum", 2)
        o_taken = pr.ev(ctx, "o_taken", 1)
        y_sum = pr.ev(ctx, "y_sum", 2)
        y_added = pr.ev(ctx, "y_added", 1)
        rec_ready = pr.ev(ctx, "rec_ready")
        turn_ps, q_ps, k_ps, o_ps = (pr.ps[:, i] for i in range(4))
        s_ps = pr.ps[:, 4:6]
        pt_ps = pr.ps[:, 6:8]

        with nc.Block() as block:
            @block.sync
            def _(sp):
                for dst, src in ((wq, "l1_wq"), (wk, "l1_wk"), (wo, "l1_wo"), (wroute, "l1_wg"), (mask, "mask_causal")):
                    sp.dma_start(dst[:], d[src]).then_inc(loaded, 16)

            @block.gpsimd
            def _(pool):
                pool.memset(kt[:, 0, 0:P], 0.0).then_inc(zeroed, 1)
                pool.memset(kn[:, 0, 0], 0.0).then_inc(zeroed, 1)
                pool.sem_inc(chunk_kept.sem, 2)
                pool.sem_inc(k_passed.sem, 1)

                def part(k, u, j):
                    hold(pool, pr.gate_p, chunk_ready.sem, chunk_ready.at(k))
                    pool.tensor_copy(pr.xt[:, ds(k * CW, CW)], chunk[:, u]).then_inc(chunk_kept.sem, 1)
                    if u == 1:
                        hold(pool, pr.gate_p, o_sum.sem, o_sum.at(k - 2))
                        hold(pool, pr.gate_p, k_taken.sem, k_taken.at(k - 1))
                        pool.tensor_copy(kt[:, 1, 0:P], kt[:, 0, CW:]).then_inc(k_passed.sem, 1)
                        hold(pool, pr.gate_p, kn_taken.sem, kn_taken.at(k - 1))
                        pool.tensor_copy(kn[:, 1, 0], kn[:, 0, CH]).then_inc(k_passed.sem, 1)

                two_a_turn(pool, part)

            @block.vector
            def _(v):
                v.sem_inc(kn_taken.sem, 1)
                v.sem_inc(y_added.sem, 1)
                v.sem_inc(p_taken.sem, 2)

                def norm(k, u):
                    v.wait_ge(turned.sem, turned.at(k - 2))
                    v.tensor_tensor(xnc[:, u], pr.X[:, ds(k * CH, CH), :], bc(pr.mean[:, ds(k * CH, CH)], D),
                                    ALU.subtract).then_inc(xn_sub.sem, 1)
                    v.wait_ge(xn_sub.sem, xn_sub.at(k))
                    v.tensor_tensor(xnc[:, u], xnc[:, u], bc(pr.rstd[:, ds(k * CH, CH)], D),
                                    ALU.mult).then_inc(xn_ready.sem, 1)

                def part(k, u, j):
                    norm(k, u)
                    v.wait_ge(o_sum.sem, o_sum.at(k - 2))
                    v.wait_ge(kn_sum.sem, kn_sum.at(k))
                    v.tensor_copy(kn[:, u, 1:], o_ps.rearrange("p (t d) -> p t d", d=D)).then_inc(kn_taken.sem, 1)
                    for half in range(2):
                        i = k * 2 + half
                        v.wait_ge(scored.sem, scored.at(i))
                        ins = v.reduce_max(mx[:, u, 2 * half:2 * half + 2],
                                           s_ps[:, half].rearrange("p (t k) -> p t k", t=2), AX)
                        ins.then_inc(maxed.sem, 1)
                    v.wait_ge(maxed.sem, maxed.at(k * 2 + 1))
                    v.tensor_scalar(nmx[:, u], mx[:, u], -SCALE, None, ALU.mult).then_inc(minus_ready.sem, 1)
                    for half in range(2):
                        v.wait_ge(p_turned.sem, p_turned.at(k * 2 + half))
                        v.tensor_copy(pt[:, u, 2 * half:2 * half + 2].rearrange("p t a q -> p (t a q)"),
                                      pt_ps[:, half]).then_inc(p_taken.sem, 1)
                    v.wait_ge(exped.sem, exped.at(k))
                    v.reciprocal(rec[:, u], sums[:, u]).then_inc(rec_ready.sem, 1)
                    v.wait_ge(rec_ready.sem, rec_ready.at(k))
                    v.wait_ge(y_sum.sem, y_sum.at(k))
                    for t in range(CH):
                        x = one(pr.X, k * CH + t)
                        ins = v.scalar_tensor_tensor(out=x, in0=turn_ps[:, t * D:(t + 1) * D],
                                                     scalar=rec[:, u, t:t + 1], in1=x, op0=ALU.mult, op1=ALU.add)
                    ins.then_inc(y_added.sem, 1)

                two_a_turn(v, part)

            @block.scalar
            def _(act):
                nc.scalar.preload_act_table(ACT.Exp)
                for e in (chunk_ready, q_taken, k_taken, r_taken, o_taken):
                    act.sem_inc(e.sem, 1)
                act.sem_inc(exped.sem, 2)
                act.wait_ge(zeroed, 2)

                def part(k, u, j):
                    act.wait_ge(r_sum.sem, r_sum.at(k - 2))
                    act.wait_ge(chunk_kept.sem, chunk_kept.at(k - 2))
                    act.wait_ge(turned.sem, turned.at(k))
                    nc.scalar.activation(chunk[:, u], turn_ps, ACT.Copy).then_inc(chunk_ready.sem, 1)
                    act.wait_ge(scored.sem, scored.at(k * 2 - 3))
                    act.wait_ge(q_sum.sem, q_sum.at(k))
                    nc.scalar.activation(qt[:, u], q_ps, ACT.Copy).then_inc(q_taken.sem, 1)
                    if u == 0:
                        act.wait_ge(k_passed.sem, j * 2 + 1)
                    act.wait_ge(k_sum.sem, k_sum.at(k))
                    nc.scalar.activation(kt[:, u, P:], k_ps, ACT.Copy).then_inc(k_taken.sem, 1)
                    hold(act, pr.gate_a, r_sum.sem, r_sum.at(k))
                    nc.scalar.activation(pr.logits[:, ds(k * CH, CH), 0:8],
                                         q_ps[:, 0:CH * 8].rearrange("p (t c) -> p t c", c=8),
                                         ACT.Copy).then_inc(r_taken.sem, 1)
                    act.wait_ge(p_turned.sem, p_turned.at(k * 2 - 3))
                    act.wait_ge(minus_ready.sem, minus_ready.at(k))
                    for t in range(CH):
                        ins = nc.scalar.activation(prob[:, u, t], s_ps[:, t // 2, (t % 2) * 2 * P:(t % 2 + 1) * 2 * P],
                                                   ACT.Exp, bias=nmx[:, u, t:t + 1], scale=SCALE,
                                                   accum_out=sums[:, u, t:t + 1])
                    ins.then_inc(exped.sem, 1)
                    act.wait_ge(y_sum.sem, y_sum.at(k - 2))
                    act.wait_ge(o_sum.sem, o_sum.at(k))
                    nc.scalar.activation(ot[:, u], o_ps, ACT.Copy).then_inc(o_taken.sem, 1)

                two_a_turn(act, part)

            @block.tensor
            def _(pe):
                for e in (turned, q_sum, k_sum, kn_sum, r_sum, scored, o_sum, y_sum):
                    pe.sem_inc(e.sem, 2)
                pe.sem_inc(p_turned.sem, 4)
                pe.wait_ge(loaded, 5 * 16)
                pe.wait_ge(zeroed, 2)

                def part(k, u, j):
                    pe.wait_ge(xn_ready.sem, xn_ready.at(k))
                    pe.wait_ge(y_added.sem, y_added.at(k - 1))
                    for t in range(CH):
                        mm = pe.transpose(turn_ps[:, t * P:(t + 1) * P], xnc[:, u, t], pr.idf[:])
                    mm.then_inc(turned.sem, 1)
                    pe.wait_ge(chunk_ready.sem, chunk_ready.at(k))
                    pe.wait_ge(r_taken.sem, r_taken.at(k - 1))
                    pe.matmul(q_ps, wq[:], chunk[:, u], start=True, stop=True).then_inc(q_sum.sem, 1)
                    pe.matmul(k_ps, wk[:], chunk[:, u], start=True, stop=True).then_inc(k_sum.sem, 1)
                    pe.wait_ge(o_taken.sem, o_taken.at(k - 1))
                    for t in range(CH):
                        mm = pe.matmul(o_ps[:, t * D:(t + 1) * D], chunk[:, u, t * P:(t + 1) * P], wk[:],
                                       start=True, stop=True)
                    mm.then_inc(kn_sum.sem, 1)
                    pe.wait_ge(q_taken.sem, q_taken.at(k))
                    for t in range(CH):
                        mm = pe.matmul(q_ps[:, t * 8:(t + 1) * 8], chunk[:, u, t * P:(t + 1) * P], wroute[:],
                                       start=True, stop=True)
                    mm.then_inc(r_sum.sem, 1)
                    pe.wait_ge(k_taken.sem, k_taken.at(k))
                    pe.wait_ge(exped.sem, exped.at(k - 1))
                    if u == 1:
                        pe.wait_ge(k_passed.sem, j * 2 + 2)
                    for t in range(CH):
                        s = s_ps[:, t // 2, (t % 2) * 2 * P:(t % 2 + 1) * 2 * P]
                        pe.matmul(s, qt[:, u, t * P:(t + 1) * P], kt[:, u, t * P:(t + 2) * P], start=True, stop=False)
                        mm = pe.matmul(s[:, P:], pr.idb[:], mask[:], start=False, stop=True)
                        if t % 2:
                            mm.then_inc(scored.sem, 1)
                    pe.wait_ge(exped.sem, exped.at(k))
                    for t in range(CH):
                        if t % 2 == 0:
                            pe.wait_ge(p_taken.sem, p_taken.at(k * 2 + t // 2 - 2))
                        for a in range(2):
                            mm = pe.transpose(pt_ps[:, t // 2, ((t % 2) * 2 + a) * P:((t % 2) * 2 + a + 1) * P],
                                              prob[:, u, t, a * P:(a + 1) * P], pr.idf[:])
                        if t % 2:
                            mm.then_inc(p_turned.sem, 1)
                    pe.wait_ge(kn_taken.sem, kn_taken.at(k))
                    if u == 1:
                        pe.wait_ge(k_passed.sem, j * 2 + 3)
                    for t in range(CH):
                        if t % 2 == 0:
                            pe.wait_ge(p_taken.sem, p_taken.at(k * 2 + t // 2))
                        for a in range(2):
                            mm = pe.matmul(o_ps[:, t * P:(t + 1) * P], kn[:, u, t + a], pt[:, u, t, a],
                                           start=a == 0, stop=a == 1)
                    mm.then_inc(o_sum.sem, 1)
                    pe.wait_ge(o_taken.sem, o_taken.at(k))
                    for t in range(CH):
                        mm = pe.matmul(turn_ps[:, t * D:(t + 1) * D], ot[:, u, t * P:(t + 1) * P], wo[:],
                                       start=True, stop=True)
                    mm.then_inc(y_sum.sem, 1)

                two_a_turn(pe, part)


def top_gates(pr, ne, top, total, bias=None, fill=None):
    nc, d = pr.nc, pr.d
    with ExitStack() as ctx:
        lg, prob, left, eq, key, gate, order = (pr.sb(ctx, n, [P, NT, ne]) for n in
                                                ("lg", "prob", "left", "eq", "key", "gate", "order"))
        m, s, r = (pr.sb(ctx, n, [P, NT]) for n in ("m", "s", "r"))
        brow = pr.sb(ctx, "bias_row", [P, ne])
        orow = pr.sb(ctx, "order_row", [P, ne])
        loaded = pr.sem(ctx, "loaded")
        shifted = pr.sem(ctx, "shifted")
        exped = pr.sem(ctx, "exped")
        dv = pr.sem(ctx, "dv_steps")
        with nc.Block() as block:
            @block.sync
            def _(sp):
                sp.dma_start(orow[:], d["order"][:, 0:ne]).then_inc(loaded, 16)
                if bias:
                    sp.dma_start(brow[:], d[bias].broadcast_to([P, ne])).then_inc(loaded, 16)

            @block.scalar
            def _(act):
                act.wait_ge(shifted, 1)
                nc.scalar.activation(prob[:], lg[:], ACT.Exp).then_inc(exped, 1)

            @block.vector
            def _(v):
                c = Chain(v, dv)
                v.wait_ge(loaded, 32 if bias else 16)
                if bias:
                    c.link(v.tensor_tensor(lg[:], pr.logits[:, :, 0:ne], brow[:].unsqueeze(1).broadcast_to([P, NT, ne]),
                                           ALU.add))
                else:
                    c.link(v.tensor_copy(lg[:], pr.logits[:, :, 0:ne]))
                c.link(v.memset(pr.gates[:], 1.0))
                c.link(v.tensor_copy(order[:], orow[:].unsqueeze(1).broadcast_to([P, NT, ne])))
                c.link(v.reduce_max(m[:], lg[:], AX))
                v.tensor_tensor(lg[:], lg[:], bc(m[:], ne), ALU.subtract).then_inc(shifted, 1)
                v.wait_ge(exped, 1)
                c.link(v.reduce_sum(s[:], prob[:], AX))
                c.link(v.reciprocal(r[:], s[:]))
                c.link(v.tensor_tensor(prob[:], prob[:], bc(r[:], ne), ALU.mult))
                c.link(v.tensor_copy(left[:], prob[:]))
                c.link(v.memset(gate[:], 0.0))
                for i in range(top):
                    c.link(v.reduce_max(m[:], left[:], AX))
                    c.link(v.tensor_tensor(eq[:], left[:], bc(m[:], ne), ALU.is_ge))
                    c.link(v.tensor_tensor(key[:], eq[:], order[:], ALU.mult))
                    c.link(v.reduce_max(m[:], key[:], AX))
                    c.link(v.tensor_tensor(eq[:], key[:], bc(m[:], ne), ALU.is_equal))
                    c.link(v.tensor_tensor(gate[:], gate[:], eq[:], ALU.add))
                    c.link(v.scalar_tensor_tensor(out=left[:], in0=eq[:], scalar=-2.0, in1=left[:], op0=ALU.mult,
                                                  op1=ALU.add))
                c.link(v.tensor_tensor(gate[:], gate[:], prob[:], ALU.mult))
                if total:
                    c.link(v.reduce_sum(s[:], gate[:], AX))
                    c.link(v.tensor_scalar(s[:], s[:], 1e-20, None, ALU.add))
                    c.link(v.reciprocal(r[:], s[:]))
                    c.link(v.tensor_tensor(gate[:], gate[:], bc(r[:], ne), ALU.mult))
                c.link(v.tensor_copy(pr.gates[:, :, 0:ne], gate[:]))


def l2_attention(pr):
    nc, d = pr.nc, pr.d
    SCALE = float(D) ** -0.5
    NH = 2
    CB = N // CW
    with ExitStack() as ctx:
        wqk = pr.sb(ctx, "wqk", [P, 2, 3, D])
        wv = pr.sb(ctx, "wv", [P, D])
        wo = pr.sb(ctx, "wo", [P, NH, D])
        wroute = pr.sb(ctx, "wroute", [P, 16])
        mask = pr.sb(ctx, "causal_mask", [P, P], BF16)
        cos = pr.sb(ctx, "cos", [P, N])
        sin = pr.sb(ctx, "sin", [P, N])
        xnc = pr.sb(ctx, "xnc", [P, CB, CH, D])
        chunk = pr.sb(ctx, "chunk", [P, CB, CW])
        qk = pr.sb(ctx, "qk_turned", [P, 3, N])
        part1 = pr.sb(ctx, "part1", [P, 2, CW])
        part2 = pr.sb(ctx, "part2", [P, 2, CW])
        vn = pr.sb(ctx, "v_by_token", [P, TPB, D])
        mx = pr.sb(ctx, "mx", [P, 2, 1])
        nmx = pr.sb(ctx, "minus_mx", [P, 2, 1])
        sums = pr.sb(ctx, "sums", [P, 2 * TPB, 1])
        rec = pr.sb(ctx, "rec", [P, 2 * TPB, 1])
        prob = pr.sb(ctx, "prob", [P, 2, N])
        pt = pr.sb(ctx, "prob_turned", [P, 2, TPB, NH, P])
        ot = pr.sb(ctx, "out_turned", [P, 2, NH * P])
        loaded = pr.sem(ctx, "weights_loaded")
        names = "xn_sub xn_ready chunk_kept rotated1 rotated2 rope_done v_taken maxed minus_ready p_taken " \
                "rec_ready y_added"
        (xn_sub, xn_ready, chunk_kept, rotated1, rotated2, rope_done, v_taken, maxed, minus_ready, p_taken,
         rec_ready, y_added) = (pr.sem(ctx, n) for n in names.split())
        names = "turned chunk_ready qk_sum v_sum r_sum r_taken scored exped p_turned o_sum o_taken y_sum batch_done"
        (turned, chunk_ready, qk_sum, v_sum, r_sum, r_taken, scored, exped, p_turned, o_sum, o_taken, y_sum,
         batch_done) = (pr.sem(ctx, n) for n in names.split())
        turn_ps = pr.ps[:, 6]
        UNITS = [(t, h) for t in range(TPB) for h in range(NH)]
        GROUPS = [(t, h, g) for t, h in UNITS for g in range(0, t + 1, CH)]
        NG = len(GROUPS)

        def batches(eng, body):
            with eng.Fori(0, B) as b:
                body(b)

        def s_ps(i):
            return pr.ps[:, 2 * (i % 2):2 * (i % 2) + 2].rearrange("p a k -> p (a k)")

        with nc.Block() as block:
            @block.sync
            def _(sp):
                for dst, src in ((wqk, "l2_wqk"), (wv, "l2_wv"), (wo, "l2_wo"), (wroute, "l2_gate"),
                                 (mask, "mask_causal"), (cos, "l2_cos"), (sin, "l2_sin")):
                    sp.dma_start(dst[:], d[src]).then_inc(loaded, 16)

            @block.gpsimd
            def _(pool):
                pool.wait_ge(loaded, 7 * 16)

                def batch(b):
                    for u in range(CB):
                        hold(pool, pr.gate_p, chunk_ready, b * CB + u + 1)
                        pool.tensor_copy(pr.xt[:, ds(b * N + u * CW, CW)], chunk[:, u]).then_inc(chunk_kept, 1)
                        for i in range(3):
                            if u == 0 and i == 0:
                                hold(pool, pr.gate_p, batch_done, b + 1)
                            hold(pool, pr.gate_p, rotated2, b * 6 + u * 3 + i + 1)
                            pool.tensor_tensor(qk[:, i, u * CW:(u + 1) * CW], part1[:, (u * 3 + i) % 2],
                                               part2[:, (u * 3 + i) % 2],
                                               ALU.add).then_inc(rope_done, 1)

                batches(pool, batch)

            @block.vector
            def _(v):
                v.wait_ge(loaded, 7 * 16)
                v.sem_inc(y_added, 1)

                def batch(b):
                    for u in range(CB):
                        v.wait_ge(batch_done, b + 1)
                        k = b * CB + u
                        v.tensor_tensor(xnc[:, u], pr.X[:, ds(k * CH, CH), :], bc(pr.mean[:, ds(k * CH, CH)], D),
                                        ALU.subtract).then_inc(xn_sub, 1)
                        v.wait_ge(xn_sub, k + 1)
                        v.tensor_tensor(xnc[:, u], xnc[:, u], bc(pr.rstd[:, ds(k * CH, CH)], D),
                                        ALU.mult).then_inc(xn_ready, 1)
                    for u in range(CB):
                        for i in range(3):
                            n = b * 6 + u * 3 + i
                            m = u * 3 + i
                            cols = slice(u * CW, (u + 1) * CW)
                            v.wait_ge(qk_sum, n + 1)
                            if m >= 2:
                                v.wait_ge(rope_done, n - 1)
                            v.tensor_tensor(part1[:, m % 2], pr.ps[:, 2 * (m % 2)], cos[:, cols],
                                            ALU.mult).then_inc(rotated1, 1)
                            v.tensor_tensor(part2[:, m % 2], pr.ps[:, 2 * (m % 2) + 1], sin[:, cols],
                                            ALU.mult).then_inc(rotated2, 1)
                        v.wait_ge(v_sum, b * CB + u + 1)
                        v.tensor_copy(vn[:, u * CH:(u + 1) * CH], pr.ps[:, 4 + u].rearrange("p (t d) -> p t d", d=D))\
                            .then_inc(v_taken, 1)

                    def highest(i):
                        t, h = UNITS[i]
                        v.wait_ge(scored, b * 16 + i + 1)
                        v.reduce_max(mx[:, h], s_ps(i)[:, 0:(t + 1) * P], AX).then_inc(maxed, 1)
                        v.wait_ge(maxed, b * 16 + i + 1)
                        v.tensor_scalar(nmx[:, h], mx[:, h], -SCALE, None, ALU.mult).then_inc(minus_ready, 1)

                    def turn(i):
                        t, h = UNITS[i]
                        for g, (gt, gh, k0) in enumerate(GROUPS):
                            if (gt, gh) == (t, h):
                                n = min(CH, t + 1 - k0)
                                v.wait_ge(p_turned, b * NG + g + 1)
                                v.tensor_copy(pt[:, t % 2, k0:k0 + n, h],
                                              pr.ps[:, 4 + g % 2, 0:n * P].rearrange("p (k q) -> p k q", q=P))\
                                    .then_inc(p_taken, 1)

                    def finish(t):
                        v.wait_ge(exped, b * 16 + 2 * t + 2)
                        v.reciprocal(rec[:, 2 * t:2 * t + 2], sums[:, 2 * t:2 * t + 2]).then_inc(rec_ready, 1)
                        v.wait_ge(rec_ready, b * TPB + t + 1)
                        v.wait_ge(y_sum, b * TPB + t + 1)
                        for h in range(NH):
                            x = one(pr.X, b * TPB + t)
                            v.scalar_tensor_tensor(out=x, in0=pr.ps[:, 7, h * D:(h + 1) * D],
                                                   scalar=rec[:, 2 * t + h], in1=x, op0=ALU.mult, op1=ALU.add)\
                                .then_inc(y_added, 1)
                            hold(v, pr.gate_v, y_added, b * 2 * TPB + 2 * t + h + 2)

                    highest(0)
                    highest(1)
                    for t in range(TPB):
                        turn(2 * t)
                        if t + 1 < TPB:
                            highest(2 * t + 2)
                        turn(2 * t + 1)
                        if t + 1 < TPB:
                            highest(2 * t + 3)
                        finish(t)

                batches(v, batch)

            @block.scalar
            def _(act):
                nc.scalar.preload_act_table(ACT.Exp)

                def batch(b):
                    for u in range(CB):
                        k = b * CB + u
                        act.wait_ge(batch_done, b + 1)
                        act.wait_ge(turned, k + 1)
                        nc.scalar.activation(chunk[:, u], turn_ps, ACT.Copy).then_inc(chunk_ready, 1)
                        hold(act, pr.gate_a, r_sum, k + 1)
                        nc.scalar.activation(pr.logits[:, ds(k * CH, CH), :],
                                             pr.ps[:, 7, 0:CH * 16].rearrange("p (t c) -> p t c", c=16),
                                             ACT.Copy).then_inc(r_taken, 1)

                    def exps(i):
                        t, h = UNITS[i]
                        act.wait_ge(minus_ready, b * 16 + i + 1)
                        if t:
                            act.wait_ge(p_turned, b * NG + len([1 for gt, gh, _ in GROUPS if (gt, gh) <= (t - 1, h)]))
                        nc.scalar.activation(prob[:, h, 0:(t + 1) * P], s_ps(i)[:, 0:(t + 1) * P], ACT.Exp,
                                             bias=nmx[:, h], scale=SCALE, accum_out=sums[:, i]).then_inc(exped, 1)

                    exps(0)
                    exps(1)
                    for t in range(TPB):
                        if t + 1 < TPB:
                            exps(2 * t + 2)
                            exps(2 * t + 3)
                        act.wait_ge(o_sum, b * TPB + t + 1)
                        if t >= 2:
                            act.wait_ge(y_sum, b * TPB + t - 1)
                        nc.scalar.activation(ot[:, t % 2], pr.ps[:, 6, 0:NH * P], ACT.Copy).then_inc(o_taken, 1)

                batches(act, batch)

            @block.tensor
            def _(pe):
                pe.wait_ge(loaded, 7 * 16)
                pe.sem_inc(batch_done, 1)

                def batch(b):
                    pe.wait_ge(y_added, b * 2 * TPB + 1)
                    for u in range(CB):
                        k = b * CB + u
                        pe.wait_ge(xn_ready, k + 1)
                        if u:
                            pe.wait_ge(chunk_ready, k)
                        for t in range(CH):
                            mm = pe.transpose(turn_ps[:, t * P:(t + 1) * P], xnc[:, u, t], pr.idf[:])
                        mm.then_inc(turned, 1)
                        pe.wait_ge(chunk_ready, k + 1)
                        for i in range(3):
                            m = u * 3 + i
                            if m >= 2:
                                pe.wait_ge(rotated2, b * 6 + m - 1)
                            pe.matmul(pr.ps[:, 2 * (m % 2)], wqk[:, 0, i], chunk[:, u], start=True, stop=True)
                            pe.matmul(pr.ps[:, 2 * (m % 2) + 1], wqk[:, 1, i], chunk[:, u], start=True, stop=True)\
                                .then_inc(qk_sum, 1)
                        for t in range(CH):
                            mm = pe.matmul(pr.ps[:, 4 + u, t * D:(t + 1) * D], chunk[:, u, t * P:(t + 1) * P], wv[:],
                                           start=True, stop=True)
                        mm.then_inc(v_sum, 1)
                        if u:
                            pe.wait_ge(r_taken, k)
                        for t in range(CH):
                            mm = pe.matmul(pr.ps[:, 7, t * 16:(t + 1) * 16], chunk[:, u, t * P:(t + 1) * P], wroute[:],
                                           start=True, stop=True)
                        mm.then_inc(r_sum, 1)

                    def score(i):
                        t, h = UNITS[i]
                        if i >= 2:
                            pe.wait_ge(exped, b * 16 + i - 1)
                        s = s_ps(i)
                        for k0 in range(0, t + 1, CH):
                            n = min(CH, t + 1 - k0)
                            last = k0 + n == t + 1
                            mm = pe.matmul(s[:, k0 * P:(k0 + n) * P], qk[:, h, t * P:(t + 1) * P],
                                           qk[:, 2, k0 * P:(k0 + n) * P], start=True, stop=not last)
                            if last:
                                mm = pe.matmul(s[:, t * P:(t + 1) * P], pr.idb[:], mask[:], start=False, stop=True)
                        mm.then_inc(scored, 1)

                    def turn(i):
                        t, h = UNITS[i]
                        pe.wait_ge(exped, b * 16 + i + 1)
                        for g, (gt, gh, k0) in enumerate(GROUPS):
                            if (gt, gh) == (t, h):
                                if g >= 2:
                                    pe.wait_ge(p_taken, b * NG + g - 1)
                                for a in range(min(CH, t + 1 - k0)):
                                    mm = pe.transpose(pr.ps[:, 4 + g % 2, a * P:(a + 1) * P],
                                                      prob[:, h, (k0 + a) * P:(k0 + a + 1) * P], pr.idf[:])
                                mm.then_inc(p_turned, 1)

                    def sum_values(t):
                        pe.wait_ge(p_taken, b * NG + len([1 for g in GROUPS if g[0] <= t]))
                        if t:
                            pe.wait_ge(o_taken, b * TPB + t)
                        for k in range(t + 1):
                            mm = pe.matmul(pr.ps[:, 6, 0:NH * P], vn[:, k], pt[:, t % 2, k].rearrange("p h q -> p (h q)"),
                                           start=k == 0, stop=k == t)
                        mm.then_inc(o_sum, 1)

                    def project(t):
                        pe.wait_ge(o_taken, b * TPB + t + 1)
                        pe.wait_ge(y_added, b * 2 * TPB + 2 * t + 1)
                        for h in range(NH):
                            mm = pe.matmul(pr.ps[:, 7, h * D:(h + 1) * D], ot[:, t % 2, h * P:(h + 1) * P], wo[:, h],
                                           start=True, stop=True)
                        mm.then_inc(y_sum, 1)

                    pe.wait_ge(rope_done, b * 6 + 6)
                    pe.wait_ge(v_taken, b * CB + CB)
                    pe.wait_ge(r_taken, b * CB + CB)
                    pe.wait_ge(chunk_kept, b * CB + CB)
                    score(0)
                    score(1)
                    for t in range(TPB):
                        turn(2 * t)
                        if t + 1 < TPB:
                            score(2 * t + 2)
                        turn(2 * t + 1)
                        if t + 1 < TPB:
                            score(2 * t + 3)
                        sum_values(t)
                        project(t)
                    pe.sem_inc(batch_done, 1)

                batches(pe, batch)


def l3_inner_statistics(pr):
    nc = pr.nc
    with ExitStack() as ctx:
        stats = pr.sb(ctx, "stats", [P, CH, 6])
        mv = pr.sb(ctx, "mv", [P, CH, 2])
        var = pr.sb(ctx, "var", [P, NT])
        std = pr.sb(ctx, "std", [P, NT])
        eps = pr.sb(ctx, "eps", [P, 1])
        dv = pr.sem(ctx, "dv_steps")
        x1_ready = pr.ev(ctx, "x1_ready")
        var_done = pr.sem(ctx, "var_done")
        std_done = pr.sem(ctx, "std_done")
        with nc.Block() as block:
            @block.gpsimd
            def _(pool):
                with pool.Fori(0, NC) as k:
                    hold(pool, pr.gate_p, x1_ready.sem, x1_ready.at(k))
                    pool.tensor_tensor(pr.X[:, ds(k * CH, CH), :], pr.X[:, ds(k * CH, CH), :],
                                       pr.x1[:, ds(k * CH, CH), :], ALU.add)

            @block.vector
            def _(v):
                v.memset(eps[:], 1e-5).then_inc(var_done, 1)
                per = 2 * CH + 3
                with v.Fori(0, NC) as k:
                    c = Chain(v, dv)
                    c.base = k * per
                    x1 = pr.x1[:, ds(k * CH, CH), :]
                    c.link(v.tensor_tensor(x1, pr.X[:, ds(k * CH, CH), :], bc(pr.mean[:, ds(k * CH, CH)], D),
                                           ALU.subtract))
                    v.tensor_tensor(x1, x1, bc(pr.rstd[:, ds(k * CH, CH)], D), ALU.mult).then_inc(x1_ready.sem, 1)
                    v.wait_ge(x1_ready.sem, x1_ready.at(k))
                    v.sem_inc(pr.gate_v, 1)
                    for t in range(CH):
                        c.step(v.bn_stats(stats[:, t, :], one(pr.x1, k * CH + t)))
                    c.wait()
                    v.sem_inc(pr.gate_v, 1)
                    for t in range(CH):
                        c.step(v.bn_aggr(mv[:, t, :], stats[:, t, :]))
                    c.wait()
                    v.sem_inc(pr.gate_v, 1)
                    c.step(v.tensor_copy(pr.mean2[:, ds(k * CH, CH)], mv[:, :, 0]))
                    c.step(v.tensor_copy(var[:, ds(k * CH, CH)], mv[:, :, 1]))
                v.wait_ge(dv, NC * per)
                v.sem_inc(var_done, 1)
                v.wait_ge(std_done, 1)
                v.reciprocal(pr.rstd2[:], std[:])

            @block.scalar
            def _(act):
                act.wait_ge(var_done, 2)
                nc.scalar.activation(std[:], var[:], ACT.Sqrt, bias=eps[:]).then_inc(std_done, 1)


def l3_project(pr):
    nc, d = pr.nc, pr.d
    VA = E + 1
    SCALE = float(E) ** -0.5
    with ExitStack() as ctx:
        wqk = pr.sb(ctx, "wqk", [P, 4, D])
        bqk = pr.sb(ctx, "bqk", [P, 4])
        wva = pr.sb(ctx, "wva", [P, D])
        bva = pr.sb(ctx, "bva", [P, D])
        wkv = pr.sb(ctx, "wkv", [P, 2 * D])
        bkv = pr.sb(ctx, "bkv", [P, 2 * D])
        wb = pr.sb(ctx, "wb", [P, D])
        wbs = pr.sb(ctx, "wbs", [P, D])
        wbias = pr.sb(ctx, "wbias", [1, D])
        ones = pr.sb(ctx, "ones", [1, P])
        g1 = pr.sb(ctx, "g1", [P, 1])
        b1 = pr.sb(ctx, "b1", [P, 1])
        own = pr.sb(ctx, "own_head", [P, H * VA])
        xnc = pr.sb(ctx, "xnc", [P, 2, CH, D])
        x2c = pr.sb(ctx, "x2c", [P, 2, CH, D])
        chunk1 = pr.sb(ctx, "chunk1", [P, 2, CW])
        chunk2 = pr.sb(ctx, "chunk2", [P, 2, CW])
        low = pr.sb(ctx, "low", [P, 2, CW])
        f32 = pr.sb(ctx, "rows32", [P, 4, CW])
        parts = pr.sb(ctx, "parts", [P, 4, 3, CW], BF16)
        rest = pr.sb(ctx, "rest", [P, CW])
        kv32 = pr.sb(ctx, "kv32", [P, CH, 2 * D])
        klow = pr.sb(ctx, "klow", [P, CH, D])
        kf = pr.sb(ctx, "k_features", [P, CH, D])
        vaug = pr.sb(ctx, "v_aug", [P, CH, H, VA])
        state = pr.sb(ctx, "state", [P, H * VA])
        outer = pr.sb(ctx, "outer", [P, H * VA])
        yc = pr.sb(ctx, "y_clipped", [P, 2, CH, D])
        loaded = pr.sem(ctx, "loaded")
        dv = pr.sem(ctx, "dv_steps")
        pl = pr.sem(ctx, "pool_steps")
        ready = pr.sem(ctx, "set_up")
        S = lambda n, p=0: pr.ev(ctx, n, p)
        xn_ready, x2_ready = S("xn_ready"), S("x2_ready")
        turned1, turned2 = S("turned1", 2), S("turned2", 2)
        c1_ready, c2_ready = S("c1_ready"), S("c2_ready", 1)
        row_sum, split = S("row_sum"), S("split", 4)
        rows_w, rows_l = S("windowed_rows_ready"), S("linear_rows_ready")
        taken_l = S("linear_rows_taken", 2)
        low_ready, low_exp = S("low_ready"), S("low_exp")
        va_sum, va_taken = S("va_sum", 2), S("va_taken", 1)
        kv_sum, kv_taken = S("kv_sum"), S("kv_taken", 1)
        klow_ready, klow_exp = S("klow_ready"), S("klow_exp")
        tok_ready = S("tok_ready")
        y_sum, y_taken, y_added = S("y_sum", 2), S("y_taken", 1), S("y_added", 2)
        st_sum, st_taken, out_sum, out_taken = S("st_sum"), S("st_taken", 1), S("out_sum"), S("out_taken", 1)
        st_ready = S("st_ready")
        stored = pr.sem(ctx, "stored")
        NW = 12

        with nc.Block() as block:
            @block.sync
            def _(sp):
                for dst, src in ((wqk, "l3_wqk"), (bqk, "l3_bqk"), (wva, "l3_wva"), (wkv, "l3_wkv"), (wb, "l3_wb"),
                                 (wbias, "l3_wbias"), (g1, "l3_g1"), (b1, "l3_b1"), (own, "own_head")):
                    sp.dma_start(dst[:], d[src]).then_inc(loaded, 16)
                sp.dma_start(bva[:], d["l3_bva"].broadcast_to([P, D])).then_inc(loaded, 16)
                sp.dma_start(bkv[:], d["l3_bkv"].broadcast_to([P, 2 * D])).then_inc(loaded, 16)
                sp.dma_start(wbs[:], d["l3_wbs"].broadcast_to([P, D])).then_inc(loaded, 16)
                sp.sem_inc(stored, 64)

                def store(k, u, j):
                    for i, t in enumerate((pr.q_dram, pr.k_dram, pr.q2_dram, pr.k2_dram)):
                        sp.wait_ge(split.sem, split.at(k * 4 + i))
                        sp.dma_start(t[:, :, ds(u * CW, CW)].rearrange("a (b p) t -> b p a t", p=P)[ds(j, 1)]
                                     .rearrange("b p a t -> (b p) a t"), parts[:, i]).then_inc(stored, 16)

                two_a_turn(sp, store)
                sp.wait_ge(stored, 64 + 64 * NC)

            @block.gpsimd
            def _(pool):
                for e, n in ((split, 4), (y_added, 2)):
                    pool.sem_inc(e.sem, n)

                def part(k, u, j):
                    c = Chain(pool, pl)
                    c.base = k * 12
                    for i in range(4):
                        e = rows_w if i < 2 else rows_l
                        hold(pool, pr.gate_p, e.sem, e.at(k * 2 + i % 2))
                        c.link(pool.tensor_tensor(rest[:], f32[:, i], parts[:, i, 0], ALU.subtract))
                        pool.sem_inc(pr.gate_p, 1)
                        c.link(pool.tensor_copy(parts[:, i, 1], rest[:]))
                        pool.sem_inc(pr.gate_p, 1)
                        c.link(pool.tensor_tensor(parts[:, i, 2], rest[:], parts[:, i, 1], ALU.subtract))
                        pool.sem_inc(split.sem, 1)
                    hold(pool, pr.gate_p, y_taken.sem, y_taken.at(k))
                    pool.tensor_tensor(pr.X[:, ds(k * CH, CH), :], pr.X[:, ds(k * CH, CH), :], yc[:, u],
                                       ALU.add).then_inc(y_added.sem, 1)

                two_a_turn(pool, part)

            @block.vector
            def _(v):
                v.wait_ge(loaded, 16 * NW)
                c = Chain(v, ready)
                c.link(v.memset(ones[:], 1.0))
                c.link(v.memset(pr.va[:, :, :, E:VA], 1.0))
                c.link(v.memset(pr.vs[:, :, :, E:VA], 1.0))
                c.link(v.memset(vaug[:], 1.0))
                c.link(v.tensor_scalar(wb[:], wb[:], 0.0, 2.0, ALU.is_ge, ALU.mult))
                c.link(v.tensor_scalar(wb[:], wb[:], -1.0, None, ALU.add))
                c.link(v.tensor_tensor(wb[:], wb[:], wbs[:], ALU.mult))
                for e in (va_taken, kv_taken, y_taken, st_taken, out_taken):
                    v.sem_inc(e.sem, 1)
                v.sem_inc(taken_l.sem, 2)
                STEPS = 29

                def part(k, u, j):
                    c = Chain(v, dv)
                    c.base = j * (2 * STEPS + 1) + u * (STEPS + 1)
                    v.wait_ge(turned2.sem, turned2.at(k - 2))
                    v.sem_inc(pr.gate_v, 1)
                    v.tensor_copy(xnc[:, u], pr.x1[:, ds(k * CH, CH), :]).then_inc(xn_ready.sem, 1)
                    c.link(v.tensor_tensor(x2c[:, u], pr.x1[:, ds(k * CH, CH), :], bc(pr.mean2[:, ds(k * CH, CH)], D),
                                           ALU.subtract))
                    v.tensor_tensor(x2c[:, u], x2c[:, u], bc(pr.rstd2[:, ds(k * CH, CH)], D),
                                    ALU.mult).then_inc(x2_ready.sem, 1)
                    v.wait_ge(va_sum.sem, va_sum.at(k))
                    c.link(v.tensor_tensor(pr.va[:, ds(j * H, H), u * CH:(u + 1) * CH, 0:E],
                                           pr.ps[:, 3].rearrange("p (t h e) -> p h t e", t=CH, e=E),
                                           bva[:].rearrange("p (h e) -> p h e", e=E).unsqueeze(2)
                                           .broadcast_to([P, H, CH, E]), ALU.add))
                    v.sem_inc(va_taken.sem, 1)
                    for i in (2, 3):
                        n = k * 4 + i
                        ps = pr.ps[:, 1 + i % 2]
                        v.wait_ge(split.sem, split.at(n - 4))
                        v.wait_ge(row_sum.sem, row_sum.at(n))
                        v.tensor_scalar(low[:, i - 2], ps, bqk[:, i:i + 1], 0.0, ALU.add, ALU.min)\
                            .then_inc(low_ready.sem, 1)
                        c.link(v.tensor_scalar(f32[:, i], ps, bqk[:, i:i + 1], 0.0, ALU.add, ALU.max))
                        v.sem_inc(taken_l.sem, 1)
                    for i in (2, 3):
                        v.wait_ge(low_exp.sem, low_exp.at(k * 2 + i - 2))
                        c.link(v.scalar_tensor_tensor(out=f32[:, i], in0=f32[:, i], scalar=SCALE if i == 2 else 1.0,
                                                      in1=low[:, i - 2], op0=ALU.mult, op1=ALU.add))
                        c.link(v.tensor_scalar(f32[:, i], f32[:, i], 1e-4, None, ALU.add))
                        v.wait_ge(stored, k * 64 + 64)
                        c.link(v.tensor_copy(parts[:, i, 0], f32[:, i]))
                        v.sem_inc(rows_l.sem, 1)
                    v.wait_ge(kv_sum.sem, kv_sum.at(k))
                    for half in range(2):
                        c.step(v.tensor_tensor(kv32[:, 2 * half:2 * half + 2],
                                               pr.ps[:, 4 + half].rearrange("p (t c) -> p t c", t=2),
                                               bkv[:].unsqueeze(1).broadcast_to([P, 2, 2 * D]), ALU.add))
                    c.wait()
                    v.sem_inc(kv_taken.sem, 1)
                    v.tensor_scalar(klow[:], kv32[:, :, 0:D], 0.0, None, ALU.min).then_inc(klow_ready.sem, 1)
                    c.step(v.tensor_copy(vaug[:, :, :, 0:E], kv32[:, :, D:].rearrange("p t (h e) -> p t h e", e=E)))
                    c.step(v.tensor_copy(pr.vs[:, ds(j * H, H), u * CH:(u + 1) * CH, 0:E],
                                         kv32[:, :, D:].rearrange("p t (h e) -> p h t e", e=E)))
                    c.step(v.tensor_scalar(kf[:], kv32[:, :, 0:D], 0.0, 1e-4, ALU.max, ALU.add))
                    if u == 0:
                        c.step(v.memset(state[:], 0.0))
                    c.wait()
                    v.wait_ge(klow_exp.sem, klow_exp.at(k))
                    c.link(v.tensor_tensor(kf[:], kf[:], klow[:], ALU.add))
                    v.sem_inc(tok_ready.sem, 1)
                    v.wait_ge(y_added.sem, y_added.at(k - 2))
                    v.wait_ge(y_sum.sem, y_sum.at(k))
                    c.link(v.tensor_scalar(yc[:, u], pr.ps[:, 6].rearrange("p (t d) -> p t d", d=D), 100.0, -100.0,
                                           ALU.min, ALU.max))
                    v.sem_inc(y_taken.sem, 1)
                    for t in range(CH):
                        v.sem_inc(st_ready.sem, 1)
                        v.wait_ge(out_sum.sem, out_sum.at(k * CH + t))
                        v.sem_inc(pr.gate_v, 1)
                        c.step(v.tensor_copy(pr.st[:, ds(j * H, H), u * CH + t, :],
                                             pr.ps[:, 7, 0:H * VA].rearrange("p (h c) -> p h c", c=VA)))
                        v.wait_ge(st_sum.sem, st_sum.at(k * CH + t))
                        c.link(v.tensor_tensor(outer[:], pr.ps[:, 3, 0:H * VA], own[:], ALU.mult))
                        v.sem_inc(st_taken.sem, 1)
                        c.link(v.tensor_tensor(state[:], state[:], outer[:], ALU.add))
                    assert c.n == STEPS + (u == 0)

                two_a_turn(v, part)

            @block.scalar
            def _(act):
                nc.scalar.preload_act_table(ACT.Exp)
                act.sem_inc(c2_ready.sem, 1)
                act.wait_ge(loaded, 16 * NW)

                def part(k, u, j):
                    act.wait_ge(y_sum.sem, y_sum.at(k - 2))
                    act.wait_ge(turned1.sem, turned1.at(k))
                    nc.scalar.activation(chunk1[:, u], pr.ps[:, 0], ACT.Copy).then_inc(c1_ready.sem, 1)
                    act.wait_ge(turned2.sem, turned2.at(k))
                    nc.scalar.activation(chunk2[:, u], pr.ps[:, 0], ACT.Identity, scale=g1[:], bias=b1[:])\
                        .then_inc(c2_ready.sem, 1)
                    act.wait_ge(stored, k * 64 + 64)
                    act.sem_inc(pr.gate_a, 1)
                    for i in range(2):
                        act.wait_ge(split.sem, split.at(k * 4 + i - 4))
                        act.wait_ge(row_sum.sem, row_sum.at(k * 4 + i))
                        nc.scalar.activation(f32[:, i], pr.ps[:, 1 + i % 2], ACT.Identity, bias=bqk[:, i:i + 1])
                        nc.scalar.activation(parts[:, i, 0], pr.ps[:, 1 + i % 2], ACT.Identity,
                                             bias=bqk[:, i:i + 1]).then_inc(rows_w.sem, 1)
                    for i in range(2):
                        act.wait_ge(low_ready.sem, low_ready.at(k * 2 + i))
                        nc.scalar.activation(low[:, i], low[:, i], ACT.Exp, scale=SCALE if i == 0 else 1.0)\
                            .then_inc(low_exp.sem, 1)
                    act.wait_ge(klow_ready.sem, klow_ready.at(k))
                    nc.scalar.activation(klow[:], klow[:], ACT.Exp).then_inc(klow_exp.sem, 1)

                two_a_turn(act, part)

            @block.tensor
            def _(pe):
                pe.wait_ge(loaded, 16 * NW)
                pe.wait_ge(ready, 7)
                for e in (turned1, turned2, va_sum, y_sum):
                    pe.sem_inc(e.sem, 2)

                def part(k, u, j):
                    pe.wait_ge(c2_ready.sem, c2_ready.at(k - 1))
                    pe.wait_ge(xn_ready.sem, xn_ready.at(k))
                    for t in range(CH):
                        mm = pe.transpose(pr.ps[:, 0, t * P:(t + 1) * P], xnc[:, u, t], pr.idf[:])
                    mm.then_inc(turned1.sem, 1)
                    pe.wait_ge(c1_ready.sem, c1_ready.at(k))
                    pe.wait_ge(x2_ready.sem, x2_ready.at(k))
                    for t in range(CH):
                        mm = pe.transpose(pr.ps[:, 0, t * P:(t + 1) * P], x2c[:, u, t], pr.idf[:])
                    mm.then_inc(turned2.sem, 1)
                    pe.wait_ge(y_taken.sem, y_taken.at(k - 1))
                    for t in range(CH):
                        s = pr.ps[:, 6, t * D:(t + 1) * D]
                        pe.matmul(s, chunk1[:, u, t * P:(t + 1) * P], wb[:], start=True, stop=False)
                        mm = pe.matmul(s, ones[:], wbias[:], start=False, stop=True)
                    mm.then_inc(y_sum.sem, 1)
                    pe.wait_ge(c2_ready.sem, c2_ready.at(k))
                    pe.wait_ge(va_taken.sem, va_taken.at(k - 1))
                    pe.wait_ge(st_taken.sem, st_taken.at(k * CH - 1))
                    for t in range(CH):
                        mm = pe.matmul(pr.ps[:, 3, t * D:(t + 1) * D], chunk2[:, u, t * P:(t + 1) * P], wva[:],
                                       start=True, stop=True)
                    mm.then_inc(va_sum.sem, 1)
                    for i in range(4):
                        e, n = (taken_l, k * 2 - 2 + i) if i < 2 else (rows_w, k * 2 + i - 2)
                        pe.wait_ge(e.sem, e.at(n))
                        pe.matmul(pr.ps[:, 1 + i % 2], wqk[:, i], chunk2[:, u], start=True, stop=True)\
                            .then_inc(row_sum.sem, 1)
                    pe.wait_ge(kv_taken.sem, kv_taken.at(k - 1))
                    for t in range(CH):
                        mm = pe.matmul(pr.ps[:, 4 + t // 2, (t % 2) * 2 * D:(t % 2 + 1) * 2 * D],
                                       chunk2[:, u, t * P:(t + 1) * P], wkv[:], start=True, stop=True)
                    mm.then_inc(kv_sum.sem, 1)
                    pe.wait_ge(rows_l.sem, rows_l.at(k * 2 + 1))
                    pe.wait_ge(tok_ready.sem, tok_ready.at(k))
                    for t in range(CH):
                        pe.wait_ge(st_ready.sem, st_ready.at(k * CH + t))
                        pe.wait_ge(st_taken.sem, st_taken.at(k * CH + t - 1))
                        pe.matmul(pr.ps[:, 7, 0:H * VA], f32[:, 2, t * P:(t + 1) * P], state[:],
                                  start=True, stop=True).then_inc(out_sum.sem, 1)
                        pe.matmul(pr.ps[:, 3, 0:H * VA], kf[:, t], vaug[:, t].rearrange("p h c -> p (h c)"),
                                  start=True, stop=True).then_inc(st_sum.sem, 1)

                two_a_turn(pe, part)


def l3_attention(pr):
    nc, d = pr.nc, pr.d
    SCALE = float(E) ** -0.5
    KM = MROW + 2
    VA = E + 1
    NG, NW, NL = 5, 4, 6
    DEPTH = 3
    with ExitStack() as ctx:
        qst, kst, qlin, klin = ([pr.sb(ctx, f"{n}{u}", [P, N], BF16) for u in range(2)]
                                for n in ("q_stack", "k_stack", "q_linear", "k_linear"))
        mask_q = pr.sb(ctx, "mask_by_query", [P, 2 * P], BF16)
        mask_k = pr.sb(ctx, "mask_by_key", [P, 2 * P], BF16)
        tri = pr.sb(ctx, "keys_up_to_query", [P, P])
        mx = pr.sb(ctx, "maxima", [P, TPB])
        mrow = [pr.sb(ctx, f"max_rows{u}", [P, TPB, KM], BF16) for u in range(2)]
        p_win = pr.sb(ctx, "p_windowed", [P, TPB, 2 * P])
        a_lin = pr.sb(ctx, "a_linear", [P, TPB, P])
        rec = pr.sb(ctx, "rec", [P, TPB])
        total = pr.sb(ctx, "total", [P, TPB, VA])
        den = pr.sb(ctx, "den", [P, TPB])
        zeroed = pr.sem(ctx, "zeroed")
        consts = pr.sem(ctx, "consts")
        stacks = [pr.sem(ctx, f"stacks{u}") for u in range(2)]
        first_part = pr.sem(ctx, "first_part")
        nsteps = pr.sem(ctx, "norm_steps")
        scored = pr.ev(ctx, "scored_by_query")
        reduced = pr.ev(ctx, "reduced", 2)
        rows_ready = pr.ev(ctx, "max_rows_ready")
        keyed = pr.ev(ctx, "scored_by_key", 2 * NL)
        exped = pr.ev(ctx, "exped", NW)
        masked = pr.ev(ctx, "masked", 2)
        summed = pr.ev(ctx, "values_summed")
        normed = pr.ev(ctx, "values_normed", 2)

        def key_ps(n, g):
            return pr.ps[:, 2 + (n * NL + g) % DEPTH]

        with nc.Block() as block:
            @block.sync
            def _(sp):
                sp.dma_start(mask_q[:], d["mask_win_q"]).then_inc(consts, 16)
                sp.dma_start(mask_k[:], d["mask_win_k"]).then_inc(consts, 16)
                sp.dma_start(tri[:], d["tri"]).then_inc(consts, 16)
                sp.wait_ge(zeroed, 12)

                def load(n, u):
                    sp.wait_ge(keyed.sem, keyed.at((n - 2) * NL + NL - 1))
                    for q, k, qd, kd in ((qst, kst, pr.q_dram, pr.k_dram), (qlin, klin, pr.q2_dram, pr.k2_dram)):
                        for a in range(3):
                            rows = slice(a * 3 * E, (a + 1) * 3 * E)
                            sp.dma_start(q[u][rows], qd[:, ds(n * E, E), :]).then_inc(stacks[u], 16)
                            sp.dma_start(k[u][rows], kd[a:a + 1, ds(n * E, E), :].broadcast_to([3, E, N]))\
                                .then_inc(stacks[u], 16)

                with sp.Fori(0, HEADS // 2) as j:
                    for u in range(2):
                        load(j * 2 + u, u)

            @block.gpsimd
            def _(pool):
                for u in range(2):
                    for t in (qst[u], kst[u], qlin[u], klin[u], mrow[u]):
                        pool.memset(t[:], 0.0).then_inc(zeroed, 1)
                pool.wait_ge(zeroed, 10)
                for u in range(2):
                    pool.memset(kst[u][MROW:KM], 1.0).then_inc(zeroed, 1)

            @block.vector
            def _(v):
                for e in (reduced, masked, normed):
                    v.sem_inc(e.sem, 2)
                v.wait_ge(zeroed, 12)
                v.wait_ge(consts, 48)

                def maxima(n, u):
                    for g in range(NW):
                        v.wait_ge(scored.sem, scored.at(n * NG + g))
                        ps = pr.ps[:, (u * NG + g) % 2]
                        if g == 0:
                            v.reduce_max(mx[:, 0:1], ps[:, P:2 * P], AX)
                            v.reduce_max(mx[:, 1:2], ps[:, 2 * P:4 * P], AX).then_inc(reduced.sem, 1)
                        else:
                            v.reduce_max(mx[:, 2 * g:2 * g + 2], ps.rearrange("p (t k) -> p t k", t=2), AX)\
                                .then_inc(reduced.sem, 1)
                    v.wait_ge(reduced.sem, reduced.at(n * NG + NW - 1))
                    v.tensor_scalar(mrow[u][:, :, MROW], mx[:], -1.0, None, ALU.mult).then_inc(first_part, 1)
                    v.wait_ge(first_part, n + 1)
                    v.scalar_tensor_tensor(out=mrow[u][:, :, MROW + 1], in0=mx[:], scalar=-1.0,
                                           in1=mrow[u][:, :, MROW], op0=ALU.mult, op1=ALU.subtract)\
                        .then_inc(rows_ready.sem, 1)
                    v.wait_ge(scored.sem, scored.at(n * NG + NW))
                    v.tensor_copy(qst[u][MROW:KM], pr.ps[MROW:KM, (u * NG + NW) % 2].bitcast(BF16))\
                        .then_inc(reduced.sem, 1)

                def triangle(n, u):
                    for g in range(NW, NL):
                        v.wait_ge(keyed.sem, keyed.at(n * NL + g))
                        t = CH * (g - NW)
                        v.tensor_tensor(a_lin[:, t:t + CH], key_ps(u, g).rearrange("p (t q) -> p t q", q=P),
                                        tri[:].unsqueeze(1).broadcast_to([P, CH, P]), ALU.mult).then_inc(masked.sem, 1)

                def normalise(n, u):
                    c = Chain(v, nsteps)
                    c.base = n * 5
                    v.wait_ge(summed.sem, summed.at(n))
                    sums = pr.ps[:, 6 + u, 0:TPB * 2 * VA].rearrange("p (t a c) -> p t a c", a=2, c=VA)
                    c.step(v.reciprocal(rec[:], sums[:, :, 0, E]))
                    c.link(v.tensor_tensor(total[:], sums[:, :, 1], one(pr.st, n), ALU.add))
                    v.tensor_tensor(one(pr.oa, n), sums[:, :, 0, 0:E], bc(rec[:], E), ALU.mult).then_inc(normed.sem, 1)
                    c.link(v.tensor_scalar(den[:], total[:, :, E], 1e-6, None, ALU.add))
                    c.link(v.reciprocal(den[:], den[:]))
                    c.link(v.tensor_tensor(one(pr.os, n), total[:, :, 0:E], bc(den[:], E), ALU.mult))

                def step(n, u):
                    maxima(n + 1, 1 - u)
                    triangle(n, u)
                    normalise(n, u)

                maxima(0, 0)
                with v.Fori(0, HEADS // 2 - 1) as j:
                    for u in range(2):
                        step(j * 2 + u, u)
                step(HEADS - 2, 0)
                triangle(HEADS - 1, 1)
                normalise(HEADS - 1, 1)

            @block.scalar
            def _(act):
                nc.scalar.preload_act_table(ACT.Exp)
                act.sem_inc(exped.sem, NW)

                def exps(n, u):
                    for g in range(NW):
                        act.wait_ge(keyed.sem, keyed.at(n * NL + g))
                        ps = key_ps(u, g)
                        if g < NW - 1:
                            ins = nc.scalar.activation(p_win[:, 2 * g:2 * g + 2].rearrange("p t q -> p (t q)"), ps,
                                                       ACT.Exp, scale=SCALE)
                        else:
                            flat = p_win[:, 2 * g:2 * g + 2].rearrange("p t q -> p (t q)")
                            ins = nc.scalar.activation(flat[:, 0:3 * P], ps[:, 0:3 * P], ACT.Exp, scale=SCALE)
                        ins.then_inc(exped.sem, 1)

                with act.Fori(0, HEADS // 2) as j:
                    for u in range(2):
                        exps(j * 2 + u, u)

            @block.tensor
            def _(pe):
                pe.sem_inc(keyed.sem, 2 * NL)
                pe.wait_ge(consts, 48)
                pe.wait_ge(zeroed, 12)

                def query_group(n, u, g, half):
                    pe.wait_ge(reduced.sem, reduced.at(n * NG + g - 2))
                    ps = pr.ps[:, (u * NG + g) % 2]
                    if g == 0:
                        pe.wait_ge(stacks[u], (half + 1) * 12 * 16)
                    if g < NW:
                        for i in range(2):
                            t = 2 * g + i
                            lo = P if t == 0 else 0
                            s = ps[:, i * 2 * P + lo:(i + 1) * 2 * P]
                            pe.matmul(s, qst[u][0:KQ, t * P:(t + 1) * P], kst[u][0:KQ, (t - 1) * P + lo:(t + 1) * P],
                                      start=True, stop=False)
                            mm = pe.matmul(s, pr.idb[:], mask_q[:, lo:], start=False, stop=True)
                    else:
                        pe.wait_ge(rows_ready.sem, rows_ready.at(n))
                        for t in range(TPB):
                            mm = pe.transpose(ps[0:KM, t * 64:(t + 1) * 64].bitcast(BF16), mrow[u][:, t], pr.idb[:])
                    mm.then_inc(scored.sem, 1)

                def key_group(n, u, g):
                    b = g - DEPTH
                    if b < 0:
                        b, m = b + NL, n - 1
                    else:
                        m = n
                    e, i = (exped, m * NW + b) if b < NW else (masked, m * 2 + b - NW)
                    pe.wait_ge(e.sem, e.at(i))
                    if g == 0:
                        pe.wait_ge(reduced.sem, reduced.at(n * NG + NW))
                    ps = key_ps(u, g)
                    if g < NW:
                        for i in range(2):
                            t = 2 * g + i
                            w = P if t == TPB - 1 else 2 * P
                            s = ps[:, i * 2 * P:i * 2 * P + w]
                            pe.matmul(s, kst[u][0:KM, t * P:(t + 1) * P], qst[u][0:KM, t * P:t * P + w],
                                      start=True, stop=False)
                            mm = pe.matmul(s, pr.idb[:], mask_k[:, 0:w], start=False, stop=True)
                    else:
                        for i in range(CH):
                            t = CH * (g - NW) + i
                            mm = pe.matmul(ps[:, i * P:(i + 1) * P], klin[u][0:KQ, t * P:(t + 1) * P],
                                           qlin[u][0:KQ, t * P:(t + 1) * P], start=True, stop=True)
                    mm.then_inc(keyed.sem, 1)

                def values(n, u, g):
                    if g == 0:
                        pe.wait_ge(normed.sem, normed.at(n - 2))
                    sums = pr.ps[:, 6 + u, 0:TPB * 2 * VA].rearrange("p (t a c) -> p t a c", a=2, c=VA)
                    if g < NW:
                        pe.wait_ge(exped.sem, exped.at(n * NW + g))
                        va = one(pr.va, n)
                        for t in (2 * g, 2 * g + 1):
                            keys = [k for k in (t - 1, t) if k >= 0]
                            for k in keys:
                                pe.matmul(sums[:, t, 0], p_win[:, k, (t - k) * P:(t - k + 1) * P], va[:, k],
                                          start=k == keys[0], stop=k == keys[-1])
                    else:
                        pe.wait_ge(masked.sem, masked.at(n * 2 + g - NW))
                        vs = one(pr.vs, n)
                        for t in range(CH * (g - NW), CH * (g - NW + 1)):
                            mm = pe.matmul(sums[:, t, 1], a_lin[:, t], vs[:, t], start=True, stop=True)
                        if g == NL - 1:
                            mm.then_inc(summed.sem, 1)

                def step(n, u, half):
                    more = not isinstance(n, int) or n + 1 < HEADS
                    for g in range(NL + 2):
                        if g < NL:
                            key_group(n, u, g)
                        if g < NG and more:
                            query_group(n + 1, 1 - u, g, half)
                        if g >= 2:
                            values(n, u, g - 2)

                for g in range(NG):
                    query_group(0, 0, g, 0)
                with pe.Fori(0, HEADS // 2 - 1) as j:
                    for u in range(2):
                        step(j * 2 + u, u, j + u)
                step(HEADS - 2, 0, HEADS // 2 - 1)
                step(HEADS - 1, 1, HEADS // 2)


def l3_mix(pr):
    nc, d = pr.nc, pr.d
    with ExitStack() as ctx:
        wp, ws, wo = (pr.sb(ctx, n, [P, D]) for n in ("wp", "ws", "wo"))
        b12 = pr.sb(ctx, "b12", [P, 2])
        bsum = pr.sb(ctx, "bsum", [P, 1])
        bo = pr.sb(ctx, "bo", [1, D])
        ones = pr.sb(ctx, "ones", [1, P])
        oc = pr.sb(ctx, "o_chunk", [P, 2, 2, CH, H, E])
        ot = pr.sb(ctx, "o_turned", [P, 2, 2, CW])
        mt = pr.sb(ctx, "mixed_turned", [P, 2, CW])
        m32 = pr.sb(ctx, "mixed", [P, 2, CH, D])
        loaded = pr.sem(ctx, "loaded")
        set_up = pr.sem(ctx, "set_up")
        gathered = pr.ev(ctx, "gathered")
        turned = pr.ev(ctx, "turned", 2)
        taken = pr.ev(ctx, "taken", 1)
        inner = pr.ev(ctx, "inner", 1)
        inner_taken = pr.ev(ctx, "inner_taken", 1)
        summed = pr.ev(ctx, "summed", 2)
        added = pr.ev(ctx, "added", 2)
        kept = pr.ev(ctx, "kept", 2)
        with nc.Block() as block:
            @block.sync
            def _(sp):
                for dst, src in ((wp, "l3_wp"), (ws, "l3_wos"), (wo, "l3_wo"), (b12, "l3_b12"), (bo, "l3_bo")):
                    sp.dma_start(dst[:], d[src]).then_inc(loaded, 16)

            @block.gpsimd
            def _(pool):
                pool.sem_inc(kept.sem, 2)

                def part(k, u, j):
                    hold(pool, pr.gate_p, added.sem, added.at(k))
                    pool.tensor_tensor(pr.x1[:, ds(k * CH, CH), :], pr.x1[:, ds(k * CH, CH), :], m32[:, u],
                                       ALU.add).then_inc(kept.sem, 1)

                two_a_turn(pool, part)

            @block.vector
            def _(v):
                v.wait_ge(loaded, 80)
                v.memset(ones[:], 1.0).then_inc(set_up, 1)
                v.tensor_tensor(bsum[:], b12[:, 0:1], b12[:, 1:2], ALU.add).then_inc(set_up, 1)
                v.sem_inc(added.sem, 2)

                def part(k, u, j):
                    v.wait_ge(turned.sem, turned.at(k - 2))
                    v.sem_inc(pr.gate_v, 1)
                    v.tensor_copy(oc[:, u, 0].rearrange("p t h e -> p h t e"),
                                  pr.oa[:, ds(j * H, H), u * CH:(u + 1) * CH, :])
                    v.tensor_copy(oc[:, u, 1].rearrange("p t h e -> p h t e"),
                                  pr.os[:, ds(j * H, H), u * CH:(u + 1) * CH, :]).then_inc(gathered.sem, 1)
                    v.wait_ge(kept.sem, kept.at(k - 2))
                    v.wait_ge(summed.sem, summed.at(k))
                    v.tensor_copy(m32[:, u], pr.ps[:, 4 + u].rearrange("p (t d) -> p t d", d=D))
                    v.tensor_tensor(pr.X[:, ds(k * CH, CH), :], pr.X[:, ds(k * CH, CH), :],
                                    pr.ps[:, 4 + u].rearrange("p (t d) -> p t d", d=D), ALU.add).then_inc(added.sem, 1)

                two_a_turn(v, part)

            @block.scalar
            def _(act):
                act.sem_inc(taken.sem, 1)
                act.sem_inc(inner_taken.sem, 1)
                act.wait_ge(set_up, 2)

                def part(k, u, j):
                    act.wait_ge(inner.sem, inner.at(k - 1))
                    act.wait_ge(turned.sem, turned.at(k))
                    nc.scalar.activation(ot[:, u], pr.ps[:, 0:2], ACT.Copy).then_inc(taken.sem, 1)
                    act.wait_ge(summed.sem, summed.at(k - 2))
                    act.wait_ge(inner.sem, inner.at(k))
                    nc.scalar.activation(mt[:, u], pr.ps[:, 2], ACT.Identity, bias=bsum[:]).then_inc(inner_taken.sem, 1)

                two_a_turn(act, part)

            @block.tensor
            def _(pe):
                pe.sem_inc(turned.sem, 2)
                pe.sem_inc(summed.sem, 2)
                pe.sem_inc(inner.sem, 1)
                pe.wait_ge(loaded, 80)
                pe.wait_ge(set_up, 2)

                def part(k, u, j):
                    pe.wait_ge(taken.sem, taken.at(k - 1))
                    pe.wait_ge(gathered.sem, gathered.at(k))
                    for a in range(2):
                        for t in range(CH):
                            mm = pe.transpose(pr.ps[:, a, t * P:(t + 1) * P],
                                              oc[:, u, a, t].rearrange("p h e -> p (h e)"), pr.idf[:])
                    mm.then_inc(turned.sem, 1)
                    pe.wait_ge(taken.sem, taken.at(k))
                    pe.wait_ge(inner_taken.sem, inner_taken.at(k - 1))
                    pe.matmul(pr.ps[:, 2], wp[:], ot[:, u, 0], start=True, stop=False)
                    pe.matmul(pr.ps[:, 2], ws[:], ot[:, u, 1], start=False, stop=True).then_inc(inner.sem, 1)
                    pe.wait_ge(inner_taken.sem, inner_taken.at(k))
                    pe.wait_ge(added.sem, added.at(k - 2))
                    for t in range(CH):
                        s = pr.ps[:, 4 + u, t * D:(t + 1) * D]
                        pe.matmul(s, mt[:, u, t * P:(t + 1) * P], wo[:], start=True, stop=False)
                        mm = pe.matmul(s, ones[:], bo[:], start=False, stop=True)
                    mm.then_inc(summed.sem, 1)

                two_a_turn(pe, part)


def l3_mlp(pr):
    nc, d = pr.nc, pr.d
    U = 4
    with ExitStack() as ctx:
        w1 = pr.sb(ctx, "w1", [P, U * D])
        b1 = pr.sb(ctx, "b1", [P, U])
        w2 = pr.sb(ctx, "w2", [P, U, D])
        b2 = pr.sb(ctx, "b2", [1, D])
        ones = pr.sb(ctx, "ones", [1, P])
        gm = pr.sb(ctx, "gm", [P, 2])
        xnc = pr.sb(ctx, "xnc", [P, 2, CH, D])
        chunk = pr.sb(ctx, "chunk", [P, 2, CW])
        hid = pr.sb(ctx, "hidden", [P, 2, U, CW])
        loaded = pr.sem(ctx, "loaded")
        set_up = pr.sem(ctx, "set_up")
        xn_sub = pr.ev(ctx, "xn_sub")
        xn_ready = pr.ev(ctx, "xn_ready")
        turned = pr.ev(ctx, "turned", 2)
        chunk_ready = pr.ev(ctx, "chunk_ready", 1)
        h_sum = pr.ev(ctx, "h_sum")
        h_ready = pr.ev(ctx, "h_ready", 4)
        y_sum = pr.ev(ctx, "y_sum", 2)
        added = pr.ev(ctx, "added", 2)
        with nc.Block() as block:
            @block.sync
            def _(sp):
                for dst, src in ((w1, "l3_w1"), (b1, "l3_b1m"), (w2, "l3_w2"), (b2, "l3_b2m"), (gm, "l3_gm")):
                    sp.dma_start(dst[:], d[src]).then_inc(loaded, 16)

            @block.vector
            def _(v):
                v.memset(ones[:], 1.0).then_inc(set_up, 1)
                v.sem_inc(added.sem, 2)

                def norm(k, u):
                    v.wait_ge(turned.sem, turned.at(k - 2))
                    v.tensor_tensor(xnc[:, u], pr.x1[:, ds(k * CH, CH), :], bc(pr.mean[:, ds(k * CH, CH)], D),
                                    ALU.subtract).then_inc(xn_sub.sem, 1)
                    v.wait_ge(xn_sub.sem, xn_sub.at(k))
                    v.tensor_tensor(xnc[:, u], xnc[:, u], bc(pr.rstd[:, ds(k * CH, CH)], D),
                                    ALU.mult).then_inc(xn_ready.sem, 1)

                def part(k, u, j):
                    norm(k, u)
                    v.wait_ge(y_sum.sem, y_sum.at(k))
                    v.tensor_tensor(pr.X[:, ds(k * CH, CH), :], pr.X[:, ds(k * CH, CH), :],
                                    pr.ps[:, 6 + u].rearrange("p (t d) -> p t d", d=D), ALU.add).then_inc(added.sem, 1)

                two_a_turn(v, part)

            @block.scalar
            def _(act):
                nc.scalar.preload_act_table(ACT.Gelu)
                act.sem_inc(chunk_ready.sem, 1)
                act.sem_inc(h_ready.sem, 4)
                act.wait_ge(loaded, 80)

                def part(k, u, j):
                    act.wait_ge(y_sum.sem, y_sum.at(k - 2))
                    act.wait_ge(turned.sem, turned.at(k))
                    nc.scalar.activation(chunk[:, u], pr.ps[:, 0], ACT.Identity, scale=gm[:, 0:1], bias=gm[:, 1:2])\
                        .then_inc(chunk_ready.sem, 1)
                    for i in range(U):
                        act.wait_ge(h_sum.sem, h_sum.at(k * U + i))
                        nc.scalar.activation(hid[:, u, i], pr.ps[:, 1 + i], ACT.Gelu, bias=b1[:, i:i + 1])\
                            .then_inc(h_ready.sem, 1)

                two_a_turn(act, part)

            @block.tensor
            def _(pe):
                pe.sem_inc(turned.sem, 2)
                pe.sem_inc(y_sum.sem, 2)
                pe.wait_ge(loaded, 80)
                pe.wait_ge(set_up, 1)

                def part(k, u, j):
                    pe.wait_ge(chunk_ready.sem, chunk_ready.at(k - 1))
                    pe.wait_ge(xn_ready.sem, xn_ready.at(k))
                    for t in range(CH):
                        mm = pe.transpose(pr.ps[:, 0, t * P:(t + 1) * P], xnc[:, u, t], pr.idf[:])
                    mm.then_inc(turned.sem, 1)
                    pe.wait_ge(chunk_ready.sem, chunk_ready.at(k))
                    for i in range(U):
                        pe.wait_ge(h_ready.sem, h_ready.at(k * U + i - U))
                        pe.matmul(pr.ps[:, 1 + i], w1[:, i * D:(i + 1) * D], chunk[:, u], start=True, stop=True)\
                            .then_inc(h_sum.sem, 1)
                    pe.wait_ge(added.sem, added.at(k - 2))
                    for t in range(CH):
                        s = pr.ps[:, 6 + u, t * D:(t + 1) * D]
                        for i in range(U):
                            if t == 0:
                                pe.wait_ge(h_ready.sem, h_ready.at(k * U + i))
                            pe.matmul(s, hid[:, u, i, t * P:(t + 1) * P], w2[:, i], start=i == 0, stop=False)
                        mm = pe.matmul(s, ones[:], b2[:], start=False, stop=True)
                    mm.then_inc(y_sum.sem, 1)

                two_a_turn(pe, part)


def program(nc, dram, out):
    pr = Prog(nc, dram, out)
    with ExitStack() as ctx:
        pr.X = pr.sb(ctx, "x", [P, NT, D])
        pr.xt = pr.sb(ctx, "xn_turned", [P, T])
        pr.mean = pr.sb(ctx, "mean", [P, NT])
        pr.rstd = pr.sb(ctx, "rstd", [P, NT])
        pr.inorm = pr.sb(ctx, "inverse_norm", [P, NT])
        pr.idf = pr.sb(ctx, "ident_f", [P, P])
        pr.idb = pr.sb(ctx, "ident_b", [P, P], BF16)
        pr.logits = pr.sb(ctx, "logits", [P, NT, 16])
        pr.gates = pr.sb(ctx, "gates", [P, NT, 17])
        pr.ps = ctx.enter_context(nc.psum_tensor("banks", [P, 8, 512], F32))
        pr.gate_v, pr.gate_p, pr.gate_a, pr.gate_e = (nc.alloc_semaphore("gate_" + e) for e in "vpae")
        pr.q_dram = nc.dram_tensor("q_parts", (3, B * P, N), BF16).ap()
        pr.k_dram = nc.dram_tensor("k_parts", (3, B * P, N), BF16).ap()
        pr.q2_dram = nc.dram_tensor("q2_parts", (3, B * P, N), BF16).ap()
        pr.k2_dram = nc.dram_tensor("k2_parts", (3, B * P, N), BF16).ap()
        pr.s_dram = nc.dram_tensor("selection_scores", (HEADS, N), F32).ap()
        load_constants(pr)
        pr.end()
        statistics(pr, norm=True)
        pr.end()
        with ExitStack() as layer:
            pr.kvp = pr.sb(layer, "kv_parts", [P, HEADS, TPB, 6 * E], BF16)
            pr.va = pr.sb(layer, "values", [P, HEADS, TPB, E + 1])
            pr.slot = pr.sb(layer, "slots", [P, HEADS, TPB])
            pr.o = pr.sb(layer, "head_outputs", [P, HEADS, TPB, E])
            l0_project(pr)
            pr.end()
            l0_select(pr)
            pr.end()
            l0_attention(pr)
            pr.end()
            out_project(pr, "wo0", "bo0", 1.0 / 3.0)
            pr.end()
        experts(pr, "m0", 8, 64, False)
        pr.end()
        statistics(pr)
        pr.end()
        l1_attention(pr)
        pr.end()
        top_gates(pr, 8, 1, False, "l1_bg")
        pr.end()
        experts(pr, "m1", 8, 128, False, 9)
        pr.end()
        statistics(pr)
        pr.end()
        l2_attention(pr)
        pr.end()
        top_gates(pr, 15, 3, True)
        pr.end()
        experts(pr, "m2", 17, 128, True)
        pr.end()
        statistics(pr)
        pr.end()
        with ExitStack() as layer:
            pr.x1 = pr.sb(layer, "x1", [P, NT, D])
            pr.mean2 = pr.sb(layer, "mean2", [P, NT])
            pr.rstd2 = pr.sb(layer, "rstd2", [P, NT])
            with ExitStack() as mixing:
                pr.va = pr.sb(mixing, "windowed_values", [P, HEADS, TPB, E + 1])
                pr.vs = pr.sb(mixing, "linear_values", [P, HEADS, TPB, E + 1])
                pr.st = pr.sb(mixing, "state_sums", [P, HEADS, TPB, E + 1])
                l3_inner_statistics(pr)
                pr.end()
                l3_project(pr)
                pr.end()
                pr.oa = pr.sb(mixing, "windowed_outputs", [P, HEADS, TPB, E])
                pr.os = pr.sb(mixing, "linear_outputs", [P, HEADS, TPB, E])
                l3_attention(pr)
                pr.end()
                l3_mix(pr)
                pr.end()
            statistics(pr, of=pr.x1)
            pr.end()
            l3_mlp(pr)
            pr.end()
        store_output(pr)


def kernel(**inputs):
    import ml_dtypes
    from concourse import bacc
    from concourse.bass_utils import run_bass_kernel_spmd

    g = {k: np.asarray(v) for k, v in inputs.items()}
    c = np.ascontiguousarray
    bf = ml_dtypes.bfloat16
    a = {}

    def heads_last(w):
        wk, wv = w
        lead = wk.shape[:-1]
        return c(np.stack([wk.reshape(*lead, H, E), wv.reshape(*lead, H, E)], -2).reshape(*lead, 2 * D))

    a["x"] = c(g["L0_attn_x"].reshape(NT, P, D).transpose(1, 0, 2).reshape(P, NT * D))
    a["ident_f"] = np.eye(P, dtype=np.float32)
    a["ident_b"] = np.eye(P, dtype=bf)
    a["wq"] = c(g["L0_attn_Wq"].T)
    a["wk"] = c(g["L0_attn_Wk"].T)
    a["wkv"] = heads_last((g["L0_attn_Wk"].T, g["L0_attn_Wv"].T))
    a["bkv"] = heads_last((g["L0_attn_bk"][None], g["L0_attn_bv"][None]))
    a["bq"] = c(g["L0_attn_bq"][:, None])
    a["bk"] = c(g["L0_attn_bk"][:, None])
    a["ws"] = c(g["L0_attn_Ws"].T)
    a["bs"] = c(g["L0_attn_bs"][:, None])
    a["cent"] = g["L0_ffn_centroids"]
    a["wroute"] = c(g["L0_ffn_w_route"].T)
    q, k = np.arange(P)[:, None], np.arange(P)[None]
    a["mask_band"] = np.concatenate([np.where(k < q, NEG, 0), 0.0 * (k + q), np.where(k > q, NEG, 0)], 1).astype(bf)
    a["places"] = c(np.broadcast_to(np.arange(N // 4, dtype=np.float32), (P, N // 4)))
    marks = np.zeros((3, 6, N), bf)
    for v in range(3):
        marks[v, v] = marks[v, 3 + v] = 1
    a["max_marks"] = marks
    a["wo0"] = c(g["L0_attn_Wo"].T)
    a["bo0"] = c(g["L0_attn_bo"][None])
    a["m0_w1"] = c(g["L0_ffn_w1"].reshape(4, 2, P, 64).transpose(2, 0, 1, 3).reshape(P, 4, P))
    a["m0_b1"] = c(g["L0_ffn_b1"].reshape(4, P).T[:, :, None])
    a["m0_w2"] = c(g["L0_ffn_w2"].reshape(4, P, D).transpose(1, 0, 2))
    a["m0_b2"] = g["L0_ffn_b2"]

    w = g["L1_attn_w_qkv"]
    a["l1_wq"], a["l1_wk"] = c(w[:, 0:D]), c(w[:, D:2 * D])
    a["l1_wo"] = g["L1_attn_w_out"]
    a["l1_wg"] = g["L1_ffn_Wg"]
    a["l1_bg"] = c(g["L1_ffn_bg"][None])
    a["mask_causal"] = np.where(k > q, NEG, 0.0).astype(bf)
    a["order"] = c(np.broadcast_to(np.arange(16, 0, -1, dtype=np.float32), (P, 16)))
    a["m1_w1"] = c(g["L1_ffn_W1"].transpose(1, 0, 2))
    a["m1_b1"] = c(g["L1_ffn_b1"].T[:, :, None])
    a["m1_w2"] = c(g["L1_ffn_W2"].transpose(1, 0, 2))
    a["m1_b2"] = np.concatenate([g["L1_ffn_b2"], g["L1_attn_b_out"][None]])

    wq = g["L2_attn_Wq"]
    three = np.stack([wq[0], wq[1], g["L2_attn_Wk"]])
    pairs = three.reshape(3, D // 2, 2, D)
    turned = np.stack([pairs[:, :, 1], pairs[:, :, 0]], 2).reshape(3, D, D)
    a["l2_wqk"] = c(np.stack([three, turned]).transpose(3, 0, 1, 2))
    a["l2_wv"] = c(g["L2_attn_Wv"].T)
    a["l2_wo"] = c(g["L2_attn_Wo"].T.reshape(2, D, D).transpose(1, 0, 2))
    a["l2_gate"] = c(np.concatenate([g["L2_ffn_gate_w"].T, np.zeros((D, 1), np.float32)], 1))
    theta = np.float32(10000.0) ** (np.float32(-2.0) * np.arange(0, D, 2, dtype=np.float32) / np.float32(D))
    angles = (np.arange(N, dtype=np.float32)[:, None] * theta.astype(np.float32)[None]).astype(np.float32)
    a["l2_cos"] = c(np.repeat(np.cos(angles), 2, axis=1).T.astype(np.float32))
    a["l2_sin"] = c(np.stack([-np.sin(angles), np.sin(angles)], 2).reshape(N, D).T.astype(np.float32))
    F, FS = P, 2 * P
    w1 = np.concatenate([g["L2_ffn_fc1_w"].reshape(15, 2, F, D),
                         g["L2_ffn_s_fc1_w"].reshape(2, 2, F, D).transpose(1, 0, 2, 3)])
    b1 = np.concatenate([g["L2_ffn_fc1_b"].reshape(15, 2, F), g["L2_ffn_s_fc1_b"].reshape(2, 2, F).transpose(1, 0, 2)])
    a["m2_w1"] = c(w1.transpose(3, 0, 1, 2).reshape(P, 17, 2 * P))
    a["m2_b1"] = c(b1.transpose(2, 0, 1))
    w2 = np.concatenate([g["L2_ffn_fc2_w"], g["L2_ffn_s_fc2_w"].reshape(D, 2, F).transpose(1, 0, 2)])
    a["m2_w2"] = c(w2.transpose(2, 0, 1))
    a["m2_b2"] = np.concatenate([g["L2_ffn_fc2_b"], g["L2_ffn_s_fc2_b"][None], np.zeros((1, D), np.float32)])
    a["m2_mult"] = c(np.concatenate([g["L2_ffn_geglu_mult"], g["L2_ffn_s_geglu_mult"].reshape(2, F)]).T)

    wa, ws = g["L3_attn_Wqkv_a"], g["L3_attn_Wqkv_s"]
    ba, bs = g["L3_attn_bqkv_a"], g["L3_attn_bqkv_s"]
    a["l3_wqk"] = c(np.stack([wa[:, :D], wa[:, D:2 * D], ws[:, :D], ws[:, D:2 * D]], 1))
    a["l3_bqk"] = c(np.stack([ba[:D], ba[D:2 * D], bs[:D], bs[D:2 * D]], 1))
    a["l3_wva"], a["l3_bva"] = c(wa[:, 2 * D:]), c(ba[None, 2 * D:])
    a["l3_wkv"], a["l3_bkv"] = c(ws[:, D:]), c(bs[None, D:])
    a["l3_wb"] = c(g["L3_ffn_weights"].T)
    a["l3_wbs"] = c(g["L3_ffn_scale"][None])
    a["l3_wbias"] = c(g["L3_ffn_bias"][None])
    a["l3_g1"], a["l3_b1"] = c(g["L3_attn_g1"][:, None]), c(g["L3_attn_b1"][:, None])
    a["own_head"] = (np.arange(P)[:, None] // E == np.arange(H * (E + 1))[None] // (E + 1)).astype(np.float32)
    a["mask_win_q"] = np.concatenate([np.where(k <= q, NEG, 0.0), np.where(k > q, NEG, 0.0)], 1).astype(bf)
    a["mask_win_k"] = np.concatenate([np.where(k < q, NEG, 0.0), np.where(k >= q, NEG, 0.0)], 1).astype(bf)
    a["tri"] = (k >= q).astype(np.float32)
    a["l3_wp"], a["l3_wos"], a["l3_wo"] = g["L3_attn_Wp_a"], g["L3_attn_Wo_s"], g["L3_attn_Wo"]
    a["l3_b12"] = c(np.stack([g["L3_attn_bp_a"], g["L3_attn_bo_s"]], 1))
    a["l3_bo"] = c(g["L3_attn_bo"][None])
    a["l3_w1"] = g["L3_attn_W1"]
    a["l3_b1m"] = c(g["L3_attn_b1m"].reshape(4, D).T)
    a["l3_w2"] = c(g["L3_attn_W2"].reshape(4, D, D).transpose(1, 0, 2))
    a["l3_b2m"] = c(g["L3_attn_b2m"][None])
    a["l3_gm"] = c(np.stack([g["L3_attn_gm"], g["L3_attn_bm"]], 1))

    nc = bacc.Bacc("TRN2", target_bir_lowering=False, num_devices=1)
    dram, arrays = {}, {}
    for name, v in a.items():
        v = c(v)
        arrays["in_" + name] = v
        dram[name] = nc.dram_tensor("in_" + name, v.shape, mybir.dt.from_np(v.dtype), kind="ExternalInput").ap()
    out = nc.dram_tensor("out_0", (P, NT * D), F32, kind="ExternalOutput").ap()
    program(nc, dram, out)
    r = run_bass_kernel_spmd(nc, [arrays], core_ids=[0])
    o = r.results[0]["out_0"]
    return o.reshape(P, NT, D).transpose(1, 0, 2).reshape(B, N, D)
```

```python
from contextlib import ExitStack

import numpy as np

import concourse.bass as bass
from concourse import mybir

F32 = mybir.dt.float32
BF16 = mybir.dt.bfloat16
ACT = mybir.ActivationFunctionType
ALU = mybir.AluOpType
AX = mybir.AxisListType.X

P = 128
B, N, D = 4, 1024, 128
T = B * N
NT = T // P
TPB = N // P
CH = 4
NC = NT // CH
CW = CH * P
H, E = 16, 8
HEADS = B * H
KQ = 9 * E
MROW = 96
NEG = -1.0e30
LOW = -3.0e38


class Ev:

    def __init__(self, sem, prime):
        self.sem, self.prime = sem, prime

    def at(self, i):
        return i + (self.prime + 1)


class Chain:

    def __init__(self, eng, sem):
        self.eng, self.sem, self.n, self.base = eng, sem, 0, 0

    def step(self, ins):
        ins.then_inc(self.sem, 1)
        self.n += 1

    def wait(self):
        self.eng.wait_ge(self.sem, self.base + self.n)

    def link(self, ins):
        self.step(ins)
        self.wait()


class Prog:

    def __init__(self, nc, dram, out):
        self.nc, self.d, self.out = nc, dram, out
        self.names = 0

        self.stage = []

    def sem(self, ctx, name):
        self.names += 1
        self.stage.append(self.nc.alloc_semaphore(f"{name}_{self.names}"))
        return self.stage[-1]

    def end(self):
        self.nc.clear_and_free_semaphores(self.stage)
        self.stage = []
        self.nc.all_engine_barrier()

    def ev(self, ctx, name, prime=0):
        return Ev(self.sem(ctx, name), prime)

    def sb(self, ctx, name, shape, dt=F32):
        self.names += 1
        return ctx.enter_context(self.nc.sbuf_tensor(f"{name}_{self.names}", shape, dt))


def hold(eng, gate, sem, value):
    eng.wait_ge(sem, value)
    eng.sem_inc(gate, 1)


def ds(i, n=1):
    return bass.ds(i, n)


def one(ap, i):
    s = ap[:, ds(i, 1)]
    names = "abcdef"[:len(s.shape) - 2]
    if len(s.shape) == 3:
        return s.rearrange("p o a -> p (o a)")
    return s.rearrange(f"p o {' '.join(names)} -> p (o {names[0]}) {' '.join(names[1:])}")


def bc(ap, n):
    return ap.unsqueeze(len(ap.shape)).broadcast_to([*ap.shape, n])


def load_constants(pr):
    nc, d = pr.nc, pr.d
    with ExitStack() as ctx:
        loaded = pr.sem(ctx, "loaded")
        with nc.Block() as block:
            @block.sync
            def _(sp):
                sp.dma_start(pr.X[:], d["x"].rearrange("p (t d) -> p t d", d=D)).then_inc(loaded, 16)
                sp.dma_start(pr.idf[:], d["ident_f"]).then_inc(loaded, 16)
                sp.dma_start(pr.idb[:], d["ident_b"]).then_inc(loaded, 16)
                sp.wait_ge(loaded, 48)


def statistics(pr, norm=False, of=None):
    nc = pr.nc
    of = pr.X if of is None else of
    with ExitStack() as ctx:
        stats = pr.sb(ctx, "stats", [P, CH, 6])
        mv = pr.sb(ctx, "mv", [P, CH, 2])
        var = pr.sb(ctx, "var", [P, NT])
        std = pr.sb(ctx, "std", [P, NT])
        ssq = pr.sb(ctx, "ssq", [P, NT])
        nrm = pr.sb(ctx, "nrm", [P, NT])
        dv = pr.sem(ctx, "dv")
        eps = pr.sb(ctx, "eps", [P, 1])
        var_done = pr.sem(ctx, "var_done")
        std_done = pr.sem(ctx, "std_done")
        with nc.Block() as block:
            @block.vector
            def _(v):
                v.memset(eps[:], 1e-5).then_inc(var_done, 1)
                per = CH + CH + 2
                with v.Fori(0, NC) as k:
                    c = Chain(v, dv)
                    c.base = k * per
                    for t in range(CH):
                        c.step(v.bn_stats(stats[:, t, :], one(of, k * CH + t)))
                    c.wait()
                    v.sem_inc(pr.gate_v, 1)
                    for t in range(CH):
                        c.step(v.bn_aggr(mv[:, t, :], stats[:, t, :]))
                    c.wait()
                    c.step(v.tensor_copy(pr.mean[:, ds(k * CH, CH)], mv[:, :, 0]))
                    c.step(v.tensor_copy(var[:, ds(k * CH, CH)], mv[:, :, 1]))
                v.wait_ge(dv, NC * per)
                v.sem_inc(var_done, 1)
                v.wait_ge(std_done, 1)
                v.reciprocal(pr.rstd[:], std[:]).then_inc(dv, 1)
                v.wait_ge(dv, NC * per + 1)
                if norm:
                    v.scalar_tensor_tensor(out=ssq[:], in0=var[:], scalar=float(D), in1=pr.rstd[:],
                                           op0=ALU.mult, op1=ALU.mult).then_inc(dv, 1)
                    v.wait_ge(dv, NC * per + 2)
                    v.tensor_tensor(ssq[:], ssq[:], pr.rstd[:], ALU.mult).then_inc(var_done, 1)
                    v.wait_ge(std_done, 2)
                    v.tensor_scalar(nrm[:], nrm[:], 1e-12, None, ALU.max).then_inc(dv, 1)
                    v.wait_ge(dv, NC * per + 3)
                    v.reciprocal(pr.inorm[:], nrm[:])

            @block.scalar
            def _(act):
                act.wait_ge(var_done, 2)
                nc.scalar.activation(std[:], var[:], ACT.Sqrt, bias=eps[:]).then_inc(std_done, 1)
                if norm:
                    act.wait_ge(var_done, 3)
                    nc.scalar.activation(nrm[:], ssq[:], ACT.Sqrt).then_inc(std_done, 1)




def split_rows(pr, ctx, name):
    return (pr.sb(ctx, name + "32", [P, 2, CW]), pr.sb(ctx, name + "_parts", [P, 2, 3, CW], BF16),
            pr.sb(ctx, name + "_rest", [P, CW]))


def l0_project(pr):
    nc, d = pr.nc, pr.d
    with ExitStack() as ctx:
        wq = pr.sb(ctx, "wq", [P, D])
        wk = pr.sb(ctx, "wk", [P, D])
        wkv = pr.sb(ctx, "wkv", [P, 2 * D])
        ws = pr.sb(ctx, "ws", [P, H])
        wroute = pr.sb(ctx, "wroute", [P, 16])
        cent = pr.sb(ctx, "cent", [8, D])
        cn2 = pr.sb(ctx, "cn2", [8, 1])
        csq = pr.sb(ctx, "csq", [8, D])
        bq = pr.sb(ctx, "bq", [P, 1])
        bk = pr.sb(ctx, "bk", [P, 1])
        bs = pr.sb(ctx, "bs", [H, 1])
        bkv = pr.sb(ctx, "bkv", [P, 2 * D])
        xnc = pr.sb(ctx, "xnc", [P, 2, CH, D])
        chunk = pr.sb(ctx, "chunk", [P, 2, CW])
        q32, qparts, qrest = split_rows(pr, ctx, "q")
        k32, kparts, krest = split_rows(pr, ctx, "k")
        kv32 = pr.sb(ctx, "kv32", [P, CH, 2 * D])
        kvrest = pr.sb(ctx, "kvrest", [P, CH, 2 * D])
        kvhalf = pr.sb(ctx, "kvhalf", [P, CH, 2 * D], BF16)
        srow = pr.sb(ctx, "srow", [H, 2, CW])
        loaded = pr.sem(ctx, "weights_loaded")
        dv = pr.sem(ctx, "dv_steps")
        pl = pr.sem(ctx, "pool_steps")
        setup = pr.sem(ctx, "centroids_steps")
        xn_ready = pr.ev(ctx, "xn_ready")
        turned = pr.ev(ctx, "xn_turned", 2)
        chunk_ready = pr.ev(ctx, "chunk_ready", 1)
        chunk_kept = pr.ev(ctx, "chunk_kept", 2)
        q_sum = pr.ev(ctx, "q_sum")
        k_sum = pr.ev(ctx, "k_sum")
        kv_sum = pr.ev(ctx, "kv_sum")
        s_sum = pr.ev(ctx, "s_sum")
        r_sum = pr.ev(ctx, "r_sum", 2)
        q_taken = pr.ev(ctx, "q_taken", 1)
        k_taken = pr.ev(ctx, "k_taken", 1)
        kv_taken = pr.ev(ctx, "kv_taken", 1)
        s_taken = pr.ev(ctx, "s_taken", 1)
        r_taken = pr.ev(ctx, "r_taken", 1)
        q_split = pr.ev(ctx, "q_split", 2)
        k_split = pr.ev(ctx, "k_split", 2)
        qk_stored = [pr.sem(ctx, f"qk_stored{u}") for u in range(2)]
        s_stored = [pr.sem(ctx, f"s_stored{u}") for u in range(2)]
        turn_ps, q_ps, k_ps, s_ps, r_ps = pr.ps[:, 0], pr.ps[:, 1], pr.ps[:, 2], pr.ps[:, 5], pr.ps[:, 6]
        kv_ps = pr.ps[:, 3:5]
        cent_ps = pr.ps[:, 7]
        WEIGHTS = 10 * 16

        def chunks(eng, body):
            with eng.Fori(0, NC // 2) as j:
                for u in range(2):
                    body(j * 2 + u, u, j)

        with nc.Block() as block:
            @block.sync
            def _(sp):
                for dst, src in ((wq, "wq"), (wk, "wk"), (wkv, "wkv"), (ws, "ws"), (cent, "cent"), (bq, "bq"),
                                 (bk, "bk"), (bs, "bs")):
                    sp.dma_start(dst[:], d[src]).then_inc(loaded, 16)
                sp.dma_start(bkv[:], d["bkv"].broadcast_to([P, 2 * D])).then_inc(loaded, 16)
                sp.dma_start(wroute[:, 0:8], d["wroute"]).then_inc(loaded, 16)
                for u in range(2):
                    sp.sem_inc(qk_stored[u], 32)
                    sp.sem_inc(s_stored[u], 16)

                def store(k, u, j):
                    sp.wait_ge(q_split.sem, q_split.at(k))
                    sp.dma_start(pr.q_dram[:, :, ds(u * CW, CW)].rearrange("a (b p) t -> b p a t", p=P)[ds(j, 1)]
                                 .rearrange("b p a t -> (b p) a t"), qparts[:, u]).then_inc(qk_stored[u], 16)
                    sp.wait_ge(k_split.sem, k_split.at(k))
                    sp.dma_start(pr.k_dram[:, :, ds(u * CW, CW)].rearrange("a (b p) t -> b p a t", p=P)[ds(j, 1)]
                                 .rearrange("b p a t -> (b p) a t"), kparts[:, u]).then_inc(qk_stored[u], 16)
                    sp.wait_ge(s_taken.sem, s_taken.at(k))
                    sp.dma_start(pr.s_dram.rearrange("(b h) t -> b h t", h=H)[ds(j, 1), :, u * CW:(u + 1) * CW]
                                 .rearrange("b h t -> (b h) t"), srow[:, u]).then_inc(s_stored[u], 16)

                chunks(sp, store)
                for u in range(2):
                    sp.wait_ge(qk_stored[u], 32 + 32 * NC // 2)
                    sp.wait_ge(s_stored[u], 16 + 16 * NC // 2)

            @block.gpsimd
            def _(pool):
                pool.sem_inc(chunk_kept.sem, 2)
                pool.sem_inc(q_split.sem, 2)
                pool.sem_inc(k_split.sem, 2)

                def part(k, u, j):
                    c = Chain(pool, pl)
                    c.base = k * 6
                    hold(pool, pr.gate_p, chunk_ready.sem, chunk_ready.at(k))
                    pool.tensor_copy(pr.xt[:, ds(k * CW, CW)], chunk[:, u]).then_inc(chunk_kept.sem, 1)
                    for taken, split, x32, parts, rest in ((q_taken, q_split, q32, qparts, qrest),
                                                           (k_taken, k_split, k32, kparts, krest)):
                        hold(pool, pr.gate_p, taken.sem, taken.at(k))
                        c.link(pool.tensor_tensor(rest[:], x32[:, u], parts[:, u, 0], ALU.subtract))
                        pool.sem_inc(pr.gate_p, 1)
                        c.link(pool.tensor_copy(parts[:, u, 1], rest[:]))
                        pool.sem_inc(pr.gate_p, 1)
                        c.step(pool.tensor_tensor(parts[:, u, 2], rest[:], parts[:, u, 1], ALU.subtract))
                        c.wait()
                        pool.sem_inc(split.sem, 1)

                chunks(pool, part)

            @block.vector
            def _(v):
                v.wait_ge(loaded, WEIGHTS)
                v.memset(pr.va[:, :, :, E:E + 1], 1.0).then_inc(dv, 1)
                v.tensor_tensor(csq[:], cent[:], cent[:], ALU.mult).then_inc(dv, 1)
                v.wait_ge(dv, 2)
                v.reduce_sum(cn2[:], csq[:], AX).then_inc(setup, 1)
                v.wait_ge(setup, 2)
                v.tensor_scalar(cn2[:], cn2[:], 1e-12, None, ALU.max).then_inc(dv, 1)
                v.wait_ge(dv, 3)
                v.reciprocal(cn2[:], cn2[:]).then_inc(dv, 1)
                v.wait_ge(dv, 4)
                v.tensor_scalar(cent[:], cent[:], cn2[:], None, ALU.mult).then_inc(setup, 1)
                v.wait_ge(setup, 4)
                v.tensor_copy(wroute[:, 8:16], cent_ps[:, 0:8]).then_inc(setup, 1)
                v.sem_inc(kv_taken.sem, 1)

                def part(k, u, j):
                    c = Chain(v, dv)
                    c.base = k * 10 + 4
                    v.wait_ge(turned.sem, turned.at(k - 2))
                    c.link(v.tensor_tensor(xnc[:, u], pr.X[:, ds(k * CH, CH), :], bc(pr.mean[:, ds(k * CH, CH)], D),
                                           ALU.subtract))
                    v.tensor_tensor(xnc[:, u], xnc[:, u], bc(pr.rstd[:, ds(k * CH, CH)], D),
                                    ALU.mult).then_inc(xn_ready.sem, 1)
                    v.wait_ge(kv_sum.sem, kv_sum.at(k))
                    c.step(v.tensor_tensor(kv32[:, 0:2], kv_ps[:, 0].rearrange("p (t c) -> p t c", t=2),
                                           bkv[:].unsqueeze(1).broadcast_to([P, 2, 2 * D]), ALU.add))
                    c.link(v.tensor_tensor(kv32[:, 2:4], kv_ps[:, 1].rearrange("p (t c) -> p t c", t=2),
                                           bkv[:].unsqueeze(1).broadcast_to([P, 2, 2 * D]), ALU.add))
                    v.sem_inc(kv_taken.sem, 1)
                    heads = kv32[:].rearrange("p t (h c) -> p h t c", c=2 * E)
                    c.step(v.tensor_copy(pr.va[:, ds(j * H, H), u * CH:(u + 1) * CH, 0:E], heads[:, :, :, E:2 * E]))
                    c.link(v.tensor_copy(kvhalf[:], kv32[:]))
                    c.step(v.tensor_tensor(kvrest[:], kv32[:], kvhalf[:], ALU.subtract))
                    pv = pr.kvp[:, ds(j * H, H), u * CH:(u + 1) * CH, :]
                    c.wait()
                    v.sem_inc(pr.gate_v, 1)
                    c.link(v.tensor_copy(pv[:, :, :, 0:16], kvhalf[:].rearrange("p t (h c) -> p h t c", c=16)))
                    c.link(v.tensor_copy(kvhalf[:], kvrest[:]))
                    v.sem_inc(pr.gate_v, 1)
                    c.step(v.tensor_copy(pv[:, :, :, 16:32], kvhalf[:].rearrange("p t (h c) -> p h t c", c=16)))
                    c.step(v.tensor_tensor(pv[:, :, :, 32:48], kvrest[:].rearrange("p t (h c) -> p h t c", c=16),
                                           kvhalf[:].rearrange("p t (h c) -> p h t c", c=16), ALU.subtract))
                    c.wait()
                    v.sem_inc(pr.gate_v, 1)
                    assert c.n == 10

                chunks(v, part)

            @block.scalar
            def _(act):
                act.wait_ge(setup, 1)
                nc.scalar.activation(cn2[:], cn2[:], ACT.Sqrt).then_inc(setup, 1)
                nc.scalar.preload_act_table(ACT.Identity)
                for e in (chunk_ready, q_taken, k_taken, s_taken, r_taken):
                    act.sem_inc(e.sem, 1)

                def part(k, u, j):
                    act.wait_ge(r_sum.sem, r_sum.at(k - 2))
                    act.wait_ge(chunk_kept.sem, chunk_kept.at(k - 2))
                    act.wait_ge(turned.sem, turned.at(k))
                    nc.scalar.activation(chunk[:, u], turn_ps, ACT.Copy).then_inc(chunk_ready.sem, 1)
                    act.wait_ge(qk_stored[u], j * 32 + 32)
                    for total, taken, split, ps, bias, x32, parts in (
                            (q_sum, q_taken, q_split, q_ps, bq, q32, qparts),
                            (k_sum, k_taken, k_split, k_ps, bk, k32, kparts)):
                        act.wait_ge(split.sem, split.at(k - 2))
                        act.wait_ge(total.sem, total.at(k))
                        nc.scalar.activation(x32[:, u], ps, ACT.Identity, bias=bias[:])
                        nc.scalar.activation(parts[:, u, 0], ps, ACT.Identity, bias=bias[:]).then_inc(taken.sem, 1)
                    act.wait_ge(s_stored[u], j * 16 + 16)
                    act.wait_ge(s_sum.sem, s_sum.at(k))
                    nc.scalar.activation(srow[:, u], s_ps[0:H], ACT.Identity, bias=bs[:]).then_inc(s_taken.sem, 1)
                    hold(act, pr.gate_a, r_sum.sem, r_sum.at(k))
                    nc.scalar.activation(pr.logits[:, ds(k * CH, CH), :],
                                         r_ps[:, 0:CH * 16].rearrange("p (t c) -> p t c", c=16),
                                         ACT.Copy).then_inc(r_taken.sem, 1)

                chunks(act, part)

            @block.tensor
            def _(pe):
                pe.wait_ge(loaded, WEIGHTS)
                pe.sem_inc(turned.sem, 2)
                pe.sem_inc(r_sum.sem, 2)
                pe.wait_ge(setup, 3)
                pe.transpose(cent_ps[:, 0:8], cent[:], pr.idf[0:8, 0:8]).then_inc(setup, 1)
                pe.wait_ge(setup, 5)

                def part(k, u, j):
                    pe.wait_ge(xn_ready.sem, xn_ready.at(k))
                    pe.wait_ge(chunk_ready.sem, chunk_ready.at(k - 1))
                    for t in range(CH):
                        mm = pe.transpose(turn_ps[:, t * P:(t + 1) * P], xnc[:, u, t], pr.idf[:])
                    mm.then_inc(turned.sem, 1)
                    pe.wait_ge(chunk_ready.sem, chunk_ready.at(k))
                    pe.wait_ge(q_taken.sem, q_taken.at(k - 1))
                    pe.matmul(q_ps, wq[:], chunk[:, u], start=True, stop=True).then_inc(q_sum.sem, 1)
                    pe.wait_ge(k_taken.sem, k_taken.at(k - 1))
                    pe.matmul(k_ps, wk[:], chunk[:, u], start=True, stop=True).then_inc(k_sum.sem, 1)
                    pe.wait_ge(kv_taken.sem, kv_taken.at(k - 1))
                    for t in range(CH):
                        mm = pe.matmul(kv_ps[:, t // 2, (t % 2) * 2 * D:(t % 2 + 1) * 2 * D],
                                       chunk[:, u, t * P:(t + 1) * P], wkv[:], start=True, stop=True)
                    mm.then_inc(kv_sum.sem, 1)
                    pe.wait_ge(s_taken.sem, s_taken.at(k - 1))
                    pe.matmul(s_ps[0:H], ws[:], chunk[:, u], start=True, stop=True).then_inc(s_sum.sem, 1)
                    pe.wait_ge(r_taken.sem, r_taken.at(k - 1))
                    for t in range(CH):
                        mm = pe.matmul(r_ps[:, t * 16:(t + 1) * 16], chunk[:, u, t * P:(t + 1) * P], wroute[:],
                                       start=True, stop=True)
                    mm.then_inc(r_sum.sem, 1)

                chunks(pe, part)


def l0_select(pr):
    nc, d = pr.nc, pr.d
    TOP = N // 4
    NE = 8
    with ExitStack() as ctx:
        s0 = pr.sb(ctx, "s0", [HEADS, N])
        s1 = pr.sb(ctx, "s1", [HEADS, N])
        ones = pr.sb(ctx, "ones", [HEADS, N])
        best = pr.sb(ctx, "best", [HEADS, 8])
        lg = pr.sb(ctx, "lg", [P, NT, NE])
        w8 = pr.sb(ctx, "w8", [P, NT, NE])
        w8b = pr.sb(ctx, "w8b", [P, NT, NE])
        m1 = pr.sb(ctx, "m1", [P, NT])
        m2 = pr.sb(ctx, "m2", [P, NT])
        cnt = pr.sb(ctx, "cnt", [P, NT])
        loaded = pr.sem(ctx, "scores_loaded")
        dv = pr.sem(ctx, "dv_steps")
        slots_ready = pr.sem(ctx, "slots_ready")
        slots_turned = pr.sem(ctx, "slots_turned")
        lg_ready = pr.sem(ctx, "lg_ready")
        exp_done = pr.sem(ctx, "exp_done")
        with nc.Block() as block:
            @block.sync
            def _(sp):
                sp.dma_start(s0[:], pr.s_dram).then_inc(loaded, 16)

            @block.vector
            def _(v):
                c = Chain(v, dv)
                c.link(v.tensor_tensor(w8[:], pr.logits[:, :, 8:16], bc(pr.inorm[:], NE), ALU.mult))
                c.link(v.tensor_tensor(lg[:], w8[:], pr.logits[:, :, 0:8], ALU.add))
                c.link(v.reduce_max(m1[:], lg[:], AX))
                v.tensor_tensor(w8[:], lg[:], bc(m1[:], NE), ALU.subtract).then_inc(lg_ready, 1)
                c.link(v.tensor_tensor(w8b[:], lg[:], bc(m1[:], NE), ALU.is_ge))
                c.link(v.reduce_sum(cnt[:], w8b[:], AX))
                c.link(v.scalar_tensor_tensor(out=w8b[:], in0=w8b[:], scalar=LOW, in1=lg[:], op0=ALU.mult,
                                              op1=ALU.add))
                c.link(v.reduce_max(m2[:], w8b[:], AX))
                c.link(v.tensor_scalar(cnt[:], cnt[:], 2.0, None, ALU.is_ge))
                c.link(v.tensor_tensor(m1[:], m1[:], cnt[:], ALU.mult))
                c.link(v.tensor_scalar(cnt[:], cnt[:], 1.0, -LOW, ALU.subtract, ALU.mult))
                c.link(v.tensor_tensor(m1[:], m1[:], cnt[:], ALU.add))
                c.link(v.tensor_tensor(m2[:], m2[:], m1[:], ALU.max))
                c.link(v.tensor_tensor(lg[:], lg[:], bc(m2[:], NE), ALU.is_ge))
                v.wait_ge(exp_done, 1)
                c.link(v.tensor_tensor(w8b[:], w8[:], lg[:], ALU.mult))
                c.link(v.reduce_sum(m1[:], w8b[:], AX))
                c.link(v.reciprocal(m2[:], m1[:]))
                c.link(v.tensor_tensor(pr.gates[:, :, 0:NE], w8b[:], bc(m2[:], NE), ALU.mult))
                v.wait_ge(loaded, 16)
                c.step(v.memset(ones[:], 1.0))
                c.link(v.tensor_copy(s1[:], s0[:]))
                for r in range(TOP // 8):
                    c.link(v.max(best[:], s1[:]))
                    c.link(v.match_replace(s1[:], best[:], s1[:], LOW))
                c.link(v.tensor_tensor(s1[:], s1[:], s0[:], ALU.not_equal))
                c.link(v.tensor_tensor_scan(s0[:], ones[:], s1[:], 0.0, ALU.mult, ALU.add))
                c.link(v.tensor_tensor(s0[:], s0[:], s1[:], ALU.mult))
                v.tensor_scalar(s0[:], s0[:], -1.0, None, ALU.add).then_inc(slots_ready, 1)
                v.wait_ge(slots_turned, 1)
                v.tensor_copy(pr.slot[:], pr.ps[:, 0].rearrange("p (t n) -> p n t", n=HEADS))

            @block.scalar
            def _(act):
                act.wait_ge(lg_ready, 1)
                nc.scalar.activation(w8[:], w8[:], ACT.Exp).then_inc(exp_done, 1)

            @block.tensor
            def _(pe):
                pe.wait_ge(slots_ready, 1)
                for t in range(TPB):
                    mm = pe.transpose(pr.ps[:, 0, t * HEADS:(t + 1) * HEADS], s0[:, t * P:(t + 1) * P],
                                      pr.idf[0:HEADS, 0:HEADS])
                mm.then_inc(slots_turned, 1)


def l0_attention(pr):
    nc, d = pr.nc, pr.d
    TOP, GLOB, V3 = N // 4, 64, 3
    SLOTS = TOP // P
    SCALE = float(E) ** -0.5
    KM = MROW + 2 * V3
    G_SEL, G_TURN, G_LOC, G_TOP, G_GLOB, G_MAX, NG = 0, 1, 2, 10, 14, 15, 16
    LG_GLOB, LG_TOP, LG_LOC, NL = 0, 1, 3, 7
    VA = E + 1
    VR = V3 * VA
    with ExitStack() as ctx:
        qst = [pr.sb(ctx, f"q_stack{u}", [P, N], BF16) for u in range(2)]
        kst = [pr.sb(ctx, f"k_stack{u}", [P, N], BF16) for u in range(2)]
        ksel = [pr.sb(ctx, f"k_selected{u}", [P, TOP], BF16) for u in range(2)]
        kglob = [pr.sb(ctx, f"k_global{u}", [P, GLOB], BF16) for u in range(2)]
        krep = pr.sb(ctx, "k_repeated", [P, SLOTS, KQ], BF16)
        kvp = [pr.sb(ctx, f"kv_parts_head{u}", [P, TPB, 6 * E], BF16) for u in range(2)]
        v_loc = [pr.sb(ctx, f"v_banded{u}", [P, TPB, VR]) for u in range(2)]
        v_top = [pr.sb(ctx, f"v_selected{u}", [P, SLOTS, VR]) for u in range(2)]
        v_glob = [pr.sb(ctx, f"v_global{u}", [GLOB, VR]) for u in range(2)]
        hot = [pr.sb(ctx, f"one_hot{u}", [P, TPB, TOP], BF16) for u in range(2)]
        slot8 = pr.sb(ctx, "slot8", [P, TPB])
        places = pr.sb(ctx, "places", [P, TOP])
        mask = pr.sb(ctx, "band_mask", [P, 3 * P], BF16)
        mx = pr.sb(ctx, "maxima", [P, V3, TPB])
        mrow = [pr.sb(ctx, f"max_rows{u}", [P, TPB, KM], BF16) for u in range(2)]
        p_loc = pr.sb(ctx, "p_local", [P, TPB, 3 * P])
        p_top = pr.sb(ctx, "p_top", [P, SLOTS, N])
        p_glob = pr.sb(ctx, "p_global", [GLOB, N])
        sums = [pr.sb(ctx, f"sums{u}", [VR, N]) for u in range(2)]
        zeroed = pr.sem(ctx, "zeroed")
        consts = pr.sem(ctx, "consts")
        stacks = [pr.sem(ctx, f"stacks{u}") for u in range(2)]
        first_part = pr.sem(ctx, "first_part")
        psteps = pr.sem(ctx, "pool_steps")
        hot_ready = pr.ev(ctx, "hot_ready", 1)
        glob_ready = pr.ev(ctx, "glob_ready")
        kvp_ready = pr.ev(ctx, "kv_parts_ready")
        v_ready = pr.ev(ctx, "values_ready")
        scored = pr.ev(ctx, "scored_by_query", 2 * NG)
        reduced = pr.ev(ctx, "reduced", 2)
        rows_ready = pr.ev(ctx, "max_rows_ready")
        keyed = pr.ev(ctx, "scored_by_key", 2 * NL)
        exped = pr.ev(ctx, "exped", 2)
        summed = pr.ev(ctx, "values_summed", 2)
        taken = pr.ev(ctx, "sums_taken", 1)
        stored = [pr.sem(ctx, f"sums_stored{u}") for u in range(2)]
        parts_q = pr.q_dram
        parts_k = pr.k_dram

        with nc.Block() as block:
            @block.sync
            def _(sp):
                sp.dma_start(mask[:], d["mask_band"]).then_inc(consts, 16)
                sp.dma_start(places[:], d["places"]).then_inc(consts, 16)
                for u in range(2):
                    sp.sem_inc(stored[u], 16)
                sp.wait_ge(zeroed, 18)
                for u in range(2):
                    for v3, t in ((0, kst[u]), (1, ksel[u]), (2, kglob[u])):
                        sp.dma_start(t[MROW:KM, :], d["max_marks"][v3, :, 0:t.shape[1]]).then_inc(consts, 16)

                def load(n, u):
                    sp.wait_ge(keyed.sem, keyed.at((n - 2) * NL + NL - 1))
                    for a in range(3):
                        rows = slice(a * 3 * E, (a + 1) * 3 * E)
                        sp.dma_start(qst[u][rows],
                                     parts_q[:, ds(n * E, E), :]).then_inc(stacks[u], 16)
                        sp.dma_start(kst[u][rows],
                                     parts_k[a:a + 1, ds(n * E, E), :].broadcast_to([3, E, N])).then_inc(stacks[u], 16)

                def store(n, u):
                    sp.wait_ge(taken.sem, taken.at(n))
                    sp.dma_start(pr.sums_dram[ds(n)].rearrange("o r t -> (o r) t"), sums[u][:])\
                        .then_inc(stored[u], 16)

                for u in range(2):
                    load(u, u)
                with sp.Fori(0, HEADS // 2 - 1) as j:
                    for u in range(2):
                        load(j * 2 + u + 2, u)
                        store(j * 2 + u, u)
                for u in range(2):
                    store(HEADS - 2 + u, u)
                    sp.wait_ge(stored[u], 16 + 16 * HEADS // 2)

            @block.gpsimd
            def _(pool):
                for u in range(2):
                    for t in (qst[u], kst[u], ksel[u], kglob[u], mrow[u]):
                        pool.memset(t[:], 0.0).then_inc(zeroed, 1)
                    for t in (v_loc[u], v_top[u], v_glob[u]):
                        pool.memset(t[:], 0.0).then_inc(zeroed, 1)
                pool.wait_ge(zeroed, 16)
                for u in range(2):
                    pool.memset(v_top[u][:, :, 2 * VA - 1], 1.0).then_inc(zeroed, 1)
                pool.wait_ge(consts, 16 * 8)
                pool.sem_inc(hot_ready.sem, 1)

                def one_hots(n, u, j):
                    c = Chain(pool, psteps)
                    c.base = n * 1
                    hold(pool, pr.gate_p, scored.sem, scored.at((n - 2) * NG + G_SEL))
                    hold(pool, pr.gate_p, hot_ready.sem, hot_ready.at(n - 1))
                    pool.tensor_copy(kvp[u][:], one(pr.kvp, n)).then_inc(kvp_ready.sem, 1)
                    c.link(pool.tensor_copy(slot8[:], one(pr.slot, n)))
                    pool.sem_inc(pr.gate_p, 1)
                    for t in range(TPB):
                        ins = pool.tensor_scalar(hot[u][:, t], places[:], slot8[:, t:t + 1], None, ALU.is_equal)
                    ins.then_inc(hot_ready.sem, 1)
                    hold(pool, pr.gate_p, keyed.sem, keyed.at((n - 2) * NL + NL - 1))
                    hold(pool, pr.gate_p, stacks[u], j * 96 + 96)
                    pool.tensor_copy(kglob[u][0:KQ], kst[u][0:KQ, 0:GLOB]).then_inc(glob_ready.sem, 1)
                    hold(pool, pr.gate_p, summed.sem, summed.at(n - 2))
                    pool.tensor_copy(v_loc[u][:, :, 0:VA], one(pr.va, n))
                    pool.tensor_copy(v_glob[u][:, 2 * VA:VR], one(pr.va, n)[0:GLOB, 0]).then_inc(v_ready.sem, 1)

                with pool.Fori(0, HEADS // 2) as j:
                    for u in range(2):
                        one_hots(j * 2 + u, u, j)

            @block.vector
            def _(v):
                v.sem_inc(reduced.sem, 2)
                v.wait_ge(zeroed, 18)

                def take(n, u, g):
                    v.wait_ge(scored.sem, scored.at(n * NG + g))
                    return pr.ps[:, g % 2]

                def maxima(n, u):
                    ps = take(n, u, G_SEL)
                    sel = ps[:, 0:SLOTS * 48].rearrange("p (s a c) -> p s a c", s=SLOTS, a=3)
                    for s in range(SLOTS):
                        v.tensor_copy(krep[:, s].rearrange("p (a i e) -> p a i e", a=3, i=3),
                                      sel[:, s, :, 0:E].unsqueeze(2).broadcast_to([P, 3, 3, E]))
                    v.tensor_reduce(v_top[u][:, :, VA:VA + E], sel[:, :, :, E:2 * E].rearrange("p s a e -> p s e a"),
                                    AX, ALU.add).then_inc(reduced.sem, 1)
                    ps = take(n, u, G_TURN)
                    v.tensor_copy(ksel[u][0:KQ], ps[0:KQ, 0:TOP // 2].bitcast(BF16)).then_inc(reduced.sem, 1)
                    for t in range(TPB):
                        ps = take(n, u, G_LOC + t)
                        lo, hi = (P if t == 0 else 0), (2 * P if t == TPB - 1 else 3 * P)
                        v.reduce_max(mx[:, 0, t:t + 1], ps[:, lo:hi], AX).then_inc(reduced.sem, 1)
                    for t in range(0, TPB, 2):
                        ps = take(n, u, G_TOP + t // 2)
                        v.reduce_max(mx[:, 1, t:t + 2], ps.rearrange("p (t k) -> p t k", t=2),
                                     AX).then_inc(reduced.sem, 1)
                    ps = take(n, u, G_GLOB)
                    v.reduce_max(mx[:, 2, :], ps.rearrange("p (t k) -> p t k", t=TPB), AX).then_inc(reduced.sem, 1)
                    v.wait_ge(reduced.sem, reduced.at(n * NG + G_GLOB))
                    first = mrow[u][:, :, MROW:MROW + V3].rearrange("p t v -> p v t")
                    second = mrow[u][:, :, MROW + V3:KM].rearrange("p t v -> p v t")
                    v.tensor_scalar(first, mx[:], -1.0, None, ALU.mult).then_inc(first_part, 1)
                    v.wait_ge(first_part, n + 1)
                    v.scalar_tensor_tensor(out=second, in0=mx[:], scalar=-1.0, in1=first, op0=ALU.mult,
                                           op1=ALU.subtract).then_inc(rows_ready.sem, 1)
                    ps = take(n, u, G_MAX)
                    v.tensor_copy(qst[u][MROW:KM], ps[MROW:KM].bitcast(BF16)).then_inc(reduced.sem, 1)

                with v.Fori(0, HEADS // 2) as j:
                    for u in range(2):
                        maxima(j * 2 + u, u)

            @block.scalar
            def _(act):
                nc.scalar.preload_act_table(ACT.Exp)
                act.sem_inc(exped.sem, 2)
                act.sem_inc(taken.sem, 1)

                def exps(n, u):
                    for g in range(NL):
                        i = u * NL + g
                        ps = pr.ps[:, 2 + 2 * (i % 2):4 + 2 * (i % 2)]
                        act.wait_ge(keyed.sem, keyed.at(n * NL + g))
                        if g == LG_GLOB:
                            ins = nc.scalar.activation(p_glob[:].rearrange("p (a t) -> p a t", a=2), ps[0:GLOB],
                                                       ACT.Exp, scale=SCALE)
                        elif g < LG_LOC:
                            ins = nc.scalar.activation(p_top[:, g - LG_TOP].rearrange("p (a t) -> p a t", a=2), ps,
                                                       ACT.Exp, scale=SCALE)
                        else:
                            a, b = 2 * (g - LG_LOC), 2 * (g - LG_LOC) + 1
                            if a == 0:
                                nc.scalar.activation(p_loc[:, a, P:], ps[:, 0, P:3 * P], ACT.Exp, scale=SCALE)
                                ins = nc.scalar.activation(p_loc[:, b], ps[:, 1, 0:3 * P], ACT.Exp, scale=SCALE)
                            elif b == TPB - 1:
                                nc.scalar.activation(p_loc[:, a], ps[:, 0, 0:3 * P], ACT.Exp, scale=SCALE)
                                ins = nc.scalar.activation(p_loc[:, b, 0:2 * P], ps[:, 1, 0:2 * P], ACT.Exp,
                                                           scale=SCALE)
                            else:
                                ins = nc.scalar.activation(p_loc[:, a:b + 1], ps[:, :, 0:3 * P], ACT.Exp, scale=SCALE)
                        ins.then_inc(exped.sem, 1)

                def take(n, u, j):
                    act.wait_ge(stored[u], j * 16 + 16)
                    act.wait_ge(summed.sem, summed.at(n))
                    nc.scalar.activation(sums[u][:].rearrange("p (a t) -> p a t", a=2), pr.ps[0:VR, 6:8],
                                         ACT.Copy).then_inc(taken.sem, 1)

                exps(0, 0)
                with act.Fori(0, HEADS // 2 - 1) as j:
                    for u in range(2):
                        take(j * 2 + u, u, j)
                        exps(j * 2 + u + 1, 1 - u)
                take(HEADS - 2, 0, HEADS // 2 - 1)
                exps(HEADS - 1, 1)
                take(HEADS - 1, 1, HEADS // 2 - 1)

            @block.tensor
            def _(pe):
                pe.sem_inc(scored.sem, 2 * NG)
                pe.sem_inc(keyed.sem, 2 * NL)
                pe.sem_inc(summed.sem, 2)
                pe.wait_ge(consts, 16 * 8)
                pe.wait_ge(zeroed, 18)

                def banded(ps, k, q, t, lo, hi):
                    pe.matmul(ps[:, lo:hi], k[:, t * P:(t + 1) * P], q[:, (t - 1) * P + lo:(t - 1) * P + hi],
                              start=True, stop=False)
                    sides = slice(2 if lo else 0, 1 if hi == 2 * P else 3, 2)
                    cut = lambda x: x[:, 0:3 * P].rearrange("p (b c) -> p b c", b=3)[:, sides]
                    return pe.matmul(cut(ps), pr.idb[:], cut(mask[:]), start=False, stop=True)

                def query_group(n, u, g):
                    pe.wait_ge(reduced.sem, reduced.at(n * NG + g - 2))
                    ps = pr.ps[:, g % 2]
                    if g == G_SEL:
                        pe.wait_ge(kvp_ready.sem, kvp_ready.at(n))
                        pe.wait_ge(hot_ready.sem, hot_ready.at(n))
                        for s in range(SLOTS):
                            for t in range(TPB):
                                mm = pe.matmul(ps[:, s * 48:(s + 1) * 48], hot[u][:, t, s * P:(s + 1) * P],
                                               kvp[u][:, t], start=t == 0, stop=t == TPB - 1)
                    elif g == G_TURN:
                        pe.wait_ge(reduced.sem, reduced.at(n * NG + G_SEL))
                        for s in range(SLOTS):
                            mm = pe.transpose(ps[0:KQ, s * 64:(s + 1) * 64].bitcast(BF16), krep[:, s], pr.idb[:])
                    elif g < G_TOP:
                        t = g - G_LOC
                        if t == 0:
                            pe.wait_ge(stacks[u], 96 * (n_half(n, u) + 1))
                        lo, hi = (P if t == 0 else 0), (2 * P if t == TPB - 1 else 3 * P)
                        mm = banded(ps, qst[u][0:KQ], kst[u][0:KQ], t, lo, hi)
                    elif g < G_GLOB:
                        if g == G_TOP:
                            pe.wait_ge(reduced.sem, reduced.at(n * NG + G_TURN))
                        for i in range(2):
                            t = 2 * (g - G_TOP) + i
                            mm = pe.matmul(ps[:, i * TOP:(i + 1) * TOP], qst[u][0:KQ, t * P:(t + 1) * P],
                                           ksel[u][0:KQ, :], start=True, stop=True)
                    elif g == G_GLOB:
                        for t in range(TPB):
                            mm = pe.matmul(ps[:, t * GLOB:(t + 1) * GLOB], qst[u][0:KQ, t * P:(t + 1) * P],
                                           kst[u][0:KQ, 0:GLOB], start=True, stop=True)
                    else:
                        pe.wait_ge(rows_ready.sem, rows_ready.at(n))
                        for t in range(TPB):
                            mm = pe.transpose(ps[0:KM, t * 64:(t + 1) * 64].bitcast(BF16), mrow[u][:, t], pr.idb[:])
                    mm.then_inc(scored.sem, 1)

                def n_half(n, u):
                    return n // 2 if isinstance(n, int) else pr.half

                def key_group(n, u, g):
                    pe.wait_ge(exped.sem, exped.at(n * NL + g - 2))
                    if g == 0:
                        pe.wait_ge(reduced.sem, reduced.at(n * NG + G_MAX))
                    i = u * NL + g
                    ps = pr.ps[:, 2 + 2 * (i % 2):4 + 2 * (i % 2)]
                    if g == LG_GLOB:
                        pe.wait_ge(glob_ready.sem, glob_ready.at(n))
                        for i in range(2):
                            mm = pe.matmul(ps[0:GLOB, i], kglob[u][0:KM, :], qst[u][0:KM, i * CW:(i + 1) * CW],
                                           start=True, stop=True)
                    elif g < LG_LOC:
                        for i in range(2):
                            mm = pe.matmul(ps[:, i], ksel[u][0:KM, (g - LG_TOP) * P:(g - LG_TOP + 1) * P],
                                           qst[u][0:KM, i * CW:(i + 1) * CW], start=True, stop=True)
                    else:
                        for i in range(2):
                            t = 2 * (g - LG_LOC) + i
                            lo, hi = (P if t == 0 else 0), (2 * P if t == TPB - 1 else 3 * P)
                            mm = banded(ps[:, i], kst[u][0:KM], qst[u][0:KM], t, lo, hi)
                    mm.then_inc(keyed.sem, 1)

                def values(n, u, g):
                    pe.wait_ge(exped.sem, exped.at(n * NL + g))
                    if g == LG_GLOB:
                        pe.wait_ge(v_ready.sem, v_ready.at(n))
                        hold(pe, pr.gate_e, taken.sem, taken.at(n - 1))
                        for i in range(2):
                            pe.matmul(pr.ps[0:VR, 6 + i], v_glob[u][:], p_glob[:, i * CW:(i + 1) * CW],
                                      start=True, stop=False)
                    elif g < LG_LOC:
                        for i in range(2):
                            pe.matmul(pr.ps[0:VR, 6 + i], v_top[u][:, g - LG_TOP],
                                      p_top[:, g - LG_TOP, i * CW:(i + 1) * CW], start=False, stop=False)
                    else:
                        for t in (2 * (g - LG_LOC), 2 * (g - LG_LOC) + 1):
                            for i in range(2):
                                lo, hi = max(t - 1, i * CH), min(t + 2, (i + 1) * CH)
                                if lo < hi:
                                    mm = pe.matmul(pr.ps[0:VR, 6 + i, (lo - i * CH) * P:(hi - i * CH) * P],
                                                   v_loc[u][:, t], p_loc[:, t, (lo - t + 1) * P:(hi - t + 1) * P],
                                                   start=False, stop=t == (CH if i == 0 else TPB - 1))
                        if g == NL - 1:
                            mm.then_inc(summed.sem, 1)

                def step(n, u):
                    for g in range(NG):
                        if g % 2 == 0 and g // 2 < NL:
                            key_group(n, u, g // 2)
                        if n_next(n):
                            query_group(n + 1, 1 - u, g)
                        if g % 2 == 1 and 1 <= g // 2 <= NL:
                            values(n, u, g // 2 - 1)

                def n_next(n):
                    return not isinstance(n, int) or n + 1 < HEADS

                for g in range(NG):
                    query_group(0, 0, g)
                with pe.Fori(0, HEADS // 2 - 1) as j:
                    for u in range(2):
                        pr.half = j + u
                        step(j * 2 + u, u)
                step(HEADS - 2, 0)
                step(HEADS - 1, 1)


def out_project(pr, w_name, bias_name):
    nc, d = pr.nc, pr.d
    V3, VA = 3, E + 1
    with ExitStack() as ctx:
        wo = pr.sb(ctx, "wo", [P, D])
        bo = pr.sb(ctx, "bo", [1, D])
        ones = pr.sb(ctx, "ones", [1, P])
        num = pr.sb(ctx, "value_sums", [P, 2, V3, CW])
        inv = pr.sb(ctx, "inverses", [P, 2, V3, CW])
        den = pr.sb(ctx, "denominators", [P, V3, CW])
        ot = pr.sb(ctx, "o_turned", [P, 2, CW])
        loaded = pr.sem(ctx, "loaded")
        read = [pr.sem(ctx, f"sums_read{u}") for u in range(2)]
        den_read = pr.sem(ctx, "denominators_read")
        inverted = pr.sem(ctx, "inverted")
        inv_stored = pr.sem(ctx, "inverses_stored")
        steps = pr.sem(ctx, "steps")
        set_up = pr.sem(ctx, "set_up")
        meant = pr.ev(ctx, "mean_ready")
        taken = pr.ev(ctx, "mean_taken", 2)
        summed = pr.ev(ctx, "summed", 2)
        added = pr.ev(ctx, "added", 2)

        def chunks(eng, body):
            with eng.Fori(0, NC // 2) as j:
                for u in range(2):
                    body(j * 2 + u, u, j)

        with nc.Block() as block:
            @block.sync
            def _(sp):
                for w in range(V3):
                    for half in range(2):
                        sp.dma_start(den[half * HEADS:(half + 1) * HEADS, w],
                                     pr.sums_dram[:, w * VA + E, half * CW:(half + 1) * CW]).then_inc(den_read, 16)
                sp.dma_start(wo[:], d[w_name]).then_inc(loaded, 16)
                sp.dma_start(bo[:], d[bias_name]).then_inc(loaded, 16)
                sp.wait_ge(inverted, 1)
                for half in range(2):
                    sp.dma_start(pr.inverse_dram[:, :, half * CW:(half + 1) * CW], den[half * HEADS:(half + 1) * HEADS])\
                        .then_inc(inv_stored, 16)
                sp.wait_ge(inv_stored, 32)

                def part(k, u, j):
                    sp.wait_ge(taken.sem, taken.at(k - 2))
                    heads = pr.sums_dram[ds(j * H, H), :, u * CW:(u + 1) * CW]
                    for w in range(V3):
                        sp.dma_start(num[:, u, w], heads[:, w * VA:w * VA + E]).then_inc(read[u], 16)
                        sp.dma_start(inv[:, u, w], pr.inverse_dram[ds(j * H, H), w:w + 1, u * CW:(u + 1) * CW]
                                     .broadcast_to([H, E, CW])).then_inc(read[u], 16)

                chunks(sp, part)

            @block.vector
            def _(v):
                v.memset(ones[:], 1.0).then_inc(set_up, 1)
                v.sem_inc(added.sem, 2)
                v.wait_ge(den_read, 96)
                v.reciprocal(den[:], den[:]).then_inc(inverted, 1)

                def mean(k, u, j):
                    c = Chain(v, steps)
                    c.base = k * 2
                    v.wait_ge(read[u], j * 96 + 96)
                    c.link(v.tensor_tensor(num[:, u], num[:, u], inv[:, u], ALU.mult))
                    c.link(v.tensor_tensor(num[:, u, 0], num[:, u, 0], num[:, u, 1], ALU.add))
                    v.tensor_tensor(num[:, u, 0], num[:, u, 0], num[:, u, 2], ALU.add).then_inc(meant.sem, 1)

                def part(k, u, j):
                    mean(k, u, j)
                    v.wait_ge(summed.sem, summed.at(k))
                    v.tensor_tensor(pr.X[:, ds(k * CH, CH), :], pr.X[:, ds(k * CH, CH), :],
                                    pr.ps[:, 2 + u].rearrange("p (t d) -> p t d", d=D), ALU.add).then_inc(added.sem, 1)

                chunks(v, part)

            @block.scalar
            def _(act):
                act.sem_inc(taken.sem, 2)

                def part(k, u, j):
                    act.wait_ge(summed.sem, summed.at(k - 2))
                    act.wait_ge(meant.sem, meant.at(k))
                    nc.scalar.activation(ot[:, u], num[:, u, 0], ACT.Copy, scale=1.0 / V3).then_inc(taken.sem, 1)

                chunks(act, part)

            @block.tensor
            def _(pe):
                pe.sem_inc(summed.sem, 2)
                pe.wait_ge(loaded, 32)
                pe.wait_ge(set_up, 1)

                def part(k, u, j):
                    pe.wait_ge(added.sem, added.at(k - 2))
                    pe.wait_ge(taken.sem, taken.at(k))
                    for t in range(CH):
                        s = pr.ps[:, 2 + u, t * D:(t + 1) * D]
                        pe.matmul(s, ot[:, u, t * P:(t + 1) * P], wo[:], start=True, stop=False)
                        mm = pe.matmul(s, ones[:], bo[:], start=False, stop=True)
                    mm.then_inc(summed.sem, 1)

                chunks(pe, part)


def experts(pr, name, ne, width, glu, nb=None):
    nc, d = pr.nc, pr.d
    UE = P // width
    NU = ne // UE
    nb = nb or ne
    with ExitStack() as ctx:
        w1 = pr.sb(ctx, "w1", [P, NU, (2 if glu else 1) * P])
        b1 = pr.sb(ctx, "b1", [P, NU, 2 if glu else 1])
        w2 = pr.sb(ctx, "w2", [P, NU, D])
        b2 = pr.sb(ctx, "b2", [nb, D])
        mult = pr.sb(ctx, "mult", [P, NU]) if glu else None
        gc = pr.sb(ctx, "gates_chunk", [P, 2, CH, nb])
        gt = pr.sb(ctx, "gates_turned", [nb, 2, CW])
        hid = pr.sb(ctx, "hidden", [P, 2, CW])
        gel = pr.sb(ctx, "gelu", [P, 2, CW]) if glu else None
        acc = pr.sb(ctx, "sums", [P, 2, CH, D])
        loaded = pr.sem(ctx, "weights_loaded")
        scaled = pr.sem(ctx, "w2_scaled")
        gates_ready = pr.ev(ctx, "gates_ready")
        gates_turned = pr.ev(ctx, "gates_turned")
        gates_kept = pr.ev(ctx, "gates_kept", 1)
        bias_sum = pr.ev(ctx, "bias_sum")
        acc_ready = pr.ev(ctx, "acc_ready", 1)
        h_sum = pr.ev(ctx, "h_sum")
        gelu_done = pr.ev(ctx, "gelu_done", 2)
        hidden_ready = pr.ev(ctx, "hidden_ready", 2) if glu else gelu_done
        y_sum = pr.ev(ctx, "y_sum", 2 * ne)
        y_added = pr.ev(ctx, "y_added", 2 * ne)
        x_added = pr.ev(ctx, "x_added", 2)

        def chunks(eng, body):
            with eng.Fori(0, NC // 2) as j:
                for u in range(2):
                    body(j * 2 + u, u)

        def h_ps(i):
            return pr.ps[:, i % 2]

        def g_ps(i):
            return pr.ps[:, 2 + i % 2]

        with nc.Block() as block:
            @block.sync
            def _(sp):
                sp.dma_start(w1[:], d[name + "_w1"]).then_inc(loaded, 16)
                sp.dma_start(b1[:], d[name + "_b1"]).then_inc(loaded, 16)
                sp.dma_start(w2[:], d[name + "_w2"]).then_inc(loaded, 16)
                sp.dma_start(b2[:], d[name + "_b2"]).then_inc(loaded, 16)
                if glu:
                    sp.dma_start(mult[:], d[name + "_mult"]).then_inc(loaded, 16)

            @block.gpsimd
            def _(pool):
                pool.sem_inc(x_added.sem, 2)

                def add(k, u):
                    hold(pool, pr.gate_p, y_added.sem, y_added.at(k * ne + ne - 1))
                    pool.tensor_tensor(pr.X[:, ds(k * CH, CH), :], pr.X[:, ds(k * CH, CH), :], acc[:, u],
                                       ALU.add).then_inc(x_added.sem, 1)

                chunks(pool, add)

            @block.vector
            def _(v):
                v.wait_ge(loaded, 16 * (5 if glu else 4))
                if glu:
                    v.tensor_tensor(w2[:], w2[:], bc(mult[:], D), ALU.mult).then_inc(scaled, 1)
                    v.sem_inc(hidden_ready.sem, 2)
                v.sem_inc(y_added.sem, 2 * ne)

                def gate_hidden(k, u, i):
                    v.wait_ge(y_sum.sem, y_sum.at(k * ne + i - 2))
                    v.wait_ge(gelu_done.sem, gelu_done.at(k * NU + i))
                    n = u * NU + i
                    v.scalar_tensor_tensor(out=hid[:, n % 2], in0=h_ps(n), scalar=b1[:, i, 0:1],
                                           in1=gel[:, n % 2], op0=ALU.add, op1=ALU.mult)\
                        .then_inc(hidden_ready.sem, 1)

                def part(k, u):
                    if glu:
                        gate_hidden(k, u, 0)
                    v.wait_ge(acc_ready.sem, acc_ready.at(k))
                    for e in range(ne):
                        if glu and e + 1 < ne:
                            gate_hidden(k, u, e + 1)
                        n = u * ne + e
                        v.wait_ge(y_added.sem, y_added.at(k * ne + e - 1))
                        v.wait_ge(y_sum.sem, y_sum.at(k * ne + e))
                        for t in range(CH):
                            ins = v.scalar_tensor_tensor(out=acc[:, u, t], in0=pr.ps[:, 4 + n % 2, t * D:(t + 1) * D],
                                                         scalar=gc[:, u, t, e:e + 1], in1=acc[:, u, t],
                                                         op0=ALU.mult, op1=ALU.add)
                        ins.then_inc(y_added.sem, 1)

                chunks(v, part)

            @block.scalar
            def _(act):
                nc.scalar.preload_act_table(ACT.Gelu)
                act.sem_inc(gates_kept.sem, 1)
                act.sem_inc(acc_ready.sem, 1)
                act.sem_inc(gelu_done.sem, 2)
                act.wait_ge(loaded, 16 * (5 if glu else 4))

                def part(k, u):
                    hold(act, pr.gate_a, y_added.sem, y_added.at((k - 2) * ne + ne - 1))
                    nc.scalar.activation(gc[:, u], pr.gates[:, ds(k * CH, CH), 0:nb], ACT.Copy)\
                        .then_inc(gates_ready.sem, 1)
                    act.wait_ge(gates_turned.sem, gates_turned.at(k))
                    nc.scalar.activation(gt[:, u], pr.ps[0:nb, 6], ACT.Copy).then_inc(gates_kept.sem, 1)
                    act.wait_ge(bias_sum.sem, bias_sum.at(k))
                    act.wait_ge(x_added.sem, x_added.at(k - 2))
                    nc.scalar.activation(acc[:, u], pr.ps[:, 7].rearrange("p (t d) -> p t d", d=D), ACT.Copy)\
                        .then_inc(acc_ready.sem, 1)
                    for i in range(NU):
                        n = u * NU + i
                        act.wait_ge(y_sum.sem, y_sum.at(k * ne + (i - 2) * UE + UE - 1))
                        act.wait_ge(h_sum.sem, h_sum.at(k * NU + i))
                        if glu:
                            act.wait_ge(hidden_ready.sem, hidden_ready.at(k * NU + i - 2))
                        nc.scalar.activation(gel[:, n % 2] if glu else hid[:, n % 2], g_ps(n) if glu else h_ps(n),
                                             ACT.Gelu, bias=b1[:, i, 1:2] if glu else b1[:, i, 0:1])\
                            .then_inc(gelu_done.sem, 1)

                chunks(act, part)

            @block.tensor
            def _(pe):
                pe.sem_inc(y_sum.sem, 2 * ne)
                pe.wait_ge(loaded, 16 * (5 if glu else 4))
                if glu:
                    pe.wait_ge(scaled, 1)

                def first(k, u, i):
                    n = u * NU + i
                    pe.wait_ge(gelu_done.sem, gelu_done.at(k * NU + i - 2))
                    if glu:
                        pe.wait_ge(hidden_ready.sem, hidden_ready.at(k * NU + i - 2))
                    x = pr.xt[:, ds(k * CW, CW)]
                    mm = pe.matmul(h_ps(n), w1[:, i, 0:P], x, start=True, stop=True)
                    if glu:
                        mm = pe.matmul(g_ps(n), w1[:, i, P:2 * P], x, start=True, stop=True)
                    mm.then_inc(h_sum.sem, 1)

                def second(k, u, i):
                    pe.wait_ge(hidden_ready.sem, hidden_ready.at(k * NU + i))
                    for s in range(UE):
                        n = u * ne + i * UE + s
                        r = slice(s * width, (s + 1) * width)
                        pe.wait_ge(y_added.sem, y_added.at(k * ne + i * UE + s - 2))
                        for t in range(CH):
                            mm = pe.matmul(pr.ps[:, 4 + n % 2, t * D:(t + 1) * D],
                                           hid[r, (u * NU + i) % 2, t * P:(t + 1) * P], w2[r, i], start=True, stop=True)
                        mm.then_inc(y_sum.sem, 1)

                def part(k, u):
                    first(k, u, 0)
                    pe.wait_ge(gates_ready.sem, gates_ready.at(k))
                    pe.wait_ge(gates_kept.sem, gates_kept.at(k - 1))
                    for t in range(CH):
                        mm = pe.transpose(pr.ps[0:nb, 6, t * P:(t + 1) * P], gc[:, u, t], pr.idf[:])
                    mm.then_inc(gates_turned.sem, 1)
                    if NU > 1:
                        first(k, u, 1)
                    pe.wait_ge(gates_kept.sem, gates_kept.at(k))
                    pe.wait_ge(acc_ready.sem, acc_ready.at(k - 1))
                    for t in range(CH):
                        mm = pe.matmul(pr.ps[:, 7, t * D:(t + 1) * D], gt[:, u, t * P:(t + 1) * P], b2[:],
                                       start=True, stop=True)
                    mm.then_inc(bias_sum.sem, 1)
                    for i in range(NU):
                        second(k, u, i)
                        if i + 2 < NU:
                            first(k, u, i + 2)

                chunks(pe, part)


def store_output(pr):
    nc = pr.nc
    with ExitStack() as ctx:
        stored = pr.sem(ctx, "stored")
        with nc.Block() as block:
            @block.sync
            def _(sp):
                sp.dma_start(pr.out.rearrange("p (t d) -> p t d", d=D), pr.X[:]).then_inc(stored, 16)
                sp.wait_ge(stored, 16)


def two_a_turn(eng, body):
    with eng.Fori(0, NC // 2) as j:
        for u in range(2):
            body(j * 2 + u, u, j)


def l1_attention(pr):
    nc, d = pr.nc, pr.d
    SCALE = float(D) ** -0.5
    with ExitStack() as ctx:
        wq, wk, wo = (pr.sb(ctx, n, [P, D]) for n in ("wq", "wk", "wo"))
        wroute = pr.sb(ctx, "wroute", [P, 8])
        mask = pr.sb(ctx, "causal_mask", [P, P], BF16)
        xnc = pr.sb(ctx, "xnc", [P, 2, CH, D])
        chunk = pr.sb(ctx, "chunk", [P, 2, CW])
        qt = pr.sb(ctx, "q_turned", [P, 2, CW])
        kt = pr.sb(ctx, "k_turned", [P, 2, P + CW])
        kn = pr.sb(ctx, "k_by_token", [P, 2, 1 + CH, D])
        mx = pr.sb(ctx, "mx", [P, 2, CH])
        nmx = pr.sb(ctx, "minus_mx", [P, 2, CH])
        sums = pr.sb(ctx, "sums", [P, 2, CH])
        rec = pr.sb(ctx, "rec", [P, 2, CH])
        prob = pr.sb(ctx, "prob", [P, 2, CH, 2 * P])
        pt = pr.sb(ctx, "prob_turned", [P, 2, CH, 2, P])
        ot = pr.sb(ctx, "out_turned", [P, 2, CW])
        loaded = pr.sem(ctx, "weights_loaded")
        zeroed = pr.sem(ctx, "zeroed")
        xn_sub = pr.ev(ctx, "xn_sub")
        xn_ready = pr.ev(ctx, "xn_ready")
        turned = pr.ev(ctx, "xn_turned", 2)
        chunk_ready = pr.ev(ctx, "chunk_ready", 1)
        chunk_kept = pr.ev(ctx, "chunk_kept", 2)
        q_sum, k_sum, kn_sum, r_sum = (pr.ev(ctx, n, 2) for n in ("q_sum", "k_sum", "kn_sum", "r_sum"))
        q_taken, k_taken, kn_taken, r_taken = (pr.ev(ctx, n, 1) for n in ("q_tak", "k_tak", "kn_tak", "r_tak"))
        k_passed = pr.ev(ctx, "k_passed", 1)
        scored = pr.ev(ctx, "scored", 2)
        maxed = pr.ev(ctx, "maxed")
        minus_ready = pr.ev(ctx, "minus_ready")
        exped = pr.ev(ctx, "exped", 2)
        p_turned = pr.ev(ctx, "p_turned", 4)
        p_taken = pr.ev(ctx, "p_taken", 2)
        o_sum = pr.ev(ctx, "o_sum", 2)
        o_taken = pr.ev(ctx, "o_taken", 1)
        y_sum = pr.ev(ctx, "y_sum", 2)
        y_added = pr.ev(ctx, "y_added", 1)
        rec_ready = pr.ev(ctx, "rec_ready")
        turn_ps, q_ps, k_ps, o_ps = (pr.ps[:, i] for i in range(4))
        s_ps = pr.ps[:, 4:6]
        pt_ps = pr.ps[:, 6:8]

        with nc.Block() as block:
            @block.sync
            def _(sp):
                for dst, src in ((wq, "l1_wq"), (wk, "l1_wk"), (wo, "l1_wo"), (wroute, "l1_wg"), (mask, "mask_causal")):
                    sp.dma_start(dst[:], d[src]).then_inc(loaded, 16)

            @block.gpsimd
            def _(pool):
                pool.memset(kt[:, 0, 0:P], 0.0).then_inc(zeroed, 1)
                pool.memset(kn[:, 0, 0], 0.0).then_inc(zeroed, 1)
                pool.sem_inc(chunk_kept.sem, 2)
                pool.sem_inc(k_passed.sem, 1)

                def part(k, u, j):
                    hold(pool, pr.gate_p, chunk_ready.sem, chunk_ready.at(k))
                    pool.tensor_copy(pr.xt[:, ds(k * CW, CW)], chunk[:, u]).then_inc(chunk_kept.sem, 1)
                    if u == 1:
                        hold(pool, pr.gate_p, o_sum.sem, o_sum.at(k - 2))
                        hold(pool, pr.gate_p, k_taken.sem, k_taken.at(k - 1))
                        pool.tensor_copy(kt[:, 1, 0:P], kt[:, 0, CW:]).then_inc(k_passed.sem, 1)
                        hold(pool, pr.gate_p, kn_taken.sem, kn_taken.at(k - 1))
                        pool.tensor_copy(kn[:, 1, 0], kn[:, 0, CH]).then_inc(k_passed.sem, 1)

                two_a_turn(pool, part)

            @block.vector
            def _(v):
                v.sem_inc(kn_taken.sem, 1)
                v.sem_inc(y_added.sem, 1)
                v.sem_inc(p_taken.sem, 2)

                def norm(k, u):
                    v.wait_ge(turned.sem, turned.at(k - 2))
                    v.tensor_tensor(xnc[:, u], pr.X[:, ds(k * CH, CH), :], bc(pr.mean[:, ds(k * CH, CH)], D),
                                    ALU.subtract).then_inc(xn_sub.sem, 1)
                    v.wait_ge(xn_sub.sem, xn_sub.at(k))
                    v.tensor_tensor(xnc[:, u], xnc[:, u], bc(pr.rstd[:, ds(k * CH, CH)], D),
                                    ALU.mult).then_inc(xn_ready.sem, 1)

                def part(k, u, j):
                    norm(k, u)
                    v.wait_ge(o_sum.sem, o_sum.at(k - 2))
                    v.wait_ge(kn_sum.sem, kn_sum.at(k))
                    v.tensor_copy(kn[:, u, 1:], o_ps.rearrange("p (t d) -> p t d", d=D)).then_inc(kn_taken.sem, 1)
                    for half in range(2):
                        i = k * 2 + half
                        v.wait_ge(scored.sem, scored.at(i))
                        ins = v.reduce_max(mx[:, u, 2 * half:2 * half + 2],
                                           s_ps[:, half].rearrange("p (t k) -> p t k", t=2), AX)
                        ins.then_inc(maxed.sem, 1)
                    v.wait_ge(maxed.sem, maxed.at(k * 2 + 1))
                    v.tensor_scalar(nmx[:, u], mx[:, u], -SCALE, None, ALU.mult).then_inc(minus_ready.sem, 1)
                    for half in range(2):
                        v.wait_ge(p_turned.sem, p_turned.at(k * 2 + half))
                        v.tensor_copy(pt[:, u, 2 * half:2 * half + 2].rearrange("p t a q -> p (t a q)"),
                                      pt_ps[:, half]).then_inc(p_taken.sem, 1)
                    v.wait_ge(exped.sem, exped.at(k))
                    v.reciprocal(rec[:, u], sums[:, u]).then_inc(rec_ready.sem, 1)
                    v.wait_ge(rec_ready.sem, rec_ready.at(k))
                    v.wait_ge(y_sum.sem, y_sum.at(k))
                    for t in range(CH):
                        x = one(pr.X, k * CH + t)
                        ins = v.scalar_tensor_tensor(out=x, in0=turn_ps[:, t * D:(t + 1) * D],
                                                     scalar=rec[:, u, t:t + 1], in1=x, op0=ALU.mult, op1=ALU.add)
                    ins.then_inc(y_added.sem, 1)

                two_a_turn(v, part)

            @block.scalar
            def _(act):
                nc.scalar.preload_act_table(ACT.Exp)
                for e in (chunk_ready, q_taken, k_taken, r_taken, o_taken):
                    act.sem_inc(e.sem, 1)
                act.sem_inc(exped.sem, 2)
                act.wait_ge(zeroed, 2)

                def part(k, u, j):
                    act.wait_ge(r_sum.sem, r_sum.at(k - 2))
                    act.wait_ge(chunk_kept.sem, chunk_kept.at(k - 2))
                    act.wait_ge(turned.sem, turned.at(k))
                    nc.scalar.activation(chunk[:, u], turn_ps, ACT.Copy).then_inc(chunk_ready.sem, 1)
                    act.wait_ge(scored.sem, scored.at(k * 2 - 3))
                    act.wait_ge(q_sum.sem, q_sum.at(k))
                    nc.scalar.activation(qt[:, u], q_ps, ACT.Copy).then_inc(q_taken.sem, 1)
                    if u == 0:
                        act.wait_ge(k_passed.sem, j * 2 + 1)
                    act.wait_ge(k_sum.sem, k_sum.at(k))
                    nc.scalar.activation(kt[:, u, P:], k_ps, ACT.Copy).then_inc(k_taken.sem, 1)
                    hold(act, pr.gate_a, r_sum.sem, r_sum.at(k))
                    nc.scalar.activation(pr.logits[:, ds(k * CH, CH), 0:8],
                                         q_ps[:, 0:CH * 8].rearrange("p (t c) -> p t c", c=8),
                                         ACT.Copy).then_inc(r_taken.sem, 1)
                    act.wait_ge(p_turned.sem, p_turned.at(k * 2 - 3))
                    act.wait_ge(minus_ready.sem, minus_ready.at(k))
                    for t in range(CH):
                        ins = nc.scalar.activation(prob[:, u, t], s_ps[:, t // 2, (t % 2) * 2 * P:(t % 2 + 1) * 2 * P],
                                                   ACT.Exp, bias=nmx[:, u, t:t + 1], scale=SCALE,
                                                   accum_out=sums[:, u, t:t + 1])
                    ins.then_inc(exped.sem, 1)
                    act.wait_ge(y_sum.sem, y_sum.at(k - 2))
                    act.wait_ge(o_sum.sem, o_sum.at(k))
                    nc.scalar.activation(ot[:, u], o_ps, ACT.Copy).then_inc(o_taken.sem, 1)

                two_a_turn(act, part)

            @block.tensor
            def _(pe):
                for e in (turned, q_sum, k_sum, kn_sum, r_sum, scored, o_sum, y_sum):
                    pe.sem_inc(e.sem, 2)
                pe.sem_inc(p_turned.sem, 4)
                pe.wait_ge(loaded, 5 * 16)
                pe.wait_ge(zeroed, 2)

                def part(k, u, j):
                    pe.wait_ge(xn_ready.sem, xn_ready.at(k))
                    pe.wait_ge(y_added.sem, y_added.at(k - 1))
                    for t in range(CH):
                        mm = pe.transpose(turn_ps[:, t * P:(t + 1) * P], xnc[:, u, t], pr.idf[:])
                    mm.then_inc(turned.sem, 1)
                    pe.wait_ge(chunk_ready.sem, chunk_ready.at(k))
                    pe.wait_ge(r_taken.sem, r_taken.at(k - 1))
                    pe.matmul(q_ps, wq[:], chunk[:, u], start=True, stop=True).then_inc(q_sum.sem, 1)
                    pe.matmul(k_ps, wk[:], chunk[:, u], start=True, stop=True).then_inc(k_sum.sem, 1)
                    pe.wait_ge(o_taken.sem, o_taken.at(k - 1))
                    for t in range(CH):
                        mm = pe.matmul(o_ps[:, t * D:(t + 1) * D], chunk[:, u, t * P:(t + 1) * P], wk[:],
                                       start=True, stop=True)
                    mm.then_inc(kn_sum.sem, 1)
                    pe.wait_ge(q_taken.sem, q_taken.at(k))
                    for t in range(CH):
                        mm = pe.matmul(q_ps[:, t * 8:(t + 1) * 8], chunk[:, u, t * P:(t + 1) * P], wroute[:],
                                       start=True, stop=True)
                    mm.then_inc(r_sum.sem, 1)
                    pe.wait_ge(k_taken.sem, k_taken.at(k))
                    pe.wait_ge(exped.sem, exped.at(k - 1))
                    if u == 1:
                        pe.wait_ge(k_passed.sem, j * 2 + 2)
                    for t in range(CH):
                        s = s_ps[:, t // 2, (t % 2) * 2 * P:(t % 2 + 1) * 2 * P]
                        pe.matmul(s, qt[:, u, t * P:(t + 1) * P], kt[:, u, t * P:(t + 2) * P], start=True, stop=False)
                        mm = pe.matmul(s[:, P:], pr.idb[:], mask[:], start=False, stop=True)
                        if t % 2:
                            mm.then_inc(scored.sem, 1)
                    pe.wait_ge(exped.sem, exped.at(k))
                    for t in range(CH):
                        if t % 2 == 0:
                            pe.wait_ge(p_taken.sem, p_taken.at(k * 2 + t // 2 - 2))
                        for a in range(2):
                            mm = pe.transpose(pt_ps[:, t // 2, ((t % 2) * 2 + a) * P:((t % 2) * 2 + a + 1) * P],
                                              prob[:, u, t, a * P:(a + 1) * P], pr.idf[:])
                        if t % 2:
                            mm.then_inc(p_turned.sem, 1)
                    pe.wait_ge(kn_taken.sem, kn_taken.at(k))
                    if u == 1:
                        pe.wait_ge(k_passed.sem, j * 2 + 3)
                    for t in range(CH):
                        if t % 2 == 0:
                            pe.wait_ge(p_taken.sem, p_taken.at(k * 2 + t // 2))
                        for a in range(2):
                            mm = pe.matmul(o_ps[:, t * P:(t + 1) * P], kn[:, u, t + a], pt[:, u, t, a],
                                           start=a == 0, stop=a == 1)
                    mm.then_inc(o_sum.sem, 1)
                    pe.wait_ge(o_taken.sem, o_taken.at(k))
                    for t in range(CH):
                        mm = pe.matmul(turn_ps[:, t * D:(t + 1) * D], ot[:, u, t * P:(t + 1) * P], wo[:],
                                       start=True, stop=True)
                    mm.then_inc(y_sum.sem, 1)

                two_a_turn(pe, part)


def top_gates(pr, ne, top, total, bias=None, fill=None):
    nc, d = pr.nc, pr.d
    with ExitStack() as ctx:
        lg, prob, left, eq, key, gate, order = (pr.sb(ctx, n, [P, NT, ne]) for n in
                                                ("lg", "prob", "left", "eq", "key", "gate", "order"))
        m, s, r = (pr.sb(ctx, n, [P, NT]) for n in ("m", "s", "r"))
        brow = pr.sb(ctx, "bias_row", [P, ne])
        orow = pr.sb(ctx, "order_row", [P, ne])
        loaded = pr.sem(ctx, "loaded")
        shifted = pr.sem(ctx, "shifted")
        exped = pr.sem(ctx, "exped")
        dv = pr.sem(ctx, "dv_steps")
        with nc.Block() as block:
            @block.sync
            def _(sp):
                sp.dma_start(orow[:], d["order"][:, 0:ne]).then_inc(loaded, 16)
                if bias:
                    sp.dma_start(brow[:], d[bias].broadcast_to([P, ne])).then_inc(loaded, 16)

            @block.scalar
            def _(act):
                act.wait_ge(shifted, 1)
                nc.scalar.activation(prob[:], lg[:], ACT.Exp).then_inc(exped, 1)

            @block.vector
            def _(v):
                c = Chain(v, dv)
                v.wait_ge(loaded, 32 if bias else 16)
                if bias:
                    c.link(v.tensor_tensor(lg[:], pr.logits[:, :, 0:ne], brow[:].unsqueeze(1).broadcast_to([P, NT, ne]),
                                           ALU.add))
                else:
                    c.link(v.tensor_copy(lg[:], pr.logits[:, :, 0:ne]))
                c.link(v.memset(pr.gates[:], 1.0))
                c.link(v.tensor_copy(order[:], orow[:].unsqueeze(1).broadcast_to([P, NT, ne])))
                c.link(v.reduce_max(m[:], lg[:], AX))
                v.tensor_tensor(lg[:], lg[:], bc(m[:], ne), ALU.subtract).then_inc(shifted, 1)
                v.wait_ge(exped, 1)
                c.link(v.reduce_sum(s[:], prob[:], AX))
                c.link(v.reciprocal(r[:], s[:]))
                c.link(v.tensor_tensor(prob[:], prob[:], bc(r[:], ne), ALU.mult))
                c.link(v.tensor_copy(left[:], prob[:]))
                c.link(v.memset(gate[:], 0.0))
                for i in range(top):
                    c.link(v.reduce_max(m[:], left[:], AX))
                    c.link(v.tensor_tensor(eq[:], left[:], bc(m[:], ne), ALU.is_ge))
                    c.link(v.tensor_tensor(key[:], eq[:], order[:], ALU.mult))
                    c.link(v.reduce_max(m[:], key[:], AX))
                    c.link(v.tensor_tensor(eq[:], key[:], bc(m[:], ne), ALU.is_equal))
                    c.link(v.tensor_tensor(gate[:], gate[:], eq[:], ALU.add))
                    c.link(v.scalar_tensor_tensor(out=left[:], in0=eq[:], scalar=-2.0, in1=left[:], op0=ALU.mult,
                                                  op1=ALU.add))
                c.link(v.tensor_tensor(gate[:], gate[:], prob[:], ALU.mult))
                if total:
                    c.link(v.reduce_sum(s[:], gate[:], AX))
                    c.link(v.tensor_scalar(s[:], s[:], 1e-20, None, ALU.add))
                    c.link(v.reciprocal(r[:], s[:]))
                    c.link(v.tensor_tensor(gate[:], gate[:], bc(r[:], ne), ALU.mult))
                c.link(v.tensor_copy(pr.gates[:, :, 0:ne], gate[:]))


def l2_attention(pr):
    nc, d = pr.nc, pr.d
    SCALE = float(D) ** -0.5
    NH = 2
    CB = N // CW
    with ExitStack() as ctx:
        wqk = pr.sb(ctx, "wqk", [P, 2, 3, D])
        wv = pr.sb(ctx, "wv", [P, D])
        wo = pr.sb(ctx, "wo", [P, NH, D])
        wroute = pr.sb(ctx, "wroute", [P, 16])
        mask = pr.sb(ctx, "causal_mask", [P, P], BF16)
        cos = pr.sb(ctx, "cos", [P, N])
        sin = pr.sb(ctx, "sin", [P, N])
        xnc = pr.sb(ctx, "xnc", [P, CB, CH, D])
        chunk = pr.sb(ctx, "chunk", [P, CB, CW])
        qk = pr.sb(ctx, "qk_turned", [P, 3, N])
        part1 = pr.sb(ctx, "part1", [P, 2, CW])
        part2 = pr.sb(ctx, "part2", [P, 2, CW])
        vn = pr.sb(ctx, "v_by_token", [P, TPB, D])
        mx = pr.sb(ctx, "mx", [P, 2, 1])
        nmx = pr.sb(ctx, "minus_mx", [P, 2, 1])
        sums = pr.sb(ctx, "sums", [P, 2 * TPB, 1])
        rec = pr.sb(ctx, "rec", [P, 2 * TPB, 1])
        prob = pr.sb(ctx, "prob", [P, 2, N])
        pt = pr.sb(ctx, "prob_turned", [P, 2, TPB, NH, P])
        ot = pr.sb(ctx, "out_turned", [P, 2, NH * P])
        loaded = pr.sem(ctx, "weights_loaded")
        names = "xn_sub xn_ready chunk_kept rotated1 rotated2 rope_done v_taken maxed minus_ready p_taken " \
                "rec_ready y_added"
        (xn_sub, xn_ready, chunk_kept, rotated1, rotated2, rope_done, v_taken, maxed, minus_ready, p_taken,
         rec_ready, y_added) = (pr.sem(ctx, n) for n in names.split())
        names = "turned chunk_ready qk_sum v_sum r_sum r_taken scored exped p_turned o_sum o_taken y_sum batch_done"
        (turned, chunk_ready, qk_sum, v_sum, r_sum, r_taken, scored, exped, p_turned, o_sum, o_taken, y_sum,
         batch_done) = (pr.sem(ctx, n) for n in names.split())
        turn_ps = pr.ps[:, 6]
        UNITS = [(t, h) for t in range(TPB) for h in range(NH)]
        GROUPS = [(t, h, g) for t, h in UNITS for g in range(0, t + 1, CH)]
        NG = len(GROUPS)

        def batches(eng, body):
            with eng.Fori(0, B) as b:
                body(b)

        def s_ps(i):
            return pr.ps[:, 2 * (i % 2):2 * (i % 2) + 2].rearrange("p a k -> p (a k)")

        with nc.Block() as block:
            @block.sync
            def _(sp):
                for dst, src in ((wqk, "l2_wqk"), (wv, "l2_wv"), (wo, "l2_wo"), (wroute, "l2_gate"),
                                 (mask, "mask_causal"), (cos, "l2_cos"), (sin, "l2_sin")):
                    sp.dma_start(dst[:], d[src]).then_inc(loaded, 16)

            @block.gpsimd
            def _(pool):
                pool.wait_ge(loaded, 7 * 16)

                def batch(b):
                    for u in range(CB):
                        hold(pool, pr.gate_p, chunk_ready, b * CB + u + 1)
                        pool.tensor_copy(pr.xt[:, ds(b * N + u * CW, CW)], chunk[:, u]).then_inc(chunk_kept, 1)
                        for i in range(3):
                            if u == 0 and i == 0:
                                hold(pool, pr.gate_p, batch_done, b + 1)
                            hold(pool, pr.gate_p, rotated2, b * 6 + u * 3 + i + 1)
                            pool.tensor_tensor(qk[:, i, u * CW:(u + 1) * CW], part1[:, (u * 3 + i) % 2],
                                               part2[:, (u * 3 + i) % 2],
                                               ALU.add).then_inc(rope_done, 1)

                batches(pool, batch)

            @block.vector
            def _(v):
                v.wait_ge(loaded, 7 * 16)
                v.sem_inc(y_added, 1)

                def batch(b):
                    for u in range(CB):
                        v.wait_ge(batch_done, b + 1)
                        k = b * CB + u
                        v.tensor_tensor(xnc[:, u], pr.X[:, ds(k * CH, CH), :], bc(pr.mean[:, ds(k * CH, CH)], D),
                                        ALU.subtract).then_inc(xn_sub, 1)
                        v.wait_ge(xn_sub, k + 1)
                        v.tensor_tensor(xnc[:, u], xnc[:, u], bc(pr.rstd[:, ds(k * CH, CH)], D),
                                        ALU.mult).then_inc(xn_ready, 1)
                    for u in range(CB):
                        for i in range(3):
                            n = b * 6 + u * 3 + i
                            m = u * 3 + i
                            cols = slice(u * CW, (u + 1) * CW)
                            v.wait_ge(qk_sum, n + 1)
                            if m >= 2:
                                v.wait_ge(rope_done, n - 1)
                            v.tensor_tensor(part1[:, m % 2], pr.ps[:, 2 * (m % 2)], cos[:, cols],
                                            ALU.mult).then_inc(rotated1, 1)
                            v.tensor_tensor(part2[:, m % 2], pr.ps[:, 2 * (m % 2) + 1], sin[:, cols],
                                            ALU.mult).then_inc(rotated2, 1)
                        v.wait_ge(v_sum, b * CB + u + 1)
                        v.tensor_copy(vn[:, u * CH:(u + 1) * CH], pr.ps[:, 4 + u].rearrange("p (t d) -> p t d", d=D))\
                            .then_inc(v_taken, 1)

                    def highest(i):
                        t, h = UNITS[i]
                        v.wait_ge(scored, b * 16 + i + 1)
                        v.reduce_max(mx[:, h], s_ps(i)[:, 0:(t + 1) * P], AX).then_inc(maxed, 1)
                        v.wait_ge(maxed, b * 16 + i + 1)
                        v.tensor_scalar(nmx[:, h], mx[:, h], -SCALE, None, ALU.mult).then_inc(minus_ready, 1)

                    def turn(i):
                        t, h = UNITS[i]
                        for g, (gt, gh, k0) in enumerate(GROUPS):
                            if (gt, gh) == (t, h):
                                n = min(CH, t + 1 - k0)
                                v.wait_ge(p_turned, b * NG + g + 1)
                                v.tensor_copy(pt[:, t % 2, k0:k0 + n, h],
                                              pr.ps[:, 4 + g % 2, 0:n * P].rearrange("p (k q) -> p k q", q=P))\
                                    .then_inc(p_taken, 1)

                    def finish(t):
                        v.wait_ge(exped, b * 16 + 2 * t + 2)
                        v.reciprocal(rec[:, 2 * t:2 * t + 2], sums[:, 2 * t:2 * t + 2]).then_inc(rec_ready, 1)
                        v.wait_ge(rec_ready, b * TPB + t + 1)
                        v.wait_ge(y_sum, b * TPB + t + 1)
                        for h in range(NH):
                            x = one(pr.X, b * TPB + t)
                            v.scalar_tensor_tensor(out=x, in0=pr.ps[:, 7, h * D:(h + 1) * D],
                                                   scalar=rec[:, 2 * t + h], in1=x, op0=ALU.mult, op1=ALU.add)\
                                .then_inc(y_added, 1)
                            hold(v, pr.gate_v, y_added, b * 2 * TPB + 2 * t + h + 2)

                    highest(0)
                    highest(1)
                    for t in range(TPB):
                        turn(2 * t)
                        if t + 1 < TPB:
                            highest(2 * t + 2)
                        turn(2 * t + 1)
                        if t + 1 < TPB:
                            highest(2 * t + 3)
                        finish(t)

                batches(v, batch)

            @block.scalar
            def _(act):
                nc.scalar.preload_act_table(ACT.Exp)

                def batch(b):
                    for u in range(CB):
                        k = b * CB + u
                        act.wait_ge(batch_done, b + 1)
                        act.wait_ge(turned, k + 1)
                        nc.scalar.activation(chunk[:, u], turn_ps, ACT.Copy).then_inc(chunk_ready, 1)
                        hold(act, pr.gate_a, r_sum, k + 1)
                        nc.scalar.activation(pr.logits[:, ds(k * CH, CH), :],
                                             pr.ps[:, 7, 0:CH * 16].rearrange("p (t c) -> p t c", c=16),
                                             ACT.Copy).then_inc(r_taken, 1)

                    def exps(i):
                        t, h = UNITS[i]
                        act.wait_ge(minus_ready, b * 16 + i + 1)
                        if t:
                            act.wait_ge(p_turned, b * NG + len([1 for gt, gh, _ in GROUPS if (gt, gh) <= (t - 1, h)]))
                        nc.scalar.activation(prob[:, h, 0:(t + 1) * P], s_ps(i)[:, 0:(t + 1) * P], ACT.Exp,
                                             bias=nmx[:, h], scale=SCALE, accum_out=sums[:, i]).then_inc(exped, 1)

                    exps(0)
                    exps(1)
                    for t in range(TPB):
                        if t + 1 < TPB:
                            exps(2 * t + 2)
                            exps(2 * t + 3)
                        act.wait_ge(o_sum, b * TPB + t + 1)
                        if t >= 2:
                            act.wait_ge(y_sum, b * TPB + t - 1)
                        nc.scalar.activation(ot[:, t % 2], pr.ps[:, 6, 0:NH * P], ACT.Copy).then_inc(o_taken, 1)

                batches(act, batch)

            @block.tensor
            def _(pe):
                pe.wait_ge(loaded, 7 * 16)
                pe.sem_inc(batch_done, 1)

                def batch(b):
                    pe.wait_ge(y_added, b * 2 * TPB + 1)
                    for u in range(CB):
                        k = b * CB + u
                        pe.wait_ge(xn_ready, k + 1)
                        if u:
                            pe.wait_ge(chunk_ready, k)
                        for t in range(CH):
                            mm = pe.transpose(turn_ps[:, t * P:(t + 1) * P], xnc[:, u, t], pr.idf[:])
                        mm.then_inc(turned, 1)
                        pe.wait_ge(chunk_ready, k + 1)
                        for i in range(3):
                            m = u * 3 + i
                            if m >= 2:
                                pe.wait_ge(rotated2, b * 6 + m - 1)
                            pe.matmul(pr.ps[:, 2 * (m % 2)], wqk[:, 0, i], chunk[:, u], start=True, stop=True)
                            pe.matmul(pr.ps[:, 2 * (m % 2) + 1], wqk[:, 1, i], chunk[:, u], start=True, stop=True)\
                                .then_inc(qk_sum, 1)
                        for t in range(CH):
                            mm = pe.matmul(pr.ps[:, 4 + u, t * D:(t + 1) * D], chunk[:, u, t * P:(t + 1) * P], wv[:],
                                           start=True, stop=True)
                        mm.then_inc(v_sum, 1)
                        if u:
                            pe.wait_ge(r_taken, k)
                        for t in range(CH):
                            mm = pe.matmul(pr.ps[:, 7, t * 16:(t + 1) * 16], chunk[:, u, t * P:(t + 1) * P], wroute[:],
                                           start=True, stop=True)
                        mm.then_inc(r_sum, 1)

                    def score(i):
                        t, h = UNITS[i]
                        if i >= 2:
                            pe.wait_ge(exped, b * 16 + i - 1)
                        s = s_ps(i)
                        for k0 in range(0, t + 1, CH):
                            n = min(CH, t + 1 - k0)
                            last = k0 + n == t + 1
                            mm = pe.matmul(s[:, k0 * P:(k0 + n) * P], qk[:, h, t * P:(t + 1) * P],
                                           qk[:, 2, k0 * P:(k0 + n) * P], start=True, stop=not last)
                            if last:
                                mm = pe.matmul(s[:, t * P:(t + 1) * P], pr.idb[:], mask[:], start=False, stop=True)
                        mm.then_inc(scored, 1)

                    def turn(i):
                        t, h = UNITS[i]
                        pe.wait_ge(exped, b * 16 + i + 1)
                        for g, (gt, gh, k0) in enumerate(GROUPS):
                            if (gt, gh) == (t, h):
                                if g >= 2:
                                    pe.wait_ge(p_taken, b * NG + g - 1)
                                for a in range(min(CH, t + 1 - k0)):
                                    mm = pe.transpose(pr.ps[:, 4 + g % 2, a * P:(a + 1) * P],
                                                      prob[:, h, (k0 + a) * P:(k0 + a + 1) * P], pr.idf[:])
                                mm.then_inc(p_turned, 1)

                    def sum_values(t):
                        pe.wait_ge(p_taken, b * NG + len([1 for g in GROUPS if g[0] <= t]))
                        if t:
                            pe.wait_ge(o_taken, b * TPB + t)
                        for k in range(t + 1):
                            mm = pe.matmul(pr.ps[:, 6, 0:NH * P], vn[:, k], pt[:, t % 2, k].rearrange("p h q -> p (h q)"),
                                           start=k == 0, stop=k == t)
                        mm.then_inc(o_sum, 1)

                    def project(t):
                        pe.wait_ge(o_taken, b * TPB + t + 1)
                        pe.wait_ge(y_added, b * 2 * TPB + 2 * t + 1)
                        for h in range(NH):
                            mm = pe.matmul(pr.ps[:, 7, h * D:(h + 1) * D], ot[:, t % 2, h * P:(h + 1) * P], wo[:, h],
                                           start=True, stop=True)
                        mm.then_inc(y_sum, 1)

                    pe.wait_ge(rope_done, b * 6 + 6)
                    pe.wait_ge(v_taken, b * CB + CB)
                    pe.wait_ge(r_taken, b * CB + CB)
                    pe.wait_ge(chunk_kept, b * CB + CB)
                    score(0)
                    score(1)
                    for t in range(TPB):
                        turn(2 * t)
                        if t + 1 < TPB:
                            score(2 * t + 2)
                        turn(2 * t + 1)
                        if t + 1 < TPB:
                            score(2 * t + 3)
                        sum_values(t)
                        project(t)
                    pe.sem_inc(batch_done, 1)

                batches(pe, batch)


def l3_inner_statistics(pr):
    nc = pr.nc
    with ExitStack() as ctx:
        stats = pr.sb(ctx, "stats", [P, CH, 6])
        mv = pr.sb(ctx, "mv", [P, CH, 2])
        var = pr.sb(ctx, "var", [P, NT])
        std = pr.sb(ctx, "std", [P, NT])
        eps = pr.sb(ctx, "eps", [P, 1])
        dv = pr.sem(ctx, "dv_steps")
        x1_ready = pr.ev(ctx, "x1_ready")
        var_done = pr.sem(ctx, "var_done")
        std_done = pr.sem(ctx, "std_done")
        with nc.Block() as block:
            @block.gpsimd
            def _(pool):
                with pool.Fori(0, NC) as k:
                    hold(pool, pr.gate_p, x1_ready.sem, x1_ready.at(k))
                    pool.tensor_tensor(pr.X[:, ds(k * CH, CH), :], pr.X[:, ds(k * CH, CH), :],
                                       pr.x1[:, ds(k * CH, CH), :], ALU.add)

            @block.vector
            def _(v):
                v.memset(eps[:], 1e-5).then_inc(var_done, 1)
                per = 2 * CH + 3
                with v.Fori(0, NC) as k:
                    c = Chain(v, dv)
                    c.base = k * per
                    x1 = pr.x1[:, ds(k * CH, CH), :]
                    c.link(v.tensor_tensor(x1, pr.X[:, ds(k * CH, CH), :], bc(pr.mean[:, ds(k * CH, CH)], D),
                                           ALU.subtract))
                    v.tensor_tensor(x1, x1, bc(pr.rstd[:, ds(k * CH, CH)], D), ALU.mult).then_inc(x1_ready.sem, 1)
                    v.wait_ge(x1_ready.sem, x1_ready.at(k))
                    v.sem_inc(pr.gate_v, 1)
                    for t in range(CH):
                        c.step(v.bn_stats(stats[:, t, :], one(pr.x1, k * CH + t)))
                    c.wait()
                    v.sem_inc(pr.gate_v, 1)
                    for t in range(CH):
                        c.step(v.bn_aggr(mv[:, t, :], stats[:, t, :]))
                    c.wait()
                    v.sem_inc(pr.gate_v, 1)
                    c.step(v.tensor_copy(pr.mean2[:, ds(k * CH, CH)], mv[:, :, 0]))
                    c.step(v.tensor_copy(var[:, ds(k * CH, CH)], mv[:, :, 1]))
                v.wait_ge(dv, NC * per)
                v.sem_inc(var_done, 1)
                v.wait_ge(std_done, 1)
                v.reciprocal(pr.rstd2[:], std[:])

            @block.scalar
            def _(act):
                act.wait_ge(var_done, 2)
                nc.scalar.activation(std[:], var[:], ACT.Sqrt, bias=eps[:]).then_inc(std_done, 1)


def l3_project(pr):
    nc, d = pr.nc, pr.d
    SC = D + H
    SCALE = float(E) ** -0.5
    with ExitStack() as ctx:
        wqk = pr.sb(ctx, "wqk", [P, 4, D])
        bqk = pr.sb(ctx, "bqk", [P, 4])
        wva = pr.sb(ctx, "wva", [P, D])
        bva = pr.sb(ctx, "bva", [P, D])
        wkv = pr.sb(ctx, "wkv", [P, 2 * D])
        bkv = pr.sb(ctx, "bkv", [P, 2 * D])
        wb = pr.sb(ctx, "wb", [P, D])
        wbs = pr.sb(ctx, "wbs", [P, D])
        wbias = pr.sb(ctx, "wbias", [1, D])
        ones = pr.sb(ctx, "ones", [1, P])
        g1 = pr.sb(ctx, "g1", [P, 1])
        b1 = pr.sb(ctx, "b1", [P, 1])
        own = pr.sb(ctx, "own_head", [P, SC])
        xnc = pr.sb(ctx, "xnc", [P, 2, CH, D])
        x2c = pr.sb(ctx, "x2c", [P, 2, CH, D])
        chunk1 = pr.sb(ctx, "chunk1", [P, 2, CW])
        chunk2 = pr.sb(ctx, "chunk2", [P, 2, CW])
        low = pr.sb(ctx, "low", [P, 2, CW])
        f32 = pr.sb(ctx, "rows32", [P, 4, CW])
        parts = pr.sb(ctx, "parts", [P, 4, 3, CW], BF16)
        rest = pr.sb(ctx, "rest", [P, CW])
        kv32 = pr.sb(ctx, "kv32", [P, CH, 2 * D])
        klow = pr.sb(ctx, "klow", [P, CH, D])
        kf = pr.sb(ctx, "k_features", [P, CH, D])
        vaug = pr.sb(ctx, "v_aug", [P, CH, SC])
        states = pr.sb(ctx, "states", [P, CH + 1, SC])
        outer = pr.sb(ctx, "outer", [P, CH, SC])
        st_den = pr.sb(ctx, "state_denominators", [H, 2, CW])
        yc = pr.sb(ctx, "y_clipped", [P, 2, CH, D])
        loaded = pr.sem(ctx, "loaded")
        dv = pr.sem(ctx, "dv_steps")
        pl = pr.sem(ctx, "pool_steps")
        ready = pr.sem(ctx, "set_up")
        S = lambda n, p=0: pr.ev(ctx, n, p)
        xn_ready, x2_ready = S("xn_ready"), S("x2_ready")
        turned1, turned2 = S("turned1", 2), S("turned2", 2)
        c1_ready, c2_ready = S("c1_ready"), S("c2_ready", 1)
        row_sum, split = S("row_sum"), S("split", 4)
        rows_w, rows_l = S("windowed_rows_ready"), S("linear_rows_ready")
        taken_l = S("linear_rows_taken", 2)
        low_ready, low_exp = S("low_ready"), S("low_exp")
        va_sum, va_taken = S("va_sum", 2), S("va_taken", 1)
        kv_sum, kv_taken = S("kv_sum"), S("kv_taken", 1)
        klow_ready, klow_exp = S("klow_ready"), S("klow_exp")
        tok_ready = S("tok_ready")
        y_sum, y_taken, y_added = S("y_sum", 2), S("y_taken", 1), S("y_added", 2)
        outer_sum, outer_taken = S("outer_sum"), S("outer_taken", 1)
        states_ready = S("states_ready")
        out_sum, out_taken = S("out_sum", 1), S("out_taken", 1)
        stored = pr.sem(ctx, "stored")
        den_stored = [pr.sem(ctx, f"den_stored{u}") for u in range(2)]
        NW = 12

        with nc.Block() as block:
            @block.sync
            def _(sp):
                for dst, src in ((wqk, "l3_wqk"), (bqk, "l3_bqk"), (wva, "l3_wva"), (wkv, "l3_wkv"), (wb, "l3_wb"),
                                 (wbias, "l3_wbias"), (g1, "l3_g1"), (b1, "l3_b1"), (own, "own_head")):
                    sp.dma_start(dst[:], d[src]).then_inc(loaded, 16)
                sp.dma_start(bva[:], d["l3_bva"].broadcast_to([P, D])).then_inc(loaded, 16)
                sp.dma_start(bkv[:], d["l3_bkv"].broadcast_to([P, 2 * D])).then_inc(loaded, 16)
                sp.dma_start(wbs[:], d["l3_wbs"].broadcast_to([P, D])).then_inc(loaded, 16)
                sp.sem_inc(stored, 64)
                for u in range(2):
                    sp.sem_inc(den_stored[u], 16)

                def store(k, u, j):
                    for i, t in enumerate((pr.q_dram, pr.k_dram, pr.q2_dram, pr.k2_dram)):
                        sp.wait_ge(split.sem, split.at(k * 4 + i))
                        sp.dma_start(t[:, :, ds(u * CW, CW)].rearrange("a (b p) t -> b p a t", p=P)[ds(j, 1)]
                                     .rearrange("b p a t -> (b p) a t"), parts[:, i]).then_inc(stored, 16)
                    sp.wait_ge(out_taken.sem, out_taken.at(k))
                    sp.dma_start(pr.state_den_dram[ds(j * H, H), u * CW:(u + 1) * CW], st_den[:, u])\
                        .then_inc(den_stored[u], 16)

                two_a_turn(sp, store)
                sp.wait_ge(stored, 64 + 64 * NC)
                for u in range(2):
                    sp.wait_ge(den_stored[u], 16 + 16 * (NC // 2))

            @block.gpsimd
            def _(pool):
                for e, n in ((split, 4), (y_added, 2)):
                    pool.sem_inc(e.sem, n)

                def part(k, u, j):
                    c = Chain(pool, pl)
                    c.base = k * 12
                    for i in range(4):
                        e = rows_w if i < 2 else rows_l
                        hold(pool, pr.gate_p, e.sem, e.at(k * 2 + i % 2))
                        c.link(pool.tensor_tensor(rest[:], f32[:, i], parts[:, i, 0], ALU.subtract))
                        pool.sem_inc(pr.gate_p, 1)
                        c.link(pool.tensor_copy(parts[:, i, 1], rest[:]))
                        pool.sem_inc(pr.gate_p, 1)
                        c.link(pool.tensor_tensor(parts[:, i, 2], rest[:], parts[:, i, 1], ALU.subtract))
                        pool.sem_inc(split.sem, 1)
                    hold(pool, pr.gate_p, y_taken.sem, y_taken.at(k))
                    pool.tensor_tensor(pr.X[:, ds(k * CH, CH), :], pr.X[:, ds(k * CH, CH), :], yc[:, u],
                                       ALU.add).then_inc(y_added.sem, 1)

                two_a_turn(pool, part)

            @block.vector
            def _(v):
                v.wait_ge(loaded, 16 * NW)
                c = Chain(v, ready)
                c.link(v.memset(ones[:], 1.0))
                c.link(v.memset(pr.va[:, :, :, E:E + 1], 1.0))
                c.link(v.memset(pr.vs[:, :, :, E:E + 1], 1.0))
                c.link(v.memset(vaug[:], 1.0))
                c.link(v.tensor_scalar(wb[:], wb[:], 0.0, 2.0, ALU.is_ge, ALU.mult))
                c.link(v.tensor_scalar(wb[:], wb[:], -1.0, None, ALU.add))
                c.link(v.tensor_tensor(wb[:], wb[:], wbs[:], ALU.mult))
                for e in (va_taken, kv_taken, y_taken, outer_taken):
                    v.sem_inc(e.sem, 1)
                v.sem_inc(taken_l.sem, 2)
                STEPS = 24

                def part(k, u, j):
                    c = Chain(v, dv)
                    c.base = k * STEPS
                    v.wait_ge(turned2.sem, turned2.at(k - 2))
                    v.sem_inc(pr.gate_v, 1)
                    v.tensor_copy(xnc[:, u], pr.x1[:, ds(k * CH, CH), :]).then_inc(xn_ready.sem, 1)
                    c.link(v.tensor_tensor(x2c[:, u], pr.x1[:, ds(k * CH, CH), :], bc(pr.mean2[:, ds(k * CH, CH)], D),
                                           ALU.subtract))
                    v.tensor_tensor(x2c[:, u], x2c[:, u], bc(pr.rstd2[:, ds(k * CH, CH)], D),
                                    ALU.mult).then_inc(x2_ready.sem, 1)
                    v.wait_ge(va_sum.sem, va_sum.at(k))
                    c.link(v.tensor_tensor(pr.va[:, ds(j * H, H), u * CH:(u + 1) * CH, 0:E],
                                           pr.ps[:, 3].rearrange("p (t h e) -> p h t e", t=CH, e=E),
                                           bva[:].rearrange("p (h e) -> p h e", e=E).unsqueeze(2)
                                           .broadcast_to([P, H, CH, E]), ALU.add))
                    v.sem_inc(va_taken.sem, 1)
                    for i in (2, 3):
                        n = k * 4 + i
                        ps = pr.ps[:, 1 + i % 2]
                        v.wait_ge(split.sem, split.at(n - 4))
                        v.wait_ge(row_sum.sem, row_sum.at(n))
                        v.tensor_scalar(low[:, i - 2], ps, bqk[:, i:i + 1], 0.0, ALU.add, ALU.min)\
                            .then_inc(low_ready.sem, 1)
                        c.link(v.tensor_scalar(f32[:, i], ps, bqk[:, i:i + 1], 0.0, ALU.add, ALU.max))
                        v.sem_inc(taken_l.sem, 1)
                    for i in (2, 3):
                        v.wait_ge(low_exp.sem, low_exp.at(k * 2 + i - 2))
                        c.link(v.scalar_tensor_tensor(out=f32[:, i], in0=f32[:, i], scalar=SCALE if i == 2 else 1.0,
                                                      in1=low[:, i - 2], op0=ALU.mult, op1=ALU.add))
                        c.link(v.tensor_scalar(f32[:, i], f32[:, i], 1e-4, None, ALU.add))
                        v.wait_ge(stored, k * 64 + 64)
                        c.link(v.tensor_copy(parts[:, i, 0], f32[:, i]))
                        v.sem_inc(rows_l.sem, 1)
                    v.wait_ge(kv_sum.sem, kv_sum.at(k))
                    for half in range(2):
                        c.step(v.tensor_tensor(kv32[:, 2 * half:2 * half + 2],
                                               pr.ps[:, 4 + half].rearrange("p (t c) -> p t c", t=2),
                                               bkv[:].unsqueeze(1).broadcast_to([P, 2, 2 * D]), ALU.add))
                    c.wait()
                    v.sem_inc(kv_taken.sem, 1)
                    v.tensor_scalar(klow[:], kv32[:, :, 0:D], 0.0, None, ALU.min).then_inc(klow_ready.sem, 1)
                    c.step(v.tensor_copy(vaug[:, :, 0:D], kv32[:, :, D:]))
                    c.step(v.tensor_copy(pr.vs[:, ds(j * H, H), u * CH:(u + 1) * CH, 0:E],
                                         kv32[:, :, D:].rearrange("p t (h e) -> p h t e", e=E)))
                    c.step(v.tensor_scalar(kf[:], kv32[:, :, 0:D], 0.0, 1e-4, ALU.max, ALU.add))
                    v.wait_ge(out_sum.sem, out_sum.at(k - 1))
                    if u == 0:
                        c.step(v.memset(states[:, 0], 0.0))
                    else:
                        c.step(v.tensor_copy(states[:, 0], states[:, CH]))
                    c.wait()
                    v.wait_ge(klow_exp.sem, klow_exp.at(k))
                    c.link(v.tensor_tensor(kf[:], kf[:], klow[:], ALU.add))
                    v.sem_inc(tok_ready.sem, 1)
                    v.wait_ge(y_added.sem, y_added.at(k - 2))
                    v.wait_ge(y_sum.sem, y_sum.at(k))
                    c.link(v.tensor_scalar(yc[:, u], pr.ps[:, 6].rearrange("p (t d) -> p t d", d=D), 100.0, -100.0,
                                           ALU.min, ALU.max))
                    v.sem_inc(y_taken.sem, 1)
                    v.wait_ge(outer_sum.sem, outer_sum.at(k))
                    for half in range(2):
                        c.step(v.tensor_tensor(outer[:, 2 * half:2 * half + 2],
                                               pr.ps[:, 4 + half, 0:2 * SC].rearrange("p (t c) -> p t c", t=2),
                                               own[:].unsqueeze(1).broadcast_to([P, 2, SC]), ALU.mult))
                    c.wait()
                    v.sem_inc(outer_taken.sem, 1)
                    for t in range(CH):
                        c.link(v.tensor_tensor(states[:, t + 1], states[:, t], outer[:, t], ALU.add))
                    v.sem_inc(states_ready.sem, 1)
                    assert c.n == STEPS

                two_a_turn(v, part)

            @block.scalar
            def _(act):
                nc.scalar.preload_act_table(ACT.Exp)
                act.sem_inc(c2_ready.sem, 1)
                act.sem_inc(out_taken.sem, 1)
                act.wait_ge(loaded, 16 * NW)

                def part(k, u, j):
                    act.wait_ge(y_sum.sem, y_sum.at(k - 2))
                    act.wait_ge(turned1.sem, turned1.at(k))
                    nc.scalar.activation(chunk1[:, u], pr.ps[:, 0], ACT.Copy).then_inc(c1_ready.sem, 1)
                    act.wait_ge(turned2.sem, turned2.at(k))
                    nc.scalar.activation(chunk2[:, u], pr.ps[:, 0], ACT.Identity, scale=g1[:], bias=b1[:])\
                        .then_inc(c2_ready.sem, 1)
                    act.wait_ge(stored, k * 64 + 64)
                    act.sem_inc(pr.gate_a, 1)
                    for i in range(2):
                        act.wait_ge(split.sem, split.at(k * 4 + i - 4))
                        act.wait_ge(row_sum.sem, row_sum.at(k * 4 + i))
                        nc.scalar.activation(f32[:, i], pr.ps[:, 1 + i % 2], ACT.Identity, bias=bqk[:, i:i + 1])
                        nc.scalar.activation(parts[:, i, 0], pr.ps[:, 1 + i % 2], ACT.Identity,
                                             bias=bqk[:, i:i + 1]).then_inc(rows_w.sem, 1)
                    for i in range(2):
                        act.wait_ge(low_ready.sem, low_ready.at(k * 2 + i))
                        nc.scalar.activation(low[:, i], low[:, i], ACT.Exp, scale=SCALE if i == 0 else 1.0)\
                            .then_inc(low_exp.sem, 1)
                    act.wait_ge(klow_ready.sem, klow_ready.at(k))
                    nc.scalar.activation(klow[:], klow[:], ACT.Exp).then_inc(klow_exp.sem, 1)
                    act.wait_ge(den_stored[u], j * 16 + 16)
                    act.wait_ge(out_sum.sem, out_sum.at(k))
                    act.sem_inc(pr.gate_a, 1)
                    nc.scalar.activation(pr.st[:, ds(k * CW, CW)], pr.ps[:, 7], ACT.Copy)
                    nc.scalar.activation(st_den[:, u], pr.ps[0:H, 3], ACT.Copy).then_inc(out_taken.sem, 1)

                two_a_turn(act, part)

            @block.tensor
            def _(pe):
                pe.wait_ge(loaded, 16 * NW)
                pe.wait_ge(ready, 7)
                for e in (turned1, turned2, va_sum, y_sum):
                    pe.sem_inc(e.sem, 2)
                pe.sem_inc(out_sum.sem, 1)

                def part(k, u, j):
                    pe.wait_ge(c2_ready.sem, c2_ready.at(k - 1))
                    pe.wait_ge(xn_ready.sem, xn_ready.at(k))
                    for t in range(CH):
                        mm = pe.transpose(pr.ps[:, 0, t * P:(t + 1) * P], xnc[:, u, t], pr.idf[:])
                    mm.then_inc(turned1.sem, 1)
                    pe.wait_ge(c1_ready.sem, c1_ready.at(k))
                    pe.wait_ge(x2_ready.sem, x2_ready.at(k))
                    for t in range(CH):
                        mm = pe.transpose(pr.ps[:, 0, t * P:(t + 1) * P], x2c[:, u, t], pr.idf[:])
                    mm.then_inc(turned2.sem, 1)
                    pe.wait_ge(y_taken.sem, y_taken.at(k - 1))
                    for t in range(CH):
                        s = pr.ps[:, 6, t * D:(t + 1) * D]
                        pe.matmul(s, chunk1[:, u, t * P:(t + 1) * P], wb[:], start=True, stop=False)
                        mm = pe.matmul(s, ones[:], wbias[:], start=False, stop=True)
                    mm.then_inc(y_sum.sem, 1)
                    pe.wait_ge(c2_ready.sem, c2_ready.at(k))
                    pe.wait_ge(va_taken.sem, va_taken.at(k - 1))
                    pe.wait_ge(out_taken.sem, out_taken.at(k - 1))
                    for t in range(CH):
                        mm = pe.matmul(pr.ps[:, 3, t * D:(t + 1) * D], chunk2[:, u, t * P:(t + 1) * P], wva[:],
                                       start=True, stop=True)
                    mm.then_inc(va_sum.sem, 1)
                    for i in range(4):
                        e, n = (taken_l, k * 2 - 2 + i) if i < 2 else (rows_w, k * 2 + i - 2)
                        pe.wait_ge(e.sem, e.at(n))
                        pe.matmul(pr.ps[:, 1 + i % 2], wqk[:, i], chunk2[:, u], start=True, stop=True)\
                            .then_inc(row_sum.sem, 1)
                    pe.wait_ge(outer_taken.sem, outer_taken.at(k - 1))
                    for t in range(CH):
                        mm = pe.matmul(pr.ps[:, 4 + t // 2, (t % 2) * 2 * D:(t % 2 + 1) * 2 * D],
                                       chunk2[:, u, t * P:(t + 1) * P], wkv[:], start=True, stop=True)
                    mm.then_inc(kv_sum.sem, 1)
                    pe.wait_ge(tok_ready.sem, tok_ready.at(k))
                    for t in range(CH):
                        mm = pe.matmul(pr.ps[:, 4 + t // 2, (t % 2) * SC:(t % 2 + 1) * SC], kf[:, t], vaug[:, t],
                                       start=True, stop=True)
                    mm.then_inc(outer_sum.sem, 1)
                    pe.wait_ge(rows_l.sem, rows_l.at(k * 2 + 1))
                    pe.wait_ge(va_taken.sem, va_taken.at(k))
                    pe.wait_ge(states_ready.sem, states_ready.at(k))
                    for t in range(CH):
                        tile = slice(t * P, (t + 1) * P)
                        pe.matmul(pr.ps[:, 7, tile], states[:, t, 0:D], f32[:, 2, tile], start=True, stop=True)
                        mm = pe.matmul(pr.ps[0:H, 3, tile], states[:, t, D:SC], f32[:, 2, tile], start=True, stop=True)
                    mm.then_inc(out_sum.sem, 1)

                two_a_turn(pe, part)


def l3_attention(pr):
    nc, d = pr.nc, pr.d
    SCALE = float(E) ** -0.5
    KM = MROW + 2
    VA = E + 1
    VR = 2 * VA
    NG, NW = 5, 4
    NT2, NL = 2, 6
    DEPTH = 4
    with ExitStack() as ctx:
        qst, kst, qlin, klin = ([pr.sb(ctx, f"{n}{u}", [P, N], BF16) for u in range(2)]
                                for n in ("q_stack", "k_stack", "q_linear", "k_linear"))
        mask_q = pr.sb(ctx, "mask_by_query", [P, 2 * P], BF16)
        mask_k = pr.sb(ctx, "mask_by_key", [P, 2 * P], BF16)
        tri = pr.sb(ctx, "keys_up_to_query", [P, P])
        mx = pr.sb(ctx, "maxima", [P, TPB])
        mrow = [pr.sb(ctx, f"max_rows{u}", [P, TPB, KM], BF16) for u in range(2)]
        p_win = pr.sb(ctx, "p_windowed", [P, TPB, 2 * P])
        a_lin = pr.sb(ctx, "a_linear", [P, TPB, P])
        v_win = [pr.sb(ctx, f"v_windowed{u}", [P, TPB, VR]) for u in range(2)]
        v_lin = [pr.sb(ctx, f"v_linear{u}", [P, TPB, VR]) for u in range(2)]
        sums = [pr.sb(ctx, f"sums{u}", [VR, N]) for u in range(2)]
        zeroed = pr.sem(ctx, "zeroed")
        consts = pr.sem(ctx, "consts")
        stacks = [pr.sem(ctx, f"stacks{u}") for u in range(2)]
        first_part = pr.sem(ctx, "first_part")
        scored = pr.ev(ctx, "scored_by_query")
        reduced = pr.ev(ctx, "reduced", 2)
        rows_ready = pr.ev(ctx, "max_rows_ready")
        keyed = pr.ev(ctx, "scored_by_key", 2 * NL)
        exped = pr.ev(ctx, "exped", NW)
        masked = pr.ev(ctx, "masked")
        v_ready = pr.ev(ctx, "values_ready")
        summed = pr.ev(ctx, "values_summed", 2)
        taken = pr.ev(ctx, "sums_taken", 1)
        stored = [pr.sem(ctx, f"sums_stored{u}") for u in range(2)]

        def key_ps(n, g):
            return pr.ps[:, 2 + (n * NL + g) % DEPTH]

        with nc.Block() as block:
            @block.sync
            def _(sp):
                sp.dma_start(mask_q[:], d["mask_win_q"]).then_inc(consts, 16)
                sp.dma_start(mask_k[:], d["mask_win_k"]).then_inc(consts, 16)
                sp.dma_start(tri[:], d["tri"]).then_inc(consts, 16)
                sp.wait_ge(zeroed, 16)

                def load(n, u):
                    sp.wait_ge(keyed.sem, keyed.at((n - 2) * NL + NL - 1))
                    for q, k, qd, kd in ((qst, kst, pr.q_dram, pr.k_dram), (qlin, klin, pr.q2_dram, pr.k2_dram)):
                        for a in range(3):
                            rows = slice(a * 3 * E, (a + 1) * 3 * E)
                            sp.dma_start(q[u][rows], qd[:, ds(n * E, E), :]).then_inc(stacks[u], 16)
                            sp.dma_start(k[u][rows], kd[a:a + 1, ds(n * E, E), :].broadcast_to([3, E, N]))\
                                .then_inc(stacks[u], 16)

                def store(n, u):
                    sp.wait_ge(taken.sem, taken.at(n))
                    sp.dma_start(pr.sums_dram[ds(n), 0:VR].rearrange("o r t -> (o r) t"), sums[u][:])\
                        .then_inc(stored[u], 16)

                for u in range(2):
                    sp.sem_inc(stored[u], 16)
                    load(u, u)
                with sp.Fori(0, HEADS // 2 - 1) as j:
                    for u in range(2):
                        load(j * 2 + u + 2, u)
                        store(j * 2 + u, u)
                for u in range(2):
                    store(HEADS - 2 + u, u)
                    sp.wait_ge(stored[u], 16 + 16 * HEADS // 2)

            @block.gpsimd
            def _(pool):
                for u in range(2):
                    for t in (qst[u], kst[u], qlin[u], klin[u], mrow[u], v_win[u], v_lin[u]):
                        pool.memset(t[:], 0.0).then_inc(zeroed, 1)
                pool.wait_ge(zeroed, 14)
                for u in range(2):
                    pool.memset(kst[u][MROW:KM], 1.0).then_inc(zeroed, 1)
                pool.wait_ge(zeroed, 16)

                def values(n, u):
                    hold(pool, pr.gate_p, summed.sem, summed.at(n - 2))
                    pool.tensor_copy(v_win[u][:, :, 0:VA], one(pr.va, n))
                    pool.tensor_copy(v_lin[u][:, :, VA:VR], one(pr.vs, n)).then_inc(v_ready.sem, 1)

                with pool.Fori(0, HEADS // 2) as j:
                    for u in range(2):
                        values(j * 2 + u, u)

            @block.vector
            def _(v):
                v.sem_inc(reduced.sem, 2)
                v.wait_ge(zeroed, 16)
                v.wait_ge(consts, 48)

                def largest(n, u, g):
                    v.wait_ge(scored.sem, scored.at(n * NG + g))
                    ps = pr.ps[:, (u * NG + g) % 2]
                    if g == 0:
                        v.reduce_max(mx[:, 0:1], ps[:, P:2 * P], AX)
                        v.reduce_max(mx[:, 1:2], ps[:, 2 * P:4 * P], AX).then_inc(reduced.sem, 1)
                    else:
                        v.reduce_max(mx[:, 2 * g:2 * g + 2], ps.rearrange("p (t k) -> p t k", t=2), AX)\
                            .then_inc(reduced.sem, 1)

                def max_rows(n, u):
                    v.wait_ge(reduced.sem, reduced.at(n * NG + NW - 1))
                    v.tensor_scalar(mrow[u][:, :, MROW], mx[:], -1.0, None, ALU.mult).then_inc(first_part, 1)
                    v.wait_ge(first_part, n + 1)
                    v.scalar_tensor_tensor(out=mrow[u][:, :, MROW + 1], in0=mx[:], scalar=-1.0,
                                           in1=mrow[u][:, :, MROW], op0=ALU.mult, op1=ALU.subtract)\
                        .then_inc(rows_ready.sem, 1)
                    v.wait_ge(scored.sem, scored.at(n * NG + NW))
                    v.tensor_copy(qst[u][MROW:KM], pr.ps[MROW:KM, (u * NG + NW) % 2].bitcast(BF16))\
                        .then_inc(reduced.sem, 1)

                def triangle(n, u, g):
                    v.wait_ge(keyed.sem, keyed.at(n * NL + g))
                    v.tensor_tensor(a_lin[:, CH * g:CH * (g + 1)], key_ps(u, g).rearrange("p (t q) -> p t q", q=P),
                                    tri[:].unsqueeze(1).broadcast_to([P, CH, P]), ALU.mult).then_inc(masked.sem, 1)

                def step(n, u):
                    for g in range(NW):
                        if g < NT2:
                            triangle(n, u, g)
                        largest(n + 1, 1 - u, g)
                    max_rows(n + 1, 1 - u)

                for g in range(NW):
                    largest(0, 0, g)
                max_rows(0, 0)
                with v.Fori(0, HEADS // 2 - 1) as j:
                    for u in range(2):
                        step(j * 2 + u, u)
                step(HEADS - 2, 0)
                for g in range(NT2):
                    triangle(HEADS - 1, 1, g)

            @block.scalar
            def _(act):
                nc.scalar.preload_act_table(ACT.Exp)
                act.sem_inc(exped.sem, NW)
                act.sem_inc(taken.sem, 1)

                def exps(n, u):
                    for g in range(NW):
                        act.wait_ge(keyed.sem, keyed.at(n * NL + NT2 + g))
                        ps = key_ps(u, NT2 + g)
                        if g < NW - 1:
                            ins = nc.scalar.activation(p_win[:, 2 * g:2 * g + 2].rearrange("p t q -> p (t q)"), ps,
                                                       ACT.Exp, scale=SCALE)
                        else:
                            flat = p_win[:, 2 * g:2 * g + 2].rearrange("p t q -> p (t q)")
                            ins = nc.scalar.activation(flat[:, 0:3 * P], ps[:, 0:3 * P], ACT.Exp, scale=SCALE)
                        ins.then_inc(exped.sem, 1)

                def take(n, u, j):
                    act.wait_ge(stored[u], j * 16 + 16)
                    act.wait_ge(summed.sem, summed.at(n))
                    nc.scalar.activation(sums[u][:].rearrange("p (a t) -> p a t", a=2), pr.ps[0:VR, 6:8],
                                         ACT.Copy).then_inc(taken.sem, 1)

                exps(0, 0)
                with act.Fori(0, HEADS // 2 - 1) as j:
                    for u in range(2):
                        take(j * 2 + u, u, j)
                        exps(j * 2 + u + 1, 1 - u)
                take(HEADS - 2, 0, HEADS // 2 - 1)
                exps(HEADS - 1, 1)
                take(HEADS - 1, 1, HEADS // 2 - 1)

            @block.tensor
            def _(pe):
                pe.sem_inc(keyed.sem, 2 * NL)
                pe.sem_inc(summed.sem, 2)
                pe.wait_ge(consts, 48)
                pe.wait_ge(zeroed, 16)

                def query_group(n, u, g, half):
                    pe.wait_ge(reduced.sem, reduced.at(n * NG + g - 2))
                    ps = pr.ps[:, (u * NG + g) % 2]
                    if g == 0:
                        pe.wait_ge(stacks[u], (half + 1) * 12 * 16)
                    if g < NW:
                        for i in range(2):
                            t = 2 * g + i
                            lo = P if t == 0 else 0
                            s = ps[:, i * 2 * P + lo:(i + 1) * 2 * P]
                            pe.matmul(s, qst[u][0:KQ, t * P:(t + 1) * P], kst[u][0:KQ, (t - 1) * P + lo:(t + 1) * P],
                                      start=True, stop=False)
                            mm = pe.matmul(s, pr.idb[:], mask_q[:, lo:], start=False, stop=True)
                    else:
                        pe.wait_ge(rows_ready.sem, rows_ready.at(n))
                        for t in range(TPB):
                            mm = pe.transpose(ps[0:KM, t * 64:(t + 1) * 64].bitcast(BF16), mrow[u][:, t], pr.idb[:])
                    mm.then_inc(scored.sem, 1)

                def key_group(n, u, g):
                    b = g - DEPTH
                    if b < 0:
                        b, m = b + NL, n - 1
                    else:
                        m = n
                    e, i = (masked, m * NT2 + b) if b < NT2 else (exped, m * NW + b - NT2)
                    pe.wait_ge(e.sem, e.at(i))
                    if g == NT2:
                        pe.wait_ge(reduced.sem, reduced.at(n * NG + NW))
                    ps = key_ps(u, g)
                    if g >= NT2:
                        for i in range(2):
                            t = 2 * (g - NT2) + i
                            w = P if t == TPB - 1 else 2 * P
                            s = ps[:, i * 2 * P:i * 2 * P + w]
                            pe.matmul(s, kst[u][0:KM, t * P:(t + 1) * P], qst[u][0:KM, t * P:t * P + w],
                                      start=True, stop=False)
                            mm = pe.matmul(s, pr.idb[:], mask_k[:, 0:w], start=False, stop=True)
                    else:
                        for i in range(CH):
                            t = CH * g + i
                            mm = pe.matmul(ps[:, i * P:(i + 1) * P], klin[u][0:KQ, t * P:(t + 1) * P],
                                           qlin[u][0:KQ, t * P:(t + 1) * P], start=True, stop=True)
                    mm.then_inc(keyed.sem, 1)

                def values(n, u, g):
                    if g < NT2:
                        if g == 0:
                            pe.wait_ge(v_ready.sem, v_ready.at(n))
                            pe.wait_ge(taken.sem, taken.at(n - 1))
                        pe.wait_ge(masked.sem, masked.at(n * NT2 + g))
                        for i in range(CH):
                            pe.matmul(pr.ps[0:VR, 6 + g, i * P:(i + 1) * P], v_lin[u][:, CH * g + i],
                                      a_lin[:, CH * g + i], start=i == 0, stop=False)
                    else:
                        w = g - NT2
                        pe.wait_ge(exped.sem, exped.at(n * NW + w))
                        for t in (2 * w, 2 * w + 1):
                            for i in range(2):
                                lo, hi = max(t, i * CH), min(t + 2, (i + 1) * CH)
                                if lo < hi:
                                    mm = pe.matmul(pr.ps[0:VR, 6 + i, (lo - i * CH) * P:(hi - i * CH) * P],
                                                   v_win[u][:, t], p_win[:, t, (lo - t) * P:(hi - t) * P],
                                                   start=False, stop=t == CH * (i + 1) - 1)
                        if g == NL - 1:
                            mm.then_inc(summed.sem, 1)

                def step(n, u, half):
                    more = not isinstance(n, int) or n + 1 < HEADS
                    for g in range(NL + 2):
                        if g < NL:
                            key_group(n, u, g)
                        if g < NG and more:
                            query_group(n + 1, 1 - u, g, half)
                        if g >= 2:
                            values(n, u, g - 2)

                for g in range(NG):
                    query_group(0, 0, g, 0)
                with pe.Fori(0, HEADS // 2 - 1) as j:
                    for u in range(2):
                        step(j * 2 + u, u, j + u)
                step(HEADS - 2, 0, HEADS // 2 - 1)
                step(HEADS - 1, 1, HEADS // 2)


def l3_mix(pr):
    nc, d = pr.nc, pr.d
    VA = E + 1
    with ExitStack() as ctx:
        wp, ws, wo = (pr.sb(ctx, n, [P, D]) for n in ("wp", "ws", "wo"))
        b12 = pr.sb(ctx, "b12", [P, 2])
        bsum = pr.sb(ctx, "bsum", [P, 1])
        bo = pr.sb(ctx, "bo", [1, D])
        ones = pr.sb(ctx, "ones", [1, P])
        num = pr.sb(ctx, "value_sums", [P, 2, 2, CW])
        inv = pr.sb(ctx, "inverses", [P, 2, 2, CW])
        den = pr.sb(ctx, "denominators", [P, 2, CW])
        st_den = pr.sb(ctx, "state_denominators", [P, CW])
        mt = pr.sb(ctx, "mixed_turned", [P, 2, CW])
        m32 = pr.sb(ctx, "mixed", [P, 2, CH, D])
        loaded = pr.sem(ctx, "loaded")
        set_up = pr.sem(ctx, "set_up")
        read = [pr.sem(ctx, f"sums_read{u}") for u in range(2)]
        den_read = pr.sem(ctx, "denominators_read")
        inverted = pr.sem(ctx, "inverted")
        inv_stored = pr.sem(ctx, "inverses_stored")
        steps = pr.sem(ctx, "steps")
        divided = pr.ev(ctx, "divided")
        inner = pr.ev(ctx, "inner", 2)
        inner_taken = pr.ev(ctx, "inner_taken", 1)
        summed = pr.ev(ctx, "summed", 2)
        added = pr.ev(ctx, "added", 2)
        kept = pr.ev(ctx, "kept", 2)
        with nc.Block() as block:
            @block.sync
            def _(sp):
                for half in range(2):
                    rows, cols = slice(half * HEADS, (half + 1) * HEADS), slice(half * CW, (half + 1) * CW)
                    for w in range(2):
                        sp.dma_start(den[rows, w], pr.sums_dram[:, w * VA + E, cols]).then_inc(den_read, 16)
                    sp.dma_start(st_den[rows], pr.state_den_dram[:, cols]).then_inc(den_read, 16)
                for dst, src in ((wp, "l3_wp"), (ws, "l3_wos"), (wo, "l3_wo"), (b12, "l3_b12"), (bo, "l3_bo")):
                    sp.dma_start(dst[:], d[src]).then_inc(loaded, 16)
                sp.wait_ge(inverted, 3)
                for half in range(2):
                    sp.dma_start(pr.inverse_dram[:, 0:2, half * CW:(half + 1) * CW],
                                 den[half * HEADS:(half + 1) * HEADS]).then_inc(inv_stored, 16)
                sp.wait_ge(inv_stored, 32)

                def part(k, u, j):
                    sp.wait_ge(inner.sem, inner.at(k - 2))
                    heads = pr.sums_dram[ds(j * H, H), :, u * CW:(u + 1) * CW]
                    for w in range(2):
                        sp.dma_start(num[:, u, w], heads[:, w * VA:w * VA + E]).then_inc(read[u], 16)
                        sp.dma_start(inv[:, u, w], pr.inverse_dram[ds(j * H, H), w:w + 1, u * CW:(u + 1) * CW]
                                     .broadcast_to([H, E, CW])).then_inc(read[u], 16)

                two_a_turn(sp, part)

            @block.gpsimd
            def _(pool):
                pool.sem_inc(kept.sem, 2)

                def part(k, u, j):
                    hold(pool, pr.gate_p, added.sem, added.at(k))
                    pool.tensor_tensor(pr.x1[:, ds(k * CH, CH), :], pr.x1[:, ds(k * CH, CH), :], m32[:, u],
                                       ALU.add).then_inc(kept.sem, 1)

                two_a_turn(pool, part)

            @block.vector
            def _(v):
                v.wait_ge(loaded, 80)
                v.memset(ones[:], 1.0).then_inc(set_up, 1)
                v.tensor_tensor(bsum[:], b12[:, 0:1], b12[:, 1:2], ALU.add).then_inc(set_up, 1)
                v.sem_inc(added.sem, 2)
                v.wait_ge(den_read, 96)
                v.tensor_tensor(den[:, 1], den[:, 1], st_den[:], ALU.add).then_inc(inverted, 1)
                v.wait_ge(inverted, 1)
                v.tensor_scalar(den[:, 1], den[:, 1], 1e-6, None, ALU.add).then_inc(inverted, 1)
                v.wait_ge(inverted, 2)
                v.reciprocal(den[:], den[:]).then_inc(inverted, 1)

                def part(k, u, j):
                    v.wait_ge(read[u], j * 64 + 64)
                    v.sem_inc(pr.gate_v, 1)
                    v.tensor_tensor(num[:, u, 1], num[:, u, 1], pr.st[:, ds(k * CW, CW)], ALU.add).then_inc(steps, 1)
                    v.wait_ge(steps, k + 1)
                    v.tensor_tensor(num[:, u], num[:, u], inv[:, u], ALU.mult).then_inc(divided.sem, 1)
                    v.wait_ge(kept.sem, kept.at(k - 2))
                    v.wait_ge(summed.sem, summed.at(k))
                    v.tensor_copy(m32[:, u], pr.ps[:, 4 + u].rearrange("p (t d) -> p t d", d=D))
                    v.tensor_tensor(pr.X[:, ds(k * CH, CH), :], pr.X[:, ds(k * CH, CH), :],
                                    pr.ps[:, 4 + u].rearrange("p (t d) -> p t d", d=D), ALU.add).then_inc(added.sem, 1)

                two_a_turn(v, part)

            @block.scalar
            def _(act):
                act.sem_inc(inner_taken.sem, 1)
                act.wait_ge(set_up, 2)

                def part(k, u, j):
                    act.wait_ge(summed.sem, summed.at(k - 2))
                    act.wait_ge(inner.sem, inner.at(k))
                    nc.scalar.activation(mt[:, u], pr.ps[:, 2], ACT.Identity, bias=bsum[:]).then_inc(inner_taken.sem, 1)

                two_a_turn(act, part)

            @block.tensor
            def _(pe):
                pe.sem_inc(summed.sem, 2)
                pe.sem_inc(inner.sem, 2)
                pe.wait_ge(loaded, 80)
                pe.wait_ge(set_up, 2)

                def part(k, u, j):
                    pe.wait_ge(divided.sem, divided.at(k))
                    pe.wait_ge(inner_taken.sem, inner_taken.at(k - 1))
                    pe.matmul(pr.ps[:, 2], wp[:], num[:, u, 0], start=True, stop=False)
                    pe.matmul(pr.ps[:, 2], ws[:], num[:, u, 1], start=False, stop=True).then_inc(inner.sem, 1)
                    pe.wait_ge(inner_taken.sem, inner_taken.at(k))
                    pe.wait_ge(added.sem, added.at(k - 2))
                    for t in range(CH):
                        s = pr.ps[:, 4 + u, t * D:(t + 1) * D]
                        pe.matmul(s, mt[:, u, t * P:(t + 1) * P], wo[:], start=True, stop=False)
                        mm = pe.matmul(s, ones[:], bo[:], start=False, stop=True)
                    mm.then_inc(summed.sem, 1)

                two_a_turn(pe, part)


def l3_mlp(pr):
    nc, d = pr.nc, pr.d
    U = 4
    with ExitStack() as ctx:
        w1 = pr.sb(ctx, "w1", [P, U * D])
        b1 = pr.sb(ctx, "b1", [P, U])
        w2 = pr.sb(ctx, "w2", [P, U, D])
        b2 = pr.sb(ctx, "b2", [1, D])
        ones = pr.sb(ctx, "ones", [1, P])
        gm = pr.sb(ctx, "gm", [P, 2])
        xnc = pr.sb(ctx, "xnc", [P, 2, CH, D])
        chunk = pr.sb(ctx, "chunk", [P, 2, CW])
        hid = pr.sb(ctx, "hidden", [P, 2, U, CW])
        loaded = pr.sem(ctx, "loaded")
        set_up = pr.sem(ctx, "set_up")
        xn_sub = pr.ev(ctx, "xn_sub")
        xn_ready = pr.ev(ctx, "xn_ready")
        turned = pr.ev(ctx, "turned", 2)
        chunk_ready = pr.ev(ctx, "chunk_ready", 1)
        h_sum = pr.ev(ctx, "h_sum")
        h_ready = pr.ev(ctx, "h_ready", 4)
        y_sum = pr.ev(ctx, "y_sum", 2)
        added = pr.ev(ctx, "added", 2)
        with nc.Block() as block:
            @block.sync
            def _(sp):
                for dst, src in ((w1, "l3_w1"), (b1, "l3_b1m"), (w2, "l3_w2"), (b2, "l3_b2m"), (gm, "l3_gm")):
                    sp.dma_start(dst[:], d[src]).then_inc(loaded, 16)

            @block.vector
            def _(v):
                v.memset(ones[:], 1.0).then_inc(set_up, 1)
                v.sem_inc(added.sem, 2)

                def norm(k, u):
                    v.wait_ge(turned.sem, turned.at(k - 2))
                    v.tensor_tensor(xnc[:, u], pr.x1[:, ds(k * CH, CH), :], bc(pr.mean[:, ds(k * CH, CH)], D),
                                    ALU.subtract).then_inc(xn_sub.sem, 1)
                    v.wait_ge(xn_sub.sem, xn_sub.at(k))
                    v.tensor_tensor(xnc[:, u], xnc[:, u], bc(pr.rstd[:, ds(k * CH, CH)], D),
                                    ALU.mult).then_inc(xn_ready.sem, 1)

                def part(k, u, j):
                    norm(k, u)
                    v.wait_ge(y_sum.sem, y_sum.at(k))
                    v.tensor_tensor(pr.X[:, ds(k * CH, CH), :], pr.X[:, ds(k * CH, CH), :],
                                    pr.ps[:, 6 + u].rearrange("p (t d) -> p t d", d=D), ALU.add).then_inc(added.sem, 1)

                two_a_turn(v, part)

            @block.scalar
            def _(act):
                nc.scalar.preload_act_table(ACT.Gelu)
                act.sem_inc(chunk_ready.sem, 1)
                act.sem_inc(h_ready.sem, 4)
                act.wait_ge(loaded, 80)

                def part(k, u, j):
                    act.wait_ge(y_sum.sem, y_sum.at(k - 2))
                    act.wait_ge(turned.sem, turned.at(k))
                    nc.scalar.activation(chunk[:, u], pr.ps[:, 0], ACT.Identity, scale=gm[:, 0:1], bias=gm[:, 1:2])\
                        .then_inc(chunk_ready.sem, 1)
                    for i in range(U):
                        act.wait_ge(h_sum.sem, h_sum.at(k * U + i))
                        nc.scalar.activation(hid[:, u, i], pr.ps[:, 1 + i], ACT.Gelu, bias=b1[:, i:i + 1])\
                            .then_inc(h_ready.sem, 1)

                two_a_turn(act, part)

            @block.tensor
            def _(pe):
                pe.sem_inc(turned.sem, 2)
                pe.sem_inc(y_sum.sem, 2)
                pe.wait_ge(loaded, 80)
                pe.wait_ge(set_up, 1)

                def part(k, u, j):
                    pe.wait_ge(chunk_ready.sem, chunk_ready.at(k - 1))
                    pe.wait_ge(xn_ready.sem, xn_ready.at(k))
                    for t in range(CH):
                        mm = pe.transpose(pr.ps[:, 0, t * P:(t + 1) * P], xnc[:, u, t], pr.idf[:])
                    mm.then_inc(turned.sem, 1)
                    pe.wait_ge(chunk_ready.sem, chunk_ready.at(k))
                    for i in range(U):
                        pe.wait_ge(h_ready.sem, h_ready.at(k * U + i - U))
                        pe.matmul(pr.ps[:, 1 + i], w1[:, i * D:(i + 1) * D], chunk[:, u], start=True, stop=True)\
                            .then_inc(h_sum.sem, 1)
                    pe.wait_ge(added.sem, added.at(k - 2))
                    for t in range(CH):
                        s = pr.ps[:, 6 + u, t * D:(t + 1) * D]
                        for i in range(U):
                            if t == 0:
                                pe.wait_ge(h_ready.sem, h_ready.at(k * U + i))
                            pe.matmul(s, hid[:, u, i, t * P:(t + 1) * P], w2[:, i], start=i == 0, stop=False)
                        mm = pe.matmul(s, ones[:], b2[:], start=False, stop=True)
                    mm.then_inc(y_sum.sem, 1)

                two_a_turn(pe, part)


def program(nc, dram, out):
    pr = Prog(nc, dram, out)
    with ExitStack() as ctx:
        pr.X = pr.sb(ctx, "x", [P, NT, D])
        pr.xt = pr.sb(ctx, "xn_turned", [P, T])
        pr.mean = pr.sb(ctx, "mean", [P, NT])
        pr.rstd = pr.sb(ctx, "rstd", [P, NT])
        pr.inorm = pr.sb(ctx, "inverse_norm", [P, NT])
        pr.idf = pr.sb(ctx, "ident_f", [P, P])
        pr.idb = pr.sb(ctx, "ident_b", [P, P], BF16)
        pr.logits = pr.sb(ctx, "logits", [P, NT, 16])
        pr.gates = pr.sb(ctx, "gates", [P, NT, 17])
        pr.ps = ctx.enter_context(nc.psum_tensor("banks", [P, 8, 512], F32))
        pr.gate_v, pr.gate_p, pr.gate_a, pr.gate_e = (nc.alloc_semaphore("gate_" + e) for e in "vpae")
        pr.q_dram = nc.dram_tensor("q_parts", (3, B * P, N), BF16).ap()
        pr.k_dram = nc.dram_tensor("k_parts", (3, B * P, N), BF16).ap()
        pr.q2_dram = nc.dram_tensor("q2_parts", (3, B * P, N), BF16).ap()
        pr.k2_dram = nc.dram_tensor("k2_parts", (3, B * P, N), BF16).ap()
        pr.s_dram = nc.dram_tensor("selection_scores", (HEADS, N), F32).ap()
        pr.sums_dram = nc.dram_tensor("head_sums", (HEADS, 3 * (E + 1), N), F32).ap()
        pr.inverse_dram = nc.dram_tensor("inverse_denominators", (HEADS, 3, N), F32).ap()
        pr.state_den_dram = nc.dram_tensor("state_denominators", (HEADS, N), F32).ap()
        load_constants(pr)
        pr.end()
        statistics(pr, norm=True)
        pr.end()
        with ExitStack() as layer:
            pr.kvp = pr.sb(layer, "kv_parts", [P, HEADS, TPB, 6 * E], BF16)
            pr.va = pr.sb(layer, "values", [P, HEADS, TPB, E + 1])
            pr.slot = pr.sb(layer, "slots", [P, HEADS, TPB])
            l0_project(pr)
            pr.end()
            l0_select(pr)
            pr.end()
            l0_attention(pr)
            pr.end()
            out_project(pr, "wo0", "bo0")
            pr.end()
        experts(pr, "m0", 8, 64, False)
        pr.end()
        statistics(pr)
        pr.end()
        l1_attention(pr)
        pr.end()
        top_gates(pr, 8, 1, False, "l1_bg")
        pr.end()
        experts(pr, "m1", 8, 128, False, 9)
        pr.end()
        statistics(pr)
        pr.end()
        l2_attention(pr)
        pr.end()
        top_gates(pr, 15, 3, True)
        pr.end()
        experts(pr, "m2", 17, 128, True)
        pr.end()
        statistics(pr)
        pr.end()
        with ExitStack() as layer:
            pr.x1 = pr.sb(layer, "x1", [P, NT, D])
            pr.mean2 = pr.sb(layer, "mean2", [P, NT])
            pr.rstd2 = pr.sb(layer, "rstd2", [P, NT])
            with ExitStack() as mixing:
                pr.va = pr.sb(mixing, "windowed_values", [P, HEADS, TPB, E + 1])
                pr.vs = pr.sb(mixing, "linear_values", [P, HEADS, TPB, E + 1])
                pr.st = pr.sb(mixing, "state_sums", [P, T])
                l3_inner_statistics(pr)
                pr.end()
                l3_project(pr)
                pr.end()
                l3_attention(pr)
                pr.end()
                l3_mix(pr)
                pr.end()
            statistics(pr, of=pr.x1)
            pr.end()
            l3_mlp(pr)
            pr.end()
        store_output(pr)


def kernel(**inputs):
    import ml_dtypes
    from concourse import bacc
    from concourse.bass_utils import run_bass_kernel_spmd

    g = {k: np.asarray(v) for k, v in inputs.items()}
    c = np.ascontiguousarray
    bf = ml_dtypes.bfloat16
    a = {}

    def heads_last(w):
        wk, wv = w
        lead = wk.shape[:-1]
        return c(np.stack([wk.reshape(*lead, H, E), wv.reshape(*lead, H, E)], -2).reshape(*lead, 2 * D))

    a["x"] = c(g["L0_attn_x"].reshape(NT, P, D).transpose(1, 0, 2).reshape(P, NT * D))
    a["ident_f"] = np.eye(P, dtype=np.float32)
    a["ident_b"] = np.eye(P, dtype=bf)
    a["wq"] = c(g["L0_attn_Wq"].T)
    a["wk"] = c(g["L0_attn_Wk"].T)
    a["wkv"] = heads_last((g["L0_attn_Wk"].T, g["L0_attn_Wv"].T))
    a["bkv"] = heads_last((g["L0_attn_bk"][None], g["L0_attn_bv"][None]))
    a["bq"] = c(g["L0_attn_bq"][:, None])
    a["bk"] = c(g["L0_attn_bk"][:, None])
    a["ws"] = c(g["L0_attn_Ws"].T)
    a["bs"] = c(g["L0_attn_bs"][:, None])
    a["cent"] = g["L0_ffn_centroids"]
    a["wroute"] = c(g["L0_ffn_w_route"].T)
    q, k = np.arange(P)[:, None], np.arange(P)[None]
    a["mask_band"] = np.concatenate([np.where(k < q, NEG, 0), 0.0 * (k + q), np.where(k > q, NEG, 0)], 1).astype(bf)
    a["places"] = c(np.broadcast_to(np.arange(N // 4, dtype=np.float32), (P, N // 4)))
    marks = np.zeros((3, 6, N), bf)
    for v in range(3):
        marks[v, v] = marks[v, 3 + v] = 1
    a["max_marks"] = marks
    a["wo0"] = c(g["L0_attn_Wo"].T)
    a["bo0"] = c(g["L0_attn_bo"][None])
    a["m0_w1"] = c(g["L0_ffn_w1"].reshape(4, 2, P, 64).transpose(2, 0, 1, 3).reshape(P, 4, P))
    a["m0_b1"] = c(g["L0_ffn_b1"].reshape(4, P).T[:, :, None])
    a["m0_w2"] = c(g["L0_ffn_w2"].reshape(4, P, D).transpose(1, 0, 2))
    a["m0_b2"] = g["L0_ffn_b2"]

    w = g["L1_attn_w_qkv"]
    a["l1_wq"], a["l1_wk"] = c(w[:, 0:D]), c(w[:, D:2 * D])
    a["l1_wo"] = g["L1_attn_w_out"]
    a["l1_wg"] = g["L1_ffn_Wg"]
    a["l1_bg"] = c(g["L1_ffn_bg"][None])
    a["mask_causal"] = np.where(k > q, NEG, 0.0).astype(bf)
    a["order"] = c(np.broadcast_to(np.arange(16, 0, -1, dtype=np.float32), (P, 16)))
    a["m1_w1"] = c(g["L1_ffn_W1"].transpose(1, 0, 2))
    a["m1_b1"] = c(g["L1_ffn_b1"].T[:, :, None])
    a["m1_w2"] = c(g["L1_ffn_W2"].transpose(1, 0, 2))
    a["m1_b2"] = np.concatenate([g["L1_ffn_b2"], g["L1_attn_b_out"][None]])

    wq = g["L2_attn_Wq"]
    three = np.stack([wq[0], wq[1], g["L2_attn_Wk"]])
    pairs = three.reshape(3, D // 2, 2, D)
    turned = np.stack([pairs[:, :, 1], pairs[:, :, 0]], 2).reshape(3, D, D)
    a["l2_wqk"] = c(np.stack([three, turned]).transpose(3, 0, 1, 2))
    a["l2_wv"] = c(g["L2_attn_Wv"].T)
    a["l2_wo"] = c(g["L2_attn_Wo"].T.reshape(2, D, D).transpose(1, 0, 2))
    a["l2_gate"] = c(np.concatenate([g["L2_ffn_gate_w"].T, np.zeros((D, 1), np.float32)], 1))
    theta = np.float32(10000.0) ** (np.float32(-2.0) * np.arange(0, D, 2, dtype=np.float32) / np.float32(D))
    angles = (np.arange(N, dtype=np.float32)[:, None] * theta.astype(np.float32)[None]).astype(np.float32)
    a["l2_cos"] = c(np.repeat(np.cos(angles), 2, axis=1).T.astype(np.float32))
    a["l2_sin"] = c(np.stack([-np.sin(angles), np.sin(angles)], 2).reshape(N, D).T.astype(np.float32))
    F, FS = P, 2 * P
    w1 = np.concatenate([g["L2_ffn_fc1_w"].reshape(15, 2, F, D),
                         g["L2_ffn_s_fc1_w"].reshape(2, 2, F, D).transpose(1, 0, 2, 3)])
    b1 = np.concatenate([g["L2_ffn_fc1_b"].reshape(15, 2, F), g["L2_ffn_s_fc1_b"].reshape(2, 2, F).transpose(1, 0, 2)])
    a["m2_w1"] = c(w1.transpose(3, 0, 1, 2).reshape(P, 17, 2 * P))
    a["m2_b1"] = c(b1.transpose(2, 0, 1))
    w2 = np.concatenate([g["L2_ffn_fc2_w"], g["L2_ffn_s_fc2_w"].reshape(D, 2, F).transpose(1, 0, 2)])
    a["m2_w2"] = c(w2.transpose(2, 0, 1))
    a["m2_b2"] = np.concatenate([g["L2_ffn_fc2_b"], g["L2_ffn_s_fc2_b"][None], np.zeros((1, D), np.float32)])
    a["m2_mult"] = c(np.concatenate([g["L2_ffn_geglu_mult"], g["L2_ffn_s_geglu_mult"].reshape(2, F)]).T)

    wa, ws = g["L3_attn_Wqkv_a"], g["L3_attn_Wqkv_s"]
    ba, bs = g["L3_attn_bqkv_a"], g["L3_attn_bqkv_s"]
    a["l3_wqk"] = c(np.stack([wa[:, :D], wa[:, D:2 * D], ws[:, :D], ws[:, D:2 * D]], 1))
    a["l3_bqk"] = c(np.stack([ba[:D], ba[D:2 * D], bs[:D], bs[D:2 * D]], 1))
    a["l3_wva"], a["l3_bva"] = c(wa[:, 2 * D:]), c(ba[None, 2 * D:])
    a["l3_wkv"], a["l3_bkv"] = c(ws[:, D:]), c(bs[None, D:])
    a["l3_wb"] = c(g["L3_ffn_weights"].T)
    a["l3_wbs"] = c(g["L3_ffn_scale"][None])
    a["l3_wbias"] = c(g["L3_ffn_bias"][None])
    a["l3_g1"], a["l3_b1"] = c(g["L3_attn_g1"][:, None]), c(g["L3_attn_b1"][:, None])
    a["own_head"] = (np.arange(P)[:, None] // E == np.concatenate([np.arange(P) // E, np.arange(H)])[None]).astype(np.float32)
    a["mask_win_q"] = np.concatenate([np.where(k <= q, NEG, 0.0), np.where(k > q, NEG, 0.0)], 1).astype(bf)
    a["mask_win_k"] = np.concatenate([np.where(k < q, NEG, 0.0), np.where(k >= q, NEG, 0.0)], 1).astype(bf)
    a["tri"] = (k >= q).astype(np.float32)
    a["l3_wp"], a["l3_wos"], a["l3_wo"] = g["L3_attn_Wp_a"], g["L3_attn_Wo_s"], g["L3_attn_Wo"]
    a["l3_b12"] = c(np.stack([g["L3_attn_bp_a"], g["L3_attn_bo_s"]], 1))
    a["l3_bo"] = c(g["L3_attn_bo"][None])
    a["l3_w1"] = g["L3_attn_W1"]
    a["l3_b1m"] = c(g["L3_attn_b1m"].reshape(4, D).T)
    a["l3_w2"] = c(g["L3_attn_W2"].reshape(4, D, D).transpose(1, 0, 2))
    a["l3_b2m"] = c(g["L3_attn_b2m"][None])
    a["l3_gm"] = c(np.stack([g["L3_attn_gm"], g["L3_attn_bm"]], 1))

    nc = bacc.Bacc("TRN2", target_bir_lowering=False, num_devices=1)
    dram, arrays = {}, {}
    for name, v in a.items():
        v = c(v)
        arrays["in_" + name] = v
        dram[name] = nc.dram_tensor("in_" + name, v.shape, mybir.dt.from_np(v.dtype), kind="ExternalInput").ap()
    out = nc.dram_tensor("out_0", (P, NT * D), F32, kind="ExternalOutput").ap()
    program(nc, dram, out)
    r = run_bass_kernel_spmd(nc, [arrays], core_ids=[0])
    o = r.results[0]["out_0"]
    return o.reshape(P, NT, D).transpose(1, 0, 2).reshape(B, N, D)
```

```python
from contextlib import ExitStack

import numpy as np

import concourse.bass as bass
from concourse import mybir

F32 = mybir.dt.float32
BF16 = mybir.dt.bfloat16
ACT = mybir.ActivationFunctionType
ALU = mybir.AluOpType
AX = mybir.AxisListType.X

P = 128
B, N, D = 4, 1024, 128
T = B * N
NT = T // P
TPB = N // P
CH = 4
NC = NT // CH
CW = CH * P
H, E = 16, 8
HEADS = B * H
KQ = 9 * E
MROW = 96
NEG = -1.0e30
LOW = -3.0e38


class Ev:

    def __init__(self, sem, prime):
        self.sem, self.prime = sem, prime

    def at(self, i):
        return i + (self.prime + 1)


class Chain:

    def __init__(self, eng, sem):
        self.eng, self.sem, self.n, self.base = eng, sem, 0, 0

    def step(self, ins):
        ins.then_inc(self.sem, 1)
        self.n += 1

    def wait(self):
        self.eng.wait_ge(self.sem, self.base + self.n)

    def link(self, ins):
        self.step(ins)
        self.wait()


class Prog:

    def __init__(self, nc, dram, out):
        self.nc, self.d, self.out = nc, dram, out
        self.names = 0

        self.stage = []

    def sem(self, ctx, name):
        self.names += 1
        self.stage.append(self.nc.alloc_semaphore(f"{name}_{self.names}"))
        return self.stage[-1]

    def end(self):
        self.nc.clear_and_free_semaphores(self.stage)
        self.stage = []
        self.nc.all_engine_barrier()

    def ev(self, ctx, name, prime=0):
        return Ev(self.sem(ctx, name), prime)

    def sb(self, ctx, name, shape, dt=F32):
        self.names += 1
        return ctx.enter_context(self.nc.sbuf_tensor(f"{name}_{self.names}", shape, dt))


def hold(eng, gate, sem, value):
    eng.wait_ge(sem, value)
    eng.sem_inc(gate, 1)


def staggered(eng, *stages):
    lagged(eng, *((s, stage) for s, stage in enumerate(stages) if stage))


def lagged(eng, *stages):
    lead = max(lag for lag, _ in stages)
    peel = lead + lead % 2

    def alone(k):
        for lag, stage in stages:
            if 0 <= k - lag < NC:
                stage(k - lag, (k - lag) % 2, (k - lag) // 2)

    for k in range(peel):
        alone(k)
    with eng.Fori(0, (NC - peel) // 2) as j:
        for u in range(2):
            for lag, stage in stages:
                off = peel + u - lag
                stage(j * 2 + off, off % 2, j + off // 2)
    for k in range(NC, NC + lead):
        alone(k)


def ds(i, n=1):
    return bass.ds(i, n)


def one(ap, i):
    s = ap[:, ds(i, 1)]
    names = "abcdef"[:len(s.shape) - 2]
    if len(s.shape) == 3:
        return s.rearrange("p o a -> p (o a)")
    return s.rearrange(f"p o {' '.join(names)} -> p (o {names[0]}) {' '.join(names[1:])}")


def bc(ap, n):
    return ap.unsqueeze(len(ap.shape)).broadcast_to([*ap.shape, n])


def store_q_parts(sp, q_dram, j, cols, parts, stored):
    sp.dma_start(q_dram[ds(j * P, P), :, cols], parts).then_inc(stored, 16)


def store_k_parts(sp, k_dram, j, cols, parts, stored):
    for a in range(3):
        sp.dma_start(k_dram[ds(j * H, H), a, :, cols], parts[:, a]).then_inc(stored, 16)


def load_stacks(sp, n, q_stack, k_stack, q_dram, k_dram, loaded):
    sp.dma_start(q_stack[0:KQ], q_dram[ds(n * E, E)].rearrange("e b t -> (e b) t").unsqueeze(0)
                 .broadcast_to([3, 3 * E, N])).then_inc(loaded, 16)
    sp.dma_start(k_stack[0:KQ], k_dram[ds(n)].rearrange("o a e t -> (o a e) t").unsqueeze(1)
                 .broadcast_to([3 * E, 3, N])).then_inc(loaded, 16)


def load_constants(pr):
    nc, d = pr.nc, pr.d
    with ExitStack() as ctx:
        loaded = pr.sem(ctx, "loaded")
        with nc.Block() as block:
            @block.sync
            def _(sp):
                sp.dma_start(pr.X[:], d["x"].rearrange("p (t d) -> p t d", d=D)).then_inc(loaded, 16)
                sp.dma_start(pr.idf[:], d["ident_f"]).then_inc(loaded, 16)
                sp.dma_start(pr.idb[:], d["ident_b"]).then_inc(loaded, 16)
                sp.wait_ge(loaded, 48)


def statistics(pr, norm=False, of=None):
    nc = pr.nc
    of = pr.X if of is None else of
    with ExitStack() as ctx:
        stats = pr.sb(ctx, "stats", [P, 2, CH, 6])
        mv = pr.sb(ctx, "mv", [P, 2, CH, 2])
        taken = pr.ev(ctx, "statistics_taken")
        aggregated = pr.ev(ctx, "aggregated", 2)
        kept = pr.ev(ctx, "kept", 2)
        var = pr.sb(ctx, "var", [P, NT])
        std = pr.sb(ctx, "std", [P, NT])
        ssq = pr.sb(ctx, "ssq", [P, NT])
        nrm = pr.sb(ctx, "nrm", [P, NT])
        dv = pr.sem(ctx, "dv")
        eps = pr.sb(ctx, "eps", [P, 1])
        var_done = pr.sem(ctx, "var_done")
        std_done = pr.sem(ctx, "std_done")
        with nc.Block() as block:
            @block.vector
            def _(v):
                v.memset(eps[:], 1e-5).then_inc(var_done, 1)
                def take(k, u, j):
                    v.wait_ge(aggregated.sem, aggregated.at(k - 2))
                    v.sem_inc(pr.gate_v, 1)
                    for t in range(CH):
                        ins = v.bn_stats(stats[:, u, t, :], one(of, k * CH + t))
                    ins.then_inc(taken.sem, 1)

                def aggregate(k, u, j):
                    v.wait_ge(kept.sem, kept.at(k - 2))
                    v.wait_ge(taken.sem, taken.at(k))
                    v.sem_inc(pr.gate_v, 1)
                    for t in range(CH):
                        ins = v.bn_aggr(mv[:, u, t, :], stats[:, u, t, :])
                    ins.then_inc(aggregated.sem, 1)

                def keep(k, u, j):
                    v.wait_ge(aggregated.sem, aggregated.at(k))
                    v.tensor_copy(pr.mean[:, ds(k * CH, CH)], mv[:, u, :, 0])
                    v.tensor_copy(var[:, ds(k * CH, CH)], mv[:, u, :, 1]).then_inc(kept.sem, 1)

                v.sem_inc(aggregated.sem, 2)
                v.sem_inc(kept.sem, 2)
                staggered(v, take, aggregate, keep)
                v.wait_ge(kept.sem, kept.at(NC - 1))
                v.sem_inc(var_done, 1)
                v.wait_ge(std_done, 1)
                v.reciprocal(pr.rstd[:], std[:]).then_inc(dv, 1)
                v.wait_ge(dv, 1)
                if norm:
                    v.scalar_tensor_tensor(out=ssq[:], in0=var[:], scalar=float(D), in1=pr.rstd[:],
                                           op0=ALU.mult, op1=ALU.mult).then_inc(dv, 1)
                    v.wait_ge(dv, 2)
                    v.tensor_tensor(ssq[:], ssq[:], pr.rstd[:], ALU.mult).then_inc(var_done, 1)
                    v.wait_ge(std_done, 2)
                    v.tensor_scalar(nrm[:], nrm[:], 1e-12, None, ALU.max).then_inc(dv, 1)
                    v.wait_ge(dv, 3)
                    v.reciprocal(pr.inorm[:], nrm[:])

            @block.scalar
            def _(act):
                act.wait_ge(var_done, 2)
                nc.scalar.activation(std[:], var[:], ACT.Sqrt, bias=eps[:]).then_inc(std_done, 1)
                if norm:
                    act.wait_ge(var_done, 3)
                    nc.scalar.activation(nrm[:], ssq[:], ACT.Sqrt).then_inc(std_done, 1)




def split_rows(pr, ctx, name):
    return (pr.sb(ctx, name + "32", [P, 2, CW]), pr.sb(ctx, name + "_parts", [P, 2, 3, CW], BF16),
            pr.sb(ctx, name + "_rest", [P, CW]))


def l0_project(pr):
    nc, d = pr.nc, pr.d
    with ExitStack() as ctx:
        wq = pr.sb(ctx, "wq", [P, D])
        wk = pr.sb(ctx, "wk", [P, D])
        wkv = pr.sb(ctx, "wkv", [P, 2 * D])
        ws = pr.sb(ctx, "ws", [P, H])
        wroute = pr.sb(ctx, "wroute", [P, 16])
        cent = pr.sb(ctx, "cent", [8, D])
        cn2 = pr.sb(ctx, "cn2", [8, 1])
        csq = pr.sb(ctx, "csq", [8, D])
        bq = pr.sb(ctx, "bq", [P, 1])
        bk = pr.sb(ctx, "bk", [P, 1])
        bs = pr.sb(ctx, "bs", [H, 1])
        bkv = pr.sb(ctx, "bkv", [P, 2 * D])
        xnc = pr.sb(ctx, "xnc", [P, 2, CH, D])
        chunk = pr.sb(ctx, "chunk", [P, 2, CW])
        q32, qparts, qrest = split_rows(pr, ctx, "q")
        k32, kparts, krest = split_rows(pr, ctx, "k")
        kv32 = pr.sb(ctx, "kv32", [P, CH, 2 * D])
        kvrest = pr.sb(ctx, "kvrest", [P, CH, 2 * D])
        kvhalf = pr.sb(ctx, "kvhalf", [P, CH, 2 * D], BF16)
        srow = pr.sb(ctx, "srow", [H, 2, CW])
        loaded = pr.sem(ctx, "weights_loaded")
        dv = pr.sem(ctx, "dv_steps")
        pl = pr.sem(ctx, "pool_steps")
        setup = pr.sem(ctx, "centroids_steps")
        xn_sub = pr.ev(ctx, "xn_sub")
        xn_ready = pr.ev(ctx, "xn_ready")
        turned = pr.ev(ctx, "xn_turned", 2)
        chunk_ready = pr.ev(ctx, "chunk_ready", 1)
        chunk_kept = pr.ev(ctx, "chunk_kept", 2)
        q_sum = pr.ev(ctx, "q_sum")
        k_sum = pr.ev(ctx, "k_sum")
        kv_sum = pr.ev(ctx, "kv_sum", 2)
        s_sum = pr.ev(ctx, "s_sum")
        r_sum = pr.ev(ctx, "r_sum", 2)
        q_taken = pr.ev(ctx, "q_taken", 1)
        k_taken = pr.ev(ctx, "k_taken", 1)
        kv_taken = pr.ev(ctx, "kv_taken", 1)
        s_taken = pr.ev(ctx, "s_taken", 1)
        r_taken = pr.ev(ctx, "r_taken", 1)
        q_split = pr.ev(ctx, "q_split", 2)
        k_split = pr.ev(ctx, "k_split", 2)
        qk_stored = [pr.sem(ctx, f"qk_stored{u}") for u in range(2)]
        s_stored = [pr.sem(ctx, f"s_stored{u}") for u in range(2)]
        turn_ps, q_ps, k_ps, s_ps, r_ps = pr.ps[:, 0], pr.ps[:, 1], pr.ps[:, 2], pr.ps[:, 5], pr.ps[:, 6]
        kv_ps = pr.ps[:, 3:5]
        cent_ps = pr.ps[:, 7]
        WEIGHTS = 10 * 16

        def chunks(eng, body):
            with eng.Fori(0, NC // 2) as j:
                for u in range(2):
                    body(j * 2 + u, u, j)

        with nc.Block() as block:
            @block.sync
            def _(sp):
                for dst, src in ((wq, "wq"), (wk, "wk"), (wkv, "wkv"), (ws, "ws"), (cent, "cent"), (bq, "bq"),
                                 (bk, "bk"), (bs, "bs")):
                    sp.dma_start(dst[:], d[src]).then_inc(loaded, 16)
                sp.dma_start(bkv[:], d["bkv"].broadcast_to([P, 2 * D])).then_inc(loaded, 16)
                sp.dma_start(wroute[:, 0:8], d["wroute"]).then_inc(loaded, 16)
                for u in range(2):
                    sp.sem_inc(qk_stored[u], 64)
                    sp.sem_inc(s_stored[u], 16)

                def store(k, u, j):
                    sp.wait_ge(q_split.sem, q_split.at(k))
                    store_q_parts(sp, pr.q_dram, j, slice(u * CW, (u + 1) * CW), qparts[:, u], qk_stored[u])
                    sp.wait_ge(k_split.sem, k_split.at(k))
                    store_k_parts(sp, pr.k_dram, j, slice(u * CW, (u + 1) * CW), kparts[:, u], qk_stored[u])
                    sp.wait_ge(s_taken.sem, s_taken.at(k))
                    sp.dma_start(pr.s_dram.rearrange("(b h) t -> b h t", h=H)[ds(j, 1), :, u * CW:(u + 1) * CW]
                                 .rearrange("b h t -> (b h) t"), srow[:, u]).then_inc(s_stored[u], 16)

                chunks(sp, store)
                for u in range(2):
                    sp.wait_ge(qk_stored[u], 64 + 64 * NC // 2)
                    sp.wait_ge(s_stored[u], 16 + 16 * NC // 2)

            @block.gpsimd
            def _(pool):
                pool.sem_inc(chunk_kept.sem, 2)
                pool.sem_inc(q_split.sem, 2)
                pool.sem_inc(k_split.sem, 2)

                def part(k, u, j):
                    c = Chain(pool, pl)
                    c.base = k * 6
                    hold(pool, pr.gate_p, chunk_ready.sem, chunk_ready.at(k))
                    pool.tensor_copy(pr.xt[:, ds(k * CW, CW)], chunk[:, u]).then_inc(chunk_kept.sem, 1)
                    for taken, split, x32, parts, rest in ((q_taken, q_split, q32, qparts, qrest),
                                                           (k_taken, k_split, k32, kparts, krest)):
                        hold(pool, pr.gate_p, taken.sem, taken.at(k))
                        c.link(pool.tensor_tensor(rest[:], x32[:, u], parts[:, u, 0], ALU.subtract))
                        pool.sem_inc(pr.gate_p, 1)
                        c.link(pool.tensor_copy(parts[:, u, 1], rest[:]))
                        pool.sem_inc(pr.gate_p, 1)
                        c.step(pool.tensor_tensor(parts[:, u, 2], rest[:], parts[:, u, 1], ALU.subtract))
                        c.wait()
                        pool.sem_inc(split.sem, 1)

                chunks(pool, part)

            @block.vector
            def _(v):
                v.wait_ge(loaded, WEIGHTS)
                v.memset(pr.va[:, :, :, E:E + 1], 1.0).then_inc(dv, 1)
                v.tensor_tensor(csq[:], cent[:], cent[:], ALU.mult).then_inc(dv, 1)
                v.wait_ge(dv, 2)
                v.reduce_sum(cn2[:], csq[:], AX).then_inc(setup, 1)
                v.wait_ge(setup, 2)
                v.tensor_scalar(cn2[:], cn2[:], 1e-12, None, ALU.max).then_inc(dv, 1)
                v.wait_ge(dv, 3)
                v.reciprocal(cn2[:], cn2[:]).then_inc(dv, 1)
                v.wait_ge(dv, 4)
                v.tensor_scalar(cent[:], cent[:], cn2[:], None, ALU.mult).then_inc(setup, 1)
                v.wait_ge(setup, 4)
                v.tensor_copy(wroute[:, 8:16], cent_ps[:, 0:8]).then_inc(setup, 1)
                v.sem_inc(kv_taken.sem, 1)

                def norm(k, u, j):
                    v.wait_ge(turned.sem, turned.at(k - 2))
                    v.tensor_tensor(xnc[:, u], pr.X[:, ds(k * CH, CH), :], bc(pr.mean[:, ds(k * CH, CH)], D),
                                    ALU.subtract).then_inc(xn_sub.sem, 1)
                    v.wait_ge(xn_sub.sem, xn_sub.at(k))
                    v.tensor_tensor(xnc[:, u], xnc[:, u], bc(pr.rstd[:, ds(k * CH, CH)], D),
                                    ALU.mult).then_inc(xn_ready.sem, 1)

                def keys_values(k, u, j):
                    c = Chain(v, dv)
                    c.base = k * 9 + 4
                    v.wait_ge(kv_sum.sem, kv_sum.at(k))
                    c.step(v.tensor_tensor(kv32[:, 0:2], kv_ps[:, 0].rearrange("p (t c) -> p t c", t=2),
                                           bkv[:].unsqueeze(1).broadcast_to([P, 2, 2 * D]), ALU.add))
                    c.link(v.tensor_tensor(kv32[:, 2:4], kv_ps[:, 1].rearrange("p (t c) -> p t c", t=2),
                                           bkv[:].unsqueeze(1).broadcast_to([P, 2, 2 * D]), ALU.add))
                    v.sem_inc(kv_taken.sem, 1)
                    heads = kv32[:].rearrange("p t (h c) -> p h t c", c=2 * E)
                    c.step(v.tensor_copy(pr.va[:, ds(j * H, H), u * CH:(u + 1) * CH, 0:E], heads[:, :, :, E:2 * E]))
                    c.link(v.tensor_copy(kvhalf[:], kv32[:]))
                    c.step(v.tensor_tensor(kvrest[:], kv32[:], kvhalf[:], ALU.subtract))
                    pv = pr.kvp[:, ds(j * H, H), u * CH:(u + 1) * CH, :]
                    c.wait()
                    v.sem_inc(pr.gate_v, 1)
                    c.link(v.tensor_copy(pv[:, :, :, 0:16], kvhalf[:].rearrange("p t (h c) -> p h t c", c=16)))
                    c.link(v.tensor_copy(kvhalf[:], kvrest[:]))
                    v.sem_inc(pr.gate_v, 1)
                    c.step(v.tensor_copy(pv[:, :, :, 16:32], kvhalf[:].rearrange("p t (h c) -> p h t c", c=16)))
                    c.step(v.tensor_tensor(pv[:, :, :, 32:48], kvrest[:].rearrange("p t (h c) -> p h t c", c=16),
                                           kvhalf[:].rearrange("p t (h c) -> p h t c", c=16), ALU.subtract))
                    c.wait()
                    v.sem_inc(pr.gate_v, 1)
                    assert c.n == 9

                lagged(v, (0, norm), (2, keys_values))

            @block.scalar
            def _(act):
                act.wait_ge(setup, 1)
                nc.scalar.activation(cn2[:], cn2[:], ACT.Sqrt).then_inc(setup, 1)
                nc.scalar.preload_act_table(ACT.Identity)
                for e in (chunk_ready, q_taken, k_taken, s_taken, r_taken):
                    act.sem_inc(e.sem, 1)

                def keep(k, u, j):
                    act.wait_ge(kv_sum.sem, kv_sum.at(k - 2))
                    act.wait_ge(chunk_kept.sem, chunk_kept.at(k - 2))
                    act.wait_ge(turned.sem, turned.at(k))
                    nc.scalar.activation(chunk[:, u], turn_ps, ACT.Copy).then_inc(chunk_ready.sem, 1)

                def rows(k, u, j):
                    act.wait_ge(qk_stored[u], j * 64 + 64)
                    for total, taken, split, ps, bias, x32, parts in (
                            (q_sum, q_taken, q_split, q_ps, bq, q32, qparts),
                            (k_sum, k_taken, k_split, k_ps, bk, k32, kparts)):
                        act.wait_ge(split.sem, split.at(k - 2))
                        act.wait_ge(total.sem, total.at(k))
                        nc.scalar.activation(x32[:, u], ps, ACT.Identity, bias=bias[:])
                        nc.scalar.activation(parts[:, u, 0], ps, ACT.Identity, bias=bias[:]).then_inc(taken.sem, 1)
                    act.wait_ge(s_stored[u], j * 16 + 16)
                    act.wait_ge(s_sum.sem, s_sum.at(k))
                    nc.scalar.activation(srow[:, u], s_ps[0:H], ACT.Identity, bias=bs[:]).then_inc(s_taken.sem, 1)
                    hold(act, pr.gate_a, r_sum.sem, r_sum.at(k))
                    nc.scalar.activation(pr.logits[:, ds(k * CH, CH), :],
                                         r_ps[:, 0:CH * 16].rearrange("p (t c) -> p t c", c=16),
                                         ACT.Copy).then_inc(r_taken.sem, 1)

                staggered(act, keep, rows)

            @block.tensor
            def _(pe):
                pe.wait_ge(loaded, WEIGHTS)
                pe.sem_inc(turned.sem, 2)
                pe.sem_inc(r_sum.sem, 2)
                pe.sem_inc(kv_sum.sem, 2)
                pe.wait_ge(setup, 3)
                pe.transpose(cent_ps[:, 0:8], cent[:], pr.idf[0:8, 0:8]).then_inc(setup, 1)
                pe.wait_ge(setup, 5)

                def turn(k, u, j):
                    pe.wait_ge(xn_ready.sem, xn_ready.at(k))
                    pe.wait_ge(chunk_ready.sem, chunk_ready.at(k - 1))
                    for t in range(CH):
                        mm = pe.transpose(turn_ps[:, t * P:(t + 1) * P], xnc[:, u, t], pr.idf[:])
                    mm.then_inc(turned.sem, 1)

                def products(k, u, j):
                    pe.wait_ge(chunk_ready.sem, chunk_ready.at(k))
                    pe.wait_ge(q_taken.sem, q_taken.at(k - 1))
                    pe.matmul(q_ps, wq[:], chunk[:, u], start=True, stop=True).then_inc(q_sum.sem, 1)
                    pe.wait_ge(k_taken.sem, k_taken.at(k - 1))
                    pe.matmul(k_ps, wk[:], chunk[:, u], start=True, stop=True).then_inc(k_sum.sem, 1)
                    pe.wait_ge(s_taken.sem, s_taken.at(k - 1))
                    pe.matmul(s_ps[0:H], ws[:], chunk[:, u], start=True, stop=True).then_inc(s_sum.sem, 1)
                    pe.wait_ge(r_taken.sem, r_taken.at(k - 1))
                    for t in range(CH):
                        mm = pe.matmul(r_ps[:, t * 16:(t + 1) * 16], chunk[:, u, t * P:(t + 1) * P], wroute[:],
                                       start=True, stop=True)
                    mm.then_inc(r_sum.sem, 1)
                    pe.wait_ge(kv_taken.sem, kv_taken.at(k - 1))
                    for t in range(CH):
                        mm = pe.matmul(kv_ps[:, t // 2, (t % 2) * 2 * D:(t % 2 + 1) * 2 * D],
                                       chunk[:, u, t * P:(t + 1) * P], wkv[:], start=True, stop=True)
                    mm.then_inc(kv_sum.sem, 1)

                staggered(pe, turn, products)


def l0_gates(pr):
    nc = pr.nc
    NE = 8
    with ExitStack() as ctx:
        lg = pr.sb(ctx, "lg", [P, NT, NE])
        w8 = pr.sb(ctx, "w8", [P, NT, NE])
        w8b = pr.sb(ctx, "w8b", [P, NT, NE])
        m1 = pr.sb(ctx, "m1", [P, NT])
        m2 = pr.sb(ctx, "m2", [P, NT])
        cnt = pr.sb(ctx, "cnt", [P, NT])
        dv = pr.sem(ctx, "dv_steps")
        lg_ready = pr.sem(ctx, "lg_ready")
        exp_done = pr.sem(ctx, "exp_done")
        with nc.Block() as block:
            @block.vector
            def _(v):
                c = Chain(v, dv)
                c.link(v.tensor_tensor(w8[:], pr.logits[:, :, 8:16], bc(pr.inorm[:], NE), ALU.mult))
                c.link(v.tensor_tensor(lg[:], w8[:], pr.logits[:, :, 0:8], ALU.add))
                c.link(v.reduce_max(m1[:], lg[:], AX))
                v.tensor_tensor(w8[:], lg[:], bc(m1[:], NE), ALU.subtract).then_inc(lg_ready, 1)
                c.link(v.tensor_tensor(w8b[:], lg[:], bc(m1[:], NE), ALU.is_ge))
                c.link(v.reduce_sum(cnt[:], w8b[:], AX))
                c.link(v.scalar_tensor_tensor(out=w8b[:], in0=w8b[:], scalar=LOW, in1=lg[:], op0=ALU.mult,
                                              op1=ALU.add))
                c.link(v.reduce_max(m2[:], w8b[:], AX))
                c.link(v.tensor_scalar(cnt[:], cnt[:], 2.0, None, ALU.is_ge))
                c.link(v.tensor_tensor(m1[:], m1[:], cnt[:], ALU.mult))
                c.link(v.tensor_scalar(cnt[:], cnt[:], 1.0, -LOW, ALU.subtract, ALU.mult))
                c.link(v.tensor_tensor(m1[:], m1[:], cnt[:], ALU.add))
                c.link(v.tensor_tensor(m2[:], m2[:], m1[:], ALU.max))
                c.link(v.tensor_tensor(lg[:], lg[:], bc(m2[:], NE), ALU.is_ge))
                v.wait_ge(exp_done, 1)
                c.link(v.tensor_tensor(w8b[:], w8[:], lg[:], ALU.mult))
                c.link(v.reduce_sum(m1[:], w8b[:], AX))
                c.link(v.reciprocal(m2[:], m1[:]))
                c.link(v.tensor_tensor(pr.gates[:, :, 0:NE], w8b[:], bc(m2[:], NE), ALU.mult))

            @block.scalar
            def _(act):
                act.wait_ge(lg_ready, 1)
                nc.scalar.activation(w8[:], w8[:], ACT.Exp).then_inc(exp_done, 1)


def l0_places(pr):
    nc = pr.nc
    with ExitStack() as ctx:
        ones = pr.sb(ctx, "ones", [HEADS, N])
        dv = pr.sem(ctx, "dv_steps")
        slots_ready = pr.sem(ctx, "slots_ready")
        slots_turned = pr.sem(ctx, "slots_turned")
        s0, s1 = pr.s0, pr.s1
        with nc.Block() as block:
            @block.vector
            def _(v):
                c = Chain(v, dv)
                c.step(v.memset(ones[:], 1.0))
                c.link(v.tensor_tensor(s1[:], s1[:], s0[:], ALU.not_equal))
                c.link(v.tensor_tensor_scan(s0[:], ones[:], s1[:], 0.0, ALU.mult, ALU.add))
                c.link(v.tensor_tensor(s0[:], s0[:], s1[:], ALU.mult))
                v.tensor_scalar(s0[:], s0[:], -1.0, None, ALU.add).then_inc(slots_ready, 1)
                v.wait_ge(slots_turned, 1)
                v.tensor_copy(pr.slot[:], pr.ps[:, 0].rearrange("p (t n) -> p n t", n=HEADS))

            @block.tensor
            def _(pe):
                pe.wait_ge(slots_ready, 1)
                for t in range(TPB):
                    mm = pe.transpose(pr.ps[:, 0, t * HEADS:(t + 1) * HEADS], s0[:, t * P:(t + 1) * P],
                                      pr.idf[0:HEADS, 0:HEADS])
                mm.then_inc(slots_turned, 1)


def l0_attention(pr):
    nc, d = pr.nc, pr.d
    TOP, GLOB, V3 = N // 4, 64, 3
    SLOTS = TOP // P
    SCALE = float(E) ** -0.5
    KM = MROW + 2 * V3
    G_SEL, G_TURN, G_TOP, G_GLOB, G_MAX, NG = 0, 3, 10, 14, 15, 16
    G_LOC = [1, 2, 4, 5, 6, 7, 8, 9]
    LG_GLOB, LG_TOP, LG_LOC, NL = 0, 1, 3, 7
    VA = E + 1
    VR = (V3 + 1) * VA
    with ExitStack() as ctx:
        qst = [pr.sb(ctx, f"q_stack{u}", [P, N], BF16) for u in range(2)]
        kst = [pr.sb(ctx, f"k_stack{u}", [P, N], BF16) for u in range(2)]
        ksel = [pr.sb(ctx, f"k_selected{u}", [P, TOP], BF16) for u in range(2)]
        kglob = [pr.sb(ctx, f"k_global{u}", [P, GLOB], BF16) for u in range(2)]
        krep = pr.sb(ctx, "k_repeated", [P, SLOTS, KQ], BF16)
        kvp = [pr.sb(ctx, f"kv_parts_head{u}", [P, TPB, 6 * E], BF16) for u in range(2)]
        v_loc = [pr.sb(ctx, f"v_banded{u}", [P, TPB, VR]) for u in range(2)]
        v_top = [pr.sb(ctx, f"v_selected{u}", [P, SLOTS, VR]) for u in range(2)]
        v_glob = [pr.sb(ctx, f"v_global{u}", [P, VR]) for u in range(2)]
        hot = [pr.sb(ctx, f"one_hot{u}", [P, TPB, TOP], BF16) for u in range(2)]
        slot8 = pr.sb(ctx, "slot8", [P, TPB])
        places = pr.sb(ctx, "places", [P, TOP])
        mask = pr.sb(ctx, "band_mask", [P, 3 * P], BF16)
        mx = pr.sb(ctx, "maxima", [P, V3, TPB])
        mrow = [pr.sb(ctx, f"max_rows{u}", [P, TPB, KM], BF16) for u in range(2)]
        p_loc = pr.sb(ctx, "p_local", [P, TPB, 3 * P])
        p_top = pr.sb(ctx, "p_top", [P, SLOTS, N])
        p_glob = pr.sb(ctx, "p_global", [P, CW])
        sums = [pr.sb(ctx, f"sums{u}", [VR, N]) for u in range(2)]
        zeroed = pr.sem(ctx, "zeroed")
        consts = pr.sem(ctx, "consts")
        stacks = [pr.sem(ctx, f"stacks{u}") for u in range(2)]
        first_part = pr.sem(ctx, "first_part")
        psteps = pr.sem(ctx, "pool_steps")
        hot_ready = pr.ev(ctx, "hot_ready", 1)
        glob_ready = pr.ev(ctx, "glob_ready")
        kvp_ready = pr.ev(ctx, "kv_parts_ready")
        v_copied = pr.ev(ctx, "values_copied")
        v_ready = pr.ev(ctx, "values_ready")
        scored = pr.ev(ctx, "scored_by_query", 2 * NG)
        reduced = pr.ev(ctx, "reduced", 2)
        rows_ready = pr.ev(ctx, "max_rows_ready")
        keyed = pr.ev(ctx, "scored_by_key", 2 * NL)
        exped = pr.ev(ctx, "exped", 2)
        summed = pr.ev(ctx, "values_summed", 2)
        taken = pr.ev(ctx, "sums_taken", 1)
        stored = [pr.sem(ctx, f"sums_stored{u}") for u in range(2)]

        with nc.Block() as block:
            @block.sync
            def _(sp):
                sp.dma_start(mask[:], d["mask_band"]).then_inc(consts, 16)
                sp.dma_start(places[:], d["places"]).then_inc(consts, 16)
                for u in range(2):
                    sp.sem_inc(stored[u], 16)
                sp.wait_ge(zeroed, 18)
                for u in range(2):
                    for v3, t in ((0, kst[u]), (1, ksel[u]), (2, kglob[u])):
                        sp.dma_start(t[MROW:KM, :], d["max_marks"][v3, :, 0:t.shape[1]]).then_inc(consts, 16)

                def load(n, u):
                    sp.wait_ge(keyed.sem, keyed.at((n - 2) * NL + NL - 1))
                    load_stacks(sp, n, qst[u], kst[u], pr.q_dram, pr.k_dram, stacks[u])

                def store(n, u):
                    sp.wait_ge(taken.sem, taken.at(n))
                    sp.dma_start(pr.sums_dram[ds(n)].rearrange("o r t -> (o r) t"), sums[u][:])\
                        .then_inc(stored[u], 16)

                for u in range(2):
                    load(u, u)
                with sp.Fori(0, HEADS // 2 - 1) as j:
                    for u in range(2):
                        load(j * 2 + u + 2, u)
                        store(j * 2 + u, u)
                for u in range(2):
                    store(HEADS - 2 + u, u)
                    sp.wait_ge(stored[u], 16 + 16 * HEADS // 2)

            @block.gpsimd
            def _(pool):
                for u in range(2):
                    for t in (qst[u], kst[u], ksel[u], kglob[u], mrow[u]):
                        pool.memset(t[:], 0.0).then_inc(zeroed, 1)
                    for t in (v_loc[u], v_top[u], v_glob[u]):
                        pool.memset(t[:], 0.0).then_inc(zeroed, 1)
                pool.wait_ge(zeroed, 16)
                for u in range(2):
                    pool.memset(v_top[u][:, :, 2 * VA - 1], 1.0).then_inc(zeroed, 1)
                pool.wait_ge(consts, 16 * 8)
                pool.sem_inc(hot_ready.sem, 1)

                def one_hots(n, u, j):
                    c = Chain(pool, psteps)
                    c.base = n * 1
                    hold(pool, pr.gate_p, scored.sem, scored.at((n - 2) * NG + G_SEL))
                    hold(pool, pr.gate_p, hot_ready.sem, hot_ready.at(n - 1))
                    pool.tensor_copy(kvp[u][:], one(pr.kvp, n)).then_inc(kvp_ready.sem, 1)
                    c.link(pool.tensor_copy(slot8[:], one(pr.slot, n)))
                    pool.sem_inc(pr.gate_p, 1)
                    for t in range(TPB):
                        ins = pool.tensor_scalar(hot[u][:, t], places[:], slot8[:, t:t + 1], None, ALU.is_equal)
                    ins.then_inc(hot_ready.sem, 1)
                    hold(pool, pr.gate_p, keyed.sem, keyed.at((n - 2) * NL + NL - 1))
                    hold(pool, pr.gate_p, stacks[u], j * 32 + 32)
                    pool.tensor_copy(kglob[u][0:KQ], kst[u][0:KQ, 0:GLOB]).then_inc(glob_ready.sem, 1)
                    hold(pool, pr.gate_p, summed.sem, summed.at(n - 2))
                    pool.tensor_copy(v_loc[u][:, :, 0:VA], one(pr.va, n))
                    pool.tensor_copy(v_glob[u][0:GLOB, 2 * VA:3 * VA], one(pr.va, n)[0:GLOB, 0])\
                        .then_inc(v_copied.sem, 1)
                    hold(pool, pr.gate_p, v_copied.sem, v_copied.at(n))
                    pool.tensor_copy(v_glob[u][GLOB:P, 3 * VA:VR], one(pr.va, n)[0:GLOB, 0])\
                        .then_inc(v_ready.sem, 1)
                    hold(pool, pr.gate_p, v_ready.sem, v_ready.at(n))

                with pool.Fori(0, HEADS // 2) as j:
                    for u in range(2):
                        one_hots(j * 2 + u, u, j)

            @block.vector
            def _(v):
                v.sem_inc(reduced.sem, 2)
                v.wait_ge(zeroed, 18)

                def take(n, u, g):
                    v.wait_ge(scored.sem, scored.at(n * NG + g))
                    return pr.ps[:, g % 2]

                def maxima(n, u):
                    ps = take(n, u, G_SEL)
                    sel = ps[:, 0:SLOTS * 48].rearrange("p (s a c) -> p s a c", s=SLOTS, a=3)
                    for s in range(SLOTS):
                        v.tensor_copy(krep[:, s].rearrange("p (a e i) -> p a e i", a=3, i=3),
                                      bc(sel[:, s, :, 0:E], 3))
                    v.tensor_reduce(v_top[u][:, :, VA:VA + E], sel[:, :, :, E:2 * E].rearrange("p s a e -> p s e a"),
                                    AX, ALU.add).then_inc(reduced.sem, 1)
                    for t in range(TPB):
                        if G_LOC[t] == G_TURN + 1:
                            ps = take(n, u, G_TURN)
                            v.tensor_copy(ksel[u][0:KQ], ps[0:KQ, 0:TOP // 2].bitcast(BF16)).then_inc(reduced.sem, 1)
                        ps = take(n, u, G_LOC[t])
                        lo, hi = (P if t == 0 else 0), (2 * P if t == TPB - 1 else 3 * P)
                        v.reduce_max(mx[:, 0, t:t + 1], ps[:, lo:hi], AX).then_inc(reduced.sem, 1)
                    for t in range(0, TPB, 2):
                        ps = take(n, u, G_TOP + t // 2)
                        v.reduce_max(mx[:, 1, t:t + 2], ps.rearrange("p (t k) -> p t k", t=2),
                                     AX).then_inc(reduced.sem, 1)
                    ps = take(n, u, G_GLOB)
                    v.reduce_max(mx[:, 2, :], ps.rearrange("p (t k) -> p t k", t=TPB), AX).then_inc(reduced.sem, 1)
                    v.wait_ge(reduced.sem, reduced.at(n * NG + G_GLOB))
                    first = mrow[u][:, :, MROW:MROW + V3].rearrange("p t v -> p v t")
                    second = mrow[u][:, :, MROW + V3:KM].rearrange("p t v -> p v t")
                    v.tensor_scalar(first, mx[:], -1.0, None, ALU.mult).then_inc(first_part, 1)
                    v.wait_ge(first_part, n + 1)
                    v.scalar_tensor_tensor(out=second, in0=mx[:], scalar=-1.0, in1=first, op0=ALU.mult,
                                           op1=ALU.subtract).then_inc(rows_ready.sem, 1)
                    ps = take(n, u, G_MAX)
                    v.tensor_copy(qst[u][MROW:KM], ps[MROW:KM].bitcast(BF16)).then_inc(reduced.sem, 1)

                with v.Fori(0, HEADS // 2) as j:
                    for u in range(2):
                        maxima(j * 2 + u, u)

            @block.scalar
            def _(act):
                nc.scalar.preload_act_table(ACT.Exp)
                act.sem_inc(exped.sem, 2)
                act.sem_inc(taken.sem, 1)

                def exps(n, u):
                    for g in range(NL):
                        i = u * NL + g
                        ps = pr.ps[:, 2 + 2 * (i % 2):4 + 2 * (i % 2)]
                        act.wait_ge(keyed.sem, keyed.at(n * NL + g))
                        if g == LG_GLOB:
                            ins = nc.scalar.activation(p_glob[:], ps[:, 0], ACT.Exp, scale=SCALE)
                        elif g < LG_LOC:
                            ins = nc.scalar.activation(p_top[:, g - LG_TOP].rearrange("p (a t) -> p a t", a=2), ps,
                                                       ACT.Exp, scale=SCALE)
                        else:
                            a, b = 2 * (g - LG_LOC), 2 * (g - LG_LOC) + 1
                            if a == 0:
                                nc.scalar.activation(p_loc[:, a, P:], ps[:, 0, P:3 * P], ACT.Exp, scale=SCALE)
                                ins = nc.scalar.activation(p_loc[:, b], ps[:, 1, 0:3 * P], ACT.Exp, scale=SCALE)
                            elif b == TPB - 1:
                                nc.scalar.activation(p_loc[:, a], ps[:, 0, 0:3 * P], ACT.Exp, scale=SCALE)
                                ins = nc.scalar.activation(p_loc[:, b, 0:2 * P], ps[:, 1, 0:2 * P], ACT.Exp,
                                                           scale=SCALE)
                            else:
                                ins = nc.scalar.activation(p_loc[:, a:b + 1], ps[:, :, 0:3 * P], ACT.Exp, scale=SCALE)
                        ins.then_inc(exped.sem, 1)

                def take(n, u, j):
                    act.wait_ge(stored[u], j * 16 + 16)
                    act.wait_ge(summed.sem, summed.at(n))
                    nc.scalar.activation(sums[u][:].rearrange("p (a t) -> p a t", a=2), pr.ps[0:VR, 6:8],
                                         ACT.Copy).then_inc(taken.sem, 1)

                exps(0, 0)
                with act.Fori(0, HEADS // 2 - 1) as j:
                    for u in range(2):
                        take(j * 2 + u, u, j)
                        exps(j * 2 + u + 1, 1 - u)
                take(HEADS - 2, 0, HEADS // 2 - 1)
                exps(HEADS - 1, 1)
                take(HEADS - 1, 1, HEADS // 2 - 1)

            @block.tensor
            def _(pe):
                pe.sem_inc(scored.sem, 2 * NG)
                pe.sem_inc(keyed.sem, 2 * NL)
                pe.sem_inc(summed.sem, 2)
                pe.wait_ge(consts, 16 * 8)
                pe.wait_ge(zeroed, 18)

                def banded(ps, k, q, t, lo, hi):
                    pe.matmul(ps[:, lo:hi], k[:, t * P:(t + 1) * P], q[:, (t - 1) * P + lo:(t - 1) * P + hi],
                              start=True, stop=False)
                    sides = slice(2 if lo else 0, 1 if hi == 2 * P else 3, 2)
                    cut = lambda x: x[:, 0:3 * P].rearrange("p (b c) -> p b c", b=3)[:, sides]
                    return pe.matmul(cut(ps), pr.idb[:], cut(mask[:]), start=False, stop=True)

                def query_group(n, u, g):
                    pe.wait_ge(reduced.sem, reduced.at(n * NG + g - 2))
                    ps = pr.ps[:, g % 2]
                    if g == G_SEL:
                        pe.wait_ge(kvp_ready.sem, kvp_ready.at(n))
                        pe.wait_ge(hot_ready.sem, hot_ready.at(n))
                        for s in range(SLOTS):
                            for t in range(TPB):
                                mm = pe.matmul(ps[:, s * 48:(s + 1) * 48], hot[u][:, t, s * P:(s + 1) * P],
                                               kvp[u][:, t], start=t == 0, stop=t == TPB - 1)
                    elif g == G_TURN:
                        pe.wait_ge(reduced.sem, reduced.at(n * NG + G_SEL))
                        for s in range(SLOTS):
                            mm = pe.transpose(ps[0:KQ, s * 64:(s + 1) * 64].bitcast(BF16), krep[:, s], pr.idb[:])
                    elif g < G_TOP:
                        t = G_LOC.index(g)
                        if t == 0:
                            pe.wait_ge(stacks[u], 32 * (n_half(n, u) + 1))
                        lo, hi = (P if t == 0 else 0), (2 * P if t == TPB - 1 else 3 * P)
                        mm = banded(ps, qst[u][0:KQ], kst[u][0:KQ], t, lo, hi)
                    elif g < G_GLOB:
                        if g == G_TOP:
                            pe.wait_ge(reduced.sem, reduced.at(n * NG + G_TURN))
                        for i in range(2):
                            t = 2 * (g - G_TOP) + i
                            mm = pe.matmul(ps[:, i * TOP:(i + 1) * TOP], qst[u][0:KQ, t * P:(t + 1) * P],
                                           ksel[u][0:KQ, :], start=True, stop=True)
                    elif g == G_GLOB:
                        for t in range(TPB):
                            mm = pe.matmul(ps[:, t * GLOB:(t + 1) * GLOB], qst[u][0:KQ, t * P:(t + 1) * P],
                                           kst[u][0:KQ, 0:GLOB], start=True, stop=True)
                    else:
                        pe.wait_ge(rows_ready.sem, rows_ready.at(n))
                        for t in range(TPB):
                            mm = pe.transpose(ps[0:KM, t * 64:(t + 1) * 64].bitcast(BF16), mrow[u][:, t], pr.idb[:])
                    mm.then_inc(scored.sem, 1)

                def n_half(n, u):
                    return n // 2 if isinstance(n, int) else pr.half

                def key_group(n, u, g):
                    pe.wait_ge(exped.sem, exped.at(n * NL + g - 2))
                    if g == 0:
                        pe.wait_ge(reduced.sem, reduced.at(n * NG + G_MAX))
                    i = u * NL + g
                    ps = pr.ps[:, 2 + 2 * (i % 2):4 + 2 * (i % 2)]
                    if g == LG_GLOB:
                        pe.wait_ge(glob_ready.sem, glob_ready.at(n))
                        for i in range(2):
                            mm = pe.matmul(ps[i * GLOB:(i + 1) * GLOB, 0], kglob[u][0:KM, :], qst[u][0:KM, i * CW:(i + 1) * CW],
                                           start=True, stop=True)
                    elif g < LG_LOC:
                        for i in range(2):
                            mm = pe.matmul(ps[:, i], ksel[u][0:KM, (g - LG_TOP) * P:(g - LG_TOP + 1) * P],
                                           qst[u][0:KM, i * CW:(i + 1) * CW], start=True, stop=True)
                    else:
                        for i in range(2):
                            t = 2 * (g - LG_LOC) + i
                            lo, hi = (P if t == 0 else 0), (2 * P if t == TPB - 1 else 3 * P)
                            mm = banded(ps[:, i], kst[u][0:KM], qst[u][0:KM], t, lo, hi)
                    mm.then_inc(keyed.sem, 1)

                def values(n, u, g):
                    pe.wait_ge(exped.sem, exped.at(n * NL + g))
                    if g == LG_GLOB:
                        pe.wait_ge(v_ready.sem, v_ready.at(n))
                        hold(pe, pr.gate_e, taken.sem, taken.at(n - 1))
                        pe.matmul(pr.ps[0:VR, 6], v_glob[u][:], p_glob[:], start=True, stop=False)
                    elif g < LG_LOC:
                        for i in range(2):
                            pe.matmul(pr.ps[0:VR, 6 + i], v_top[u][:, g - LG_TOP],
                                      p_top[:, g - LG_TOP, i * CW:(i + 1) * CW],
                                      start=i == 1 and g == LG_TOP, stop=False)
                    else:
                        for t in (2 * (g - LG_LOC), 2 * (g - LG_LOC) + 1):
                            for i in range(2):
                                lo, hi = max(t - 1, i * CH), min(t + 2, (i + 1) * CH)
                                if lo < hi:
                                    mm = pe.matmul(pr.ps[0:VR, 6 + i, (lo - i * CH) * P:(hi - i * CH) * P],
                                                   v_loc[u][:, t], p_loc[:, t, (lo - t + 1) * P:(hi - t + 1) * P],
                                                   start=False, stop=t == (CH if i == 0 else TPB - 1))
                        if g == NL - 1:
                            mm.then_inc(summed.sem, 1)

                def step(n, u):
                    done = dict(k=0, q=0, v=0)
                    for part in "kqkqvqkqvqqkqvqkqvqkqqvqkqqvqv":
                        g = done[part]
                        done[part] += 1
                        if part == "k":
                            key_group(n, u, g)
                        elif part == "v":
                            values(n, u, g)
                        elif n_next(n):
                            query_group(n + 1, 1 - u, g)
                    assert done == dict(k=NL, q=NG, v=NL)

                def n_next(n):
                    return not isinstance(n, int) or n + 1 < HEADS

                for g in range(NG):
                    query_group(0, 0, g)
                with pe.Fori(0, HEADS // 2 - 1) as j:
                    for u in range(2):
                        pr.half = j + u
                        step(j * 2 + u, u)
                step(HEADS - 2, 0)
                step(HEADS - 1, 1)


def out_project(pr, w_name, bias_name):
    nc, d = pr.nc, pr.d
    V3, VA = 3, E + 1
    with ExitStack() as ctx:
        wo = pr.sb(ctx, "wo", [P, D])
        bo = pr.sb(ctx, "bo", [1, D])
        ones = pr.sb(ctx, "ones", [1, P])
        num = pr.sb(ctx, "value_sums", [P, 2, V3, CW])
        inv = pr.sb(ctx, "inverses", [H, 2, V3, CW])
        spread = pr.sb(ctx, "spread_heads", [H, P])
        den = pr.sb(ctx, "denominators", [P, V3, CW])
        ot = pr.sb(ctx, "o_turned", [P, 2, CW])
        loaded = pr.sem(ctx, "loaded")
        read = [pr.sem(ctx, f"sums_read{u}") for u in range(2)]
        den_read = pr.sem(ctx, "denominators_read")
        inverted = pr.sem(ctx, "inverted")
        inv_stored = pr.sem(ctx, "inverses_stored")
        steps = pr.sem(ctx, "steps")
        set_up = pr.sem(ctx, "set_up")
        spread_out = pr.ev(ctx, "inverses_spread")
        divided = pr.ev(ctx, "divided", 1)
        meant = pr.ev(ctx, "mean_ready")
        taken = pr.ev(ctx, "mean_taken", 2)
        summed = pr.ev(ctx, "summed", 2)
        added = pr.ev(ctx, "added", 2)

        def chunks(eng, body):
            with eng.Fori(0, NC // 2) as j:
                for u in range(2):
                    body(j * 2 + u, u, j)

        def sums_of(heads, w, half):
            if w == V3 - 1:
                return heads[:, (w + half) * VA:(w + half + 1) * VA, 0:CW]
            return heads[:, w * VA:(w + 1) * VA, half * CW:(half + 1) * CW]

        with nc.Block() as block:
            @block.sync
            def _(sp):
                for w in range(V3):
                    for half in range(2):
                        sp.dma_start(den[half * HEADS:(half + 1) * HEADS, w],
                                     sums_of(pr.sums_dram, w, half)[:, E]).then_inc(den_read, 16)
                sp.dma_start(wo[:], d[w_name]).then_inc(loaded, 16)
                sp.dma_start(bo[:], d[bias_name]).then_inc(loaded, 16)
                sp.dma_start(spread[:], d["spread"]).then_inc(loaded, 16)
                sp.wait_ge(inverted, 1)
                for half in range(2):
                    sp.dma_start(pr.inverse_dram[:, :, half * CW:(half + 1) * CW], den[half * HEADS:(half + 1) * HEADS])\
                        .then_inc(inv_stored, 16)
                sp.wait_ge(inv_stored, 32)

                def part(k, u, j):
                    sp.wait_ge(taken.sem, taken.at(k - 2))
                    heads = pr.sums_dram[ds(j * H, H)]
                    sp.dma_start(inv[:, u], pr.inverse_dram[ds(j * H, H), :, u * CW:(u + 1) * CW]).then_inc(read[u], 16)
                    for w in range(V3):
                        sp.dma_start(num[:, u, w], sums_of(heads, w, u)[:, 0:E]).then_inc(read[u], 16)

                chunks(sp, part)

            @block.vector
            def _(v):
                v.memset(ones[:], 1.0).then_inc(set_up, 1)
                v.sem_inc(added.sem, 2)
                v.sem_inc(divided.sem, 1)
                v.wait_ge(den_read, 96)
                v.reciprocal(den[:], den[:]).then_inc(inverted, 1)

                def mean(k, u, j):
                    c = Chain(v, steps)
                    c.base = k * 2
                    v.wait_ge(spread_out.sem, spread_out.at(k))
                    c.link(v.tensor_tensor(num[:, u], num[:, u], pr.ps[:, 4:4 + V3], ALU.mult))
                    v.sem_inc(divided.sem, 1)
                    c.link(v.tensor_tensor(num[:, u, 0], num[:, u, 0], num[:, u, 1], ALU.add))
                    v.tensor_tensor(num[:, u, 0], num[:, u, 0], num[:, u, 2], ALU.add).then_inc(meant.sem, 1)

                def add(k, u, j):
                    v.wait_ge(summed.sem, summed.at(k))
                    v.tensor_tensor(pr.X[:, ds(k * CH, CH), :], pr.X[:, ds(k * CH, CH), :],
                                    pr.ps[:, 2 + u].rearrange("p (t d) -> p t d", d=D), ALU.add).then_inc(added.sem, 1)

                staggered(v, mean, add)

            @block.scalar
            def _(act):
                act.sem_inc(taken.sem, 2)

                def part(k, u, j):
                    act.wait_ge(summed.sem, summed.at(k - 2))
                    act.wait_ge(meant.sem, meant.at(k))
                    nc.scalar.activation(ot[:, u], num[:, u, 0], ACT.Copy, scale=1.0 / V3).then_inc(taken.sem, 1)

                chunks(act, part)

            @block.tensor
            def _(pe):
                pe.sem_inc(summed.sem, 2)
                pe.wait_ge(loaded, 48)
                pe.wait_ge(set_up, 1)

                def spread_inverses(k, u, j):
                    pe.wait_ge(divided.sem, divided.at(k - 1))
                    hold(pe, pr.gate_e, read[u], j * 64 + 64)
                    for w in range(V3):
                        mm = pe.matmul(pr.ps[:, 4 + w], spread[:], inv[:, u, w], start=True, stop=True)
                    mm.then_inc(spread_out.sem, 1)

                def products(k, u, j):
                    pe.wait_ge(added.sem, added.at(k - 2))
                    pe.wait_ge(taken.sem, taken.at(k))
                    for t in range(CH):
                        s = pr.ps[:, 2 + u, t * D:(t + 1) * D]
                        pe.matmul(s, ot[:, u, t * P:(t + 1) * P], wo[:], start=True, stop=False)
                        mm = pe.matmul(s, ones[:], bo[:], start=False, stop=True)
                    mm.then_inc(summed.sem, 1)

                staggered(pe, spread_inverses, products)


def experts(pr, name, ne, width, glu, nb=None, select=0):
    nc, d = pr.nc, pr.d
    UE = P // width
    NU = ne // UE
    nb = nb or ne
    with ExitStack() as ctx:
        w1 = pr.sb(ctx, "w1", [P, NU, (2 if glu else 1) * P])
        b1 = pr.sb(ctx, "b1", [P, NU, 2 if glu else 1])
        w2 = pr.sb(ctx, "w2", [P, NU, D])
        b2 = pr.sb(ctx, "b2", [nb, D])
        mult = pr.sb(ctx, "mult", [P, NU]) if glu else None
        gc = pr.sb(ctx, "gates_chunk", [P, 2, CH, nb])
        gt = pr.sb(ctx, "gates_turned", [nb, 2, CW])
        hid = pr.sb(ctx, "hidden", [P, 2, CW])
        gel = pr.sb(ctx, "gelu", [P, 2, CW]) if glu else None
        acc = pr.sb(ctx, "sums", [P, 2, CH, D])
        loaded = pr.sem(ctx, "weights_loaded")
        scaled = pr.sem(ctx, "w2_scaled")
        gates_ready = pr.ev(ctx, "gates_ready")
        gates_turned = pr.ev(ctx, "gates_turned")
        gates_kept = pr.ev(ctx, "gates_kept", 1)
        bias_sum = pr.ev(ctx, "bias_sum")
        acc_ready = pr.ev(ctx, "acc_ready", 1)
        h_sum = pr.ev(ctx, "h_sum")
        gelu_done = pr.ev(ctx, "gelu_done", 2)
        hidden_ready = pr.ev(ctx, "hidden_ready", 2) if glu else gelu_done
        y_sum = pr.ev(ctx, "y_sum", 2 * ne)
        y_added = pr.ev(ctx, "y_added", 2 * ne)
        x_added = pr.ev(ctx, "x_added", 2)
        scores_loaded = pr.sem(ctx, "scores_loaded")
        selects = pr.sem(ctx, "selection_steps")
        assert not select or select // 8 * 2 == NC * ne

        def chunks(eng, body):
            with eng.Fori(0, NC // 2) as j:
                for u in range(2):
                    body(j * 2 + u, u)

        def ahead(eng, prepare, body):
            for step in prepare:
                step(0, 0)
            with eng.Fori(0, NC // 2 - 1) as j:
                for u in range(2):
                    body(j * 2 + u, u, prepare)
            body(NC - 2, 0, prepare)
            body(NC - 1, 1, ())

        def h_ps(i):
            return pr.ps[:, i % 2]

        def g_ps(i):
            return pr.ps[:, 2 + i % 2]

        with nc.Block() as block:
            @block.sync
            def _(sp):
                if select:
                    sp.dma_start(pr.s0[:], pr.s_dram).then_inc(scores_loaded, 16)
                sp.dma_start(w1[:], d[name + "_w1"]).then_inc(loaded, 16)
                sp.dma_start(b1[:], d[name + "_b1"]).then_inc(loaded, 16)
                sp.dma_start(w2[:], d[name + "_w2"]).then_inc(loaded, 16)
                sp.dma_start(b2[:], d[name + "_b2"]).then_inc(loaded, 16)
                if glu:
                    sp.dma_start(mult[:], d[name + "_mult"]).then_inc(loaded, 16)

            @block.gpsimd
            def _(pool):
                pool.sem_inc(x_added.sem, 2)

                def add(k, u):
                    hold(pool, pr.gate_p, y_added.sem, y_added.at(k * ne + ne - 1))
                    pool.tensor_tensor(pr.X[:, ds(k * CH, CH), :], pr.X[:, ds(k * CH, CH), :], acc[:, u],
                                       ALU.add).then_inc(x_added.sem, 1)

                chunks(pool, add)

            @block.vector
            def _(v):
                v.wait_ge(loaded, 16 * (5 if glu else 4))
                if glu:
                    v.tensor_tensor(w2[:], w2[:], bc(mult[:], D), ALU.mult).then_inc(scaled, 1)
                    v.sem_inc(hidden_ready.sem, 2)
                v.sem_inc(y_added.sem, 2 * ne)
                if select:
                    v.wait_ge(scores_loaded, 16)
                    v.tensor_copy(pr.s1[:], pr.s0[:]).then_inc(selects, 1)

                def select_step(k, e):
                    hold(v, pr.gate_v, selects, k * ne + e + 1)
                    if e % 2 == 0:
                        ins = v.max(pr.best[:], pr.s1[:])
                    else:
                        ins = v.match_replace(pr.s1[:], pr.best[:], pr.s1[:], LOW)
                    ins.then_inc(selects, 1)

                def gate_hidden(k, u, i):
                    v.wait_ge(y_sum.sem, y_sum.at(k * ne + i - 2))
                    v.wait_ge(gelu_done.sem, gelu_done.at(k * NU + i))
                    n = u * NU + i
                    v.scalar_tensor_tensor(out=hid[:, n % 2], in0=h_ps(n), scalar=b1[:, i, 0:1],
                                           in1=gel[:, n % 2], op0=ALU.add, op1=ALU.mult)\
                        .then_inc(hidden_ready.sem, 1)

                def part(k, u):
                    if glu:
                        gate_hidden(k, u, 0)
                    v.wait_ge(acc_ready.sem, acc_ready.at(k))
                    for e in range(ne):
                        if glu and e + 1 < ne:
                            gate_hidden(k, u, e + 1)
                        n = u * ne + e
                        v.wait_ge(y_added.sem, y_added.at(k * ne + e - 1))
                        v.wait_ge(y_sum.sem, y_sum.at(k * ne + e))
                        for t in range(CH):
                            ins = v.scalar_tensor_tensor(out=acc[:, u, t], in0=pr.ps[:, 4 + n % 2, t * D:(t + 1) * D],
                                                         scalar=gc[:, u, t, e:e + 1], in1=acc[:, u, t],
                                                         op0=ALU.mult, op1=ALU.add)
                        ins.then_inc(y_added.sem, 1)
                        if select:
                            select_step(k, e)

                chunks(v, part)

            @block.scalar
            def _(act):
                nc.scalar.preload_act_table(ACT.Gelu)
                act.sem_inc(gates_kept.sem, 1)
                act.sem_inc(acc_ready.sem, 1)
                act.sem_inc(gelu_done.sem, 2)
                act.wait_ge(loaded, 16 * (5 if glu else 4))

                def keep_gates(k, u):
                    hold(act, pr.gate_a, y_added.sem, y_added.at((k - 2) * ne + ne - 1))
                    nc.scalar.activation(gc[:, u], pr.gates[:, ds(k * CH, CH), 0:nb], ACT.Copy)\
                        .then_inc(gates_ready.sem, 1)

                def keep_turned(k, u):
                    act.wait_ge(gates_turned.sem, gates_turned.at(k))
                    nc.scalar.activation(gt[:, u], pr.ps[0:nb, 6], ACT.Copy).then_inc(gates_kept.sem, 1)

                def start_sums(k, u):
                    act.wait_ge(bias_sum.sem, bias_sum.at(k))
                    act.wait_ge(x_added.sem, x_added.at(k - 2))
                    nc.scalar.activation(acc[:, u], pr.ps[:, 7].rearrange("p (t d) -> p t d", d=D), ACT.Copy)\
                        .then_inc(acc_ready.sem, 1)

                def part(k, u, steps):
                    for i in range(NU):
                        n = u * NU + i
                        act.wait_ge(y_sum.sem, y_sum.at(k * ne + (i - 2) * UE + UE - 1))
                        act.wait_ge(h_sum.sem, h_sum.at(k * NU + i))
                        if glu:
                            act.wait_ge(hidden_ready.sem, hidden_ready.at(k * NU + i - 2))
                        nc.scalar.activation(gel[:, n % 2] if glu else hid[:, n % 2], g_ps(n) if glu else h_ps(n),
                                             ACT.Gelu, bias=b1[:, i, 1:2] if glu else b1[:, i, 0:1])\
                            .then_inc(gelu_done.sem, 1)
                        if i < len(steps):
                            steps[i](k + 1, 1 - u)

                ahead(act, (keep_gates, keep_turned, start_sums), part)

            @block.tensor
            def _(pe):
                pe.sem_inc(y_sum.sem, 2 * ne)
                pe.wait_ge(loaded, 16 * (5 if glu else 4))
                if glu:
                    pe.wait_ge(scaled, 1)

                def first(k, u, i):
                    n = u * NU + i
                    pe.wait_ge(gelu_done.sem, gelu_done.at(k * NU + i - 2))
                    if glu:
                        pe.wait_ge(hidden_ready.sem, hidden_ready.at(k * NU + i - 2))
                    x = pr.xt[:, ds(k * CW, CW)]
                    mm = pe.matmul(h_ps(n), w1[:, i, 0:P], x, start=True, stop=True)
                    if glu:
                        mm = pe.matmul(g_ps(n), w1[:, i, P:2 * P], x, start=True, stop=True)
                    mm.then_inc(h_sum.sem, 1)

                def second(k, u, i):
                    pe.wait_ge(hidden_ready.sem, hidden_ready.at(k * NU + i))
                    for s in range(UE):
                        n = u * ne + i * UE + s
                        r = slice(s * width, (s + 1) * width)
                        pe.wait_ge(y_added.sem, y_added.at(k * ne + i * UE + s - 2))
                        for t in range(CH):
                            mm = pe.matmul(pr.ps[:, 4 + n % 2, t * D:(t + 1) * D],
                                           hid[r, (u * NU + i) % 2, t * P:(t + 1) * P], w2[r, i], start=True, stop=True)
                        mm.then_inc(y_sum.sem, 1)

                def turn_gates(k, u):
                    pe.wait_ge(gates_ready.sem, gates_ready.at(k))
                    pe.wait_ge(gates_kept.sem, gates_kept.at(k - 1))
                    for t in range(CH):
                        mm = pe.transpose(pr.ps[0:nb, 6, t * P:(t + 1) * P], gc[:, u, t], pr.idf[:])
                    mm.then_inc(gates_turned.sem, 1)

                def sum_biases(k, u):
                    pe.wait_ge(gates_kept.sem, gates_kept.at(k))
                    pe.wait_ge(acc_ready.sem, acc_ready.at(k - 1))
                    for t in range(CH):
                        mm = pe.matmul(pr.ps[:, 7, t * D:(t + 1) * D], gt[:, u, t * P:(t + 1) * P], b2[:],
                                       start=True, stop=True)
                    mm.then_inc(bias_sum.sem, 1)

                def part(k, u, steps):
                    for i in range(NU):
                        second(k, u, i)
                        if i + 2 < NU:
                            first(k, u, i + 2)
                        elif steps:
                            first(k + 1, 1 - u, i + 2 - NU)
                        if i < len(steps):
                            steps[i](k + 1, 1 - u)

                first(0, 0, 0)
                first(0, 0, 1)
                ahead(pe, (turn_gates, sum_biases), part)


def store_output(pr):
    nc = pr.nc
    with ExitStack() as ctx:
        stored = pr.sem(ctx, "stored")
        with nc.Block() as block:
            @block.sync
            def _(sp):
                sp.dma_start(pr.out.rearrange("p (t d) -> p t d", d=D), pr.X[:]).then_inc(stored, 16)
                sp.wait_ge(stored, 16)


def two_a_turn(eng, body):
    with eng.Fori(0, NC // 2) as j:
        for u in range(2):
            body(j * 2 + u, u, j)


def l1_attention(pr):
    nc, d = pr.nc, pr.d
    SCALE = float(D) ** -0.5
    with ExitStack() as ctx:
        wq, wk, wo = (pr.sb(ctx, n, [P, D]) for n in ("wq", "wk", "wo"))
        wroute = pr.sb(ctx, "wroute", [P, 8])
        mask = pr.sb(ctx, "causal_mask", [P, P], BF16)
        xnc = pr.sb(ctx, "xnc", [P, 2, CH, D])
        chunk = pr.sb(ctx, "chunk", [P, 2, CW])
        qt = pr.sb(ctx, "q_turned", [P, 2, CW])
        kt = pr.sb(ctx, "k_turned", [P, 2, P + CW])
        kn = pr.sb(ctx, "k_by_token", [P, 2, 1 + CH, D])
        mx = pr.sb(ctx, "mx", [P, 2, CH])
        nmx = pr.sb(ctx, "minus_mx", [P, 2, CH])
        sums = pr.sb(ctx, "sums", [P, 2, CH])
        rec = pr.sb(ctx, "rec", [P, 2, CH])
        prob = pr.sb(ctx, "prob", [P, 2, CH, 2 * P])
        pt = pr.sb(ctx, "prob_turned", [P, 2, CH, 2, P])
        ot = pr.sb(ctx, "out_turned", [P, 2, CW])
        loaded = pr.sem(ctx, "weights_loaded")
        zeroed = pr.sem(ctx, "zeroed")
        xn_sub = pr.ev(ctx, "xn_sub")
        xn_ready = pr.ev(ctx, "xn_ready")
        turned = pr.ev(ctx, "xn_turned", 2)
        chunk_ready = pr.ev(ctx, "chunk_ready", 1)
        chunk_kept = pr.ev(ctx, "chunk_kept", 2)
        q_sum, k_sum, kn_sum, r_sum = (pr.ev(ctx, n, 2) for n in ("q_sum", "k_sum", "kn_sum", "r_sum"))
        q_taken, k_taken, kn_taken, r_taken = (pr.ev(ctx, n, 1) for n in ("q_tak", "k_tak", "kn_tak", "r_tak"))
        k_passed = pr.ev(ctx, "k_passed", 1)
        scored = pr.ev(ctx, "scored", 2)
        maxed = pr.ev(ctx, "maxed")
        minus_ready = pr.ev(ctx, "minus_ready")
        exped = pr.ev(ctx, "exped", 2)
        p_turned = pr.ev(ctx, "p_turned", 4)
        p_taken = pr.ev(ctx, "p_taken", 2)
        o_sum = pr.ev(ctx, "o_sum", 2)
        o_taken = pr.ev(ctx, "o_taken", 2)
        y_sum = pr.ev(ctx, "y_sum", 2)
        y_added = pr.ev(ctx, "y_added", 2)
        rec_ready = pr.ev(ctx, "rec_ready")
        turn_ps, q_ps, k_ps, o_ps = (pr.ps[:, i] for i in range(4))
        y_ps = k_ps
        s_ps = pr.ps[:, 4:6]
        pt_ps = pr.ps[:, 6:8]

        with nc.Block() as block:
            @block.sync
            def _(sp):
                for dst, src in ((wq, "l1_wq"), (wk, "l1_wk"), (wo, "l1_wo"), (wroute, "l1_wg"), (mask, "mask_causal")):
                    sp.dma_start(dst[:], d[src]).then_inc(loaded, 16)

            @block.gpsimd
            def _(pool):
                pool.memset(kt[:, 0, 0:P], 0.0).then_inc(zeroed, 1)
                pool.memset(kn[:, 0, 0], 0.0).then_inc(zeroed, 1)
                pool.sem_inc(chunk_kept.sem, 2)
                pool.sem_inc(k_passed.sem, 1)

                def part(k, u, j):
                    hold(pool, pr.gate_p, chunk_ready.sem, chunk_ready.at(k))
                    pool.tensor_copy(pr.xt[:, ds(k * CW, CW)], chunk[:, u]).then_inc(chunk_kept.sem, 1)
                    if u == 1:
                        hold(pool, pr.gate_p, o_sum.sem, o_sum.at(k - 2))
                        hold(pool, pr.gate_p, k_taken.sem, k_taken.at(k - 1))
                        pool.tensor_copy(kt[:, 1, 0:P], kt[:, 0, CW:]).then_inc(k_passed.sem, 1)
                        hold(pool, pr.gate_p, kn_taken.sem, kn_taken.at(k - 1))
                        pool.tensor_copy(kn[:, 1, 0], kn[:, 0, CH]).then_inc(k_passed.sem, 1)

                two_a_turn(pool, part)

            @block.vector
            def _(v):
                v.sem_inc(kn_taken.sem, 1)
                v.sem_inc(y_added.sem, 2)
                v.sem_inc(p_taken.sem, 2)

                def norm(k, u, j):
                    v.wait_ge(turned.sem, turned.at(k - 2))
                    v.tensor_tensor(xnc[:, u], pr.X[:, ds(k * CH, CH), :], bc(pr.mean[:, ds(k * CH, CH)], D),
                                    ALU.subtract).then_inc(xn_sub.sem, 1)
                    v.wait_ge(xn_sub.sem, xn_sub.at(k))
                    v.tensor_tensor(xnc[:, u], xnc[:, u], bc(pr.rstd[:, ds(k * CH, CH)], D),
                                    ALU.mult).then_inc(xn_ready.sem, 1)

                def keep_keys(k, u, j):
                    v.wait_ge(o_sum.sem, o_sum.at(k - 2))
                    if u == 0:
                        v.wait_ge(k_passed.sem, j * 2 + 1)
                    v.wait_ge(kn_sum.sem, kn_sum.at(k))
                    v.tensor_copy(kn[:, u, 1:], o_ps.rearrange("p (t d) -> p t d", d=D)).then_inc(kn_taken.sem, 1)

                def highest(k, u, j):
                    for half in range(2):
                        i = k * 2 + half
                        v.wait_ge(scored.sem, scored.at(i))
                        ins = v.reduce_max(mx[:, u, 2 * half:2 * half + 2],
                                           s_ps[:, half].rearrange("p (t k) -> p t k", t=2), AX)
                        ins.then_inc(maxed.sem, 1)
                    v.wait_ge(maxed.sem, maxed.at(k * 2 + 1))
                    v.tensor_scalar(nmx[:, u], mx[:, u], -SCALE, None, ALU.mult).then_inc(minus_ready.sem, 1)

                def finish(k, u, j):
                    for half in range(2):
                        v.wait_ge(p_turned.sem, p_turned.at(k * 2 + half))
                        v.tensor_copy(pt[:, u, 2 * half:2 * half + 2].rearrange("p t a q -> p (t a q)"),
                                      pt_ps[:, half]).then_inc(p_taken.sem, 1)
                    v.wait_ge(exped.sem, exped.at(k))
                    v.reciprocal(rec[:, u], sums[:, u]).then_inc(rec_ready.sem, 1)
                    v.wait_ge(rec_ready.sem, rec_ready.at(k))
                    v.wait_ge(y_sum.sem, y_sum.at(k))
                    for t in range(CH):
                        x = one(pr.X, k * CH + t)
                        ins = v.scalar_tensor_tensor(out=x, in0=y_ps[:, t * D:(t + 1) * D],
                                                     scalar=rec[:, u, t:t + 1], in1=x, op0=ALU.mult, op1=ALU.add)
                    ins.then_inc(y_added.sem, 1)

                lagged(v, (0, norm), (1, highest), (2, finish), (0, keep_keys))

            @block.scalar
            def _(act):
                nc.scalar.preload_act_table(ACT.Exp)
                for e in (chunk_ready, q_taken, k_taken, r_taken):
                    act.sem_inc(e.sem, 1)
                act.sem_inc(o_taken.sem, 2)
                act.sem_inc(exped.sem, 2)
                act.wait_ge(zeroed, 2)

                def project(k, u, j):
                    act.wait_ge(r_sum.sem, r_sum.at(k - 2))
                    act.wait_ge(chunk_kept.sem, chunk_kept.at(k - 2))
                    act.wait_ge(turned.sem, turned.at(k))
                    nc.scalar.activation(chunk[:, u], turn_ps, ACT.Copy).then_inc(chunk_ready.sem, 1)
                    act.wait_ge(scored.sem, scored.at(k * 2 - 3))
                    act.wait_ge(q_sum.sem, q_sum.at(k))
                    nc.scalar.activation(qt[:, u], q_ps, ACT.Copy).then_inc(q_taken.sem, 1)
                    if u == 0:
                        act.wait_ge(k_passed.sem, j * 2 + 1)
                    act.wait_ge(k_sum.sem, k_sum.at(k))
                    nc.scalar.activation(kt[:, u, P:], k_ps, ACT.Copy).then_inc(k_taken.sem, 1)
                    hold(act, pr.gate_a, r_sum.sem, r_sum.at(k))
                    nc.scalar.activation(pr.logits[:, ds(k * CH, CH), 0:8],
                                         q_ps[:, 0:CH * 8].rearrange("p (t c) -> p t c", c=8),
                                         ACT.Copy).then_inc(r_taken.sem, 1)

                def exps(k, u, j):
                    act.wait_ge(p_turned.sem, p_turned.at(k * 2 - 3))
                    act.wait_ge(minus_ready.sem, minus_ready.at(k))
                    for t in range(CH):
                        ins = nc.scalar.activation(prob[:, u, t], s_ps[:, t // 2, (t % 2) * 2 * P:(t % 2 + 1) * 2 * P],
                                                   ACT.Exp, bias=nmx[:, u, t:t + 1], scale=SCALE,
                                                   accum_out=sums[:, u, t:t + 1])
                    ins.then_inc(exped.sem, 1)

                def keep_outputs(k, u, j):
                    act.wait_ge(y_sum.sem, y_sum.at(k - 2))
                    act.wait_ge(o_sum.sem, o_sum.at(k))
                    nc.scalar.activation(ot[:, u], o_ps, ACT.Copy).then_inc(o_taken.sem, 1)

                lagged(act, (1, exps), (2, keep_outputs), (0, project))

            @block.tensor
            def _(pe):
                for e in (turned, q_sum, k_sum, kn_sum, r_sum, scored, o_sum, y_sum):
                    pe.sem_inc(e.sem, 2)
                pe.sem_inc(p_turned.sem, 4)
                pe.wait_ge(loaded, 5 * 16)
                pe.wait_ge(zeroed, 2)

                def turn(k, u, j):
                    pe.wait_ge(xn_ready.sem, xn_ready.at(k))
                    pe.wait_ge(chunk_ready.sem, chunk_ready.at(k - 1))
                    for t in range(CH):
                        mm = pe.transpose(turn_ps[:, t * P:(t + 1) * P], xnc[:, u, t], pr.idf[:])
                    mm.then_inc(turned.sem, 1)

                def project(k, u, j):
                    pe.wait_ge(chunk_ready.sem, chunk_ready.at(k))
                    pe.wait_ge(r_taken.sem, r_taken.at(k - 1))
                    pe.matmul(q_ps, wq[:], chunk[:, u], start=True, stop=True).then_inc(q_sum.sem, 1)
                    pe.wait_ge(y_added.sem, y_added.at(k - 2))
                    pe.matmul(k_ps, wk[:], chunk[:, u], start=True, stop=True).then_inc(k_sum.sem, 1)
                    pe.wait_ge(o_taken.sem, o_taken.at(k - 2))
                    for t in range(CH):
                        mm = pe.matmul(o_ps[:, t * D:(t + 1) * D], chunk[:, u, t * P:(t + 1) * P], wk[:],
                                       start=True, stop=True)
                    mm.then_inc(kn_sum.sem, 1)
                    pe.wait_ge(q_taken.sem, q_taken.at(k))
                    for t in range(CH):
                        mm = pe.matmul(q_ps[:, t * 8:(t + 1) * 8], chunk[:, u, t * P:(t + 1) * P], wroute[:],
                                       start=True, stop=True)
                    mm.then_inc(r_sum.sem, 1)

                def scores(k, u, j):
                    pe.wait_ge(k_taken.sem, k_taken.at(k))
                    pe.wait_ge(exped.sem, exped.at(k - 1))
                    if u == 1:
                        pe.wait_ge(k_passed.sem, j * 2 + 2)
                    for t in range(CH):
                        s = s_ps[:, t // 2, (t % 2) * 2 * P:(t % 2 + 1) * 2 * P]
                        pe.matmul(s, qt[:, u, t * P:(t + 1) * P], kt[:, u, t * P:(t + 2) * P], start=True, stop=False)
                        mm = pe.matmul(s[:, P:], pr.idb[:], mask[:], start=False, stop=True)
                        if t % 2:
                            mm.then_inc(scored.sem, 1)

                def sum_values(k, u, j):
                    pe.wait_ge(exped.sem, exped.at(k))
                    for t in range(CH):
                        if t % 2 == 0:
                            pe.wait_ge(p_taken.sem, p_taken.at(k * 2 + t // 2 - 2))
                        for a in range(2):
                            mm = pe.transpose(pt_ps[:, t // 2, ((t % 2) * 2 + a) * P:((t % 2) * 2 + a + 1) * P],
                                              prob[:, u, t, a * P:(a + 1) * P], pr.idf[:])
                        if t % 2:
                            mm.then_inc(p_turned.sem, 1)
                    pe.wait_ge(kn_taken.sem, kn_taken.at(min(k + 1, NC - 1) if isinstance(k, int) else k + 1))
                    if u == 1:
                        pe.wait_ge(k_passed.sem, j * 2 + 3)
                    for t in range(CH):
                        if t % 2 == 0:
                            pe.wait_ge(p_taken.sem, p_taken.at(k * 2 + t // 2))
                        for a in range(2):
                            mm = pe.matmul(o_ps[:, t * P:(t + 1) * P], kn[:, u, t + a], pt[:, u, t, a],
                                           start=a == 0, stop=a == 1)
                    mm.then_inc(o_sum.sem, 1)

                def outputs(k, u, j):
                    pe.wait_ge(o_taken.sem, o_taken.at(k))
                    for t in range(CH):
                        mm = pe.matmul(y_ps[:, t * D:(t + 1) * D], ot[:, u, t * P:(t + 1) * P], wo[:],
                                       start=True, stop=True)
                    mm.then_inc(y_sum.sem, 1)

                lagged(pe, (1, scores), (2, sum_values), (0, turn), (2, outputs), (0, project))


def top_gates(pr, ne, top, total, bias=None, fill=None):
    nc, d = pr.nc, pr.d
    with ExitStack() as ctx:
        lg, prob, left, eq, key, gate, order = (pr.sb(ctx, n, [P, NT, ne]) for n in
                                                ("lg", "prob", "left", "eq", "key", "gate", "order"))
        m, s, r = (pr.sb(ctx, n, [P, NT]) for n in ("m", "s", "r"))
        brow = pr.sb(ctx, "bias_row", [P, ne])
        orow = pr.sb(ctx, "order_row", [P, ne])
        loaded = pr.sem(ctx, "loaded")
        shifted = pr.sem(ctx, "shifted")
        exped = pr.sem(ctx, "exped")
        dv = pr.sem(ctx, "dv_steps")
        with nc.Block() as block:
            @block.sync
            def _(sp):
                sp.dma_start(orow[:], d["order"][:, 0:ne]).then_inc(loaded, 16)
                if bias:
                    sp.dma_start(brow[:], d[bias].broadcast_to([P, ne])).then_inc(loaded, 16)

            @block.scalar
            def _(act):
                act.wait_ge(shifted, 1)
                nc.scalar.activation(prob[:], lg[:], ACT.Exp).then_inc(exped, 1)

            @block.vector
            def _(v):
                c = Chain(v, dv)
                v.wait_ge(loaded, 32 if bias else 16)
                if bias:
                    c.link(v.tensor_tensor(lg[:], pr.logits[:, :, 0:ne], brow[:].unsqueeze(1).broadcast_to([P, NT, ne]),
                                           ALU.add))
                else:
                    c.link(v.tensor_copy(lg[:], pr.logits[:, :, 0:ne]))
                c.link(v.memset(pr.gates[:], 1.0))
                c.link(v.tensor_copy(order[:], orow[:].unsqueeze(1).broadcast_to([P, NT, ne])))
                c.link(v.reduce_max(m[:], lg[:], AX))
                v.tensor_tensor(lg[:], lg[:], bc(m[:], ne), ALU.subtract).then_inc(shifted, 1)
                v.wait_ge(exped, 1)
                c.link(v.reduce_sum(s[:], prob[:], AX))
                c.link(v.reciprocal(r[:], s[:]))
                c.link(v.tensor_tensor(prob[:], prob[:], bc(r[:], ne), ALU.mult))
                c.link(v.tensor_copy(left[:], prob[:]))
                c.link(v.memset(gate[:], 0.0))
                for i in range(top):
                    c.link(v.reduce_max(m[:], left[:], AX))
                    c.link(v.tensor_tensor(eq[:], left[:], bc(m[:], ne), ALU.is_ge))
                    c.link(v.tensor_tensor(key[:], eq[:], order[:], ALU.mult))
                    c.link(v.reduce_max(m[:], key[:], AX))
                    c.link(v.tensor_tensor(eq[:], key[:], bc(m[:], ne), ALU.is_equal))
                    c.link(v.tensor_tensor(gate[:], gate[:], eq[:], ALU.add))
                    c.link(v.scalar_tensor_tensor(out=left[:], in0=eq[:], scalar=-2.0, in1=left[:], op0=ALU.mult,
                                                  op1=ALU.add))
                c.link(v.tensor_tensor(gate[:], gate[:], prob[:], ALU.mult))
                if total:
                    c.link(v.reduce_sum(s[:], gate[:], AX))
                    c.link(v.tensor_scalar(s[:], s[:], 1e-20, None, ALU.add))
                    c.link(v.reciprocal(r[:], s[:]))
                    c.link(v.tensor_tensor(gate[:], gate[:], bc(r[:], ne), ALU.mult))
                c.link(v.tensor_copy(pr.gates[:, :, 0:ne], gate[:]))


def l2_attention(pr):
    nc, d = pr.nc, pr.d
    SCALE = float(D) ** -0.5
    NH = 2
    CB = N // CW
    with ExitStack() as ctx:
        wqk = pr.sb(ctx, "wqk", [P, 2, 3, D])
        wv = pr.sb(ctx, "wv", [P, D])
        wo = pr.sb(ctx, "wo", [P, NH, D])
        wroute = pr.sb(ctx, "wroute", [P, 16])
        mask = pr.sb(ctx, "causal_mask", [P, P], BF16)
        cos = pr.sb(ctx, "cos", [P, N])
        sin = pr.sb(ctx, "sin", [P, N])
        xnc = pr.sb(ctx, "xnc", [P, CB, CH, D])
        chunk = pr.sb(ctx, "chunk", [P, CB, CW])
        qk = pr.sb(ctx, "qk_turned", [P, 3, N])
        part1 = pr.sb(ctx, "part1", [P, 2, CW])
        part2 = pr.sb(ctx, "part2", [P, 2, CW])
        vn = pr.sb(ctx, "v_by_token", [P, TPB, D])
        mx = pr.sb(ctx, "mx", [P, 2, 1])
        nmx = pr.sb(ctx, "minus_mx", [P, 2, 1])
        sums = pr.sb(ctx, "sums", [P, 2 * TPB, 1])
        rec = pr.sb(ctx, "rec", [P, 2 * TPB, 1])
        prob = pr.sb(ctx, "prob", [P, 2, N])
        pt = pr.sb(ctx, "prob_turned", [P, 2, TPB, NH, P])
        ot = pr.sb(ctx, "out_turned", [P, 2, NH * P])
        loaded = pr.sem(ctx, "weights_loaded")
        names = "xn_sub xn_ready chunk_kept rotated1 rotated2 rope_done v_taken maxed minus_ready p_taken " \
                "rec_ready y_added"
        (xn_sub, xn_ready, chunk_kept, rotated1, rotated2, rope_done, v_taken, maxed, minus_ready, p_taken,
         rec_ready, y_added) = (pr.sem(ctx, n) for n in names.split())
        names = "turned chunk_ready qk_sum v_sum r_sum r_taken scored exped p_turned o_sum o_taken y_sum batch_done"
        (turned, chunk_ready, qk_sum, v_sum, r_sum, r_taken, scored, exped, p_turned, o_sum, o_taken, y_sum,
         batch_done) = (pr.sem(ctx, n) for n in names.split())
        turn_ps = pr.ps[:, 6]
        UNITS = [(t, h) for t in range(TPB) for h in range(NH)]
        GROUPS = [(t, h, g) for t, h in UNITS for g in range(0, t + 1, CH)]
        NG = len(GROUPS)

        def batches(eng, body):
            with eng.Fori(0, B) as b:
                body(b)

        def s_ps(i):
            return pr.ps[:, 2 * (i % 2):2 * (i % 2) + 2].rearrange("p a k -> p (a k)")

        with nc.Block() as block:
            @block.sync
            def _(sp):
                for dst, src in ((wqk, "l2_wqk"), (wv, "l2_wv"), (wo, "l2_wo"), (wroute, "l2_gate"),
                                 (mask, "mask_causal"), (cos, "l2_cos"), (sin, "l2_sin")):
                    sp.dma_start(dst[:], d[src]).then_inc(loaded, 16)

            @block.gpsimd
            def _(pool):
                pool.wait_ge(loaded, 7 * 16)

                def batch(b):
                    for u in range(CB):
                        hold(pool, pr.gate_p, chunk_ready, b * CB + u + 1)
                        pool.tensor_copy(pr.xt[:, ds(b * N + u * CW, CW)], chunk[:, u]).then_inc(chunk_kept, 1)
                        for i in range(3):
                            if u == 0 and i == 0:
                                hold(pool, pr.gate_p, batch_done, b + 1)
                            hold(pool, pr.gate_p, rotated2, b * 6 + u * 3 + i + 1)
                            pool.tensor_tensor(qk[:, i, u * CW:(u + 1) * CW], part1[:, (u * 3 + i) % 2],
                                               part2[:, (u * 3 + i) % 2],
                                               ALU.add).then_inc(rope_done, 1)

                batches(pool, batch)

            @block.vector
            def _(v):
                v.wait_ge(loaded, 7 * 16)
                v.sem_inc(y_added, 1)

                def batch(b):
                    for u in range(CB):
                        v.wait_ge(batch_done, b + 1)
                        k = b * CB + u
                        v.tensor_tensor(xnc[:, u], pr.X[:, ds(k * CH, CH), :], bc(pr.mean[:, ds(k * CH, CH)], D),
                                        ALU.subtract).then_inc(xn_sub, 1)
                        v.wait_ge(xn_sub, k + 1)
                        v.tensor_tensor(xnc[:, u], xnc[:, u], bc(pr.rstd[:, ds(k * CH, CH)], D),
                                        ALU.mult).then_inc(xn_ready, 1)
                    for u in range(CB):
                        for i in range(3):
                            n = b * 6 + u * 3 + i
                            m = u * 3 + i
                            cols = slice(u * CW, (u + 1) * CW)
                            v.wait_ge(qk_sum, n + 1)
                            if m >= 2:
                                v.wait_ge(rope_done, n - 1)
                            v.tensor_tensor(part1[:, m % 2], pr.ps[:, 2 * (m % 2)], cos[:, cols],
                                            ALU.mult).then_inc(rotated1, 1)
                            v.tensor_tensor(part2[:, m % 2], pr.ps[:, 2 * (m % 2) + 1], sin[:, cols],
                                            ALU.mult).then_inc(rotated2, 1)
                        v.wait_ge(v_sum, b * CB + u + 1)
                        v.tensor_copy(vn[:, u * CH:(u + 1) * CH], pr.ps[:, 4 + u].rearrange("p (t d) -> p t d", d=D))\
                            .then_inc(v_taken, 1)

                    def highest(i):
                        t, h = UNITS[i]
                        v.wait_ge(scored, b * 16 + i + 1)
                        v.reduce_max(mx[:, h], s_ps(i)[:, 0:(t + 1) * P], AX).then_inc(maxed, 1)
                        v.wait_ge(maxed, b * 16 + i + 1)
                        v.tensor_scalar(nmx[:, h], mx[:, h], -SCALE, None, ALU.mult).then_inc(minus_ready, 1)

                    def turn(i):
                        t, h = UNITS[i]
                        for g, (gt, gh, k0) in enumerate(GROUPS):
                            if (gt, gh) == (t, h):
                                n = min(CH, t + 1 - k0)
                                v.wait_ge(p_turned, b * NG + g + 1)
                                v.tensor_copy(pt[:, t % 2, k0:k0 + n, h],
                                              pr.ps[:, 4 + g % 2, 0:n * P].rearrange("p (k q) -> p k q", q=P))\
                                    .then_inc(p_taken, 1)

                    def finish(t):
                        v.wait_ge(exped, b * 16 + 2 * t + 2)
                        v.reciprocal(rec[:, 2 * t:2 * t + 2], sums[:, 2 * t:2 * t + 2]).then_inc(rec_ready, 1)
                        v.wait_ge(rec_ready, b * TPB + t + 1)
                        v.wait_ge(y_sum, b * TPB + t + 1)
                        for h in range(NH):
                            x = one(pr.X, b * TPB + t)
                            v.scalar_tensor_tensor(out=x, in0=pr.ps[:, 7, h * D:(h + 1) * D],
                                                   scalar=rec[:, 2 * t + h], in1=x, op0=ALU.mult, op1=ALU.add)\
                                .then_inc(y_added, 1)
                            hold(v, pr.gate_v, y_added, b * 2 * TPB + 2 * t + h + 2)

                    highest(0)
                    highest(1)
                    for t in range(TPB):
                        turn(2 * t)
                        if t + 1 < TPB:
                            highest(2 * t + 2)
                        turn(2 * t + 1)
                        if t + 1 < TPB:
                            highest(2 * t + 3)
                        if t:
                            finish(t - 1)
                    finish(TPB - 1)

                batches(v, batch)

            @block.scalar
            def _(act):
                nc.scalar.preload_act_table(ACT.Exp)

                def batch(b):
                    for u in range(CB):
                        k = b * CB + u
                        act.wait_ge(batch_done, b + 1)
                        act.wait_ge(turned, k + 1)
                        nc.scalar.activation(chunk[:, u], turn_ps, ACT.Copy).then_inc(chunk_ready, 1)
                        hold(act, pr.gate_a, r_sum, k + 1)
                        nc.scalar.activation(pr.logits[:, ds(k * CH, CH), :],
                                             pr.ps[:, 7, 0:CH * 16].rearrange("p (t c) -> p t c", c=16),
                                             ACT.Copy).then_inc(r_taken, 1)

                    def exps(i):
                        t, h = UNITS[i]
                        act.wait_ge(minus_ready, b * 16 + i + 1)
                        if t:
                            act.wait_ge(p_turned, b * NG + len([1 for gt, gh, _ in GROUPS if (gt, gh) <= (t - 1, h)]))
                        nc.scalar.activation(prob[:, h, 0:(t + 1) * P], s_ps(i)[:, 0:(t + 1) * P], ACT.Exp,
                                             bias=nmx[:, h], scale=SCALE, accum_out=sums[:, i]).then_inc(exped, 1)

                    exps(0)
                    exps(1)
                    for t in range(TPB):
                        if t + 1 < TPB:
                            exps(2 * t + 2)
                            exps(2 * t + 3)
                        act.wait_ge(o_sum, b * TPB + t + 1)
                        if t >= 2:
                            act.wait_ge(y_sum, b * TPB + t - 1)
                        nc.scalar.activation(ot[:, t % 2], pr.ps[:, 6, 0:NH * P], ACT.Copy).then_inc(o_taken, 1)

                batches(act, batch)

            @block.tensor
            def _(pe):
                pe.wait_ge(loaded, 7 * 16)
                pe.sem_inc(batch_done, 1)

                def batch(b):
                    pe.wait_ge(y_added, b * 2 * TPB + 1)
                    for u in range(CB):
                        k = b * CB + u
                        pe.wait_ge(xn_ready, k + 1)
                        if u:
                            pe.wait_ge(chunk_ready, k)
                        for t in range(CH):
                            mm = pe.transpose(turn_ps[:, t * P:(t + 1) * P], xnc[:, u, t], pr.idf[:])
                        mm.then_inc(turned, 1)
                        pe.wait_ge(chunk_ready, k + 1)
                        for i in range(3):
                            m = u * 3 + i
                            if m >= 2:
                                pe.wait_ge(rotated2, b * 6 + m - 1)
                            pe.matmul(pr.ps[:, 2 * (m % 2)], wqk[:, 0, i], chunk[:, u], start=True, stop=True)
                            pe.matmul(pr.ps[:, 2 * (m % 2) + 1], wqk[:, 1, i], chunk[:, u], start=True, stop=True)\
                                .then_inc(qk_sum, 1)
                        for t in range(CH):
                            mm = pe.matmul(pr.ps[:, 4 + u, t * D:(t + 1) * D], chunk[:, u, t * P:(t + 1) * P], wv[:],
                                           start=True, stop=True)
                        mm.then_inc(v_sum, 1)
                        if u:
                            pe.wait_ge(r_taken, k)
                        for t in range(CH):
                            mm = pe.matmul(pr.ps[:, 7, t * 16:(t + 1) * 16], chunk[:, u, t * P:(t + 1) * P], wroute[:],
                                           start=True, stop=True)
                        mm.then_inc(r_sum, 1)

                    def score(i):
                        t, h = UNITS[i]
                        if i >= 2:
                            pe.wait_ge(exped, b * 16 + i - 1)
                        s = s_ps(i)
                        for k0 in range(0, t + 1, CH):
                            n = min(CH, t + 1 - k0)
                            last = k0 + n == t + 1
                            mm = pe.matmul(s[:, k0 * P:(k0 + n) * P], qk[:, h, t * P:(t + 1) * P],
                                           qk[:, 2, k0 * P:(k0 + n) * P], start=True, stop=not last)
                            if last:
                                mm = pe.matmul(s[:, t * P:(t + 1) * P], pr.idb[:], mask[:], start=False, stop=True)
                        mm.then_inc(scored, 1)

                    def turn(i):
                        t, h = UNITS[i]
                        pe.wait_ge(exped, b * 16 + i + 1)
                        for g, (gt, gh, k0) in enumerate(GROUPS):
                            if (gt, gh) == (t, h):
                                if g >= 2:
                                    pe.wait_ge(p_taken, b * NG + g - 1)
                                for a in range(min(CH, t + 1 - k0)):
                                    mm = pe.transpose(pr.ps[:, 4 + g % 2, a * P:(a + 1) * P],
                                                      prob[:, h, (k0 + a) * P:(k0 + a + 1) * P], pr.idf[:])
                                mm.then_inc(p_turned, 1)

                    def sum_values(t):
                        pe.wait_ge(p_taken, b * NG + len([1 for g in GROUPS if g[0] <= t]))
                        if t:
                            pe.wait_ge(o_taken, b * TPB + t)
                        for k in range(t + 1):
                            mm = pe.matmul(pr.ps[:, 6, 0:NH * P], vn[:, k], pt[:, t % 2, k].rearrange("p h q -> p (h q)"),
                                           start=k == 0, stop=k == t)
                        mm.then_inc(o_sum, 1)

                    def project(t):
                        pe.wait_ge(o_taken, b * TPB + t + 1)
                        pe.wait_ge(y_added, b * 2 * TPB + 2 * t + 1)
                        for h in range(NH):
                            mm = pe.matmul(pr.ps[:, 7, h * D:(h + 1) * D], ot[:, t % 2, h * P:(h + 1) * P], wo[:, h],
                                           start=True, stop=True)
                        mm.then_inc(y_sum, 1)

                    pe.wait_ge(rotated2, b * 6 + 6)
                    pe.wait_ge(v_taken, b * CB + CB)
                    pe.wait_ge(r_taken, b * CB + CB)
                    pe.wait_ge(rope_done, b * 6 + 3)
                    score(0)
                    score(1)
                    for t in range(TPB):
                        turn(2 * t)
                        if t + 1 == CH:
                            pe.wait_ge(rope_done, b * 6 + 6)
                        if t + 1 < TPB:
                            score(2 * t + 2)
                        turn(2 * t + 1)
                        if t + 1 < TPB:
                            score(2 * t + 3)
                        if t:
                            project(t - 1)
                        sum_values(t)
                    project(TPB - 1)
                    pe.wait_ge(chunk_kept, b * CB + CB)
                    pe.sem_inc(batch_done, 1)

                batches(pe, batch)


def l3_inner_statistics(pr):
    nc = pr.nc
    with ExitStack() as ctx:
        stats = pr.sb(ctx, "stats", [P, CH, 6])
        mv = pr.sb(ctx, "mv", [P, CH, 2])
        var = pr.sb(ctx, "var", [P, NT])
        std = pr.sb(ctx, "std", [P, NT])
        eps = pr.sb(ctx, "eps", [P, 1])
        dv = pr.sem(ctx, "dv_steps")
        x1_ready = pr.ev(ctx, "x1_ready")
        var_done = pr.sem(ctx, "var_done")
        std_done = pr.sem(ctx, "std_done")
        with nc.Block() as block:
            @block.gpsimd
            def _(pool):
                with pool.Fori(0, NC) as k:
                    hold(pool, pr.gate_p, x1_ready.sem, x1_ready.at(k))
                    pool.tensor_tensor(pr.X[:, ds(k * CH, CH), :], pr.X[:, ds(k * CH, CH), :],
                                       pr.x1[:, ds(k * CH, CH), :], ALU.add)

            @block.vector
            def _(v):
                v.memset(eps[:], 1e-5).then_inc(var_done, 1)
                per = 2 * CH + 3
                with v.Fori(0, NC) as k:
                    c = Chain(v, dv)
                    c.base = k * per
                    x1 = pr.x1[:, ds(k * CH, CH), :]
                    c.link(v.tensor_tensor(x1, pr.X[:, ds(k * CH, CH), :], bc(pr.mean[:, ds(k * CH, CH)], D),
                                           ALU.subtract))
                    v.tensor_tensor(x1, x1, bc(pr.rstd[:, ds(k * CH, CH)], D), ALU.mult).then_inc(x1_ready.sem, 1)
                    v.wait_ge(x1_ready.sem, x1_ready.at(k))
                    v.sem_inc(pr.gate_v, 1)
                    for t in range(CH):
                        c.step(v.bn_stats(stats[:, t, :], one(pr.x1, k * CH + t)))
                    c.wait()
                    v.sem_inc(pr.gate_v, 1)
                    for t in range(CH):
                        c.step(v.bn_aggr(mv[:, t, :], stats[:, t, :]))
                    c.wait()
                    v.sem_inc(pr.gate_v, 1)
                    c.step(v.tensor_copy(pr.mean2[:, ds(k * CH, CH)], mv[:, :, 0]))
                    c.step(v.tensor_copy(var[:, ds(k * CH, CH)], mv[:, :, 1]))
                v.wait_ge(dv, NC * per)
                v.sem_inc(var_done, 1)
                v.wait_ge(std_done, 1)
                v.reciprocal(pr.rstd2[:], std[:])

            @block.scalar
            def _(act):
                act.wait_ge(var_done, 2)
                nc.scalar.activation(std[:], var[:], ACT.Sqrt, bias=eps[:]).then_inc(std_done, 1)


def l3_project(pr):
    nc, d = pr.nc, pr.d
    SC = D + H
    SCALE = float(E) ** -0.5
    with ExitStack() as ctx:
        wqk = pr.sb(ctx, "wqk", [P, 4, D])
        bqk = pr.sb(ctx, "bqk", [P, 4])
        wva = pr.sb(ctx, "wva", [P, D])
        bva = pr.sb(ctx, "bva", [P, D])
        wkv = pr.sb(ctx, "wkv", [P, 2 * D])
        bkv = pr.sb(ctx, "bkv", [P, 2 * D])
        wb = pr.sb(ctx, "wb", [P, D])
        wbs = pr.sb(ctx, "wbs", [P, D])
        wbias = pr.sb(ctx, "wbias", [1, D])
        ones = pr.sb(ctx, "ones", [1, P])
        g1 = pr.sb(ctx, "g1", [P, 1])
        b1 = pr.sb(ctx, "b1", [P, 1])
        own = pr.sb(ctx, "own_head", [P, SC])
        xnc = pr.sb(ctx, "xnc", [P, 2, CH, D])
        x2c = pr.sb(ctx, "x2c", [P, 2, CH, D])
        chunk1 = pr.sb(ctx, "chunk1", [P, 2, CW])
        chunk2 = pr.sb(ctx, "chunk2", [P, 2, CW])
        low = pr.sb(ctx, "low", [P, 2, CW])
        f32 = pr.sb(ctx, "rows32", [P, 4, CW])
        parts = pr.sb(ctx, "parts", [P, 2, 4, 3, CW], BF16)
        rest = pr.sb(ctx, "rest", [P, 3, CW])
        kv32 = pr.sb(ctx, "kv32", [P, CH, 2 * D])
        klow = pr.sb(ctx, "klow", [P, CH, D])
        kf = pr.sb(ctx, "k_features", [P, CH, D])
        vaug = pr.sb(ctx, "v_aug", [P, CH, SC])
        states = pr.sb(ctx, "states", [P, CH + 1, SC])
        outer = pr.sb(ctx, "outer", [P, CH, SC])
        st_den = pr.sb(ctx, "state_denominators", [H, 2, CW])
        yc = pr.sb(ctx, "y_clipped", [P, 2, CH, D])
        loaded = pr.sem(ctx, "loaded")
        dv = pr.sem(ctx, "dv_steps")
        state_steps = pr.sem(ctx, "state_steps")
        pl = pr.sem(ctx, "pool_steps")
        ready = pr.sem(ctx, "set_up")
        S = lambda n, p=0: pr.ev(ctx, n, p)
        xn_ready, x2_sub, x2_ready = S("xn_ready"), S("x2_sub"), S("x2_ready")
        turned1, turned2 = S("turned1", 2), S("turned2", 2)
        c1_ready, c2_ready = S("c1_ready"), S("c2_ready", 1)
        row_sum, split = S("row_sum"), S("split", 4)
        rows_w, rows_l = S("windowed_rows_ready", 2), S("linear_rows_ready")
        taken_l = S("linear_rows_taken", 2)
        low_ready, low_exp = S("low_ready"), S("low_exp")
        va_sum, va_taken = S("va_sum", 2), S("va_taken", 1)
        kv_sum, kv_taken = S("kv_sum"), S("kv_taken", 1)
        klow_ready, klow_exp = S("klow_ready"), S("klow_exp")
        tok_ready = S("tok_ready")
        y_sum, y_taken, y_added = S("y_sum", 2), S("y_taken", 1), S("y_added", 2)
        outer_sum, outer_taken = S("outer_sum"), S("outer_taken", 1)
        states_ready = S("states_ready")
        out_sum, out_taken = S("out_sum", 1), S("out_taken", 1)
        stored = [pr.sem(ctx, f"stored{u}") for u in range(2)]
        den_stored = [pr.sem(ctx, f"den_stored{u}") for u in range(2)]
        NW = 12
        ORDER = (2, 3, 0, 1)

        with nc.Block() as block:
            @block.sync
            def _(sp):
                for dst, src in ((wqk, "l3_wqk"), (bqk, "l3_bqk"), (wva, "l3_wva"), (wkv, "l3_wkv"), (wb, "l3_wb"),
                                 (wbias, "l3_wbias"), (g1, "l3_g1"), (b1, "l3_b1"), (own, "own_head")):
                    sp.dma_start(dst[:], d[src]).then_inc(loaded, 16)
                sp.dma_start(bva[:], d["l3_bva"].broadcast_to([P, D])).then_inc(loaded, 16)
                sp.dma_start(bkv[:], d["l3_bkv"].broadcast_to([P, 2 * D])).then_inc(loaded, 16)
                sp.dma_start(wbs[:], d["l3_wbs"].broadcast_to([P, D])).then_inc(loaded, 16)
                for u in range(2):
                    sp.sem_inc(stored[u], 128)
                    sp.sem_inc(den_stored[u], 16)

                def store(k, u, j):
                    cols = slice(u * CW, (u + 1) * CW)
                    drams = (pr.q_dram, pr.k_dram, pr.q2_dram, pr.k2_dram)
                    for n, i in enumerate(ORDER):
                        t = drams[i]
                        sp.wait_ge(split.sem, split.at(k * 4 + n))
                        (store_k_parts if i % 2 else store_q_parts)(sp, t, j, cols, parts[:, u, i], stored[u])
                    sp.wait_ge(out_taken.sem, out_taken.at(k))
                    sp.dma_start(pr.state_den_dram[ds(j * H, H), u * CW:(u + 1) * CW], st_den[:, u])\
                        .then_inc(den_stored[u], 16)

                two_a_turn(sp, store)
                for u in range(2):
                    sp.wait_ge(stored[u], 128 + 128 * (NC // 2))
                    sp.wait_ge(den_stored[u], 16 + 16 * (NC // 2))

            @block.gpsimd
            def _(pool):
                for e, n in ((split, 4), (y_added, 2)):
                    pool.sem_inc(e.sem, n)

                def part(k, u, j):
                    c = Chain(pool, pl)
                    c.base = k * 10
                    for i in ORDER:
                        e = rows_w if i < 2 else rows_l
                        left = rest[:, max(i - 1, 0)]
                        hold(pool, pr.gate_p, e.sem, e.at(k * 2 + i % 2))
                        if i < 2:
                            c.link(pool.tensor_tensor(left, f32[:, i], parts[:, u, i, 0], ALU.subtract))
                            pool.sem_inc(pr.gate_p, 1)
                        c.link(pool.tensor_copy(parts[:, u, i, 1], left))
                        pool.sem_inc(pr.gate_p, 1)
                        c.link(pool.tensor_tensor(parts[:, u, i, 2], left, parts[:, u, i, 1], ALU.subtract))
                        pool.sem_inc(split.sem, 1)
                    hold(pool, pr.gate_p, y_taken.sem, y_taken.at(k))
                    pool.tensor_tensor(pr.X[:, ds(k * CH, CH), :], pr.X[:, ds(k * CH, CH), :], yc[:, u],
                                       ALU.add).then_inc(y_added.sem, 1)

                two_a_turn(pool, part)

            @block.vector
            def _(v):
                v.wait_ge(loaded, 16 * NW)
                c = Chain(v, ready)
                c.link(v.memset(ones[:], 1.0))
                c.link(v.memset(pr.va[:, :, :, E:E + 1], 1.0))
                c.link(v.memset(pr.vs[:, :, :, E:E + 1], 1.0))
                c.link(v.memset(vaug[:], 1.0))
                c.link(v.tensor_scalar(wb[:], wb[:], 0.0, 2.0, ALU.is_ge, ALU.mult))
                c.link(v.tensor_scalar(wb[:], wb[:], -1.0, None, ALU.add))
                c.link(v.tensor_tensor(wb[:], wb[:], wbs[:], ALU.mult))
                for e in (va_taken, kv_taken, y_taken, outer_taken):
                    v.sem_inc(e.sem, 1)
                v.sem_inc(taken_l.sem, 2)
                def norm(k, u, j):
                    v.wait_ge(turned2.sem, turned2.at(k - 2))
                    v.sem_inc(pr.gate_v, 1)
                    v.tensor_copy(xnc[:, u], pr.x1[:, ds(k * CH, CH), :]).then_inc(xn_ready.sem, 1)
                    v.tensor_tensor(x2c[:, u], pr.x1[:, ds(k * CH, CH), :], bc(pr.mean2[:, ds(k * CH, CH)], D),
                                    ALU.subtract).then_inc(x2_sub.sem, 1)
                    v.wait_ge(x2_sub.sem, x2_sub.at(k))
                    v.tensor_tensor(x2c[:, u], x2c[:, u], bc(pr.rstd2[:, ds(k * CH, CH)], D),
                                    ALU.mult).then_inc(x2_ready.sem, 1)

                def features(k, u, j):
                    c = Chain(v, dv)
                    c.base = k * 18
                    v.wait_ge(kv_sum.sem, kv_sum.at(k))
                    for half in range(2):
                        c.step(v.tensor_tensor(kv32[:, 2 * half:2 * half + 2],
                                               pr.ps[:, 4 + half].rearrange("p (t c) -> p t c", t=2),
                                               bkv[:].unsqueeze(1).broadcast_to([P, 2, 2 * D]), ALU.add))
                    c.wait()
                    v.sem_inc(kv_taken.sem, 1)
                    v.tensor_scalar(klow[:], kv32[:, :, 0:D], 0.0, None, ALU.min).then_inc(klow_ready.sem, 1)
                    c.step(v.tensor_copy(vaug[:, :, 0:D], kv32[:, :, D:]))
                    c.step(v.tensor_copy(pr.vs[:, ds(j * H, H), u * CH:(u + 1) * CH, 0:E],
                                         kv32[:, :, D:].rearrange("p t (h e) -> p h t e", e=E)))
                    c.step(v.tensor_scalar(kf[:], kv32[:, :, 0:D], 0.0, 1e-4, ALU.max, ALU.add))
                    c.wait()
                    v.wait_ge(klow_exp.sem, klow_exp.at(k))
                    c.link(v.tensor_tensor(kf[:], kf[:], klow[:], ALU.add))
                    v.sem_inc(tok_ready.sem, 1)
                    v.wait_ge(out_sum.sem, out_sum.at(k - 1))
                    for i in (2, 3):
                        n = k * 4 + i - 2
                        ps = pr.ps[:, 1 + i % 2]
                        v.wait_ge(split.sem, split.at(n - 4))
                        v.wait_ge(row_sum.sem, row_sum.at(n))
                        v.tensor_scalar(low[:, i - 2], ps, bqk[:, i:i + 1], 0.0, ALU.add, ALU.min)\
                            .then_inc(low_ready.sem, 1)
                        c.link(v.tensor_scalar(f32[:, i], ps, bqk[:, i:i + 1], 0.0, ALU.add, ALU.max))
                        v.sem_inc(taken_l.sem, 1)
                    for i in (2, 3):
                        v.wait_ge(low_exp.sem, low_exp.at(k * 2 + i - 2))
                        c.link(v.scalar_tensor_tensor(out=f32[:, i], in0=f32[:, i], scalar=SCALE if i == 2 else 1.0,
                                                      in1=low[:, i - 2], op0=ALU.mult, op1=ALU.add))
                        c.link(v.tensor_scalar(f32[:, i], f32[:, i], 1e-4, None, ALU.add))
                        v.wait_ge(stored[u], j * 128 + 128)
                        c.link(v.tensor_copy(parts[:, u, i, 0], f32[:, i]))
                        c.link(v.tensor_tensor(rest[:, i - 1], f32[:, i], parts[:, u, i, 0], ALU.subtract))
                        v.sem_inc(rows_l.sem, 1)
                    v.wait_ge(va_sum.sem, va_sum.at(k))
                    c.link(v.tensor_tensor(pr.va[:, ds(j * H, H), u * CH:(u + 1) * CH, 0:E],
                                           pr.ps[:, 3].rearrange("p (t h e) -> p h t e", t=CH, e=E),
                                           bva[:].rearrange("p (h e) -> p h e", e=E).unsqueeze(2)
                                           .broadcast_to([P, H, CH, E]), ALU.add))
                    v.sem_inc(va_taken.sem, 1)
                    v.wait_ge(y_added.sem, y_added.at(k - 2))
                    v.wait_ge(y_sum.sem, y_sum.at(k))
                    c.link(v.tensor_scalar(yc[:, u], pr.ps[:, 6].rearrange("p (t d) -> p t d", d=D), 100.0, -100.0,
                                           ALU.min, ALU.max))
                    v.sem_inc(y_taken.sem, 1)
                    assert c.n == 18

                def add_states(k, u, j):
                    c = Chain(v, state_steps)
                    c.base = k * 7
                    v.wait_ge(out_sum.sem, out_sum.at(k - 1))
                    if u == 0:
                        c.step(v.memset(states[:, 0], 0.0))
                    else:
                        c.step(v.tensor_copy(states[:, 0], states[:, CH]))
                    v.wait_ge(outer_sum.sem, outer_sum.at(k))
                    for half in range(2):
                        c.step(v.tensor_tensor(outer[:, 2 * half:2 * half + 2],
                                               pr.ps[:, 4 + half, 0:2 * SC].rearrange("p (t c) -> p t c", t=2),
                                               own[:].unsqueeze(1).broadcast_to([P, 2, SC]), ALU.mult))
                    c.wait()
                    v.sem_inc(outer_taken.sem, 1)
                    for t in range(CH):
                        c.link(v.tensor_tensor(states[:, t + 1], states[:, t], outer[:, t], ALU.add))
                    v.sem_inc(states_ready.sem, 1)
                    assert c.n == 7

                lagged(v, (3, add_states), (0, norm), (2, features))

            @block.scalar
            def _(act):
                nc.scalar.preload_act_table(ACT.Exp)
                act.sem_inc(c2_ready.sem, 1)
                act.sem_inc(out_taken.sem, 1)
                act.sem_inc(rows_w.sem, 2)
                act.wait_ge(loaded, 16 * NW)

                def keep(k, u, j):
                    act.wait_ge(va_sum.sem, va_sum.at(k - 2))
                    act.wait_ge(turned1.sem, turned1.at(k))
                    nc.scalar.activation(chunk1[:, u], pr.ps[:, 0], ACT.Copy).then_inc(c1_ready.sem, 1)
                    act.wait_ge(turned2.sem, turned2.at(k))
                    nc.scalar.activation(chunk2[:, u], pr.ps[:, 0], ACT.Identity, scale=g1[:], bias=b1[:])\
                        .then_inc(c2_ready.sem, 1)

                def rows(k, u, j):
                    act.wait_ge(klow_ready.sem, klow_ready.at(k))
                    nc.scalar.activation(klow[:], klow[:], ACT.Exp).then_inc(klow_exp.sem, 1)
                    for i in range(2):
                        act.wait_ge(low_ready.sem, low_ready.at(k * 2 + i))
                        nc.scalar.activation(low[:, i], low[:, i], ACT.Exp, scale=SCALE if i == 0 else 1.0)\
                            .then_inc(low_exp.sem, 1)
                    act.wait_ge(stored[u], j * 128 + 128)
                    act.sem_inc(pr.gate_a, 1)
                    for i in range(2):
                        act.wait_ge(split.sem, split.at(k * 4 + i - 2))
                        act.wait_ge(row_sum.sem, row_sum.at(k * 4 + i + 2))
                        nc.scalar.activation(f32[:, i], pr.ps[:, 1 + i % 2], ACT.Identity, bias=bqk[:, i:i + 1])
                        nc.scalar.activation(parts[:, u, i, 0], pr.ps[:, 1 + i % 2], ACT.Identity,
                                             bias=bqk[:, i:i + 1]).then_inc(rows_w.sem, 1)

                def keep_state_sums(k, u, j):
                    act.wait_ge(den_stored[u], j * 16 + 16)
                    act.wait_ge(out_sum.sem, out_sum.at(k))
                    act.sem_inc(pr.gate_a, 1)
                    nc.scalar.activation(pr.st[:, ds(k * CW, CW)], pr.ps[:, 7], ACT.Copy)
                    nc.scalar.activation(st_den[:, u], pr.ps[0:H, 3], ACT.Copy).then_inc(out_taken.sem, 1)

                lagged(act, (1, keep), (3, keep_state_sums), (2, rows))

            @block.tensor
            def _(pe):
                pe.wait_ge(loaded, 16 * NW)
                pe.wait_ge(ready, 7)
                for e in (turned1, turned2, va_sum, y_sum):
                    pe.sem_inc(e.sem, 2)
                pe.sem_inc(out_sum.sem, 1)

                def turn(k, u, j):
                    pe.wait_ge(c2_ready.sem, c2_ready.at(k - 1))
                    pe.wait_ge(xn_ready.sem, xn_ready.at(k))
                    for t in range(CH):
                        mm = pe.transpose(pr.ps[:, 0, t * P:(t + 1) * P], xnc[:, u, t], pr.idf[:])
                    mm.then_inc(turned1.sem, 1)
                    pe.wait_ge(c1_ready.sem, c1_ready.at(k))
                    pe.wait_ge(x2_ready.sem, x2_ready.at(k))
                    for t in range(CH):
                        mm = pe.transpose(pr.ps[:, 0, t * P:(t + 1) * P], x2c[:, u, t], pr.idf[:])
                    mm.then_inc(turned2.sem, 1)

                def rows(k, u, n, e, before):
                    pe.wait_ge(e.sem, e.at(before))
                    pe.matmul(pr.ps[:, 1 + n % 2], wqk[:, ORDER[n]], chunk2[:, u], start=True, stop=True)\
                        .then_inc(row_sum.sem, 1)

                def linear(k, u, j):
                    pe.wait_ge(c2_ready.sem, c2_ready.at(k))
                    rows(k, u, 0, rows_w, k * 2 - 2)
                    rows(k, u, 1, rows_w, k * 2 - 1)
                    pe.wait_ge(outer_taken.sem, outer_taken.at(k - 1))
                    for t in range(CH):
                        mm = pe.matmul(pr.ps[:, 4 + t // 2, (t % 2) * 2 * D:(t % 2 + 1) * 2 * D],
                                       chunk2[:, u, t * P:(t + 1) * P], wkv[:], start=True, stop=True)
                    mm.then_inc(kv_sum.sem, 1)

                def others(k, u, j):
                    pe.wait_ge(y_taken.sem, y_taken.at(k - 1))
                    for t in range(CH):
                        s = pr.ps[:, 6, t * D:(t + 1) * D]
                        pe.matmul(s, chunk1[:, u, t * P:(t + 1) * P], wb[:], start=True, stop=False)
                        mm = pe.matmul(s, ones[:], wbias[:], start=False, stop=True)
                    mm.then_inc(y_sum.sem, 1)
                    rows(k, u, 2, taken_l, k * 2)
                    rows(k, u, 3, taken_l, k * 2 + 1)
                    pe.wait_ge(va_taken.sem, va_taken.at(k - 1))
                    pe.wait_ge(out_taken.sem, out_taken.at(k - 1))
                    for t in range(CH):
                        mm = pe.matmul(pr.ps[:, 3, t * D:(t + 1) * D], chunk2[:, u, t * P:(t + 1) * P], wva[:],
                                       start=True, stop=True)
                    mm.then_inc(va_sum.sem, 1)

                def tile_products(k, u, j):
                    pe.wait_ge(tok_ready.sem, tok_ready.at(k))
                    for t in range(CH):
                        mm = pe.matmul(pr.ps[:, 4 + t // 2, (t % 2) * SC:(t % 2 + 1) * SC], kf[:, t], vaug[:, t],
                                       start=True, stop=True)
                    mm.then_inc(outer_sum.sem, 1)

                def state_sums(k, u, j):
                    pe.wait_ge(rows_l.sem, rows_l.at(k * 2 + 1))
                    pe.wait_ge(va_taken.sem, va_taken.at(k))
                    pe.wait_ge(states_ready.sem, states_ready.at(k))
                    pe.wait_ge(out_taken.sem, out_taken.at(k - 1))
                    for t in range(CH):
                        tile = slice(t * P, (t + 1) * P)
                        pe.matmul(pr.ps[:, 7, tile], states[:, t, 0:D], f32[:, 2, tile], start=True, stop=True)
                        mm = pe.matmul(pr.ps[0:H, 3, tile], states[:, t, D:SC], f32[:, 2, tile], start=True, stop=True)
                    mm.then_inc(out_sum.sem, 1)

                lagged(pe, (3, tile_products), (1, turn), (2, linear), (3, state_sums), (2, others))


def l3_attention(pr):
    nc, d = pr.nc, pr.d
    SCALE = float(E) ** -0.5
    KM = MROW + 2
    VA = E + 1
    VR = 2 * VA
    NG, NW = 5, 4
    NT2, NL = 2, 6
    SETS = 4
    DEPTH = 4
    with ExitStack() as ctx:
        qst, kst, qlin, klin = ([pr.sb(ctx, f"{n}{u}", [P, N], BF16) for u in range(SETS)]
                                for n in ("q_stack", "k_stack", "q_linear", "k_linear"))
        mask_q = pr.sb(ctx, "mask_by_query", [P, 2 * P], BF16)
        mask_k = pr.sb(ctx, "mask_by_key", [P, 2 * P], BF16)
        tri = pr.sb(ctx, "keys_up_to_query", [P, P])
        mx = pr.sb(ctx, "maxima", [P, TPB])
        mrow = [pr.sb(ctx, f"max_rows{u}", [P, TPB, KM], BF16) for u in range(2)]
        p_win = pr.sb(ctx, "p_windowed", [P, TPB, 2 * P])
        a_lin = pr.sb(ctx, "a_linear", [P, TPB, P])
        v_win = [pr.sb(ctx, f"v_windowed{u}", [P, TPB, VR]) for u in range(2)]
        v_lin = [pr.sb(ctx, f"v_linear{u}", [P, TPB, VR]) for u in range(2)]
        sums = [pr.sb(ctx, f"sums{u}", [VR, N]) for u in range(2)]
        zeroed = pr.sem(ctx, "zeroed")
        consts = pr.sem(ctx, "consts")
        stacks = [pr.sem(ctx, f"stacks{u}") for u in range(SETS)]
        first_part = pr.sem(ctx, "first_part")
        scored = pr.ev(ctx, "scored_by_query")
        reduced = pr.ev(ctx, "reduced", 2)
        rows_ready = pr.ev(ctx, "max_rows_ready")
        keyed = pr.ev(ctx, "scored_by_key", SETS * NL)
        exped = pr.ev(ctx, "exped", NW)
        masked = pr.ev(ctx, "masked")
        v_ready = pr.ev(ctx, "values_ready")
        summed = pr.ev(ctx, "values_summed", 2)
        taken = pr.ev(ctx, "sums_taken", 1)
        stored = [pr.sem(ctx, f"sums_stored{u}") for u in range(2)]

        def key_ps(n, g):
            return pr.ps[:, 2 + (n * NL + g) % DEPTH]

        with nc.Block() as block:
            @block.sync
            def _(sp):
                sp.dma_start(mask_q[:], d["mask_win_q"]).then_inc(consts, 16)
                sp.dma_start(mask_k[:], d["mask_win_k"]).then_inc(consts, 16)
                sp.dma_start(tri[:], d["tri"]).then_inc(consts, 16)
                sp.wait_ge(zeroed, 4 * SETS + 2 * 3 + SETS)

                def load(n, u):
                    sp.wait_ge(keyed.sem, keyed.at((n - SETS) * NL + NL - 1))
                    for q, k, qd, kd in ((qst, kst, pr.q_dram, pr.k_dram), (qlin, klin, pr.q2_dram, pr.k2_dram)):
                        load_stacks(sp, n, q[u], k[u], qd, kd, stacks[u])

                def store(n, u):
                    sp.wait_ge(taken.sem, taken.at(n))
                    sp.dma_start(pr.sums_dram[ds(n), 0:VR].rearrange("o r t -> (o r) t"), sums[u][:])\
                        .then_inc(stored[u], 16)

                for u in range(2):
                    sp.sem_inc(stored[u], 16)
                for n in range(SETS):
                    load(n, n)
                with sp.Fori(0, HEADS // SETS - 1) as j:
                    for u in range(SETS):
                        store(j * SETS + u, u % 2)
                        load(j * SETS + u + SETS, u)
                for u in range(SETS):
                    store(HEADS - SETS + u, u % 2)
                for u in range(2):
                    sp.wait_ge(stored[u], 16 + 16 * HEADS // 2)

            @block.gpsimd
            def _(pool):
                for u in range(SETS):
                    for t in (qst[u], kst[u], qlin[u], klin[u]):
                        pool.memset(t[:], 0.0).then_inc(zeroed, 1)
                for u in range(2):
                    for t in (mrow[u], v_win[u], v_lin[u]):
                        pool.memset(t[:], 0.0).then_inc(zeroed, 1)
                pool.wait_ge(zeroed, 4 * SETS + 2 * 3)
                for u in range(SETS):
                    pool.memset(kst[u][MROW:KM], 1.0).then_inc(zeroed, 1)
                pool.wait_ge(zeroed, 4 * SETS + 2 * 3 + SETS)

                def values(n, u):
                    hold(pool, pr.gate_p, summed.sem, summed.at(n - 2))
                    pool.tensor_copy(v_win[u][:, :, 0:VA], one(pr.va, n))
                    pool.tensor_copy(v_lin[u][:, :, VA:VR], one(pr.vs, n)).then_inc(v_ready.sem, 1)

                with pool.Fori(0, HEADS // 2) as j:
                    for u in range(2):
                        values(j * 2 + u, u)

            @block.vector
            def _(v):
                v.sem_inc(reduced.sem, 2)
                v.wait_ge(zeroed, 4 * SETS + 2 * 3 + SETS)
                v.wait_ge(consts, 48)

                def largest(n, u, g):
                    v.wait_ge(scored.sem, scored.at(n * NG + g))
                    ps = pr.ps[:, (u * NG + g) % 2]
                    if g == 0:
                        v.reduce_max(mx[:, 0:1], ps[:, P:2 * P], AX)
                        v.reduce_max(mx[:, 1:2], ps[:, 2 * P:4 * P], AX).then_inc(reduced.sem, 1)
                    else:
                        v.reduce_max(mx[:, 2 * g:2 * g + 2], ps.rearrange("p (t k) -> p t k", t=2), AX)\
                            .then_inc(reduced.sem, 1)

                def max_rows(n, u):
                    v.wait_ge(reduced.sem, reduced.at(n * NG + NW - 1))
                    v.tensor_scalar(mrow[u % 2][:, :, MROW], mx[:], -1.0, None, ALU.mult).then_inc(first_part, 1)
                    v.wait_ge(first_part, n + 1)
                    v.scalar_tensor_tensor(out=mrow[u % 2][:, :, MROW + 1], in0=mx[:], scalar=-1.0,
                                           in1=mrow[u % 2][:, :, MROW], op0=ALU.mult, op1=ALU.subtract)\
                        .then_inc(rows_ready.sem, 1)
                    v.wait_ge(scored.sem, scored.at(n * NG + NW))
                    v.tensor_copy(qst[u][MROW:KM], pr.ps[MROW:KM, (u * NG + NW) % 2].bitcast(BF16))\
                        .then_inc(reduced.sem, 1)

                def triangle(n, u, g):
                    v.wait_ge(keyed.sem, keyed.at(n * NL + g))
                    v.tensor_tensor(a_lin[:, CH * g:CH * (g + 1)], key_ps(u, g).rearrange("p (t q) -> p t q", q=P),
                                    tri[:].unsqueeze(1).broadcast_to([P, CH, P]), ALU.mult).then_inc(masked.sem, 1)

                def step(n, u):
                    for g in range(NW):
                        if g < NT2:
                            triangle(n, u, g)
                        largest(n + 1, (u + 1) % SETS, g)
                    max_rows(n + 1, (u + 1) % SETS)

                for g in range(NW):
                    largest(0, 0, g)
                max_rows(0, 0)
                with v.Fori(0, HEADS // SETS - 1) as j:
                    for u in range(SETS):
                        step(j * SETS + u, u)
                for u in range(SETS - 1):
                    step(HEADS - SETS + u, u)
                for g in range(NT2):
                    triangle(HEADS - 1, SETS - 1, g)

            @block.scalar
            def _(act):
                nc.scalar.preload_act_table(ACT.Exp)
                act.sem_inc(exped.sem, NW)
                act.sem_inc(taken.sem, 1)

                def exps(n, u):
                    for g in range(NW):
                        act.wait_ge(keyed.sem, keyed.at(n * NL + NT2 + g))
                        ps = key_ps(u, NT2 + g)
                        if g < NW - 1:
                            ins = nc.scalar.activation(p_win[:, 2 * g:2 * g + 2].rearrange("p t q -> p (t q)"), ps,
                                                       ACT.Exp, scale=SCALE)
                        else:
                            flat = p_win[:, 2 * g:2 * g + 2].rearrange("p t q -> p (t q)")
                            ins = nc.scalar.activation(flat[:, 0:3 * P], ps[:, 0:3 * P], ACT.Exp, scale=SCALE)
                        ins.then_inc(exped.sem, 1)

                def take(n, u, j):
                    act.wait_ge(stored[u], j * 16 + 16)
                    act.wait_ge(summed.sem, summed.at(n))
                    nc.scalar.activation(sums[u][:].rearrange("p (a t) -> p a t", a=2), pr.ps[0:VR, 6:8],
                                         ACT.Copy).then_inc(taken.sem, 1)

                exps(0, 0)
                with act.Fori(0, HEADS // 2 - 1) as j:
                    for u in range(2):
                        take(j * 2 + u, u, j)
                        exps(j * 2 + u + 1, 1 - u)
                take(HEADS - 2, 0, HEADS // 2 - 1)
                exps(HEADS - 1, 1)
                take(HEADS - 1, 1, HEADS // 2 - 1)

            @block.tensor
            def _(pe):
                pe.sem_inc(keyed.sem, SETS * NL)
                pe.sem_inc(summed.sem, 2)
                pe.wait_ge(consts, 48)
                pe.wait_ge(zeroed, 4 * SETS + 2 * 3 + SETS)

                def query_group(n, u, g, turn):
                    pe.wait_ge(reduced.sem, reduced.at(n * NG + g - 2))
                    ps = pr.ps[:, (u * NG + g) % 2]
                    if g == 0:
                        pe.wait_ge(stacks[u], (turn + 1) * 4 * 16)
                    if g < NW:
                        for i in range(2):
                            t = 2 * g + i
                            lo = P if t == 0 else 0
                            s = ps[:, i * 2 * P + lo:(i + 1) * 2 * P]
                            pe.matmul(s, qst[u][0:KQ, t * P:(t + 1) * P], kst[u][0:KQ, (t - 1) * P + lo:(t + 1) * P],
                                      start=True, stop=False)
                            mm = pe.matmul(s, pr.idb[:], mask_q[:, lo:], start=False, stop=True)
                    else:
                        pe.wait_ge(rows_ready.sem, rows_ready.at(n))
                        for t in range(TPB):
                            mm = pe.transpose(ps[0:KM, t * 64:(t + 1) * 64].bitcast(BF16), mrow[u % 2][:, t], pr.idb[:])
                    mm.then_inc(scored.sem, 1)

                def key_group(n, u, g):
                    b = g - DEPTH
                    if b < 0:
                        b, m = b + NL, n - 1
                    else:
                        m = n
                    e, i = (masked, m * NT2 + b) if b < NT2 else (exped, m * NW + b - NT2)
                    pe.wait_ge(e.sem, e.at(i))
                    if g == NT2:
                        pe.wait_ge(reduced.sem, reduced.at(n * NG + NW))
                    ps = key_ps(u, g)
                    if g >= NT2:
                        for i in range(2):
                            t = 2 * (g - NT2) + i
                            w = P if t == TPB - 1 else 2 * P
                            s = ps[:, i * 2 * P:i * 2 * P + w]
                            pe.matmul(s, kst[u][0:KM, t * P:(t + 1) * P], qst[u][0:KM, t * P:t * P + w],
                                      start=True, stop=False)
                            mm = pe.matmul(s, pr.idb[:], mask_k[:, 0:w], start=False, stop=True)
                    else:
                        for i in range(CH):
                            t = CH * g + i
                            mm = pe.matmul(ps[:, i * P:(i + 1) * P], klin[u][0:KQ, t * P:(t + 1) * P],
                                           qlin[u][0:KQ, t * P:(t + 1) * P], start=True, stop=True)
                    mm.then_inc(keyed.sem, 1)

                def values(n, u, g):
                    if g < NT2:
                        if g == 0:
                            pe.wait_ge(v_ready.sem, v_ready.at(n))
                            pe.wait_ge(taken.sem, taken.at(n - 1))
                        pe.wait_ge(masked.sem, masked.at(n * NT2 + g))
                        for i in range(CH):
                            pe.matmul(pr.ps[0:VR, 6 + g, i * P:(i + 1) * P], v_lin[u % 2][:, CH * g + i],
                                      a_lin[:, CH * g + i], start=i == 0, stop=False)
                    else:
                        w = g - NT2
                        pe.wait_ge(exped.sem, exped.at(n * NW + w))
                        for t in (2 * w, 2 * w + 1):
                            for i in range(2):
                                lo, hi = max(t, i * CH), min(t + 2, (i + 1) * CH)
                                if lo < hi:
                                    mm = pe.matmul(pr.ps[0:VR, 6 + i, (lo - i * CH) * P:(hi - i * CH) * P],
                                                   v_win[u % 2][:, t], p_win[:, t, (lo - t) * P:(hi - t) * P],
                                                   start=False, stop=t == CH * (i + 1) - 1)
                        if g == NL - 1:
                            mm.then_inc(summed.sem, 1)

                def step(n, u, turn):
                    more = not isinstance(n, int) or n + 1 < HEADS
                    for g in range(NL + 2):
                        if g < NL:
                            key_group(n, u, g)
                        if g < NG and more:
                            query_group(n + 1, (u + 1) % SETS, g, turn)
                        if g >= 2:
                            values(n, u, g - 2)

                for g in range(NG):
                    query_group(0, 0, g, 0)
                with pe.Fori(0, HEADS // SETS - 1) as j:
                    for u in range(SETS):
                        step(j * SETS + u, u, j + (u + 1) // SETS)
                for u in range(SETS):
                    step(HEADS - SETS + u, u, HEADS // SETS - 1)


def l3_mix(pr):
    nc, d = pr.nc, pr.d
    VA = E + 1
    with ExitStack() as ctx:
        wp, ws, wo = (pr.sb(ctx, n, [P, D]) for n in ("wp", "ws", "wo"))
        b12 = pr.sb(ctx, "b12", [P, 2])
        bsum = pr.sb(ctx, "bsum", [P, 1])
        bo = pr.sb(ctx, "bo", [1, D])
        ones = pr.sb(ctx, "ones", [1, P])
        num = pr.sb(ctx, "value_sums", [P, 2, 2, CW])
        inv = pr.sb(ctx, "inverses", [H, 2, 2, CW])
        spread = pr.sb(ctx, "spread_heads", [H, P])
        den = pr.sb(ctx, "denominators", [P, 2, CW])
        st_den = pr.sb(ctx, "state_denominators", [P, CW])
        mt = pr.sb(ctx, "mixed_turned", [P, 2, CW])
        m32 = pr.sb(ctx, "mixed", [P, 2, CH, D])
        loaded = pr.sem(ctx, "loaded")
        set_up = pr.sem(ctx, "set_up")
        read = [pr.sem(ctx, f"sums_read{u}") for u in range(2)]
        den_read = pr.sem(ctx, "denominators_read")
        inverted = pr.sem(ctx, "inverted")
        inv_stored = pr.sem(ctx, "inverses_stored")
        steps = pr.sem(ctx, "steps")
        spread_out = pr.ev(ctx, "inverses_spread")
        divided = pr.ev(ctx, "divided", 1)
        inner = pr.ev(ctx, "inner", 2)
        inner_taken = pr.ev(ctx, "inner_taken", 1)
        summed = pr.ev(ctx, "summed", 2)
        added = pr.ev(ctx, "added", 2)
        kept = pr.ev(ctx, "kept", 2)
        with nc.Block() as block:
            @block.sync
            def _(sp):
                for half in range(2):
                    rows, cols = slice(half * HEADS, (half + 1) * HEADS), slice(half * CW, (half + 1) * CW)
                    for w in range(2):
                        sp.dma_start(den[rows, w], pr.sums_dram[:, w * VA + E, cols]).then_inc(den_read, 16)
                    sp.dma_start(st_den[rows], pr.state_den_dram[:, cols]).then_inc(den_read, 16)
                for dst, src in ((wp, "l3_wp"), (ws, "l3_wos"), (wo, "l3_wo"), (b12, "l3_b12"), (bo, "l3_bo"),
                                 (spread, "spread")):
                    sp.dma_start(dst[:], d[src]).then_inc(loaded, 16)
                sp.wait_ge(inverted, 3)
                for half in range(2):
                    sp.dma_start(pr.inverse_dram[:, 0:2, half * CW:(half + 1) * CW],
                                 den[half * HEADS:(half + 1) * HEADS]).then_inc(inv_stored, 16)
                sp.wait_ge(inv_stored, 32)

                def part(k, u, j):
                    sp.wait_ge(inner.sem, inner.at(k - 2))
                    heads = pr.sums_dram[ds(j * H, H), :, u * CW:(u + 1) * CW]
                    sp.dma_start(inv[:, u], pr.inverse_dram[ds(j * H, H), 0:2, u * CW:(u + 1) * CW])\
                        .then_inc(read[u], 16)
                    for w in range(2):
                        sp.dma_start(num[:, u, w], heads[:, w * VA:w * VA + E]).then_inc(read[u], 16)

                two_a_turn(sp, part)

            @block.gpsimd
            def _(pool):
                pool.sem_inc(kept.sem, 2)

                def part(k, u, j):
                    hold(pool, pr.gate_p, added.sem, added.at(k))
                    pool.tensor_tensor(pr.x1[:, ds(k * CH, CH), :], pr.x1[:, ds(k * CH, CH), :], m32[:, u],
                                       ALU.add).then_inc(kept.sem, 1)

                two_a_turn(pool, part)

            @block.vector
            def _(v):
                v.wait_ge(loaded, 96)
                v.memset(ones[:], 1.0).then_inc(set_up, 1)
                v.tensor_tensor(bsum[:], b12[:, 0:1], b12[:, 1:2], ALU.add).then_inc(set_up, 1)
                v.sem_inc(added.sem, 2)
                v.sem_inc(divided.sem, 1)
                v.wait_ge(den_read, 96)
                v.tensor_tensor(den[:, 1], den[:, 1], st_den[:], ALU.add).then_inc(inverted, 1)
                v.wait_ge(inverted, 1)
                v.tensor_scalar(den[:, 1], den[:, 1], 1e-6, None, ALU.add).then_inc(inverted, 1)
                v.wait_ge(inverted, 2)
                v.reciprocal(den[:], den[:]).then_inc(inverted, 1)

                def divide(k, u, j):
                    v.wait_ge(spread_out.sem, spread_out.at(k))
                    v.sem_inc(pr.gate_v, 1)
                    v.tensor_tensor(num[:, u, 1], num[:, u, 1], pr.st[:, ds(k * CW, CW)], ALU.add).then_inc(steps, 1)
                    v.wait_ge(steps, k + 1)
                    v.tensor_tensor(num[:, u], num[:, u], pr.ps[:, 0:2], ALU.mult).then_inc(divided.sem, 1)

                def add(k, u, j):
                    v.wait_ge(kept.sem, kept.at(k - 2))
                    v.wait_ge(summed.sem, summed.at(k))
                    v.tensor_copy(m32[:, u], pr.ps[:, 4 + u].rearrange("p (t d) -> p t d", d=D))
                    v.tensor_tensor(pr.X[:, ds(k * CH, CH), :], pr.X[:, ds(k * CH, CH), :],
                                    pr.ps[:, 4 + u].rearrange("p (t d) -> p t d", d=D), ALU.add).then_inc(added.sem, 1)

                staggered(v, divide, None, add)

            @block.scalar
            def _(act):
                act.sem_inc(inner_taken.sem, 1)
                act.wait_ge(set_up, 2)

                def part(k, u, j):
                    act.wait_ge(summed.sem, summed.at(k - 2))
                    act.wait_ge(inner.sem, inner.at(k))
                    nc.scalar.activation(mt[:, u], pr.ps[:, 2], ACT.Identity, bias=bsum[:]).then_inc(inner_taken.sem, 1)

                two_a_turn(act, part)

            @block.tensor
            def _(pe):
                pe.sem_inc(summed.sem, 2)
                pe.sem_inc(inner.sem, 2)
                pe.wait_ge(loaded, 96)
                pe.wait_ge(set_up, 2)

                def spread_inverses(k, u, j):
                    pe.wait_ge(divided.sem, divided.at(k - 1))
                    hold(pe, pr.gate_e, read[u], j * 48 + 48)
                    for w in range(2):
                        mm = pe.matmul(pr.ps[:, w], spread[:], inv[:, u, w], start=True, stop=True)
                    mm.then_inc(spread_out.sem, 1)

                def inner_products(k, u, j):
                    pe.wait_ge(divided.sem, divided.at(k))
                    pe.wait_ge(inner_taken.sem, inner_taken.at(k - 1))
                    pe.matmul(pr.ps[:, 2], wp[:], num[:, u, 0], start=True, stop=False)
                    pe.matmul(pr.ps[:, 2], ws[:], num[:, u, 1], start=False, stop=True).then_inc(inner.sem, 1)

                def products(k, u, j):
                    pe.wait_ge(inner_taken.sem, inner_taken.at(k))
                    pe.wait_ge(added.sem, added.at(k - 2))
                    for t in range(CH):
                        s = pr.ps[:, 4 + u, t * D:(t + 1) * D]
                        pe.matmul(s, mt[:, u, t * P:(t + 1) * P], wo[:], start=True, stop=False)
                        mm = pe.matmul(s, ones[:], bo[:], start=False, stop=True)
                    mm.then_inc(summed.sem, 1)

                staggered(pe, spread_inverses, inner_products, products)


def l3_mlp(pr):
    nc, d = pr.nc, pr.d
    U = 4
    with ExitStack() as ctx:
        w1 = pr.sb(ctx, "w1", [P, U * D])
        b1 = pr.sb(ctx, "b1", [P, U])
        w2 = pr.sb(ctx, "w2", [P, U, D])
        b2 = pr.sb(ctx, "b2", [1, D])
        ones = pr.sb(ctx, "ones", [1, P])
        gm = pr.sb(ctx, "gm", [P, 2])
        xnc = pr.sb(ctx, "xnc", [P, 2, CH, D])
        chunk = pr.sb(ctx, "chunk", [P, 2, CW])
        hid = pr.sb(ctx, "hidden", [P, 2, U, CW])
        loaded = pr.sem(ctx, "loaded")
        set_up = pr.sem(ctx, "set_up")
        xn_sub = pr.ev(ctx, "xn_sub")
        xn_ready = pr.ev(ctx, "xn_ready")
        turned = pr.ev(ctx, "turned", 2)
        chunk_ready = pr.ev(ctx, "chunk_ready", 1)
        h_sum = pr.ev(ctx, "h_sum", 2 * U)
        h_ready = pr.ev(ctx, "h_ready", 4)
        y_sum = pr.ev(ctx, "y_sum", 2)
        added = pr.ev(ctx, "added", 2)
        with nc.Block() as block:
            @block.sync
            def _(sp):
                for dst, src in ((w1, "l3_w1"), (b1, "l3_b1m"), (w2, "l3_w2"), (b2, "l3_b2m"), (gm, "l3_gm")):
                    sp.dma_start(dst[:], d[src]).then_inc(loaded, 16)

            @block.vector
            def _(v):
                v.memset(ones[:], 1.0).then_inc(set_up, 1)
                v.sem_inc(added.sem, 2)

                def norm(k, u, j):
                    v.wait_ge(turned.sem, turned.at(k - 2))
                    v.tensor_tensor(xnc[:, u], pr.x1[:, ds(k * CH, CH), :], bc(pr.mean[:, ds(k * CH, CH)], D),
                                    ALU.subtract).then_inc(xn_sub.sem, 1)
                    v.wait_ge(xn_sub.sem, xn_sub.at(k))
                    v.tensor_tensor(xnc[:, u], xnc[:, u], bc(pr.rstd[:, ds(k * CH, CH)], D),
                                    ALU.mult).then_inc(xn_ready.sem, 1)

                def add(k, u, j):
                    v.wait_ge(y_sum.sem, y_sum.at(k))
                    v.tensor_tensor(pr.X[:, ds(k * CH, CH), :], pr.X[:, ds(k * CH, CH), :],
                                    pr.ps[:, 6 + u].rearrange("p (t d) -> p t d", d=D), ALU.add).then_inc(added.sem, 1)

                staggered(v, norm, None, add)

            @block.scalar
            def _(act):
                nc.scalar.preload_act_table(ACT.Gelu)
                act.sem_inc(chunk_ready.sem, 1)
                act.sem_inc(h_ready.sem, 4)
                act.wait_ge(loaded, 80)

                def keep(k, u, j):
                    act.wait_ge(h_sum.sem, h_sum.at((k - 2) * U + U - 1))
                    act.wait_ge(turned.sem, turned.at(k))
                    nc.scalar.activation(chunk[:, u], pr.ps[:, 0], ACT.Identity, scale=gm[:, 0:1], bias=gm[:, 1:2])\
                        .then_inc(chunk_ready.sem, 1)

                def gelu(k, u, j):
                    act.wait_ge(y_sum.sem, y_sum.at(k - 2))
                    for i in range(U):
                        act.wait_ge(h_sum.sem, h_sum.at(k * U + i))
                        nc.scalar.activation(hid[:, u, i], pr.ps[:, 1 + i], ACT.Gelu, bias=b1[:, i:i + 1])\
                            .then_inc(h_ready.sem, 1)

                staggered(act, keep, gelu)

            @block.tensor
            def _(pe):
                pe.sem_inc(turned.sem, 2)
                pe.sem_inc(y_sum.sem, 2)
                pe.sem_inc(h_sum.sem, 2 * U)
                pe.wait_ge(loaded, 80)
                pe.wait_ge(set_up, 1)

                def turn(k, u, j):
                    pe.wait_ge(chunk_ready.sem, chunk_ready.at(k - 1))
                    pe.wait_ge(xn_ready.sem, xn_ready.at(k))
                    for t in range(CH):
                        mm = pe.transpose(pr.ps[:, 0, t * P:(t + 1) * P], xnc[:, u, t], pr.idf[:])
                    mm.then_inc(turned.sem, 1)

                def first_products(k, u, j):
                    pe.wait_ge(chunk_ready.sem, chunk_ready.at(k))
                    for i in range(U):
                        pe.wait_ge(h_ready.sem, h_ready.at(k * U + i - U))
                        pe.matmul(pr.ps[:, 1 + i], w1[:, i * D:(i + 1) * D], chunk[:, u], start=True, stop=True)\
                            .then_inc(h_sum.sem, 1)

                def second_products(k, u, j):
                    pe.wait_ge(added.sem, added.at(k - 2))
                    for t in range(CH):
                        s = pr.ps[:, 6 + u, t * D:(t + 1) * D]
                        for i in range(U):
                            if t == 0:
                                pe.wait_ge(h_ready.sem, h_ready.at(k * U + i))
                            pe.matmul(s, hid[:, u, i, t * P:(t + 1) * P], w2[:, i], start=i == 0, stop=False)
                        mm = pe.matmul(s, ones[:], b2[:], start=False, stop=True)
                    mm.then_inc(y_sum.sem, 1)

                staggered(pe, turn, first_products, second_products)


def program(nc, dram, out):
    pr = Prog(nc, dram, out)
    with ExitStack() as ctx:
        pr.X = pr.sb(ctx, "x", [P, NT, D])
        pr.xt = pr.sb(ctx, "xn_turned", [P, T])
        pr.mean = pr.sb(ctx, "mean", [P, NT])
        pr.rstd = pr.sb(ctx, "rstd", [P, NT])
        pr.inorm = pr.sb(ctx, "inverse_norm", [P, NT])
        pr.idf = pr.sb(ctx, "ident_f", [P, P])
        pr.idb = pr.sb(ctx, "ident_b", [P, P], BF16)
        pr.logits = pr.sb(ctx, "logits", [P, NT, 16])
        pr.gates = pr.sb(ctx, "gates", [P, NT, 17])
        pr.ps = ctx.enter_context(nc.psum_tensor("banks", [P, 8, 512], F32))
        pr.gate_v, pr.gate_p, pr.gate_a, pr.gate_e = (nc.alloc_semaphore("gate_" + e) for e in "vpae")
        pr.q_dram = nc.dram_tensor("q_parts", (B * P, 3, N), BF16).ap()
        pr.k_dram = nc.dram_tensor("k_parts", (HEADS, 3, E, N), BF16).ap()
        pr.q2_dram = nc.dram_tensor("q2_parts", (B * P, 3, N), BF16).ap()
        pr.k2_dram = nc.dram_tensor("k2_parts", (HEADS, 3, E, N), BF16).ap()
        pr.s_dram = nc.dram_tensor("selection_scores", (HEADS, N), F32).ap()
        pr.sums_dram = nc.dram_tensor("head_sums", (HEADS, 4 * (E + 1), N), F32).ap()
        pr.inverse_dram = nc.dram_tensor("inverse_denominators", (HEADS, 3, N), F32).ap()
        pr.state_den_dram = nc.dram_tensor("state_denominators", (HEADS, N), F32).ap()
        load_constants(pr)
        pr.end()
        statistics(pr, norm=True)
        pr.end()
        with ExitStack() as layer:
            pr.kvp = pr.sb(layer, "kv_parts", [P, HEADS, TPB, 6 * E], BF16)
            pr.va = pr.sb(layer, "values", [P, HEADS, TPB, E + 1])
            pr.slot = pr.sb(layer, "slots", [P, HEADS, TPB])
            pr.s0 = pr.sb(layer, "selection_scores", [HEADS, N])
            pr.s1 = pr.sb(layer, "scores_left", [HEADS, N])
            pr.best = pr.sb(layer, "best_scores", [HEADS, 8])
            l0_project(pr)
            pr.end()
            l0_gates(pr)
            pr.end()
            experts(pr, "m0", 8, 64, False, select=N // 4)
            pr.end()
            l0_places(pr)
            pr.end()
            l0_attention(pr)
            pr.end()
            out_project(pr, "wo0", "bo0")
            pr.end()
        statistics(pr)
        pr.end()
        l1_attention(pr)
        pr.end()
        top_gates(pr, 8, 1, False, "l1_bg")
        pr.end()
        experts(pr, "m1", 8, 128, False, 9)
        pr.end()
        statistics(pr)
        pr.end()
        l2_attention(pr)
        pr.end()
        top_gates(pr, 15, 3, True)
        pr.end()
        experts(pr, "m2", 17, 128, True)
        pr.end()
        statistics(pr)
        pr.end()
        with ExitStack() as layer:
            pr.x1 = pr.sb(layer, "x1", [P, NT, D])
            pr.mean2 = pr.sb(layer, "mean2", [P, NT])
            pr.rstd2 = pr.sb(layer, "rstd2", [P, NT])
            with ExitStack() as mixing:
                pr.va = pr.sb(mixing, "windowed_values", [P, HEADS, TPB, E + 1])
                pr.vs = pr.sb(mixing, "linear_values", [P, HEADS, TPB, E + 1])
                pr.st = pr.sb(mixing, "state_sums", [P, T])
                l3_inner_statistics(pr)
                pr.end()
                l3_project(pr)
                pr.end()
                l3_attention(pr)
                pr.end()
                l3_mix(pr)
                pr.end()
            statistics(pr, of=pr.x1)
            pr.end()
            l3_mlp(pr)
            pr.end()
        store_output(pr)


def kernel(**inputs):
    import ml_dtypes
    from concourse import bacc
    from concourse.bass_utils import run_bass_kernel_spmd

    g = {k: np.asarray(v) for k, v in inputs.items()}
    c = np.ascontiguousarray
    bf = ml_dtypes.bfloat16
    a = {}

    def heads_last(w):
        wk, wv = w
        lead = wk.shape[:-1]
        return c(np.stack([wk.reshape(*lead, H, E), wv.reshape(*lead, H, E)], -2).reshape(*lead, 2 * D))

    a["x"] = c(g["L0_attn_x"].reshape(NT, P, D).transpose(1, 0, 2).reshape(P, NT * D))
    a["ident_f"] = np.eye(P, dtype=np.float32)
    a["ident_b"] = np.eye(P, dtype=bf)
    a["wq"] = c(g["L0_attn_Wq"].T)
    a["wk"] = c(g["L0_attn_Wk"].T)
    a["wkv"] = heads_last((g["L0_attn_Wk"].T, g["L0_attn_Wv"].T))
    a["bkv"] = heads_last((g["L0_attn_bk"][None], g["L0_attn_bv"][None]))
    a["bq"] = c(g["L0_attn_bq"][:, None])
    a["bk"] = c(g["L0_attn_bk"][:, None])
    a["ws"] = c(g["L0_attn_Ws"].T)
    a["bs"] = c(g["L0_attn_bs"][:, None])
    a["cent"] = g["L0_ffn_centroids"]
    a["wroute"] = c(g["L0_ffn_w_route"].T)
    q, k = np.arange(P)[:, None], np.arange(P)[None]
    a["mask_band"] = np.concatenate([np.where(k < q, NEG, 0), 0.0 * (k + q), np.where(k > q, NEG, 0)], 1).astype(bf)
    a["places"] = c(np.broadcast_to(np.arange(N // 4, dtype=np.float32), (P, N // 4)))
    marks = np.zeros((3, 6, N), bf)
    for v in range(3):
        marks[v, v] = marks[v, 3 + v] = 1
    a["max_marks"] = marks
    a["spread"] = (np.arange(H)[:, None] == np.arange(P)[None] // E).astype(np.float32)
    a["wo0"] = c(g["L0_attn_Wo"].T)
    a["bo0"] = c(g["L0_attn_bo"][None])
    a["m0_w1"] = c(g["L0_ffn_w1"].reshape(4, 2, P, 64).transpose(2, 0, 1, 3).reshape(P, 4, P))
    a["m0_b1"] = c(g["L0_ffn_b1"].reshape(4, P).T[:, :, None])
    a["m0_w2"] = c(g["L0_ffn_w2"].reshape(4, P, D).transpose(1, 0, 2))
    a["m0_b2"] = g["L0_ffn_b2"]

    w = g["L1_attn_w_qkv"]
    a["l1_wq"], a["l1_wk"] = c(w[:, 0:D]), c(w[:, D:2 * D])
    a["l1_wo"] = g["L1_attn_w_out"]
    a["l1_wg"] = g["L1_ffn_Wg"]
    a["l1_bg"] = c(g["L1_ffn_bg"][None])
    a["mask_causal"] = np.where(k > q, NEG, 0.0).astype(bf)
    a["order"] = c(np.broadcast_to(np.arange(16, 0, -1, dtype=np.float32), (P, 16)))
    a["m1_w1"] = c(g["L1_ffn_W1"].transpose(1, 0, 2))
    a["m1_b1"] = c(g["L1_ffn_b1"].T[:, :, None])
    a["m1_w2"] = c(g["L1_ffn_W2"].transpose(1, 0, 2))
    a["m1_b2"] = np.concatenate([g["L1_ffn_b2"], g["L1_attn_b_out"][None]])

    wq = g["L2_attn_Wq"]
    three = np.stack([wq[0], wq[1], g["L2_attn_Wk"]])
    pairs = three.reshape(3, D // 2, 2, D)
    turned = np.stack([pairs[:, :, 1], pairs[:, :, 0]], 2).reshape(3, D, D)
    a["l2_wqk"] = c(np.stack([three, turned]).transpose(3, 0, 1, 2))
    a["l2_wv"] = c(g["L2_attn_Wv"].T)
    a["l2_wo"] = c(g["L2_attn_Wo"].T.reshape(2, D, D).transpose(1, 0, 2))
    a["l2_gate"] = c(np.concatenate([g["L2_ffn_gate_w"].T, np.zeros((D, 1), np.float32)], 1))
    theta = np.float32(10000.0) ** (np.float32(-2.0) * np.arange(0, D, 2, dtype=np.float32) / np.float32(D))
    angles = (np.arange(N, dtype=np.float32)[:, None] * theta.astype(np.float32)[None]).astype(np.float32)
    a["l2_cos"] = c(np.repeat(np.cos(angles), 2, axis=1).T.astype(np.float32))
    a["l2_sin"] = c(np.stack([-np.sin(angles), np.sin(angles)], 2).reshape(N, D).T.astype(np.float32))
    F, FS = P, 2 * P
    w1 = np.concatenate([g["L2_ffn_fc1_w"].reshape(15, 2, F, D),
                         g["L2_ffn_s_fc1_w"].reshape(2, 2, F, D).transpose(1, 0, 2, 3)])
    b1 = np.concatenate([g["L2_ffn_fc1_b"].reshape(15, 2, F), g["L2_ffn_s_fc1_b"].reshape(2, 2, F).transpose(1, 0, 2)])
    a["m2_w1"] = c(w1.transpose(3, 0, 1, 2).reshape(P, 17, 2 * P))
    a["m2_b1"] = c(b1.transpose(2, 0, 1))
    w2 = np.concatenate([g["L2_ffn_fc2_w"], g["L2_ffn_s_fc2_w"].reshape(D, 2, F).transpose(1, 0, 2)])
    a["m2_w2"] = c(w2.transpose(2, 0, 1))
    a["m2_b2"] = np.concatenate([g["L2_ffn_fc2_b"], g["L2_ffn_s_fc2_b"][None], np.zeros((1, D), np.float32)])
    a["m2_mult"] = c(np.concatenate([g["L2_ffn_geglu_mult"], g["L2_ffn_s_geglu_mult"].reshape(2, F)]).T)

    wa, ws = g["L3_attn_Wqkv_a"], g["L3_attn_Wqkv_s"]
    ba, bs = g["L3_attn_bqkv_a"], g["L3_attn_bqkv_s"]
    a["l3_wqk"] = c(np.stack([wa[:, :D], wa[:, D:2 * D], ws[:, :D], ws[:, D:2 * D]], 1))
    a["l3_bqk"] = c(np.stack([ba[:D], ba[D:2 * D], bs[:D], bs[D:2 * D]], 1))
    a["l3_wva"], a["l3_bva"] = c(wa[:, 2 * D:]), c(ba[None, 2 * D:])
    a["l3_wkv"], a["l3_bkv"] = c(ws[:, D:]), c(bs[None, D:])
    a["l3_wb"] = c(g["L3_ffn_weights"].T)
    a["l3_wbs"] = c(g["L3_ffn_scale"][None])
    a["l3_wbias"] = c(g["L3_ffn_bias"][None])
    a["l3_g1"], a["l3_b1"] = c(g["L3_attn_g1"][:, None]), c(g["L3_attn_b1"][:, None])
    a["own_head"] = (np.arange(P)[:, None] // E == np.concatenate([np.arange(P) // E, np.arange(H)])[None]).astype(np.float32)
    a["mask_win_q"] = np.concatenate([np.where(k <= q, NEG, 0.0), np.where(k > q, NEG, 0.0)], 1).astype(bf)
    a["mask_win_k"] = np.concatenate([np.where(k < q, NEG, 0.0), np.where(k >= q, NEG, 0.0)], 1).astype(bf)
    a["tri"] = (k >= q).astype(np.float32)
    a["l3_wp"], a["l3_wos"], a["l3_wo"] = g["L3_attn_Wp_a"], g["L3_attn_Wo_s"], g["L3_attn_Wo"]
    a["l3_b12"] = c(np.stack([g["L3_attn_bp_a"], g["L3_attn_bo_s"]], 1))
    a["l3_bo"] = c(g["L3_attn_bo"][None])
    a["l3_w1"] = g["L3_attn_W1"]
    a["l3_b1m"] = c(g["L3_attn_b1m"].reshape(4, D).T)
    a["l3_w2"] = c(g["L3_attn_W2"].reshape(4, D, D).transpose(1, 0, 2))
    a["l3_b2m"] = c(g["L3_attn_b2m"][None])
    a["l3_gm"] = c(np.stack([g["L3_attn_gm"], g["L3_attn_bm"]], 1))

    nc = bacc.Bacc("TRN2", target_bir_lowering=False, num_devices=1)
    dram, arrays = {}, {}
    for name, v in a.items():
        v = c(v)
        arrays["in_" + name] = v
        dram[name] = nc.dram_tensor("in_" + name, v.shape, mybir.dt.from_np(v.dtype), kind="ExternalInput").ap()
    out = nc.dram_tensor("out_0", (P, NT * D), F32, kind="ExternalOutput").ap()
    program(nc, dram, out)
    r = run_bass_kernel_spmd(nc, [arrays], core_ids=[0])
    o = r.results[0]["out_0"]
    return o.reshape(P, NT, D).transpose(1, 0, 2).reshape(B, N, D)
```
